# Optimizing a Trainium2 kernel written in Bass

```python
import numpy as np
import jax
import jax.numpy as jnp

def _softmax(x, axis=-1):
    return jax.nn.softmax(x, axis=axis)

def _gelu(x):
    return jax.nn.gelu(x, approximate=True)

def _silu(x):
    return jax.nn.silu(x)

def _sigmoid(x):
    return jax.nn.sigmoid(x)

def _layernorm(x, axis=-1, eps=1e-05):
    m = jnp.mean(x, axis=axis, keepdims=True)
    v = jnp.var(x, axis=axis, keepdims=True)
    return (x - m) / jnp.sqrt(v + eps)

def _scatter_add(tgt, idx, src, axis=0):
    return tgt.at[idx].add(src)

def _segment_sum(src, seg, n):
    return jax.ops.segment_sum(src, seg, n)
kernel_name = 'mk_flamingo_gated_d4_seqx_r8_2b45c0'

def setup_inputs(seed: int=0):
    np.random.seed(seed)
    _w = jnp.asarray

    def _rec_inputs():
        import jax
        import jax.numpy as jnp
        _rk = jax.random.key(seed)
        x = -0.0002928 + 1 * jax.random.normal(jax.random.fold_in(_rk, 1), (32, 64, 128), jnp.float32)
        _lenS = 64 - jax.random.randint(jax.random.fold_in(_rk, 7), (32,), 0, max(1, 64 // 4) + 1, jnp.int32)
        _lenS2 = 64 - jax.random.randint(jax.random.fold_in(_rk, 8), (32,), 0, max(1, 64 // 4) + 1, jnp.int32)
        _ctx_1024P = jax.random.normal(jax.random.fold_in(_rk, 11), (32, 16, 128), jnp.float32)
        _ctx_1024c = jax.random.dirichlet(jax.random.fold_in(_rk, 511), 0.3 * jnp.ones((16,), jnp.float32), (32, 64))
        _ctx_1024t = jnp.einsum('bsk,bkd->bsd', _ctx_1024c, _ctx_1024P)
        _ctx_1024t = _ctx_1024t * jax.lax.rsqrt(jnp.mean(jnp.square(_ctx_1024t)) + 1e-12) * 0.953939
        ctx_1024 = -0.000514642 + 1.00011 * (_ctx_1024t + 0.3 * jax.random.normal(jax.random.fold_in(_rk, 611), (32, 64, 128), jnp.float32))
        fside_BxS2_0 = jax.random.uniform(jax.random.fold_in(_rk, 13), (32, 64), jnp.float32, 0.0, 0.499917)
        itok_BxS2_0_7 = jax.random.randint(jax.random.fold_in(_rk, 15), (32, 64), 0, 8, jnp.int32)
        _validS = jnp.arange(64)[None, :] < _lenS[:, None]
        _validS2 = jnp.arange(64)[None, :] < _lenS2[:, None]
        _causal = jnp.tril(jnp.ones((64, 64), dtype=bool))
        mask_BxS2_fk1 = jnp.where(jnp.broadcast_to(_validS2[:, :], (32, 64)), 1.0, 0.0).astype(jnp.float32)
        mask_BxS2_bf0 = jnp.logical_not(jnp.ones((32, 64), dtype=bool))
        _g = jax.random.normal(jax.random.fold_in(_rk, 9001), (2, 4), jnp.float32)
        _g = jnp.sign(_g) * jnp.maximum(jnp.abs(_g), 1.0) + (_g == 0) * 1.0
        g_xattn = _g[0]
        g_ffn = _g[1]
        return (x, ctx_1024, fside_BxS2_0, itok_BxS2_0_7, mask_BxS2_fk1, mask_BxS2_bf0, g_xattn, g_ffn)
    x, ctx_1024, fside_BxS2_0, itok_BxS2_0_7, mask_BxS2_fk1, mask_BxS2_bf0, g_xattn, g_ffn = _rec_inputs()

    def _L0_xattn_setup():
        import jax, jax.numpy as jnp
        import numpy as np
        DIM = 128
        HEADS = 16
        DIM_HEAD = 64
        FF_MULT = 4
        CTX_DIM = 128
        INNER = HEADS * DIM_HEAD
        FF_INNER = DIM * FF_MULT
        FUSED = INNER + 2 * DIM_HEAD + 2 * FF_INNER
        SCALE = DIM_HEAD ** (-0.5)

        def layer_norm(x, gamma, eps=1e-05):
            mu = jnp.mean(x, axis=-1, keepdims=True)
            var = jnp.var(x, axis=-1, keepdims=True)
            return (x - mu) * jax.lax.rsqrt(var + eps) * gamma

        def swiglu(x):
            a, gate = jnp.split(x, 2, axis=-1)
            return jax.nn.silu(gate) * a

        def parallel_block(x, gamma, W_fused, W_attn_out, W_ff_out):
            B, N, D = x.shape
            h = layer_norm(x, gamma)
            fused = h @ W_fused
            q = fused[..., :INNER]
            k = fused[..., INNER:INNER + DIM_HEAD]
            v = fused[..., INNER + DIM_HEAD:INNER + 2 * DIM_HEAD]
            ff = fused[..., INNER + 2 * DIM_HEAD:]
            q = q.reshape(B, N, HEADS, DIM_HEAD).transpose(0, 2, 1, 3) * SCALE
            sim = jnp.einsum('bhid,bjd->bhij', q, k)
            causal = jnp.triu(jnp.ones((N, N), dtype=bool), k=1)
            neg = -jnp.finfo(sim.dtype).max
            sim = jnp.where(causal, neg, sim)
            sim = sim - jax.lax.stop_gradient(jnp.max(sim, axis=-1, keepdims=True))
            attn = jax.nn.softmax(sim, axis=-1)
            out = jnp.einsum('bhij,bjd->bhid', attn, v)
            out = out.transpose(0, 2, 1, 3).reshape(B, N, INNER)
            return out @ W_attn_out + swiglu(ff) @ W_ff_out

        def cross_attention(x, context, gamma, ctx_gamma, W_q, W_kv, W_out):
            B, N, D = x.shape
            xq = layer_norm(x, gamma)
            c = layer_norm(context, ctx_gamma)
            q = (xq @ W_q).reshape(B, N, HEADS, DIM_HEAD).transpose(0, 2, 1, 3) * SCALE
            kv = c @ W_kv
            k, v = (kv[..., :DIM_HEAD], kv[..., DIM_HEAD:])
            sim = jnp.einsum('bhid,bjd->bhij', q, k)
            attn = jax.nn.softmax(sim, axis=-1)
            out = jnp.einsum('bhij,bjd->bhid', attn, v)
            out = out.transpose(0, 2, 1, 3).reshape(B, N, INNER)
            return out @ W_out
        key = jax.random.key(seed)
        ks = jax.random.split(key, 12)
        w = lambda k, shape: jax.random.normal(k, shape, dtype=jnp.float32) * 0.02
        return {'x': jax.random.normal(ks[0], (4, 128, DIM), dtype=jnp.float32), 'context': jax.random.normal(ks[1], (4, 64, CTX_DIM), dtype=jnp.float32), 'ptb_gamma': jnp.ones((DIM,), dtype=jnp.float32), 'W_fused': w(ks[2], (DIM, FUSED)), 'W_attn_out': w(ks[3], (INNER, DIM)), 'W_ff_out': w(ks[4], (FF_INNER, DIM)), 'ca_gamma': jnp.ones((DIM,), dtype=jnp.float32), 'ca_ctx_gamma': jnp.ones((CTX_DIM,), dtype=jnp.float32), 'W_q': w(ks[5], (DIM, INNER)), 'W_kv': w(ks[6], (CTX_DIM, 2 * DIM_HEAD)), 'W_out': w(ks[7], (INNER, DIM))}
    _L0_xattn_all = _L0_xattn_setup()
    _L0_xattn_in = {k: v for k, v in _L0_xattn_all.items() if k in ('ptb_gamma', 'W_fused', 'W_attn_out', 'W_ff_out', 'ca_gamma', 'ca_ctx_gamma', 'W_q', 'W_kv', 'W_out')}
    del _L0_xattn_all

    def _L0_ffn_setup():
        import jax, jax.numpy as jnp
        import numpy as np
        H, KVH, HD, D = (8, 2, 128, 128)
        E, TOPK, FFN = (8, 2, 448)
        THETA, EPS = (1000000.0, 1e-05)
        NBITS, GS = (4, 128)
        QMAX = float(2 ** NBITS - 1)
        NEG = -1e+30

        def qgroup(w):
            shp = w.shape
            w2 = w.reshape(-1, GS)
            wmax = jnp.max(w2, -1, keepdims=True)
            wmin = jnp.min(w2, -1, keepdims=True)
            scales = jnp.clip(wmax - wmin, 1e-05, None) / QMAX
            base = jnp.clip(jnp.round(-wmin / scales), 0.0, QMAX)
            wq = (jnp.clip(jnp.round(w2 / scales) + base, 0.0, QMAX) - base) * scales
            return wq.reshape(shp)

        def rms(x, g):
            return x * jax.lax.rsqrt(jnp.mean(x * x, -1, keepdims=True) + EPS) * g

        def rot_half(x):
            h = x.shape[-1] // 2
            return jnp.concatenate([-x[..., h:], x[..., :h]], axis=-1)
        key = jax.random.key(seed)
        ks = jax.random.split(key, 12)
        B, S = (2, 128)
        n = lambda k, s: 0.02 * jax.random.normal(k, s, dtype=jnp.float32)
        return {'hidden_states': jax.random.normal(ks[0], (B, S, D), dtype=jnp.float32), 'w_q': n(ks[1], (H * HD, D)), 'w_k': n(ks[2], (KVH * HD, D)), 'w_v': n(ks[3], (KVH * HD, D)), 'w_o': n(ks[4], (D, H * HD)), 'g1': jnp.ones((D,), jnp.float32), 'g2': jnp.ones((D,), jnp.float32), 'w_gate': n(ks[5], (E, D)), 'w1': n(ks[6], (E, FFN, D)), 'w3': n(ks[7], (E, FFN, D)), 'w2': n(ks[8], (E, D, FFN))}
    _L0_ffn_all = _L0_ffn_setup()
    _L0_ffn_in = {k: v for k, v in _L0_ffn_all.items() if k in ('w_q', 'w_k', 'w_v', 'w_o', 'g1', 'g2', 'w_gate', 'w1', 'w3', 'w2')}
    del _L0_ffn_all

    def _L1_xattn_setup():
        import jax, jax.numpy as jnp
        import numpy as np
        HEADS = 16
        DIM_HEAD = 64
        DIM = 128
        INNER = HEADS * DIM_HEAD

        def _split_heads(t):
            b, n, _ = t.shape
            return t.reshape(b, n, HEADS, DIM_HEAD).transpose(0, 2, 1, 3)
        key = jax.random.key(seed)
        ks = jax.random.split(key, 8)
        B, N, M = (4, 256, 256)
        x = jax.random.normal(ks[0], (B, N, DIM), dtype=jnp.float32)
        context = jax.random.normal(ks[1], (B, M, DIM), dtype=jnp.float32)
        x_mask = (jax.random.uniform(ks[2], (B, N)) > 0.1).astype(jnp.float32)
        context_mask = (jax.random.uniform(ks[3], (B, M)) > 0.1).astype(jnp.float32)
        s = 0.02
        Wq = jax.random.normal(ks[4], (DIM, INNER), dtype=jnp.float32) * s
        Wkv = jax.random.normal(ks[5], (DIM, 2 * INNER), dtype=jnp.float32) * s
        Wo = jax.random.normal(ks[6], (INNER, DIM), dtype=jnp.float32) * s
        bo = jnp.zeros((DIM,), dtype=jnp.float32)
        return {'x': x, 'context': context, 'x_mask': x_mask, 'context_mask': context_mask, 'Wq': Wq, 'Wkv': Wkv, 'Wo': Wo, 'bo': bo}
    _L1_xattn_all = _L1_xattn_setup()
    _L1_xattn_in = {k: v for k, v in _L1_xattn_all.items() if k in ('Wq', 'Wkv', 'Wo', 'bo')}
    del _L1_xattn_all

    def _L1_ffn_setup():
        import jax, jax.numpy as jnp
        import numpy as np
        import math
        B, S, H, I, E = (4, 256, 128, 512, 8)
        TOP_K = 2
        CAPACITY_FACTOR = 1.25
        key = jax.random.key(seed)
        k1, k2, k3, k4, k5 = jax.random.split(key, 5)
        x = jax.random.normal(k1, (B, S, H), dtype=jnp.float32)
        W_router = jax.random.normal(k2, (E, H), dtype=jnp.float32) * (1.0 / math.sqrt(H))
        b_router = jnp.zeros((E,), dtype=jnp.float32)
        experts_inter = jax.random.normal(k3, (E, H, I), dtype=jnp.float32) * 0.02
        experts_out = jax.random.normal(k4, (E, I, H), dtype=jnp.float32) * 0.02
        return {'x': x, 'W_router': W_router, 'b_router': b_router, 'experts_inter': experts_inter, 'experts_out': experts_out}
    _L1_ffn_all = _L1_ffn_setup()
    _L1_ffn_in = {k: v for k, v in _L1_ffn_all.items() if k in ('W_router', 'b_router', 'experts_inter', 'experts_out')}
    del _L1_ffn_all

    def _L2_xattn_setup():
        import jax, jax.numpy as jnp
        import numpy as np
        D_MODEL = 128
        NUM_HEADS = 16
        DEPTH = D_MODEL // NUM_HEADS
        key = jax.random.key(seed)
        ks = jax.random.split(key, 10)
        B, T, C = (2, 256, 384)
        s = 1.0 / np.sqrt(D_MODEL)
        inp = {'x': jax.random.normal(ks[0], (B, T, D_MODEL), dtype=jnp.float32), 'context': jax.random.normal(ks[1], (B, C, D_MODEL), dtype=jnp.float32), 'Wq': jax.random.normal(ks[2], (D_MODEL, D_MODEL), dtype=jnp.float32) * s, 'bq': jnp.zeros((D_MODEL,), dtype=jnp.float32), 'Wk': jax.random.normal(ks[3], (D_MODEL, D_MODEL), dtype=jnp.float32) * s, 'bk': jnp.zeros((D_MODEL,), dtype=jnp.float32), 'Wv': jax.random.normal(ks[4], (D_MODEL, D_MODEL), dtype=jnp.float32) * s, 'bv': jnp.zeros((D_MODEL,), dtype=jnp.float32), 'Wo': jax.random.normal(ks[5], (D_MODEL, D_MODEL), dtype=jnp.float32) * s, 'bo': jnp.zeros((D_MODEL,), dtype=jnp.float32)}
        return inp
    _L2_xattn_all = _L2_xattn_setup()
    _L2_xattn_in = {k: v for k, v in _L2_xattn_all.items() if k in ('Wq', 'bq', 'Wk', 'bk', 'Wv', 'bv', 'Wo', 'bo')}
    del _L2_xattn_all

    def _L2_ffn_setup():
        import jax, jax.numpy as jnp
        import numpy as np
        D = 128
        E = 8
        K = 2
        NUM_ITER = 2
        DT = 0.1
        H = 64
        CTX = 2 * D

        def _gelu(t):
            return jax.nn.gelu(t, approximate=False)

        def _inl(ctrl, x, v, mu):
            alpha_raw, beta_raw, gate_raw = jnp.split(ctrl, 3, axis=-1)
            alpha = jax.nn.sigmoid(alpha_raw)
            beta = jax.nn.softplus(beta_raw)
            gate = jax.nn.sigmoid(gate_raw)
            error = x - mu
            v_next = alpha * v - beta * error
            x_next = x + DT * gate * v_next
            return (x_next, v_next)
        key = jax.random.key(seed)
        ks = jax.random.split(key, 20)
        s = 0.02
        inp = {'x': jax.random.normal(ks[0], (4, 512, D), jnp.float32), 'w_r1': jax.random.normal(ks[1], (D, D // 4), jnp.float32) * s, 'b_r1': jnp.zeros((D // 4,), jnp.float32), 'w_r2': jax.random.normal(ks[2], (D // 4, E), jnp.float32) * s, 'b_r2': jnp.zeros((E,), jnp.float32), 'w_h1': jax.random.normal(ks[3], (D, D // 4), jnp.float32) * s, 'b_h1': jnp.zeros((D // 4,), jnp.float32), 'w_h2': jax.random.normal(ks[4], (D // 4, 1), jnp.float32) * s, 'b_h2': jnp.zeros((1,), jnp.float32), 'expert_w1': jax.random.normal(ks[5], (E, CTX, H), jnp.float32) * s, 'expert_b1': jnp.zeros((E, H), jnp.float32), 'expert_w2': jax.random.normal(ks[6], (E, H, 3 * D), jnp.float32) * s, 'expert_b2': jnp.zeros((E, 3 * D), jnp.float32), 'w_s1': jax.random.normal(ks[7], (CTX, H), jnp.float32) * s, 'b_s1': jnp.zeros((H,), jnp.float32), 'w_s2': jax.random.normal(ks[8], (H, 3 * D), jnp.float32) * s, 'b_s2': jnp.zeros((3 * D,), jnp.float32), 'shared_weight': jnp.asarray(0.5, jnp.float32), 'w_f1': jax.random.normal(ks[9], (D, 2 * D), jnp.float32) * s, 'b_f1': jnp.zeros((2 * D,), jnp.float32), 'w_f2': jax.random.normal(ks[10], (2 * D, D), jnp.float32) * s, 'b_f2': jnp.zeros((D,), jnp.float32), 'integration_weight': jnp.full((D,), 0.5, jnp.float32), 'mu': jnp.zeros((D,), jnp.float32)}
        return inp
    _L2_ffn_all = _L2_ffn_setup()
    _L2_ffn_in = {k: v for k, v in _L2_ffn_all.items() if k in ('w_r1', 'b_r1', 'w_r2', 'b_r2', 'w_h1', 'b_h1', 'w_h2', 'b_h2', 'expert_w1', 'expert_b1', 'expert_w2', 'expert_b2', 'w_s1', 'b_s1', 'w_s2', 'b_s2', 'shared_weight', 'w_f1', 'b_f1', 'w_f2', 'b_f2', 'integration_weight', 'mu')}
    del _L2_ffn_all

    def _L3_xattn_setup():
        import math
        import jax, jax.numpy as jnp
        import numpy as np
        D_MODEL = 128
        NUM_HEADS = 16
        N_BUCKETS = 8
        B, L, S = (2, 256, 256)
        NEG_INF = -1e+30
        key = jax.random.key(seed)
        ks = jax.random.split(key, 12)
        inv = 1.0 / math.sqrt(D_MODEL)
        return {'query': jax.random.normal(ks[0], (B, L, D_MODEL), jnp.float32), 'key': jax.random.normal(ks[1], (B, S, D_MODEL), jnp.float32), 'value': jax.random.normal(ks[2], (B, S, D_MODEL), jnp.float32), 'query_times': jax.random.uniform(ks[3], (B, L), jnp.float32) * 0.5, 'key_times': jax.random.uniform(ks[4], (B, S), jnp.float32), 'key_padding_mask': jnp.zeros((B, S), dtype=bool), 'source_bucket_ids': jax.random.randint(ks[5], (B, S), 0, N_BUCKETS, jnp.int32), 'Wq': jax.random.normal(ks[6], (D_MODEL, D_MODEL), jnp.float32) * inv, 'Wk_b': jax.random.normal(ks[7], (N_BUCKETS, D_MODEL, D_MODEL), jnp.float32) * inv, 'Wv_b': jax.random.normal(ks[8], (N_BUCKETS, D_MODEL, D_MODEL), jnp.float32) * inv, 'Wo': jax.random.normal(ks[9], (D_MODEL, D_MODEL), jnp.float32) * inv, 'bo': jnp.zeros((D_MODEL,), jnp.float32)}
    _L3_xattn_all = _L3_xattn_setup()
    _L3_xattn_in = {k: v for k, v in _L3_xattn_all.items() if k in ('Wq', 'Wk_b', 'Wv_b', 'Wo', 'bo')}
    del _L3_xattn_all

    def _L3_ffn_setup():
        import jax, jax.numpy as jnp
        import numpy as np
        EMBED_DIM = 128
        HIDDEN = 4 * EMBED_DIM
        BATCH, SEQ = (4, 512)
        EPS = 1e-05

        def _quant_weight(w):
            s = jnp.clip(jnp.mean(jnp.abs(w)), EPS, None)
            wq = jnp.clip(jnp.round(w / s), -1.0, 1.0) * s
            return w + jax.lax.stop_gradient(wq - w)

        def _quant_act(x):
            scale = 127.0 / jnp.clip(jnp.max(jnp.abs(x), axis=-1, keepdims=True), EPS, None)
            xq = jnp.clip(jnp.round(x * scale), -128.0, 127.0) / scale
            return x + jax.lax.stop_gradient(xq - x)

        def _bitlinear(x, w):
            return jnp.einsum('bsi,oi->bso', _quant_act(x), _quant_weight(w))
        key = jax.random.key(seed)
        k1, k2, k3 = jax.random.split(key, 3)
        x = jax.random.normal(k1, (BATCH, SEQ, EMBED_DIM), dtype=jnp.float32)
        w1 = jax.random.normal(k2, (HIDDEN, EMBED_DIM), dtype=jnp.float32) * (1.0 / np.sqrt(EMBED_DIM))
        w2 = jax.random.normal(k3, (EMBED_DIM, HIDDEN), dtype=jnp.float32) * (1.0 / np.sqrt(HIDDEN))
        return {'x': x, 'w1': w1, 'w2': w2}
    _L3_ffn_all = _L3_ffn_setup()
    _L3_ffn_in = {k: v for k, v in _L3_ffn_all.items() if k in ('w1', 'w2')}
    del _L3_ffn_all
    return {'x': x, 'ctx_1024': ctx_1024, 'fside_BxS2_0': fside_BxS2_0, 'itok_BxS2_0_7': itok_BxS2_0_7, 'mask_BxS2_fk1': mask_BxS2_fk1, 'mask_BxS2_bf0': mask_BxS2_bf0, 'g_xattn': g_xattn, 'g_ffn': g_ffn, 'L0_xattn_ptb_gamma': _L0_xattn_in['ptb_gamma'], 'L0_xattn_W_fused': _L0_xattn_in['W_fused'], 'L0_xattn_W_attn_out': _L0_xattn_in['W_attn_out'], 'L0_xattn_W_ff_out': _L0_xattn_in['W_ff_out'], 'L0_xattn_ca_gamma': _L0_xattn_in['ca_gamma'], 'L0_xattn_ca_ctx_gamma': _L0_xattn_in['ca_ctx_gamma'], 'L0_xattn_W_q': _L0_xattn_in['W_q'], 'L0_xattn_W_kv': _L0_xattn_in['W_kv'], 'L0_xattn_W_out': _L0_xattn_in['W_out'], 'L0_ffn_w_q': _L0_ffn_in['w_q'], 'L0_ffn_w_k': _L0_ffn_in['w_k'], 'L0_ffn_w_v': _L0_ffn_in['w_v'], 'L0_ffn_w_o': _L0_ffn_in['w_o'], 'L0_ffn_g1': _L0_ffn_in['g1'], 'L0_ffn_g2': _L0_ffn_in['g2'], 'L0_ffn_w_gate': _L0_ffn_in['w_gate'], 'L0_ffn_w1': _L0_ffn_in['w1'], 'L0_ffn_w3': _L0_ffn_in['w3'], 'L0_ffn_w2': _L0_ffn_in['w2'], 'L1_xattn_Wq': _L1_xattn_in['Wq'], 'L1_xattn_Wkv': _L1_xattn_in['Wkv'], 'L1_xattn_Wo': _L1_xattn_in['Wo'], 'L1_xattn_bo': _L1_xattn_in['bo'], 'L1_ffn_W_router': _L1_ffn_in['W_router'], 'L1_ffn_b_router': _L1_ffn_in['b_router'], 'L1_ffn_experts_inter': _L1_ffn_in['experts_inter'], 'L1_ffn_experts_out': _L1_ffn_in['experts_out'], 'L2_xattn_Wq': _L2_xattn_in['Wq'], 'L2_xattn_bq': _L2_xattn_in['bq'], 'L2_xattn_Wk': _L2_xattn_in['Wk'], 'L2_xattn_bk': _L2_xattn_in['bk'], 'L2_xattn_Wv': _L2_xattn_in['Wv'], 'L2_xattn_bv': _L2_xattn_in['bv'], 'L2_xattn_Wo': _L2_xattn_in['Wo'], 'L2_xattn_bo': _L2_xattn_in['bo'], 'L2_ffn_w_r1': _L2_ffn_in['w_r1'], 'L2_ffn_b_r1': _L2_ffn_in['b_r1'], 'L2_ffn_w_r2': _L2_ffn_in['w_r2'], 'L2_ffn_b_r2': _L2_ffn_in['b_r2'], 'L2_ffn_w_h1': _L2_ffn_in['w_h1'], 'L2_ffn_b_h1': _L2_ffn_in['b_h1'], 'L2_ffn_w_h2': _L2_ffn_in['w_h2'], 'L2_ffn_b_h2': _L2_ffn_in['b_h2'], 'L2_ffn_expert_w1': _L2_ffn_in['expert_w1'], 'L2_ffn_expert_b1': _L2_ffn_in['expert_b1'], 'L2_ffn_expert_w2': _L2_ffn_in['expert_w2'], 'L2_ffn_expert_b2': _L2_ffn_in['expert_b2'], 'L2_ffn_w_s1': _L2_ffn_in['w_s1'], 'L2_ffn_b_s1': _L2_ffn_in['b_s1'], 'L2_ffn_w_s2': _L2_ffn_in['w_s2'], 'L2_ffn_b_s2': _L2_ffn_in['b_s2'], 'L2_ffn_shared_weight': _L2_ffn_in['shared_weight'], 'L2_ffn_w_f1': _L2_ffn_in['w_f1'], 'L2_ffn_b_f1': _L2_ffn_in['b_f1'], 'L2_ffn_w_f2': _L2_ffn_in['w_f2'], 'L2_ffn_b_f2': _L2_ffn_in['b_f2'], 'L2_ffn_integration_weight': _L2_ffn_in['integration_weight'], 'L2_ffn_mu': _L2_ffn_in['mu'], 'L3_xattn_Wq': _L3_xattn_in['Wq'], 'L3_xattn_Wk_b': _L3_xattn_in['Wk_b'], 'L3_xattn_Wv_b': _L3_xattn_in['Wv_b'], 'L3_xattn_Wo': _L3_xattn_in['Wo'], 'L3_xattn_bo': _L3_xattn_in['bo'], 'L3_ffn_w1': _L3_ffn_in['w1'], 'L3_ffn_w2': _L3_ffn_in['w2']}

def reference(x, ctx_1024, fside_BxS2_0, itok_BxS2_0_7, mask_BxS2_fk1, mask_BxS2_bf0, g_xattn, g_ffn, L0_xattn_ptb_gamma, L0_xattn_W_fused, L0_xattn_W_attn_out, L0_xattn_W_ff_out, L0_xattn_ca_gamma, L0_xattn_ca_ctx_gamma, L0_xattn_W_q, L0_xattn_W_kv, L0_xattn_W_out, L0_ffn_w_q, L0_ffn_w_k, L0_ffn_w_v, L0_ffn_w_o, L0_ffn_g1, L0_ffn_g2, L0_ffn_w_gate, L0_ffn_w1, L0_ffn_w3, L0_ffn_w2, L1_xattn_Wq, L1_xattn_Wkv, L1_xattn_Wo, L1_xattn_bo, L1_ffn_W_router, L1_ffn_b_router, L1_ffn_experts_inter, L1_ffn_experts_out, L2_xattn_Wq, L2_xattn_bq, L2_xattn_Wk, L2_xattn_bk, L2_xattn_Wv, L2_xattn_bv, L2_xattn_Wo, L2_xattn_bo, L2_ffn_w_r1, L2_ffn_b_r1, L2_ffn_w_r2, L2_ffn_b_r2, L2_ffn_w_h1, L2_ffn_b_h1, L2_ffn_w_h2, L2_ffn_b_h2, L2_ffn_expert_w1, L2_ffn_expert_b1, L2_ffn_expert_w2, L2_ffn_expert_b2, L2_ffn_w_s1, L2_ffn_b_s1, L2_ffn_w_s2, L2_ffn_b_s2, L2_ffn_shared_weight, L2_ffn_w_f1, L2_ffn_b_f1, L2_ffn_w_f2, L2_ffn_b_f2, L2_ffn_integration_weight, L2_ffn_mu, L3_xattn_Wq, L3_xattn_Wk_b, L3_xattn_Wv_b, L3_xattn_Wo, L3_xattn_bo, L3_ffn_w1, L3_ffn_w2):
    import jax
    import jax.numpy as jnp

    def _L0_xattn_ref(x, context, ptb_gamma, W_fused, W_attn_out, W_ff_out, ca_gamma, ca_ctx_gamma, W_q, W_kv, W_out):
        import jax, jax.numpy as jnp
        import numpy as np
        DIM = 128
        HEADS = 16
        DIM_HEAD = 64
        FF_MULT = 4
        CTX_DIM = 128
        INNER = HEADS * DIM_HEAD
        FF_INNER = DIM * FF_MULT
        FUSED = INNER + 2 * DIM_HEAD + 2 * FF_INNER
        SCALE = DIM_HEAD ** (-0.5)

        def layer_norm(x, gamma, eps=1e-05):
            mu = jnp.mean(x, axis=-1, keepdims=True)
            var = jnp.var(x, axis=-1, keepdims=True)
            return (x - mu) * jax.lax.rsqrt(var + eps) * gamma

        def swiglu(x):
            a, gate = jnp.split(x, 2, axis=-1)
            return jax.nn.silu(gate) * a

        def parallel_block(x, gamma, W_fused, W_attn_out, W_ff_out):
            B, N, D = x.shape
            h = layer_norm(x, gamma)
            fused = h @ W_fused
            q = fused[..., :INNER]
            k = fused[..., INNER:INNER + DIM_HEAD]
            v = fused[..., INNER + DIM_HEAD:INNER + 2 * DIM_HEAD]
            ff = fused[..., INNER + 2 * DIM_HEAD:]
            q = q.reshape(B, N, HEADS, DIM_HEAD).transpose(0, 2, 1, 3) * SCALE
            sim = jnp.einsum('bhid,bjd->bhij', q, k)
            causal = jnp.triu(jnp.ones((N, N), dtype=bool), k=1)
            neg = -jnp.finfo(sim.dtype).max
            sim = jnp.where(causal, neg, sim)
            sim = sim - jax.lax.stop_gradient(jnp.max(sim, axis=-1, keepdims=True))
            attn = jax.nn.softmax(sim, axis=-1)
            out = jnp.einsum('bhij,bjd->bhid', attn, v)
            out = out.transpose(0, 2, 1, 3).reshape(B, N, INNER)
            return out @ W_attn_out + swiglu(ff) @ W_ff_out

        def cross_attention(x, context, gamma, ctx_gamma, W_q, W_kv, W_out):
            B, N, D = x.shape
            xq = layer_norm(x, gamma)
            c = layer_norm(context, ctx_gamma)
            q = (xq @ W_q).reshape(B, N, HEADS, DIM_HEAD).transpose(0, 2, 1, 3) * SCALE
            kv = c @ W_kv
            k, v = (kv[..., :DIM_HEAD], kv[..., DIM_HEAD:])
            sim = jnp.einsum('bhid,bjd->bhij', q, k)
            attn = jax.nn.softmax(sim, axis=-1)
            out = jnp.einsum('bhij,bjd->bhid', attn, v)
            out = out.transpose(0, 2, 1, 3).reshape(B, N, INNER)
            return out @ W_out
        y = x + parallel_block(x, ptb_gamma, W_fused, W_attn_out, W_ff_out)
        return cross_attention(y, context, ca_gamma, ca_ctx_gamma, W_q, W_kv, W_out)

    def _L0_ffn_ref(hidden_states, w_q, w_k, w_v, w_o, g1, g2, w_gate, w1, w3, w2):
        import jax, jax.numpy as jnp
        import numpy as np
        H, KVH, HD, D = (8, 2, 128, 128)
        E, TOPK, FFN = (8, 2, 448)
        THETA, EPS = (1000000.0, 1e-05)
        NBITS, GS = (4, 128)
        QMAX = float(2 ** NBITS - 1)
        NEG = -1e+30

        def qgroup(w):
            shp = w.shape
            w2 = w.reshape(-1, GS)
            wmax = jnp.max(w2, -1, keepdims=True)
            wmin = jnp.min(w2, -1, keepdims=True)
            scales = jnp.clip(wmax - wmin, 1e-05, None) / QMAX
            base = jnp.clip(jnp.round(-wmin / scales), 0.0, QMAX)
            wq = (jnp.clip(jnp.round(w2 / scales) + base, 0.0, QMAX) - base) * scales
            return wq.reshape(shp)

        def rms(x, g):
            return x * jax.lax.rsqrt(jnp.mean(x * x, -1, keepdims=True) + EPS) * g

        def rot_half(x):
            h = x.shape[-1] // 2
            return jnp.concatenate([-x[..., h:], x[..., :h]], axis=-1)
        B, S, _ = hidden_states.shape
        T = B * S
        xn = rms(hidden_states, g1)
        q = (xn @ qgroup(w_q).T).reshape(B, S, H, HD).transpose(0, 2, 1, 3)
        k = (xn @ qgroup(w_k).T).reshape(B, S, KVH, HD).transpose(0, 2, 1, 3)
        v = (xn @ qgroup(w_v).T).reshape(B, S, KVH, HD).transpose(0, 2, 1, 3)
        k = qgroup(k)
        pos = jnp.arange(S, dtype=jnp.float32)
        inv = 1.0 / THETA ** (jnp.arange(0, HD, 2, dtype=jnp.float32) / HD)
        freqs = pos[:, None] * inv[None, :]
        emb = jnp.concatenate([freqs, freqs], axis=-1)
        cos = jnp.cos(emb)[None, None]
        sin = jnp.sin(emb)[None, None]
        q = q * cos + rot_half(q) * sin
        k = k * cos + rot_half(k) * sin
        rep = H // KVH
        k = jnp.repeat(k, rep, axis=1)
        v = jnp.repeat(v, rep, axis=1)
        v = qgroup(v)
        scores = jnp.einsum('bhqd,bhkd->bhqk', q, k) / np.float32(np.sqrt(HD))
        causal = jnp.tril(jnp.ones((S, S), dtype=bool))
        scores = jnp.where(causal[None, None], scores, NEG)
        attn = jax.nn.softmax(scores, axis=-1)
        o = jnp.einsum('bhqk,bhkd->bhqd', attn, v).transpose(0, 2, 1, 3).reshape(B, S, H * HD)
        h = hidden_states + o @ qgroup(w_o).T
        hn = rms(h, g2).reshape(T, D)
        logits = hn @ w_gate.T
        probs = jax.nn.softmax(logits, axis=-1)
        tv, ti = jax.lax.top_k(probs, TOPK)
        tv = tv / jnp.sum(tv, axis=-1, keepdims=True)
        rw = jnp.zeros((T, E), hn.dtype).at[jnp.arange(T)[:, None], ti].set(tv)
        moe = jnp.zeros((T, D), hn.dtype)
        for e in range(E):
            up = jax.nn.silu(hn @ qgroup(w1[e]).T) * (hn @ qgroup(w3[e]).T)
            moe = moe + rw[:, e:e + 1] * (up @ qgroup(w2[e]).T)
        return h + moe.reshape(B, S, D)

    def _L1_xattn_ref(x, context, x_mask, context_mask, Wq, Wkv, Wo, bo):
        import jax, jax.numpy as jnp
        import numpy as np
        HEADS = 16
        DIM_HEAD = 64
        DIM = 128
        INNER = HEADS * DIM_HEAD

        def _split_heads(t):
            b, n, _ = t.shape
            return t.reshape(b, n, HEADS, DIM_HEAD).transpose(0, 2, 1, 3)
        scale = DIM_HEAD ** (-0.5)
        q = _split_heads(x @ Wq)
        kv = context @ Wkv
        k = _split_heads(kv[..., :INNER])
        v = _split_heads(kv[..., INNER:])
        dots = jnp.einsum('bhnd,bhmd->bhnm', q, k) * scale
        prod = x_mask[:, None, :, None] * context_mask[:, None, None, :]
        masked = jnp.isclose(1.0 - prod, 1.0)
        dots = jnp.where(masked, -jnp.inf, dots)
        valid = jnp.any(~masked, axis=-1, keepdims=True)
        dots = jnp.where(valid, dots, 0.0)
        attn = jax.nn.softmax(dots, axis=-1)
        attn = jnp.where(valid, attn, 0.0)
        out = jnp.einsum('bhnm,bhmd->bhnd', attn, v)
        b, h, n, d = out.shape
        out = out.transpose(0, 2, 1, 3).reshape(b, n, h * d)
        return out @ Wo + bo

    def _L1_ffn_ref(x, W_router, b_router, experts_inter, experts_out):
        import jax, jax.numpy as jnp
        import numpy as np
        import math
        B, S, H, I, E = (4, 256, 128, 512, 8)
        TOP_K = 2
        CAPACITY_FACTOR = 1.25
        b, s, h = x.shape
        e = experts_inter.shape[0]
        T = b * s
        capacity = math.ceil(T / e * CAPACITY_FACTOR)
        x_flat = x.reshape(T, h)
        logits = x_flat @ W_router.T + b_router
        weights_flat = jax.nn.softmax(logits, axis=-1)
        top_vals, top_idx = jax.lax.top_k(weights_flat, TOP_K)
        topk_flat = jnp.zeros_like(weights_flat).at[jnp.arange(T)[:, None], top_idx].set(top_vals)
        routing_mask = (topk_flat > 0).astype(jnp.int32)
        order = jnp.argsort(-routing_mask, axis=0, stable=True)
        sorted_mask = jnp.take_along_axis(routing_mask, order, axis=0)
        sorted_mask = sorted_mask[:capacity]
        sorted_idx = order[:capacity]
        used_tokens = (sorted_idx * sorted_mask).reshape(-1)
        mask_flat = sorted_mask.reshape(-1).astype(x.dtype)
        inputs_tokens = x_flat[used_tokens] * mask_flat[:, None]
        inputs_tokens = inputs_tokens.reshape(capacity, e, h)
        inputs_weights = jnp.take_along_axis(topk_flat, sorted_idx, axis=0)
        hmid = jnp.einsum('ceh,ehi->cei', inputs_tokens, experts_inter)
        hmid = jax.nn.relu(hmid)
        out = jnp.einsum('cei,eih->ceh', hmid, experts_out)
        out = out * inputs_weights[:, :, None]
        combined = jnp.zeros((T, h), dtype=x.dtype).at[used_tokens].add(out.reshape(-1, h))
        return combined.reshape(b, s, h)

    def _L2_xattn_ref(x, context, Wq, bq, Wk, bk, Wv, bv, Wo, bo):
        import jax, jax.numpy as jnp
        import numpy as np
        D_MODEL = 128
        NUM_HEADS = 16
        DEPTH = D_MODEL // NUM_HEADS
        B, T, D = x.shape
        C = context.shape[1]
        H, d = (NUM_HEADS, DEPTH)
        q = x @ Wq.T + bq
        k = context @ Wk.T + bk
        v = context @ Wv.T + bv
        q = q.reshape(B, T, H, d).transpose(0, 2, 1, 3)
        k = k.reshape(B, C, H, d).transpose(0, 2, 1, 3)
        v = v.reshape(B, C, H, d).transpose(0, 2, 1, 3)
        scores = jnp.einsum('bhtd,bhcd->bhtc', q, k) / jnp.sqrt(jnp.asarray(d, x.dtype))
        attn = jax.nn.softmax(scores, axis=-1)
        out = jnp.einsum('bhtc,bhcd->bhtd', attn, v)
        out = out.transpose(0, 2, 1, 3).reshape(B, T, D)
        return out @ Wo.T + bo

    def _L2_ffn_ref(x, w_r1, b_r1, w_r2, b_r2, w_h1, b_h1, w_h2, b_h2, expert_w1, expert_b1, expert_w2, expert_b2, w_s1, b_s1, w_s2, b_s2, shared_weight, w_f1, b_f1, w_f2, b_f2, integration_weight, mu):
        import jax, jax.numpy as jnp
        import numpy as np
        D = 128
        E = 8
        K = 2
        NUM_ITER = 2
        DT = 0.1
        H = 64
        CTX = 2 * D

        def _gelu(t):
            return jax.nn.gelu(t, approximate=False)

        def _inl(ctrl, x, v, mu):
            alpha_raw, beta_raw, gate_raw = jnp.split(ctrl, 3, axis=-1)
            alpha = jax.nn.sigmoid(alpha_raw)
            beta = jax.nn.softplus(beta_raw)
            gate = jax.nn.sigmoid(gate_raw)
            error = x - mu
            v_next = alpha * v - beta * error
            x_next = x + DT * gate * v_next
            return (x_next, v_next)
        B, N, Dm = x.shape
        xf = x.reshape(B * N, Dm)
        logits = _gelu(xf @ w_r1 + b_r1) @ w_r2 + b_r2
        probs = jax.nn.softmax(logits, axis=-1)
        top_p, top_i = jax.lax.top_k(probs, K)
        top_p = top_p / jnp.sum(top_p, axis=-1, keepdims=True)
        flat_idx = top_i.reshape(-1)
        flat_w = top_p.reshape(-1, 1)
        v = jnp.zeros_like(xf)
        integrated = xf
        for _ in range(NUM_ITER):
            ctx = jnp.concatenate([integrated, v], axis=-1)
            shared_ctrl = _gelu(ctx @ w_s1 + b_s1) @ w_s2 + b_s2
            x_shared, v_shared = _inl(shared_ctrl, integrated, v, mu)
            sw = jax.nn.sigmoid(shared_weight)
            ctx_e = jnp.repeat(ctx, K, axis=0)
            x_e = jnp.repeat(integrated, K, axis=0)
            v_e = jnp.repeat(v, K, axis=0)
            w1 = expert_w1[flat_idx]
            b1 = expert_b1[flat_idx]
            w2 = expert_w2[flat_idx]
            b2 = expert_b2[flat_idx]
            hidden = _gelu(jnp.einsum('tc,tch->th', ctx_e, w1) + b1)
            ctrl = jnp.einsum('th,tho->to', hidden, w2) + b2
            x_r, v_r = _inl(ctrl, x_e, v_e, mu)
            x_r = (x_r * flat_w).reshape(B * N, K, Dm).sum(axis=1)
            v_r = (v_r * flat_w).reshape(B * N, K, Dm).sum(axis=1)
            x_next = sw * x_shared + (1.0 - sw) * x_r
            v_next = sw * v_shared + (1.0 - sw) * v_r
            halt = jax.nn.sigmoid(_gelu(x_next @ w_h1 + b_h1) @ w_h2 + b_h2)
            refined = _gelu(x_next @ w_f1 + b_f1) @ w_f2 + b_f2
            integrated = integrated + halt * refined * integration_weight
            v = v_next
        return integrated.reshape(B, N, Dm)

    def _L3_xattn_ref(query, key, value, query_times, key_times, key_padding_mask, source_bucket_ids, Wq, Wk_b, Wv_b, Wo, bo):
        import math
        import jax, jax.numpy as jnp
        import numpy as np
        D_MODEL = 128
        NUM_HEADS = 16
        N_BUCKETS = 8
        B, L, S = (2, 256, 256)
        NEG_INF = -1e+30
        Bq, Lq, D = query.shape
        Sq = key.shape[1]
        H = NUM_HEADS
        dk = D // H
        Q = (query @ Wq).reshape(Bq, Lq, H, dk).transpose(0, 2, 1, 3)
        N = Bq * Sq
        kf = key.reshape(N, D)
        vf = value.reshape(N, D)
        buckets = source_bucket_ids.reshape(N)
        K_all = jnp.einsum('nd,edk->enk', kf, Wk_b)
        V_all = jnp.einsum('nd,edk->enk', vf, Wv_b)
        rows = jnp.arange(N)
        Kf = K_all[buckets, rows]
        Vf = V_all[buckets, rows]
        K = Kf.reshape(Bq, Sq, H, dk).transpose(0, 2, 1, 3)
        V = Vf.reshape(Bq, Sq, H, dk).transpose(0, 2, 1, 3)
        time_diff = query_times[:, :, None] - key_times[:, None, :]
        attend = (time_diff < 0)[:, None, :, :] | key_padding_mask[:, None, None, :]
        scores = jnp.einsum('bhld,bhsd->bhls', Q, K) / math.sqrt(dk)
        scores = jnp.where(attend, scores, NEG_INF)
        attn = jax.nn.softmax(scores, axis=-1)
        ctx = jnp.einsum('bhls,bhsd->bhld', attn, V)
        ctx = ctx.transpose(0, 2, 1, 3).reshape(Bq, Lq, D)
        return ctx @ Wo + bo

    def _L3_ffn_ref(x, w1, w2):
        import jax, jax.numpy as jnp
        import numpy as np
        EMBED_DIM = 128
        HIDDEN = 4 * EMBED_DIM
        BATCH, SEQ = (4, 512)
        EPS = 1e-05

        def _quant_weight(w):
            s = jnp.clip(jnp.mean(jnp.abs(w)), EPS, None)
            wq = jnp.clip(jnp.round(w / s), -1.0, 1.0) * s
            return w + jax.lax.stop_gradient(wq - w)

        def _quant_act(x):
            scale = 127.0 / jnp.clip(jnp.max(jnp.abs(x), axis=-1, keepdims=True), EPS, None)
            xq = jnp.clip(jnp.round(x * scale), -128.0, 127.0) / scale
            return x + jax.lax.stop_gradient(xq - x)

        def _bitlinear(x, w):
            return jnp.einsum('bsi,oi->bso', _quant_act(x), _quant_weight(w))
        h = jax.nn.gelu(_bitlinear(x, w1), approximate=False)
        return _bitlinear(h, w2)
    x = x + jnp.tanh(g_xattn[0]) * _L0_xattn_ref(_layernorm(x, axis=-1), ctx_1024, L0_xattn_ptb_gamma, L0_xattn_W_fused, L0_xattn_W_attn_out, L0_xattn_W_ff_out, L0_xattn_ca_gamma, L0_xattn_ca_ctx_gamma, L0_xattn_W_q, L0_xattn_W_kv, L0_xattn_W_out)
    x = x + jnp.tanh(g_ffn[0]) * _L0_ffn_ref(_layernorm(x, axis=-1), L0_ffn_w_q, L0_ffn_w_k, L0_ffn_w_v, L0_ffn_w_o, L0_ffn_g1, L0_ffn_g2, L0_ffn_w_gate, L0_ffn_w1, L0_ffn_w3, L0_ffn_w2)
    x = x + jnp.tanh(g_xattn[1]) * _L1_xattn_ref(_layernorm(x, axis=-1), ctx_1024, mask_BxS2_fk1, mask_BxS2_fk1, L1_xattn_Wq, L1_xattn_Wkv, L1_xattn_Wo, L1_xattn_bo)
    x = x + jnp.tanh(g_ffn[1]) * _L1_ffn_ref(_layernorm(x, axis=-1), L1_ffn_W_router, L1_ffn_b_router, L1_ffn_experts_inter, L1_ffn_experts_out)
    x = x + jnp.tanh(g_xattn[2]) * _L2_xattn_ref(_layernorm(x, axis=-1), ctx_1024, L2_xattn_Wq, L2_xattn_bq, L2_xattn_Wk, L2_xattn_bk, L2_xattn_Wv, L2_xattn_bv, L2_xattn_Wo, L2_xattn_bo)
    x = x + jnp.tanh(g_ffn[2]) * _L2_ffn_ref(_layernorm(x, axis=-1), L2_ffn_w_r1, L2_ffn_b_r1, L2_ffn_w_r2, L2_ffn_b_r2, L2_ffn_w_h1, L2_ffn_b_h1, L2_ffn_w_h2, L2_ffn_b_h2, L2_ffn_expert_w1, L2_ffn_expert_b1, L2_ffn_expert_w2, L2_ffn_expert_b2, L2_ffn_w_s1, L2_ffn_b_s1, L2_ffn_w_s2, L2_ffn_b_s2, L2_ffn_shared_weight, L2_ffn_w_f1, L2_ffn_b_f1, L2_ffn_w_f2, L2_ffn_b_f2, L2_ffn_integration_weight, L2_ffn_mu)
    x = x + jnp.tanh(g_xattn[3]) * _L3_xattn_ref(_layernorm(x, axis=-1), ctx_1024, ctx_1024, fside_BxS2_0, fside_BxS2_0, mask_BxS2_bf0, itok_BxS2_0_7, L3_xattn_Wq, L3_xattn_Wk_b, L3_xattn_Wv_b, L3_xattn_Wo, L3_xattn_bo)
    x = x + jnp.tanh(g_ffn[3]) * _L3_ffn_ref(_layernorm(x, axis=-1), L3_ffn_w1, L3_ffn_w2)
    return x

_drawn_inputs = setup_inputs


def setup_inputs(seed=0):
    import zlib

    import numpy as np

    out = dict(_drawn_inputs(seed))
    spreads = {'L0_xattn_ptb_gamma': (1.0, 0.6),
     'L0_xattn_ca_gamma': (1.0, 0.6),
     'L0_xattn_ca_ctx_gamma': (1.0, 0.6),
     'L0_ffn_g1': (1.0, 0.6),
     'L0_ffn_g2': (1.0, 0.6),
     'L1_xattn_bo': (0.0, 0.1),
     'L1_ffn_b_router': (0.0, 1.819),
     'L2_xattn_bq': (0.0, 0.377),
     'L2_xattn_bk': (0.0, 2.0),
     'L2_xattn_bv': (0.0, 0.1),
     'L2_xattn_bo': (0.0, 0.1),
     'L2_ffn_b_r1': (0.0, 2.0),
     'L2_ffn_b_r2': (0.0, 2.0),
     'L2_ffn_b_h1': (0.0, 0.8),
     'L2_ffn_expert_b1': (0.0, 2.0),
     'L2_ffn_expert_b2': (0.0, 2.0),
     'L2_ffn_b_s1': (0.0, 2.0),
     'L2_ffn_b_s2': (0.0, 2.0),
     'L2_ffn_b_f1': (0.0, 0.478),
     'L2_ffn_b_f2': (0.0, 0.1),
     'L2_ffn_integration_weight': (0.5, 0.541),
     'L2_ffn_mu': (0.0, 2.0),
     'L3_xattn_bo': (0.0, 0.1)}
    factors = {'g_ffn': 21.416,
     'L0_xattn_W_fused': 8.0,
     'L0_xattn_W_attn_out': 8.0,
     'L0_xattn_W_ff_out': 8.0,
     'L0_xattn_W_q': 8.0,
     'L0_ffn_w_q': 8.0,
     'L0_ffn_w_k': 8.0,
     'L0_ffn_w_gate': 4.005,
     'L0_ffn_w1': 3.538,
     'L0_ffn_w3': 3.512,
     'L0_ffn_w2': 3.434,
     'L1_xattn_Wq': 35.359,
     'L2_ffn_w_r1': 53.707,
     'L2_ffn_w_r2': 46.616,
     'L2_ffn_w_h1': 8.0,
     'L2_ffn_w_h2': 8.0,
     'L2_ffn_expert_w1': 50.91,
     'L2_ffn_expert_w2': 45.029,
     'L2_ffn_w_s1': 32.111,
     'L2_ffn_w_s2': 28.598}
    for name, (base, spread) in spreads.items():
        noise = np.random.default_rng([zlib.crc32(name.encode()), seed]).standard_normal(out[name].shape)
        drawn = base * np.exp(spread * noise) if base else spread * noise
        out[name] = jnp.asarray(drawn.astype(out[name].dtype))
    for name, factor in factors.items():
        out[name] = (out[name] * factor).astype(out[name].dtype)
    return out
```

```python
from contextlib import ExitStack

import concourse.bass as bass
from concourse import mybir
import numpy as np

ALU = mybir.AluOpType
ACT = mybir.ActivationFunctionType
AX = mybir.AxisListType
F32 = mybir.dt.float32
BF16 = mybir.dt.bfloat16
I32 = mybir.dt.int32
U8 = mybir.dt.uint8

P = 128
D = 128
B, S = 32, 64
TILE_B = P // S
NT = B // TILE_B
H = 16
E = 8
NEG = -1.0e30
GROUP = 4
NG = NT // GROUP
GT = GROUP * P


def some(count):
    return not isinstance(count, int) or count > 0


class Own:

    def __init__(self, eng, sem):
        self.eng, self.sem, self.n = eng, sem, 0

    def one(self):
        self.n += 1
        return 1

    def restart(self):
        if self.n:
            self.eng.wait_ge(self.sem, self.n)
            self.eng.sem_clear(self.sem)
            self.n = 0


class Machine:
    pass


class Attention:

    def __init__(self, pieces, scale, q_ready, v_ready, w_out, normalise, finish, heads="pair", many_k=False,
                 ctx="none", cx_base=0, extra=(), x_gain=None, c_gain=None, mask=None, rowscale=None, dve_front=None,
                 pool_front=None, more_out=None, out_order=None):
        self.pieces, self.scale, self.q_ready, self.v_ready, self.w_out = pieces, scale, q_ready, v_ready, w_out
        self.normalise, self.finish, self.heads, self.many_k = normalise, finish, heads, many_k
        self.ctx, self.cx_base, self.extra, self.x_gain, self.c_gain = ctx, cx_base, extra, x_gain, c_gain
        self.mask, self.rowscale, self.dve_front, self.pool_front = mask, rowscale, dve_front, pool_front
        self.more_out, self.out_order = more_out, out_order


def pipeline(eng, own, step):
    def static(n):
        step(n, n % 2, [0 <= n + k < NT for k in range(3)])
        if own:
            own.restart()
    for n in range(-2, 2):
        static(n)
    with eng.Fori(1, NT // 2 - 1) as i:
        for u in range(2):
            step(2 * i + u, u, [True] * 3)
            if own:
                own.restart()
    for n in range(NT - 2, NT):
        static(n)


class Event:

    def __init__(self, sem):
        self.sem, self.base = sem, 0


def attention(m, a):
    ev = m.ev
    used = ["xn", "x_turned", "xT", "scores", "shifted", "exped", "rinv", "probs", "p_turned", "pT",
            "pv", "oT", "out", "done"]
    used += ["piece%d" % j for j in range(len(a.pieces))] + ["kept%d" % j for j in range(len(a.pieces))]
    used += list(a.extra)
    if a.heads == "narrow":
        used += ["o_turned", "onat"]
    npc = len(a.pieces)
    nb = 4 if a.heads == "wide" else 8
    nh = 2 * nb
    PSv = (m.PS[:, 0:512].rearrange("q (c p k) -> q c p k", c=4, p=2) if a.heads == "wide"
           else m.PS[:, :].rearrange("q (p c k) -> q c p k", p=2, c=8))
    Pv = m.PROB[:, 0:nb * 128].rearrange("q (c p k) -> q c p k", c=nb, p=2)
    mx = m.mx[:, 0:nh].rearrange("q (c p) -> q c p", p=2)
    rs = m.rs[:, 0:nh].rearrange("q (c p) -> q c p", p=2)

    def bk(ap):
        return ap.unsqueeze(3).to_broadcast([128, nb, 2, S])

    def pe(p):
        def step(n, u, on):
            if on[1]:
                t, v = n + 1, 1 - u
                p.wait_ge(ev["xn"].sem, ev["xn"].base + t + 1)
                if a.ctx == "load":
                    p.wait_ge(m.cx_loaded[v], a.cx_base + 8 * t - 8 * v + 16)
                if some(t):
                    p.wait_ge(ev["xT"].sem, ev["xT"].base + t)
                if "kT" in a.extra:
                    if some(t):
                        p.wait_ge(ev["kT"].sem, ev["kT"].base + t)
                ins = p.transpose(m.TPS[:, 0:128], m.xn[:, v, :], m.ident[:, :])
                if a.ctx != "none":
                    ins = p.transpose(m.TPS[:, 128:256], m.cx[:, v, :], m.ident[:, :])
                ins.then_inc(ev["x_turned"].sem, 1)
                for j, piece in enumerate(a.pieces):
                    if j == 0:
                        p.wait_ge(ev["xT"].sem, ev["xT"].base + t + 1)
                        if some(t - 1):
                            p.wait_ge(ev["oT"].sem, ev["oT"].base + t - 1)
                        if a.heads == "narrow":
                            if some(t - 1):
                                p.wait_ge(ev["onat"].sem, ev["onat"].base + t - 1)
                    if j >= 2:
                        p.wait_ge(ev["kept%d" % (j - 2)].sem, ev["kept%d" % (j - 2)].base + t + 1)
                    for w in piece.get("needs", []):
                        p.wait_ge(ev[w].sem, ev[w].base + t + 1)
                    ins = piece["pe"](p, m.RING[:, (j % 2) * 512:(j % 2) * 512 + 512], t, v)
                    ins.then_inc(ev["piece%d" % j].sem, 1)
            if on[0]:
                t = n
                p.wait_ge(ev["probs"].sem, ev["probs"].base + t + 1)
                if some(t):
                    p.wait_ge(ev["pT"].sem, ev["pT"].base + t)
                for c in range(nb):
                    ins = p.transpose(m.PTP[:, c * 128:(c + 1) * 128], m.PROB[:, c * 128:(c + 1) * 128],
                                      m.ident[:, :])
                ins.then_inc(ev["p_turned"].sem, 1)
            if on[1]:
                t, v = n + 1, 1 - u
                if "kT" in a.extra:
                    p.wait_ge(ev["knat"].sem, ev["knat"].base + t + 1)
                    p.wait_ge(ev["xT"].sem, ev["xT"].base + t + 1)
                    for g in range(2):
                        ins = p.transpose(m.TPS[:, 256 + g * 128:384 + g * 128], m.KN[:, g * 128:(g + 1) * 128],
                                          m.ident[:, :])
                    ins.then_inc(ev["k_turned"].sem, 1)
                for w in a.q_ready:
                    p.wait_ge(ev[w].sem, ev[w].base + t + 1)
                if some(t):
                    p.wait_ge(ev["shifted"].sem, ev["shifted"].base + t)
                m.hold(p)
                for c in range(nb):
                    for h in range(2):
                        for b in range(2):
                            if a.heads == "wide":
                                hd = 2 * c + h
                                ins = p.matmul(m.PS[64 * b:64 * b + 64, hd * 64:hd * 64 + 64],
                                               m.QT[:, hd, 64 * b:64 * b + 64],
                                               m.KT[:, hd // 4, 64 * b:64 * b + 64], start=True, stop=True)
                            else:
                                r = slice(64 * h, 64 * h + 64)
                                ins = p.matmul(m.PS[64 * b:64 * b + 64, h * 512 + c * 64:h * 512 + c * 64 + 64],
                                               m.QT[r, c, 64 * b:64 * b + 64],
                                               m.KT[r, c if a.many_k else 0, 64 * b:64 * b + 64],
                                               start=True, stop=True)
                ins.then_inc(ev["scores"].sem, 1)
            if on[0]:
                t = n
                p.wait_ge(ev["pT"].sem, ev["pT"].base + t + 1)
                kept = {w: t + 1 for w in a.v_ready}
                if on[1]:
                    kept.update({"kept%d" % j: t + 2 for j in range(max(0, npc - 2), npc)})
                for w, k in kept.items():
                    if some(k):
                        p.wait_ge(ev[w].sem, ev[w].base + k)
                if a.heads == "narrow":
                    if some(t):
                        p.wait_ge(ev["onat"].sem, ev["onat"].base + t)
                if some(t):
                    p.wait_ge(ev["oT"].sem, ev["oT"].base + t)
                m.hold(p)
                for c in range(nb):
                    for h in range(2):
                        r = slice(64 * h, 64 * h + 64)
                        for b in range(2):
                            ptb = m.PT[r, c, 64 * b:64 * b + 64]
                            if a.heads == "wide":
                                ins = p.matmul(m.RING[:, h * 512 + c * 128 + 64 * b:h * 512 + c * 128 + 64 * b + 64],
                                               m.VW[r, u, 2 * b + (2 * c) // 4, :], ptb,
                                               start=True, stop=True)
                            elif a.heads == "narrow":
                                ins = p.matmul(m.RING[64 * b:64 * b + 64, h * 512 + c * 8:h * 512 + c * 8 + 8],
                                               ptb, m.V[r, u, b, c * 8:c * 8 + 8], start=True, stop=True)
                            else:
                                vo = c * 64 if a.many_k else 0
                                ins = p.matmul(m.RING[r, c * 128 + 64 * b:c * 128 + 64 * b + 64],
                                               m.V[r, u, b, vo:vo + 64], ptb, start=True, stop=True)
                ins.then_inc(ev["pv"].sem, 1)
                if a.heads == "narrow":
                    p.wait_ge(ev["onat"].sem, ev["onat"].base + t + 1)
                    if some(t):
                        p.wait_ge(ev["done"].sem, ev["done"].base + t)
                    ins = p.transpose(m.OPS[:, 128:256], m.ON[:, :], m.ident[:, :])
                    ins.then_inc(ev["o_turned"].sem, 1)
                p.wait_ge(ev["oT"].sem, ev["oT"].base + t + 1)
                if some(t):
                    p.wait_ge(ev["done"].sem, ev["done"].base + t)
                n_out = 1 if a.heads == "narrow" else 8
                mats = [(m.OT[:, a.out_order[c] if a.out_order else c, :], a.w_out[:, c, :]) for c in range(n_out)]
                if a.more_out:
                    mats += a.more_out(u)
                for k, (l, r) in enumerate(mats):
                    ins = p.matmul(m.OPS[:, 0:128], l, r, start=(k == 0), stop=(k == len(mats) - 1))
                ins.then_inc(ev["out"].sem, 1)
        pipeline(p, None, step)

    def act(s):
        own = Own(s, m.own_act)

        def step(n, u, on):
            if on[1]:
                t, v = n + 1, 1 - u
                s.wait_ge(ev["x_turned"].sem, ev["x_turned"].base + t + 1)
                if a.ctx != "none":
                    (s.activation(m.cT[:, :], m.TPS[:, 128:256], ACT.Copy if a.c_gain is None else ACT.Identity,
                                          scale=1.0 if a.c_gain is None else a.c_gain))
                s.activation(m.xT[:, :], m.TPS[:, 0:128], ACT.Copy if a.x_gain is None else ACT.Identity,
                                             scale=1.0 if a.x_gain is None else a.x_gain).then_inc(ev["xT"].sem, 1)
                for j, piece in enumerate(a.pieces):
                    if "act" in piece:
                        s.wait_ge(ev["piece%d" % j].sem, ev["piece%d" % j].base + t + 1)
                        ins = piece["act"](s, m.RING[:, (j % 2) * 512:(j % 2) * 512 + 512], t, v, own)
                        ins.then_inc(ev[piece.get("raises", "kept%d" % j)].sem, 1)
                if "kT" in a.extra:
                    s.wait_ge(ev["k_turned"].sem, ev["k_turned"].base + t + 1)
                    s.activation(m.KT[:, 0:2, :], m.TPS[:, 256:512].rearrange("p (g k) -> p g k", g=2),
                                                 ACT.Copy).then_inc(ev["kT"].sem, 1)
            if on[0]:
                t = n
                s.wait_ge(ev["p_turned"].sem, ev["p_turned"].base + t + 1)
                s.activation(m.PT[:, 0:nb, :], m.PTP[:, 0:nb * 128].rearrange("p (c q) -> p c q", c=nb),
                                             ACT.Copy).then_inc(ev["pT"].sem, 1)
                if a.heads == "narrow":
                    s.wait_ge(ev["pv"].sem, ev["pv"].base + t + 1)
                    s.activation(m.ON[:, 0:64], m.RING[:, 0:64], ACT.Copy)
                    s.activation(m.ON[:, 64:128], m.RING[:, 512:576], ACT.Copy).then_inc(ev["onat"].sem, 1)
                    s.wait_ge(ev["o_turned"].sem, ev["o_turned"].base + t + 1)
                    s.activation(m.OT[:, 0, :], m.OPS[:, 128:256], ACT.Copy).then_inc(ev["oT"].sem, 1)
            if on[1]:
                t = n + 1
                s.wait_ge(ev["shifted"].sem, ev["shifted"].base + t + 1)
                s.activation(m.PROB[:, 0:nb * 128], m.PROB[:, 0:nb * 128], ACT.Exp, scale=a.scale).then_inc(ev["exped"].sem, 1)
        pipeline(s, own, step)

    def dve(v):
        own = Own(v, m.own_dve)

        def step(n, u, on):
            if on[2]:
                t = n + 2
                if some(t - 1):
                    v.wait_ge(ev["x_turned"].sem, ev["x_turned"].base + t - 1)
                a.normalise(v, own, t, u)
            if on[1]:
                t, w = n + 1, 1 - u
                if a.dve_front:
                    a.dve_front(v, own, t, w)
                for j, piece in enumerate(a.pieces):
                    if "dve" in piece:
                        v.wait_ge(ev["piece%d" % j].sem, ev["piece%d" % j].base + t + 1)
                        ins = piece["dve"](v, m.RING[:, (j % 2) * 512:(j % 2) * 512 + 512], t, w, own)
                        ins.then_inc(ev["kept%d" % j].sem, 1)
                        if "dve_after" in piece:
                            piece["dve_after"](v, t, own)
                v.wait_ge(ev["scores"].sem, ev["scores"].base + t + 1)
                if a.mask:
                    v.tensor_tensor(Pv, PSv, a.mask(t).to_broadcast([128, nb, 2, S]), ALU.add).then_inc(own.sem, own.one())
                    v.wait_ge(own.sem, own.n)
                    v.tensor_reduce(mx, Pv, AX.X, ALU.max).then_inc(own.sem, own.one())
                    v.wait_ge(own.sem, own.n)
                    ins = v.tensor_tensor(Pv, Pv, bk(mx), ALU.subtract)
                else:
                    v.tensor_reduce(mx, PSv, AX.X, ALU.max).then_inc(own.sem, own.one())
                    v.wait_ge(own.sem, own.n)
                    ins = v.tensor_tensor(Pv, PSv, bk(mx), ALU.subtract)
                ins.then_inc(ev["shifted"].sem, 1)
            if on[0] and a.heads != "narrow":
                if some(n + 1):
                    v.wait_ge(ev["pv"].sem, ev["pv"].base + n + 1)
                v.tensor_copy(m.OT[:, :, :], m.RING[:, :].rearrange("p (c q) -> p c q", c=8)).then_inc(ev["oT"].sem, 1)
            if on[1]:
                t = n + 1
                v.wait_ge(ev["exped"].sem, ev["exped"].base + t + 1)
                v.tensor_reduce(rs, Pv, AX.X, ALU.add).then_inc(own.sem, own.one())
                v.wait_ge(own.sem, own.n)
                if a.rowscale:
                    v.reciprocal(rs, rs).then_inc(own.sem, own.one())
                    v.wait_ge(own.sem, own.n)
                    ins = v.tensor_scalar(rs, rs, a.rowscale(t), None, ALU.mult)
                else:
                    ins = v.reciprocal(rs, rs)
                ins.then_inc(ev["rinv"].sem, 1)
            if on[0]:
                if some(n + 1):
                    v.wait_ge(ev["out"].sem, ev["out"].base + n + 1)
                a.finish(v, own, n).then_inc(ev["done"].sem, 1)
        pipeline(v, own, step)

    def pool(g):
        def step(n, u, on):
            if on[1]:
                t = n + 1
                if a.pool_front:
                    a.pool_front(g, t, 1 - u)
                g.wait_ge(ev["rinv"].sem, ev["rinv"].base + t + 1)
                g.tensor_tensor(Pv, Pv, bk(rs), ALU.mult).then_inc(ev["probs"].sem, 1)
        pipeline(g, None, step)

    def sp(q):
        if a.ctx == "load":
            def step(n, u, on):
                if on[2]:
                    t = n + 2
                    if some(t - 1):
                        q.wait_ge(ev["x_turned"].sem, ev["x_turned"].base + t - 1)
                    src = m.ctx_tiles[bass.ds(t, 1), :, :].rearrange("a p d -> (a p) d")
                    q.dma_start(m.cx[:, u, :], src).then_inc(m.cx_loaded[u], 16)
            pipeline(q, None, step)

    programs = dict(pe=pe, act=act, dve=dve, pool=pool, sp=sp)
    return programs, used


def constants():
    q = np.arange(P)
    k = np.arange(S)
    pos = (q % S).astype(np.float32)
    inv = (1.0 / np.float32(1000000.0) ** (np.arange(0, D, 2, dtype=np.float32) / np.float32(D))).astype(np.float32)
    freqs = pos[:, None] * inv[None, :]
    emb = np.concatenate([freqs, freqs], 1).astype(np.float32)
    cos, sin = np.cos(emb).astype(np.float32), np.sin(emb).astype(np.float32)
    half = np.where(np.arange(D) < D // 2, -1.0, 1.0).astype(np.float32)
    e = np.arange(E)
    tie = (e[None, :] < e[:, None]).astype(np.float32).reshape(1, E * E).repeat(P, 0)
    return dict(
        ident=np.eye(P, dtype=np.float32),
        causal=np.where(k[None, :] > (q % S)[:, None], np.float32(NEG), np.float32(0)).astype(np.float32),
        before=(q[:, None] < q[None, :]).astype(np.float32),
        cosT=np.ascontiguousarray(cos.T), sinT=np.ascontiguousarray(sin.T),
        cosN=cos, sinN=(sin * half[None, :]).astype(np.float32),
        tie=tie,
        own_dims=((q[:, None] % 64) // 8 == np.arange(8)[None, :]).astype(np.float32),
        ones=np.ones((P, P), np.float32),
        zeros=np.zeros((P, 3 * P), np.float32),
        pick=(np.arange(P)[:, None] % E == (np.arange(512)[None, :] // 64)).astype(np.float32),
    )


CONST = constants()
ON_CHIP = [n for n in CONST if n != "zeros"]


def program(nc, t, out, stop=99):
    m = Machine()
    ctx = ExitStack()
    with ctx:
        def sb(name, shape, dt=F32, stack=ctx):
            return stack.enter_context(nc.sbuf_tensor(name, shape, dt))

        class Arena:

            def __init__(self, name, floats):
                self.buf, self.at, self.floats = sb(name, [P, floats]), 0, floats

            def cut(self, shape):
                n = int(np.prod(shape[1:]))
                assert self.at + n <= self.floats, (self.at, n)
                ap = self.buf[0:shape[0], self.at:self.at + n]
                self.at += n
                if len(shape) == 2:
                    return ap
                names = "abcd"[:len(shape) - 1]
                return ap.rearrange("p (%s) -> p %s" % (" ".join(names), " ".join(names)),
                                    **{k: v for k, v in zip(names, shape[1:])})

            def again(self):
                self.at = 0

        def ps(name, shape):
            return ctx.enter_context(nc.psum_tensor(name, shape, F32))

        def sem(name):
            return ctx.enter_context(nc.semaphore(name))

        X = m.X = sb("X", [P, NT * D])
        XIN = m.XIN = sb("XIN", [P, NT * D])
        table = {name: sb("table_" + name, [P, CONST[name].shape[1]]) for name in ON_CHIP}
        m.ident, m.causal, m.before, m.ones = table["ident"], table["causal"], table["before"], table["ones"]
        m.cosT, m.sinT, m.cosN, m.sinN = table["cosT"], table["sinT"], table["cosN"], table["sinN"]
        m.tie, m.own_dims, m.pick = table["tie"], table["own_dims"], table["pick"]
        m.g_all = sb("g_all", [P, 8])
        m.tg = sb("tg", [P, 8])
        m.gains = sb("gains", [P, 8])
        m.mhalf = sb("mhalf", [P, NT])
        m.st = sb("st", [P, NT, 6])
        m.mv = sb("mv", [P, NT, 2])
        m.rstd = sb("rstd", [P, NT])
        m.cmv = sb("cmv", [P, NT, 2])
        m.crstd = sb("crstd", [P, NT])
        m.anchor = sb("anchor", [P, 32], BF16)
        m.xn = sb("xn", [P, 2, D])
        m.cx = sb("cx", [P, 2, D])
        m.xT = sb("xT", [P, P])
        m.cT = sb("cT", [P, P])
        m.mx = sb("mx", [P, H])
        m.rs = sb("rs", [P, H])
        m.TPS = ps("TPS", [P, 512])
        m.RING = ps("RING", [P, 1024])
        m.PS = ps("PS", [P, 1024])
        m.PTP = ps("PTP", [P, 1024])
        m.OPS = ps("OPS", [P, 512])

        names = ["xn", "x_turned", "xT", "scores", "shifted", "exped", "rinv", "probs", "p_turned", "pT",
                 "pv", "oT", "out", "done", "o_turned", "onat", "kT", "knat", "k_turned", "gate_exped",
                 "q_turned_by_pos", "q_biased", "q_split", "kv_biased", "masked_ctx"]
        names += ["piece%d" % j for j in range(6)] + ["kept%d" % j for j in range(6)]
        m.ev = {n: Event(sem(n)) for n in names}
        ev = m.ev
        m.own_act, m.own_dve, m.own_pool = sem("own_act"), sem("own_dve"), sem("own_pool")
        m.cx_loaded = [sem("even_context_loaded"), sem("odd_context_loaded")]
        s_const, s_x, s_ready = sem("constants_loaded"), sem("x_loaded"), sem("setup_done")
        s_var, s_rstd = sem("variance_ready"), sem("rstd_ready")
        s_stored = sem("stored")
        m.weights = {}
        prog = dict(pe=[], act=[], dve=[], pool=[], sp=[])
        m.nvar = 0

        def hold(p):
            p.ldweights(m.anchor[:, :], tile_position=(0, 0))
        m.hold = hold

        def load(group, pairs):
            s = sem("loaded_" + group)
            m.weights[group] = (s, 16 * len(pairs))

            def f(q):
                for dst, src in pairs:
                    q.dma_start(dst, src, allow_slow_non_contiguous=True).then_inc(s, 16)
            prog["sp"].append(f)

        def loaded(eng, group):
            s, n = m.weights[group]
            eng.wait_ge(s, n)
        m.loaded = loaded

        def row(ap, n):
            return ap.rearrange("(a n) -> a n", a=1).to_broadcast([P, n])

        def col(ap):
            return ap.rearrange("(p a) -> p a", a=1)

        def barrier():
            v = ev["done"].base
            for k in prog:
                prog[k].append(lambda eng, v=v: eng.wait_ge(ev["done"].sem, v))

        load("constants", [(table[n][:, :], t["const_" + n]) for n in ON_CHIP]
             + [(m.g_all[:, 0:4], row(t["g_xattn"], 4)), (m.g_all[:, 4:8], row(t["g_ffn"], 4))]
             + [(m.gains[:, i:i + 1], col(t[n])) for i, n in enumerate(
                 ["L0_xattn_ptb_gamma", "L0_xattn_ca_gamma", "L0_xattn_ca_ctx_gamma", "L0_ffn_g1", "L0_ffn_g2"])])
        load("x", [(X[:, :].rearrange("p (t d) -> p t d", d=D), t["x"].rearrange("(t b) s d -> (b s) t d", b=TILE_B))])
        m.ctx_tiles = t["ctx_1024"].rearrange("(t b) s d -> t (b s) d", b=TILE_B)

        def setup_dve(v):
            v.memset(m.mhalf[:, :], -0.5).then_inc(s_ready, 1)
            v.memset(m.anchor[:, :], 0.0).then_inc(s_ready, 1)
        prog["dve"].append(setup_dve)

        def setup_act(s):
            loaded(s, "constants")
            s.activation(m.tg[:, :], m.g_all[:, :], ACT.Tanh).then_inc(s_ready, 1)
        prog["act"].append(setup_act)
        for k in ("pe", "dve", "pool", "act"):
            prog[k].append(lambda eng: (loaded(eng, "constants"), eng.wait_ge(s_ready, 3)))

        def tile_of(buf, i, width=D):
            return buf[:, bass.ds(i * width, width)]
        m.tile_of = tile_of

        def statistics(src, mv, rstd, eps, rms=False):
            k = m.nvar = m.nvar + 1

            def dve(v):
                own = Own(v, m.own_dve)
                for i in range(NT):
                    v.bn_stats(m.st[:, i, :], src[:, i * D:(i + 1) * D]).then_inc(own.sem, own.one())
                v.wait_ge(own.sem, own.n)
                for i in range(NT):
                    v.bn_aggr(mv[:, i, :], m.st[:, i, :]).then_inc(own.sem, own.one())
                v.wait_ge(own.sem, own.n)
                if rms:
                    v.tensor_tensor(rstd[:, :], mv[:, :, 0], mv[:, :, 0], ALU.mult).then_inc(own.sem, own.one())
                    v.wait_ge(own.sem, own.n)
                    v.tensor_tensor(mv[:, :, 1], rstd[:, :], mv[:, :, 1], ALU.add).then_inc(own.sem, own.one())
                    v.wait_ge(own.sem, own.n)
                v.tensor_scalar(rstd[:, :], mv[:, :, 1], eps, None, ALU.add).then_inc(s_var, 1)
                own.restart()
                v.wait_ge(s_rstd, k)

            def pool(g):
                g.wait_ge(s_var, k)
                g.tensor_tensor(rstd[:, :], rstd[:, :], m.mhalf[:, :], ALU.pow).then_inc(s_rstd, 1)
            prog["dve"].append(dve)
            prog["pool"].append(pool)

        def norm_to_xin():
            def dve(v):
                own = Own(v, m.own_dve)
                x3 = X[:, :].rearrange("p (t d) -> p t d", d=D)
                y3 = XIN[:, :].rearrange("p (t d) -> p t d", d=D)
                v.tensor_tensor(y3, x3, m.mv[:, :, 0:1].to_broadcast([P, NT, D]), ALU.subtract).then_inc(own.sem, own.one())
                v.wait_ge(own.sem, own.n)
                v.tensor_tensor(y3, y3, m.rstd[:, :].unsqueeze(2).to_broadcast([P, NT, D]), ALU.mult).then_inc(own.sem, own.one())
                v.wait_ge(own.sem, own.n)
                own.restart()
            prog["dve"].append(dve)

        mv2 = m.mv[:, :, :].rearrange("p t s -> p (t s)")
        cmv2 = m.cmv[:, :, :].rearrange("p t s -> p (t s)")

        def norm_tile(v, dst, src, i, mvf, rstd):
            return v.tensor_scalar(dst, tile_of(src, i), mvf[:, bass.ds(2 * i, 1)], rstd[:, bass.ds(i, 1)],
                                   ALU.subtract, ALU.mult)

        def run(a):
            progs, used = attention(m, a)
            for k in prog:
                def go(eng, f=progs[k], bases={n: ev[n].base for n in ev}):
                    for n, b in bases.items():
                        ev[n].base = b
                    f(eng)
                prog[k].append(go)
            for n in used:
                ev[n].base += NT

        def q_piece(w, j, col0=0):
            def f(p, bank, i, u):
                for c in range(4):
                    ins = p.matmul(bank[:, c * P:(c + 1) * P], w[:, col0 + (4 * j + c) * P:col0 + (4 * j + c + 1) * P],
                                   m.xT[:, :], start=True, stop=True)
                return ins
            return f

        def q_keep(j):
            def f(s, bank, i, u, own):
                return s.activation(m.QT[:, 4 * j:4 * j + 4, :], bank.rearrange("p (c q) -> p c q", c=4), ACT.Copy)
            return f

        WORK, RB, RA = Arena("work_arena", 11300), Arena("arena_b", 8400), Arena("arena_a", 25000)
        Wf = RB.cut([P, 2176])
        Wao = RB.cut([P, 8, D])
        Wffo = RB.cut([P, 4, D])
        Wq0 = RB.cut([P, 1024])
        Wkv0 = RB.cut([P, 128])
        Wo0 = RB.cut([P, 8, D])
        m.QT = WORK.cut([P, 8, P])
        m.KT = WORK.cut([P, 8, P])
        m.V = WORK.cut([P, 2, 2, 512])
        m.VW = m.V[:, :, :, :].rearrange("p u b w -> p u (b w)")[:, :, 0:512].rearrange("p u (k d) -> p u k d", d=D)
        m.PROB = WORK.cut([P, 1024])
        m.PT = WORK.cut([P, 8, P])
        m.OT = WORK.cut([P, 8, P])
        m.ON = WORK.cut([P, P])
        m.KN = WORK.cut([P, 256])
        EG = WORK.cut([P, 512])
        UT = WORK.cut([P, 2, 4, P])
        m.CTX = WORK.cut([P, NT * D])
        load("layer0_fused", [(Wf[:, :], t["L0_xattn_W_fused"]),
                              (Wao[:, :, :], t["L0_xattn_W_attn_out"].rearrange("(c p) d -> p c d", p=P)),
                              (Wffo[:, :, :], t["L0_xattn_W_ff_out"].rearrange("(c p) d -> p c d", p=P))])
        load("layer0_cross", [(Wq0[:, :], t["L0_xattn_W_q"]), (Wkv0[:, :], t["L0_xattn_W_kv"]),
                              (Wo0[:, :, :], t["L0_xattn_W_out"].rearrange("(c p) d -> p c d", p=P)),
                              (m.CTX[:, :].rearrange("p (t d) -> p t d", d=D),
                               t["ctx_1024"].rearrange("(t b) s d -> (b s) t d", b=TILE_B))])
        prog["dve"].append(lambda v: loaded(v, "x"))
        statistics(X, m.mv, m.rstd, 1e-5)
        norm_to_xin()
        statistics(XIN, m.mv, m.rstd, 1e-5)
        prog["pe"].append(lambda p: loaded(p, "layer0_fused"))

        def mqa_kv(w, src, k0):
            def f(p, bank, i, u):
                for h in range(2):
                    p.matmul(bank[64 * h:64 * h + 64, 0:P], w[:, k0:k0 + 64], src[:, :], start=True, stop=True)
                for b in range(2):
                    for h in range(2):
                        ins = p.matmul(bank[64 * h:64 * h + 64, 128 + 64 * b:192 + 64 * b],
                                       src[:, 64 * b:64 * b + 64], w[:, k0 + 64:k0 + 128], start=True, stop=True)
                return ins
            return f

        def mqa_keep(s, bank, i, u, own):
            s.activation(m.KT[:, 0, :], bank[:, 0:P], ACT.Copy)
            return s.activation(m.V[:, u, :, 0:64], bank[:, 128:256].rearrange("p (b d) -> p b d", b=2), ACT.Copy)

        def gate_exp(s, bank, i, u, own):
            return s.activation(EG[:, :], bank, ACT.Exp, scale=-1.0)

        def gate_times(v, bank, i, u, own):
            v.wait_ge(ev["gate_exped"].sem, ev["gate_exped"].base + i + 1)
            v.tensor_scalar(EG[:, :], EG[:, :], 1.0, None, ALU.add).then_inc(own.sem, own.one())
            v.wait_ge(own.sem, own.n)
            v.reciprocal(EG[:, :], EG[:, :]).then_inc(own.sem, own.one())
            v.wait_ge(own.sem, own.n)
            return v.tensor_tensor(EG[:, :], bank, EG[:, :], ALU.mult)

        def up_times(v, bank, i, u, own):
            v.wait_ge(ev["kept3"].sem, ev["kept3"].base + i + 1)
            return v.tensor_tensor(UT[:, u, :, :].rearrange("p c q -> p (c q)"), bank, EG[:, :], ALU.mult)

        def finish_into_xin(v, own, i):
            return v.tensor_tensor(tile_of(XIN, i), m.OPS[:, 0:128], tile_of(XIN, i), ALU.add)

        def finish_into_x(gate):
            def f(v, own, i):
                return v.scalar_tensor_tensor(tile_of(X, i), m.OPS[:, 0:128], m.tg[:, gate:gate + 1], tile_of(X, i),
                                              ALU.mult, ALU.add)
            return f

        def normalise(src):
            def f(v, own, i, u):
                norm_tile(v, m.xn[:, u, :], src, i, mv2, m.rstd).then_inc(ev["xn"].sem, 1)
            return f

        def normalise_both(v, own, i, u):
            norm_tile(v, m.cx[:, u, :], m.CTX, i, cmv2, m.crstd)
            norm_tile(v, m.xn[:, u, :], XIN, i, mv2, m.rstd).then_inc(ev["xn"].sem, 1)

        def causal_mask(i):
            return m.causal[:, :].unsqueeze(1).unsqueeze(1)

        run(Attention(extra=["gate_exped"], x_gain=m.gains[:, 0:1], mask=causal_mask, scale=64 ** -0.5,
                 pieces=[dict(pe=q_piece(Wf, 0), act=q_keep(0)), dict(pe=q_piece(Wf, 1), act=q_keep(1)),
                         dict(pe=mqa_kv(Wf, m.xT, 1024), act=mqa_keep),
                         dict(pe=q_piece(Wf, 0, 1664), act=gate_exp, raises="gate_exped", dve=gate_times),
                         dict(pe=q_piece(Wf, 0, 1152), dve=up_times)],
                 q_ready=["kept0", "kept1", "kept2"], v_ready=["kept2"], w_out=Wao,
                 more_out=lambda u: [(UT[:, u, c, :], Wffo[:, c, :]) for c in range(4)],
                 normalise=normalise(XIN), finish=finish_into_xin))
        barrier()
        if stop >= 1:
            prog["dve"].append(lambda v: loaded(v, "layer0_cross"))
            prog["pe"].append(lambda v: loaded(v, "layer0_cross"))
            statistics(m.CTX, m.cmv, m.crstd, 1e-5)
            statistics(XIN, m.mv, m.rstd, 1e-5)
            run(Attention(ctx="normed", x_gain=m.gains[:, 1:2], c_gain=m.gains[:, 2:3], scale=64 ** -0.5,
                     pieces=[dict(pe=q_piece(Wq0, 0), act=q_keep(0)), dict(pe=q_piece(Wq0, 1), act=q_keep(1)),
                             dict(pe=mqa_kv(Wkv0, m.cT, 0), act=mqa_keep)],
                     q_ready=["kept0", "kept1", "kept2"], v_ready=["kept2"], w_out=Wo0,
                     normalise=normalise_both, finish=finish_into_x(0)))
            barrier()
        wqT = RA.cut([P, 8 * P])
        wqrT = RA.cut([P, 8 * P])
        wkT = RA.cut([P, 2 * P])
        wvT = RA.cut([P, 2 * P])
        woT = RA.cut([P, 8, D])
        KF, CF = 112, 4
        F0 = KF * CF
        w1T = RA.cut([P, E * F0])
        w3T = RA.cut([P, E * F0])
        w2T = RA.cut([P, E, CF, D])
        NGR = E * F0 // P
        small = RA.cut([P, 20, P])
        stage = [RA.cut([P, NGR, P]) for i in range(2)]
        wgT = sb("wgT", [P, 2, E])
        wg_n = sb("wg_n", [E, 2, D])
        qp = sb("qp", [P, 5, NGR])
        s_turned, s_kept_w, s_quant = sem("weights_turned"), sem("weights_kept"), sem("weights_quantised")
        s_stage, s_rotated = sem("staged_again"), sem("rotation_ready")
        m.n_turned = 0
        m.n_quant = 0

        def turn(sources, dst, rows=P, cols=P):
            n = m.n_turned = m.n_turned + 1
            bank = m.PTP[:, (n % 2) * 512:(n % 2) * 512 + 512]

            def pe(p):
                if some(n - 2):
                    p.wait_ge(s_kept_w, n - 2)
                for k, src in enumerate(sources):
                    ins = p.transpose(bank[0:cols, k * rows:(k + 1) * rows], src, m.ident[0:rows, 0:rows])
                ins.then_inc(s_turned, 1)

            def act(s):
                s.wait_ge(s_turned, n)
                s.activation(dst[0], dst[1](bank[0:cols, 0:rows * len(sources)]), ACT.Copy).then_inc(s_kept_w, 1)
            prog["pe"].append(pe)
            prog["act"].append(act)

        def kept_weights():
            n = m.n_turned
            prog["pe"].append(lambda p: p.wait_ge(s_kept_w, n))

        MAGIC = 12582912.0

        def quantise(v, own, w, g, prm=None):
            rows = w.shape[0]
            mx, mn, sc, ri, bs = [qp[0:rows, k, 0:g] for k in range(5)]

            def wide(x):
                return x.unsqueeze(2).to_broadcast([rows, g, P])
            v.tensor_reduce(mx, w, AX.X, ALU.max).then_inc(own.sem, own.one())
            v.wait_ge(own.sem, own.n)
            v.tensor_reduce(mn, w, AX.X, ALU.min).then_inc(own.sem, own.one())
            v.wait_ge(own.sem, own.n)
            v.tensor_tensor(sc, mx, mn, ALU.subtract).then_inc(own.sem, own.one())
            v.wait_ge(own.sem, own.n)
            v.tensor_scalar(sc, sc, 1e-5, 1.0 / 15.0, ALU.max, ALU.mult).then_inc(own.sem, own.one())
            v.wait_ge(own.sem, own.n)
            v.reciprocal(ri, sc).then_inc(own.sem, own.one())
            v.wait_ge(own.sem, own.n)
            v.tensor_tensor(bs, mn, ri, ALU.mult).then_inc(own.sem, own.one())
            v.wait_ge(own.sem, own.n)
            v.tensor_scalar(bs, bs, -1.0, MAGIC, ALU.mult, ALU.add).then_inc(own.sem, own.one())
            v.wait_ge(own.sem, own.n)
            v.tensor_scalar(bs, bs, MAGIC, 0.0, ALU.subtract, ALU.max).then_inc(own.sem, own.one())
            v.wait_ge(own.sem, own.n)
            v.tensor_scalar(bs, bs, 15.0, None, ALU.min).then_inc(own.sem, own.one())
            v.wait_ge(own.sem, own.n)
            v.tensor_tensor(w, w, wide(ri), ALU.mult).then_inc(own.sem, own.one())
            v.wait_ge(own.sem, own.n)
            v.tensor_scalar(w, w, MAGIC, MAGIC, ALU.add, ALU.subtract).then_inc(own.sem, own.one())
            v.wait_ge(own.sem, own.n)
            v.tensor_tensor(w, w, wide(bs), ALU.add).then_inc(own.sem, own.one())
            v.wait_ge(own.sem, own.n)
            v.tensor_scalar(w, w, 0.0, 15.0, ALU.max, ALU.min).then_inc(own.sem, own.one())
            v.wait_ge(own.sem, own.n)
            v.tensor_tensor(w, w, wide(bs), ALU.subtract).then_inc(own.sem, own.one())
            v.wait_ge(own.sem, own.n)
            return v.tensor_tensor(w, w, wide(sc), ALU.mult)

        def quantised(w, g, group, extra_wait=None):
            k = m.n_quant = m.n_quant + 1

            def dve(v):
                if group:
                    loaded(v, group)
                if extra_wait:
                    v.wait_ge(*extra_wait)
                own = Own(v, m.own_dve)
                quantise(v, own, w, g).then_inc(s_quant, 1)
                own.restart()
            prog["dve"].append(dve)
            prog["pe"].append(lambda p: p.wait_ge(s_quant, k))

        if stop >= 2:
            if stop >= 4:
                RB.again()
                Wq1 = RB.cut([P, 1024])
                Wkv1 = RB.cut([P, 2048])
                Wo1 = RB.cut([P, 8, D])
                WiE = RB.cut([P, E, 4 * P])
            load("layer0_small", [(small[:, 0:8, :], t["L0_ffn_w_q"].rearrange("(k p) d -> p k d", p=P)),
                                  (small[:, 8:10, :], t["L0_ffn_w_k"].rearrange("(k p) d -> p k d", p=P)),
                                  (small[:, 10:12, :], t["L0_ffn_w_v"].rearrange("(k p) d -> p k d", p=P)),
                                  (small[:, 12:20, :], t["L0_ffn_w_o"].rearrange("p (k d) -> p k d", k=8)),
                                  (wg_n[:, 0, :], t["L0_ffn_w_gate"]), (wg_n[:, 1, :], t["L1_ffn_W_router"])])
            rows = "e f d -> (e f) d"
            load("layer0_w1", [(stage[0][:, :, :], t["L0_ffn_w1"].rearrange(rows).rearrange("(k p) d -> p k d", p=P))])
            load("layer0_w3", [(stage[1][:, :, :], t["L0_ffn_w3"].rearrange(rows).rearrange("(k p) d -> p k d", p=P))])
            quantised(small[:, :, :], 20, "layer0_small")

            def flat(k):
                return lambda b: b.rearrange("p (k q) -> p k q", k=k)
            for k in range(0, 8, 4):
                turn([small[:, k + i, :] for i in range(4)], (wqT[:, k * P:(k + 4) * P], lambda b: b))
            turn([small[:, 8 + i, :] for i in range(2)], (wkT[:, :], lambda b: b))
            turn([small[:, 10 + i, :] for i in range(2)], (wvT[:, :], lambda b: b))
            for k in range(0, 8, 4):
                turn([small[:, 12 + k + i, :] for i in range(4)], (woT[:, k:k + 4, :], flat(4)))
            prog["pe"].append(lambda p: loaded(p, "layer0_small"))
            turn([wg_n[:, i, :] for i in range(2)], (wgT[:, :, :], flat(2)), rows=E)
            n_q = m.n_turned

            def rotate(s):
                s.wait_ge(s_kept_w, n_q)
                a4 = wqT[:, :].rearrange("p (h r d) -> p h r d", h=8, r=2)
                b4 = wqrT[:, :].rearrange("p (h r d) -> p h r d", h=8, r=2)
                s.activation(b4[:, :, 0, :], a4[:, :, 1, :], ACT.Copy, scale=-1.0).then_inc(s_rotated, 1)
                s.activation(b4[:, :, 1, :], a4[:, :, 0, :], ACT.Copy).then_inc(s_rotated, 1)
            prog["act"].append(rotate)
            prog["pe"].append(lambda p: p.wait_ge(s_rotated, 2))
            quantised(stage[0][:, :, :], NGR, "layer0_w1")
            for k in range(0, NGR, 4):
                turn([stage[0][:, k + i, :] for i in range(4)], (w1T[:, k * P:(k + 4) * P], lambda b: b))
            n_w1 = m.n_turned
            quantised(stage[1][:, :, :], NGR, "layer0_w3")
            for k in range(0, NGR, 4):
                turn([stage[1][:, k + i, :] for i in range(4)], (w3T[:, k * P:(k + 4) * P], lambda b: b))
            if stop >= 4:
                load("layer1_attention", [(Wq1[:, :], t["L1_xattn_Wq"]), (Wkv1[:, :], t["L1_xattn_Wkv"]),
                                          (Wo1[:, :, :], t["L1_xattn_Wo"].rearrange("(c p) d -> p c d", p=P))])
                load("layer1_experts", [(WiE[:, :, :], t["L1_ffn_experts_inter"].rearrange("e h i -> h e i"))])
            st2 = stage[0][:, :, :].rearrange("p (e g) q -> p e (g q)", e=4)

            def load_w2(q):
                q.wait_ge(s_turned, n_w1)
                for eh in range(2):
                    for el in range(4):
                        q.dma_start(st2[64 * eh:64 * eh + 64, el, :],
                                    t["L0_ffn_w2"][4 * eh + el].rearrange("(p r) f -> p (r f)", r=2))\
                            .then_inc(s_stage, 16)
            prog["sp"].append(load_w2)
            quantised(stage[0][:, :, :], NGR, None, (s_stage, 128))
            for el in range(4):
                for par in range(2):
                    dst = w2T[0:KF, :, :, :].rearrange("f (a e) c (q r) -> f a e c q r", a=2, r=2)[:, :, el, :, :, par]
                    turn([st2[:, el, par * F0 + c * KF:par * F0 + (c + 1) * KF] for c in range(CF)],
                         (dst.rearrange("f a c q -> f c a q"),
                          lambda b: b.rearrange("f (c a q) -> f c a q", c=CF, a=2)), cols=KF)
            kept_weights()

            statistics(X, m.mv, m.rstd, 1e-5)
            norm_to_xin()
            statistics(XIN, m.mv, m.rstd, 1e-5, rms=True)
            TR = UT[:, :, :, :].rearrange("p u c q -> p (u c) q")
            KR = EG[:, 0:256]

            def with_table(table, dst):
                def f(v, bank, i, u, own):
                    return v.tensor_tensor(dst, bank.rearrange("p (c q) -> p c q", c=4),
                                           table[:, :].unsqueeze(1).to_broadcast([P, 4, P]), ALU.mult)
                return f

            def k_piece(p, bank, i, u):
                return p.matmul(bank[:, 0:256], m.xT[:, :], wkT[:, :], start=True, stop=True)

            def k_keep(v, bank, i, u, own):
                return v.tensor_copy(m.KN[:, :], bank[:, 0:256])

            def v_piece(p, bank, i, u):
                for b in range(2):
                    for h in range(2):
                        ins = p.matmul(bank[64 * h:64 * h + 64, 256 * b:256 * b + 256], m.xT[:, 64 * b:64 * b + 64],
                                       wvT[:, :], start=True, stop=True)
                return ins

            def v_keep(v, bank, i, u, own):
                v.tensor_copy(m.VW[:, u, :, :], bank.rearrange("p (k d) -> p k d", d=D)).then_inc(own.sem, own.one())
                v.wait_ge(own.sem, own.n)
                return quantise(v, own, m.VW[:, u, :, :], 4)

            def k_finish(v, i, own):
                v.wait_ge(ev["kept4"].sem, ev["kept4"].base + i + 1)
                k3 = m.KN[:, :].rearrange("p (g d) -> p g d", g=2)
                r3 = KR.rearrange("p (g d) -> p g d", g=2)
                quantise(v, own, k3, 2).then_inc(own.sem, own.one())
                v.wait_ge(own.sem, own.n)
                for h in range(2):
                    v.tensor_tensor(r3[:, :, 64 * h:64 * h + 64], k3[:, :, 64 - 64 * h:128 - 64 * h],
                                             m.sinN[:, 64 * h:64 * h + 64].unsqueeze(1).to_broadcast([P, 2, 64]),
                                             ALU.mult).then_inc(own.sem, own.one())
                v.wait_ge(own.sem, own.n)
                v.tensor_tensor(k3, k3, m.cosN[:, :].unsqueeze(1).to_broadcast([P, 2, P]), ALU.mult).then_inc(own.sem, own.one())
                v.wait_ge(own.sem, own.n)
                v.tensor_tensor(k3, k3, r3, ALU.add).then_inc(ev["knat"].sem, 1)

            def pool_rope(g, i, u):
                g.wait_ge(ev["kept3"].sem, ev["kept3"].base + i + 1)
                g.tensor_tensor(m.QT[:, :, :], m.QT[:, :, :], TR, ALU.add).then_inc(ev["q_turned_by_pos"].sem, 1)

            def scaled(src):
                def f(v, own, i, u):
                    v.tensor_scalar(m.xn[:, u, :], tile_of(src, i), m.rstd[:, bass.ds(i, 1)], None,
                                                    ALU.mult).then_inc(ev["xn"].sem, 1)
                return f

            run(Attention(heads="wide", extra=["kT", "knat", "k_turned", "q_turned_by_pos"],
                     x_gain=m.gains[:, 3:4], mask=causal_mask, scale=float(1 / np.float32(np.sqrt(128))),
                     pieces=[dict(pe=q_piece(wqT, 0), dve=with_table(m.cosT, m.QT[:, 0:4, :])),
                             dict(pe=q_piece(wqrT, 0), dve=with_table(m.sinT, TR[:, 0:4, :])),
                             dict(pe=q_piece(wqT, 1), dve=with_table(m.cosT, m.QT[:, 4:8, :])),
                             dict(pe=q_piece(wqrT, 1), dve=with_table(m.sinT, TR[:, 4:8, :])),
                             dict(pe=k_piece, dve=k_keep), dict(pe=v_piece, dve=v_keep, dve_after=k_finish)],
                     q_ready=["q_turned_by_pos", "kT"], v_ready=["kept5"], w_out=woT, pool_front=pool_rope,
                     out_order=[4 * (c % 2) + c // 2 for c in range(8)],
                     normalise=scaled(XIN), finish=finish_into_xin))
            barrier()
        LG = sb("LG", [P, NT * E])
        PR = sb("PR", [P, NT * E])
        RW = sb("RW", [P, NT * E])
        SEL = sb("SEL", [P, 2, NT * E])
        rt = sb("rt", [P, 4, NT])
        s_rt_ready, s_rt_exped = sem("logits_ready"), sem("logits_exped")
        m.n_rt = 0

        def by_tile(buf):
            return buf.rearrange("p (t e) -> p t e", e=E)

        def routing(x_src, w_router, gain, norm, bias=None, hidden=None):
            used = ["xn", "x_turned", "xT", "piece0", "kept0"] + (["piece1", "kept1"] if hidden else [])

            def pe(p):
                def step(n, u, on):
                    if on[1]:
                        t, v = n + 1, 1 - u
                        p.wait_ge(ev["xn"].sem, ev["xn"].base + t + 1)
                        if some(t):
                            p.wait_ge(ev["xT"].sem, ev["xT"].base + t)
                        p.transpose(m.TPS[:, 0:128], m.xn[:, v, :], m.ident[:, :]).then_inc(ev["x_turned"].sem, 1)
                        p.wait_ge(ev["xT"].sem, ev["xT"].base + t + 1)
                        if hidden:
                            if some(t):
                                p.wait_ge(ev["kept1"].sem, ev["kept1"].base + t)
                            p.matmul(m.PS[0:32, 0:128], hidden[0], m.xT[:, :], start=True, stop=True).then_inc(ev["piece1"].sem, 1)
                            p.wait_ge(ev["kept1"].sem, ev["kept1"].base + t + 1)
                        if some(t - 1):
                            p.wait_ge(ev["kept0"].sem, ev["kept0"].base + t - 1)
                        l, r = (hidden[2], hidden[3]) if hidden else (m.xT[:, :], w_router)
                        p.matmul(m.RING[:, v * 512:v * 512 + E], l, r, start=True, stop=True).then_inc(ev["piece0"].sem, 1)
                pipeline(p, None, step)

            def act(s):
                def step(n, u, on):
                    if on[1]:
                        t = n + 1
                        s.wait_ge(ev["x_turned"].sem, ev["x_turned"].base + t + 1)
                        s.activation(m.xT[:, :], m.TPS[:, 0:128], ACT.Copy if gain is None else
                                                     ACT.Identity, scale=1.0 if gain is None else gain).then_inc(ev["xT"].sem, 1)
                        if hidden:
                            s.wait_ge(ev["piece1"].sem, ev["piece1"].base + t + 1)
                            s.activation(hidden[2], m.PS[0:32, 0:128], ACT.Gelu, bias=hidden[1]).then_inc(ev["kept1"].sem, 1)
                pipeline(s, None, step)

            def dve(v):
                own = Own(v, m.own_dve)

                def step(n, u, on):
                    if on[2]:
                        if some(n + 1):
                            v.wait_ge(ev["x_turned"].sem, ev["x_turned"].base + n + 1)
                        norm(v, own, n + 2, u)
                    if on[0]:
                        if some(n + 1):
                            v.wait_ge(ev["piece0"].sem, ev["piece0"].base + n + 1)
                        ps = m.RING[:, u * 512:u * 512 + E]
                        dst = LG[:, bass.ds(n * E, E)]
                        if bias is not None:
                            v.tensor_tensor(dst, ps, bias, ALU.add).then_inc(ev["kept0"].sem, 1)
                        else:
                            v.tensor_scalar(dst, ps, 1.0, None, ALU.mult).then_inc(ev["kept0"].sem, 1)
                pipeline(v, own, step)
            bases = {n: ev[n].base for n in ev}
            for k, f in (("pe", pe), ("act", act), ("dve", dve)):
                def go(eng, f=f):
                    for n, b in bases.items():
                        ev[n].base = b
                    f(eng)
                prog[k].append(go)
            for n in used:
                ev[n].base += NT

        def softmax_and_ranks():
            k = m.n_rt = m.n_rt + 1
            lg, pr = by_tile(LG[:, :]), by_tile(PR[:, :])

            def wide(x):
                return x.unsqueeze(2).to_broadcast([P, NT, E])

            def dve(v):
                own = Own(v, m.own_dve)
                v.wait_ge(ev["kept0"].sem, kept)
                v.tensor_reduce(rt[:, 0, :], lg, AX.X, ALU.max).then_inc(own.sem, own.one())
                v.wait_ge(own.sem, own.n)
                v.tensor_tensor(lg, lg, wide(rt[:, 0, :]), ALU.subtract).then_inc(s_rt_ready, 1)
                v.wait_ge(s_rt_exped, k)
                v.tensor_reduce(rt[:, 1, :], lg, AX.X, ALU.add).then_inc(own.sem, own.one())
                v.wait_ge(own.sem, own.n)
                v.reciprocal(rt[:, 1, :], rt[:, 1, :]).then_inc(own.sem, own.one())
                v.wait_ge(own.sem, own.n)
                v.tensor_tensor(pr, lg, wide(rt[:, 1, :]), ALU.mult).then_inc(own.sem, own.one())
                v.wait_ge(own.sem, own.n)
                above, level = m.R1[:, :].rearrange("p (t e f) -> p t e f", e=E, f=E), \
                    m.R2[:, :].rearrange("p (t e f) -> p t e f", e=E, f=E)
                f_ = pr.unsqueeze(2).to_broadcast([P, NT, E, E])
                e_ = pr.unsqueeze(3).to_broadcast([P, NT, E, E])
                v.tensor_tensor(above, f_, e_, ALU.is_gt).then_inc(own.sem, own.one())
                v.tensor_tensor(level, f_, e_, ALU.is_equal).then_inc(own.sem, own.one())
                v.wait_ge(own.sem, own.n)
                tie = m.tie[:, :].unsqueeze(1).to_broadcast([P, NT, E * E])
                l3 = m.R2[:, :].rearrange("p (t g) -> p t g", g=E * E)
                v.tensor_tensor(l3, l3, tie, ALU.mult).then_inc(own.sem, own.one())
                v.wait_ge(own.sem, own.n)
                v.tensor_tensor(m.R1[:, :], m.R1[:, :], m.R2[:, :], ALU.add).then_inc(own.sem, own.one())
                v.wait_ge(own.sem, own.n)
                v.tensor_reduce(by_tile(RW[:, :]), above, AX.X, ALU.add).then_inc(own.sem, own.one())
                v.wait_ge(own.sem, own.n)
                v.tensor_scalar(SEL[:, 0, :], RW[:, :], 0.0, None, ALU.is_equal).then_inc(own.sem, own.one())
                v.tensor_scalar(SEL[:, 1, :], RW[:, :], 1.0, None, ALU.is_equal).then_inc(own.sem, own.one())
                v.wait_ge(own.sem, own.n)
                own.restart()
            kept = ev["kept0"].base

            def act(s):
                s.wait_ge(s_rt_ready, k)
                s.activation(LG[:, :], LG[:, :], ACT.Exp).then_inc(s_rt_exped, 1)
            prog["dve"].append(dve)
            prog["act"].append(act)

        def top2_weights(normed):
            def dve(v):
                own = Own(v, m.own_dve)
                v.tensor_tensor(RW[:, :], SEL[:, 0, :], SEL[:, 1, :], ALU.add).then_inc(own.sem, own.one())
                v.wait_ge(own.sem, own.n)
                v.tensor_tensor(RW[:, :], RW[:, :], PR[:, :], ALU.mult).then_inc(own.sem, own.one())
                v.wait_ge(own.sem, own.n)
                if normed:
                    v.tensor_reduce(rt[:, 2, :], by_tile(RW[:, :]), AX.X, ALU.add).then_inc(own.sem, own.one())
                    v.wait_ge(own.sem, own.n)
                    v.reciprocal(rt[:, 2, :], rt[:, 2, :]).then_inc(own.sem, own.one())
                    v.wait_ge(own.sem, own.n)
                    v.tensor_tensor(by_tile(RW[:, :]), by_tile(RW[:, :]),
                                             rt[:, 2, :].unsqueeze(2).to_broadcast([P, NT, E]), ALU.mult).then_inc(own.sem, own.one())
                    v.wait_ge(own.sem, own.n)
                own.restart()
            prog["dve"].append(dve)

        for n in ("group_normed", "group_turned", "group_T", "up", "silued", "hidden", "down", "summed", "group_done"):
            ev[n] = Event(sem(n))

        def one_ahead(v):
            v.memset(rt[:, 2, :], 0.0).then_inc(ev["group_done"].sem, 1)
            v.memset(rt[:, 3, :], 0.0).then_inc(ev["group_turned"].sem, 1)
            v.wait_ge(ev["group_done"].sem, 1)
            v.wait_ge(ev["group_turned"].sem, 1)
        prog["dve"].append(one_ahead)
        ev["group_done"].base = ev["group_turned"].base = 1

        def experts(kf, w_in, w_gate, w_out, gain, norm, gate, residual):
            base = {n: ev[n].base for n in ("group_normed", "group_turned", "group_T", "up", "silued", "hidden",
                                                     "down", "summed", "group_done", "done")}
            XG, XGT = m.XG, m.XGT

            def pe(p):
                def up(g, e):
                    for c in range(4):
                        j = 32 * g + 4 * e + c
                        if not (e == 0 and c < 2):
                            if w_gate is not None:
                                p.wait_ge(ev["silued"].sem, base["silued"] + j - 1)
                            p.wait_ge(ev["hidden"].sem, base["hidden"] + j - 1)
                        bank = (c % 2) * 512
                        ins = p.matmul(m.RING[0:kf, bank:bank + 512], w_in(e, c), XGT[:, :], start=True, stop=True)
                        if w_gate is not None:
                            ins = p.matmul(m.PS[0:kf, bank:bank + 512], w_gate(e, c), XGT[:, :], start=True, stop=True)
                        ins.then_inc(ev["up"].sem, 1)

                def down(g, e):
                    p.wait_ge(ev["hidden"].sem, base["hidden"] + 32 * g + 4 * e + 4)
                    if e >= 2:
                        p.wait_ge(ev["summed"].sem, base["summed"] + 8 * g + e - 1)
                    for i in range(GROUP):
                        for c in range(4):
                            ins = p.matmul(m.PTP[:, (e % 2) * 512 + i * P:(e % 2) * 512 + (i + 1) * P],
                                           m.UTE[0:kf, e % 2, c, i * P:(i + 1) * P], w_out(e, c),
                                           start=(c == 0), stop=(c == 3))
                    ins.then_inc(ev["down"].sem, 1)
                with p.Fori(0, NG) as g:
                    p.wait_ge(ev["group_normed"].sem, base["group_normed"] + g + 1)
                    p.wait_ge(ev["group_done"].sem, base["group_done"] + g)
                    for i in range(GROUP):
                        ins = p.transpose(m.TPS[:, i * P:(i + 1) * P], XG[:, i, :], m.ident[:, :])
                    ins.then_inc(ev["group_turned"].sem, 1)
                    p.wait_ge(ev["group_T"].sem, base["group_T"] + g + 1)
                    up(g, 0)
                    for e in range(E):
                        if e + 1 < E:
                            up(g, e + 1)
                        down(g, e)

            def act(s):
                with s.Fori(0, NG) as g:
                    s.wait_ge(ev["group_turned"].sem, base["group_turned"] + g + 1)
                    s.activation(XGT[:, :], m.TPS[:, :], ACT.Copy if gain is None else ACT.Identity,
                                 scale=1.0 if gain is None else gain).then_inc(ev["group_T"].sem, 1)
                    for e in range(E):
                        for c in range(4):
                            j = 32 * g + 4 * e + c
                            s.wait_ge(ev["up"].sem, base["up"] + j + 1)
                            src = m.RING[0:kf, (c % 2) * 512:(c % 2) * 512 + 512]
                            if w_gate is not None:
                                s.activation(m.SG[0:kf, c % 2, :], src, ACT.Silu).then_inc(ev["silued"].sem, 1)
                            else:
                                s.activation(m.UTE[0:kf, e % 2, c, :], src, ACT.Relu).then_inc(ev["hidden"].sem, 1)

            def dve(v):
                own = Own(v, m.own_dve)
                acc = m.ACC

                def add(g, e):
                    v.wait_ge(ev["down"].sem, base["down"] + 8 * g + e + 1)
                    for i in range(GROUP):
                        scalar = RW[:, bass.ds((4 * g + i) * E + e, 1)]
                        src = m.PTP[:, (e % 2) * 512 + i * P:(e % 2) * 512 + (i + 1) * P]
                        if e == 0:
                            ins = v.tensor_scalar(acc[:, i, :], src, scalar, None, ALU.mult)
                        else:
                            ins = v.scalar_tensor_tensor(acc[:, i, :], src, scalar, acc[:, i, :], ALU.mult, ALU.add)
                    ins.then_inc(ev["summed"].sem, 1)
                    v.wait_ge(ev["summed"].sem, base["summed"] + 8 * g + e + 1)
                with v.Fori(0, NG) as g:
                    v.wait_ge(ev["group_turned"].sem, base["group_turned"] + g)
                    for i in range(GROUP):
                        ins = norm(v, XG[:, i, :], 4 * g + i)
                    ins.then_inc(ev["group_normed"].sem, 1)
                    for e in range(E):
                        if w_gate is not None:
                            for c in range(4):
                                j = 32 * g + 4 * e + c
                                v.wait_ge(ev["silued"].sem, base["silued"] + j + 1)
                                v.tensor_tensor(m.UTE[0:kf, e % 2, c, :], m.PS[0:kf, (c % 2) * 512:(c % 2) * 512 + 512],
                                                m.SG[0:kf, c % 2, :], ALU.mult).then_inc(ev["hidden"].sem, 1)
                        if e:
                            add(g, e - 1)
                    add(g, E - 1)
                    a2 = acc.rearrange("p i d -> p (i d)")
                    if residual is not None:
                        v.tensor_tensor(a2, a2, tile_of(residual, g, GT), ALU.add).then_inc(own.sem, own.one())
                        v.wait_ge(own.sem, own.n)
                    v.scalar_tensor_tensor(tile_of(X, g, GT), a2, m.tg[:, gate:gate + 1], tile_of(X, g, GT),
                                           ALU.mult, ALU.add).then_inc(ev["group_done"].sem, 1)
                    own.restart()
                v.wait_ge(ev["group_done"].sem, base["group_done"] + NG)
            for k, f in (("pe", pe), ("act", act), ("dve", dve)):
                prog[k].append(f)
            per = dict(group_normed=NG, group_turned=NG, group_T=NG, up=32 * NG, hidden=32 * NG, down=E * NG, summed=E * NG,
                       group_done=NG, silued=32 * NG if w_gate is not None else 0)
            for n, k in per.items():
                ev[n].base += k

        def group_barrier():
            v = ev["group_done"].base
            for k in prog:
                prog[k].append(lambda eng, v=v: eng.wait_ge( ev["group_done"].sem, v))

        def again():
            WORK.again()
            m.XG = WORK.cut([P, GROUP, D])
            m.XGT = WORK.cut([P, GT])
            m.SG = WORK.cut([P, 2, GT])
            m.UTE = WORK.cut([P, 2, 4, GT])
            m.ACC = WORK.cut([P, GROUP, D])
            m.R1 = WORK.cut([P, NT * E * E])
            m.R2 = WORK.cut([P, NT * E * E])

        def attention_buffers():
            WORK.again()
            m.QT = WORK.cut([P, 8, P])
            m.KT = WORK.cut([P, 8, P])
            m.V = WORK.cut([P, 2, 2, 512])
            m.PROB = WORK.cut([P, 1024])
            m.PT = WORK.cut([P, 8, P])
            m.OT = WORK.cut([P, 8, P])
            m.ON = WORK.cut([P, P])

        if stop >= 3:
            again()
            statistics(XIN, m.mv, m.rstd, 1e-5, rms=True)
            routing(XIN, wgT[:, 0, :], m.gains[:, 4:5], scaled(XIN))
            softmax_and_ranks()
            top2_weights(True)
            experts(KF, lambda e, c: w1T[:, e * F0 + c * KF:e * F0 + (c + 1) * KF],
                    lambda e, c: w3T[:, e * F0 + c * KF:e * F0 + (c + 1) * KF],
                    lambda e, c: w2T[0:KF, e, c, :], m.gains[:, 4:5],
                    lambda v, dst, i: v.tensor_scalar(dst, tile_of(XIN, i), m.rstd[:, bass.ds(i, 1)], None, ALU.mult),
                    4, XIN)
            group_barrier()
        if stop >= 4:
            attention_buffers()
            RA.again()
            TMPO = RA.cut([P, D])
            WoE = RA.cut([P, E, 4, D])
            xm = RA.cut([P, NT])
            cm = RA.cut([P, NT, S])
            valid = RA.cut([P, NT])
            bo1 = RA.cut([P, D])
            br1 = RA.cut([P, E])
            NEXT_A = RA.at
            w_done = ev["group_done"].base
            halves = "(t b) s -> b t s"

            def of_keys(name, hb, words=S):
                return t[name].rearrange(halves, b=2)[hb].unsqueeze(0).to_broadcast([64, NT, words])

            def of_queries(name):
                return t[name].rearrange("(t b) s -> (b s) t", b=2)
            load("layer1_masks", [(xm[:, :], of_queries("mask_BxS2_fk1")),
                                  (cm[0:64], of_keys("mask_BxS2_fk1", 0)), (cm[64:128], of_keys("mask_BxS2_fk1", 1)),
                                  (bo1[:, :], row(t["L1_xattn_bo"], D)), (br1[:, :], row(t["L1_ffn_b_router"], E))])
            load("layer1_expert_out", [(WoE[:, e, :, :], t["L1_ffn_experts_out"][e].rearrange("(c p) h -> p c h", p=P))
                                       for e in range(E)])

            def mask1(v):
                loaded(v, "layer1_masks")
                own = Own(v, m.own_dve)
                v.tensor_tensor(cm[:, :, :], cm[:, :, :], xm[:, :].unsqueeze(2).to_broadcast([P, NT, S]), ALU.mult).then_inc(own.sem, own.one())
                v.wait_ge(own.sem, own.n)
                v.tensor_scalar(cm[:, :, :], cm[:, :, :], -1.0, 1.0, ALU.mult, ALU.add).then_inc(own.sem, own.one())
                v.wait_ge(own.sem, own.n)
                v.tensor_scalar(cm[:, :, :], cm[:, :, :], 1.0, None, ALU.subtract).then_inc(own.sem, own.one())
                v.wait_ge(own.sem, own.n)
                minus = m.PROB[:, :].rearrange("p (t k) -> p t k", k=S)
                v.tensor_scalar(minus, cm[:, :, :], -1.0, None, ALU.mult).then_inc(own.sem, own.one())
                v.wait_ge(own.sem, own.n)
                v.tensor_tensor(cm[:, :, :], cm[:, :, :], minus, ALU.max).then_inc(own.sem, own.one())
                v.wait_ge(own.sem, own.n)
                v.tensor_scalar(cm[:, :, :], cm[:, :, :], 1e-8 + 1e-5, NEG, ALU.is_le, ALU.mult).then_inc(own.sem, own.one())
                v.wait_ge(own.sem, own.n)
                v.tensor_reduce(valid[:, :], cm[:, :, :], AX.X, ALU.max).then_inc(own.sem, own.one())
                v.wait_ge(own.sem, own.n)
                v.tensor_scalar(valid[:, :], valid[:, :], NEG / 2, None, ALU.is_gt).then_inc(own.sem, own.one())
                v.wait_ge(own.sem, own.n)
                own.restart()
            prog["dve"].append(mask1)
            statistics(X, m.mv, m.rstd, 1e-5)
            prog["pe"].append(lambda p: loaded(p, "layer1_attention"))
            m.cx_phase = 0

            def kv1_piece(j):
                def f(p, bank, i, u):
                    for c in range(4):
                        ins = p.matmul(bank[:, c * P:(c + 1) * P], Wkv1[:, (4 * j + c) * P:(4 * j + c + 1) * P], m.cT[:, :],
                                       start=True, stop=True)
                    return ins
                return f

            def k1_keep(j):
                def f(s, bank, i, u, own):
                    return s.activation(m.KT[:, 4 * j:4 * j + 4, :], bank.rearrange("p (c q) -> p c q", c=4), ACT.Copy)
                return f

            def v1_piece(b):
                def f(p, bank, i, u):
                    w = Wkv1[:, 1024:2048].rearrange("p (c h d) -> p c h d", c=8, h=2)
                    for h in range(2):
                        ins = p.matmul(bank[64 * h:64 * h + 64, :].rearrange("p (c d) -> p c d", c=8),
                                       m.cT[:, 64 * b:64 * b + 64], w[:, :, h, :], start=True, stop=True)
                    return ins
                return f

            def v1_keep(b):
                def f(s, bank, i, u, own):
                    return s.activation(m.V[:, u, b, :], bank, ACT.Copy)
                return f

            def finish_biased(gate, bias):
                def f(v, own, i):
                    v.tensor_tensor(TMPO[:, :], m.OPS[:, 0:128], bias[:, :], ALU.add).then_inc(own.sem, own.one())
                    v.wait_ge(own.sem, own.n)
                    return v.scalar_tensor_tensor(tile_of(X, i), TMPO[:, :], m.tg[:, gate:gate + 1], tile_of(X, i),
                                                  ALU.mult, ALU.add)
                return f

            def next_ctx():
                k = m.cx_phase
                m.cx_phase += 1
                return k * 8 * NT

            run(Attention(ctx="load", cx_base=next_ctx(), many_k=True, scale=64 ** -0.5,
                     mask=lambda i: cm[:, bass.ds(i, 1), :].unsqueeze(1),
                     rowscale=lambda i: valid[:, bass.ds(i, 1)],
                     pieces=[dict(pe=q_piece(Wq1, 0), act=q_keep(0)), dict(pe=q_piece(Wq1, 1), act=q_keep(1)),
                             dict(pe=kv1_piece(0), act=k1_keep(0)), dict(pe=kv1_piece(1), act=k1_keep(1)),
                             dict(pe=v1_piece(0), act=v1_keep(0)), dict(pe=v1_piece(1), act=v1_keep(1))],
                     q_ready=["kept0", "kept1", "kept2", "kept3"], v_ready=["kept4", "kept5"], w_out=Wo1,
                     normalise=normalise(X), finish=finish_biased(1, bo1)))
            barrier()
        if stop >= 5:
            again()
            CAP = int(np.ceil(B * S / E * 1.25))
            statistics(X, m.mv, m.rstd, 1e-5)
            prog["dve"].append(lambda v: loaded(v, "layer1_masks"))
            routing(X, wgT[:, 1, :], None, normalise(X), bias=br1[:, :])
            softmax_and_ranks()
            top2_weights(False)
            s_chosen, s_counted = sem("chosen"), sem("counted")

            def chosen(v):
                own = Own(v, m.own_dve)
                v.tensor_scalar(SEL[:, 0, :], RW[:, :], 0.0, None, ALU.is_gt).then_inc(s_chosen, 1)
                v.wait_ge(s_counted, 1)
                cnt = m.PS[:, 512:640].rearrange("p (t e) -> p t e", e=E)
                a = [m.R1[:, 0:128].rearrange("p (t e) -> p t e", e=E), m.R2[:, 0:128].rearrange("p (t e) -> p t e", e=E)]
                v.tensor_copy(a[0], cnt).then_inc(own.sem, own.one())
                v.wait_ge(own.sem, own.n)
                for k, d in enumerate((1, 2, 4, 8)):
                    x, y = a[k % 2], a[1 - k % 2]
                    v.tensor_copy(y[:, 0:d, :], x[:, 0:d, :]).then_inc(own.sem, own.one())
                    v.tensor_tensor(y[:, d:NT, :], x[:, d:NT, :], x[:, 0:NT - d, :], ALU.add).then_inc(own.sem, own.one())
                    v.wait_ge(own.sem, own.n)
                v.tensor_tensor(a[0], a[0], cnt, ALU.subtract).then_inc(own.sem, own.one())
                v.wait_ge(own.sem, own.n)
                v.tensor_tensor(a[0], a[0], m.PS[:, 0:128].rearrange("p (t e) -> p t e", e=E), ALU.add).then_inc(own.sem, own.one())
                v.wait_ge(own.sem, own.n)
                v.tensor_scalar(m.R1[:, 0:128], m.R1[:, 0:128], float(CAP), None, ALU.is_lt).then_inc(own.sem, own.one())
                v.wait_ge(own.sem, own.n)
                v.tensor_tensor(RW[:, :], RW[:, :], m.R1[:, 0:128], ALU.mult).then_inc(own.sem, own.one())
                v.wait_ge(own.sem, own.n)
                own.restart()
            prog["dve"].append(chosen)

            def count(p):
                p.wait_ge(s_chosen, 1)
                p.matmul(m.PS[:, 0:128], m.before[:, :], SEL[:, 0, :], start=True, stop=True)
                p.matmul(m.PS[:, 512:640], m.ones[:, :], SEL[:, 0, :], start=True, stop=True).then_inc(s_counted, 1)
            prog["pe"].append(count)
            prog["pe"].append(lambda p: (loaded(p, "layer1_experts"), loaded(p, "layer1_expert_out")))
            experts(P, lambda e, c: WiE[:, e, c * P:(c + 1) * P], None, lambda e, c: WoE[:, e, c, :], None,
                    lambda v, dst, i: norm_tile(v, dst, X, i, mv2, m.rstd), 5, None)
            group_barrier()
        if stop >= 6:
            attention_buffers()
            RB.again()
            RA.again()
            TMPO = RA.cut([P, D])
            nat2 = RA.cut([P, 4, D])
            wT2 = RA.cut([P, 4, D])
            bq2, bk2 = RA.cut([P, 1]), RA.cut([P, 1])
            bv2 = RA.cut([P, 64])
            bo2 = RA.cut([P, D])
            QB = RA.cut([P, P])
            wr1, br1c, wr2, br2 = RA.cut([P, 32]), RA.cut([P, 1]), RA.cut([P, E]), RA.cut([P, E])
            hr = RA.cut([P, P])
            wh1, bh1, wh2c, wh2, bh2 = RA.cut([P, 32]), RA.cut([P, 1]), RA.cut([P, 1]), RA.cut([P, P]), RA.cut([P, 1])
            e1, be1 = RA.cut([P, 2, 512]), RA.cut([P, 4])
            e2, be2 = RA.cut([P, 4, 384]), RA.cut([P, 384])
            s1, bs1 = RA.cut([P, 2, 64]), RA.cut([P, 1])
            s2, bs2 = RA.cut([P, 384]), RA.cut([P, 3])
            f1, bf1, f2, bf2 = RA.cut([P, 256]), RA.cut([P, 2]), RA.cut([P, 2, D]), RA.cut([P, 1])
            iw, mu, sw = RA.cut([P, 1]), RA.cut([P, 1]), RA.cut([P, 1])
            wq3, wk3, wv3, wo3, bo3 = (RA.cut([P, D]), RA.cut([P, E, D]), RA.cut([P, E, D]), RA.cut([P, 1, D]),
                                       RA.cut([P, D]))
            kt3, qt3 = RA.cut([P, NT, S]), RA.cut([P, NT])
            pad = RA.cut([P, NT, S])
            BK = RA.cut([P, NT * P])
            cmT = RA.cut([P, E, P])
            nat3 = RA.cut([P, 2, 512])
            pad8 = RA.cut([P, NT * S // 4])
            LEFT_A = RA.at
            tok_row = t["itok_BxS2_0_7"].rearrange("b s -> (b s)")
            load("layer2_attention", [(nat2[:, i, :], t["L2_xattn_W" + n]) for i, n in enumerate("qkvo")]
                 + [(bq2[:, :], col(t["L2_xattn_bq"])), (bk2[:, :], col(t["L2_xattn_bk"])),
                    (bv2[0:64], row(t["L2_xattn_bv"][0:64], 64)[0:64]), (bv2[64:128], row(t["L2_xattn_bv"][64:128], 64)[0:64]),
                    (bo2[:, :], row(t["L2_xattn_bo"], D))])
            A2 = "L2_ffn_"
            load("layer2_ffn", [
                (wr1[:, :], t[A2 + "w_r1"]), (br1c[0:32], col(t[A2 + "b_r1"])), (wr2[0:32], t[A2 + "w_r2"]),
                (br2[:, :], row(t[A2 + "b_r2"], E)), (wh1[:, :], t[A2 + "w_h1"]), (bh1[0:32], col(t[A2 + "b_h1"])),
                (wh2c[0:32], t[A2 + "w_h2"]), (bh2[:, :], row(t[A2 + "b_h2"], 1))]
                + [(e1[:, k, :].rearrange("p (e h) -> p e h", e=E), t[A2 + "expert_w1"].rearrange("e (k p) h -> k p e h", k=2)[k])
                   for k in range(2)]
                + [(be1[:, :], t[A2 + "expert_b1"].rearrange("(c a) h -> (a h) c", a=2)),
                   (e2[:, :, :], t[A2 + "expert_w2"].rearrange("(c a) h o -> (a h) c o", a=2)),
                   (be2[0:E], t[A2 + "expert_b2"]), (be2[E:P], t["const_zeros"][E:P]),
                   (s1[:, :, :], t[A2 + "w_s1"].rearrange("(k p) h -> p k h", p=P)), (bs1[0:64], col(t[A2 + "b_s1"])),
                   (s2[0:64], t[A2 + "w_s2"]), (bs2[:, :], t[A2 + "b_s2"].rearrange("(j p) -> p j", p=P)),
                   (f1[:, :], t[A2 + "w_f1"]), (bf1[:, :], t[A2 + "b_f1"].rearrange("(j p) -> p j", p=P)),
                   (f2[:, :, :], t[A2 + "w_f2"].rearrange("(k p) d -> p k d", p=P)), (bf2[:, :], col(t[A2 + "b_f2"])),
                   (iw[:, :], col(t[A2 + "integration_weight"])), (mu[:, :], col(t[A2 + "mu"])),
                   (sw[:, :], row(t[A2 + "shared_weight"], 1))])
            load("layer3", [
                (wq3[:, :], t["L3_xattn_Wq"]), (wk3[:, :, :], t["L3_xattn_Wk_b"].rearrange("e d k -> d e k")),
                (wv3[:, :, :], t["L3_xattn_Wv_b"].rearrange("e d k -> d e k")), (wo3[:, 0, :], t["L3_xattn_Wo"]),
                (bo3[:, :], row(t["L3_xattn_bo"], D)), (qt3[:, :], of_queries("fside_BxS2_0")),
                (kt3[0:64], of_keys("fside_BxS2_0", 0)), (kt3[64:128], of_keys("fside_BxS2_0", 1)),
                (pad8.bitcast(I32)[0:64].rearrange("p (t k) -> p t k", t=NT), of_keys("mask_BxS2_bf0", 0, S // 4)),
                (pad8.bitcast(I32)[64:128].rearrange("p (t k) -> p t k", t=NT), of_keys("mask_BxS2_bf0", 1, S // 4)),
                (cmT[:, :, :].rearrange("p e q -> p (e q)").bitcast(I32), row(tok_row[0:1024], 1024)),
                (pad[:, :, :].rearrange("p t k -> p (t k)").bitcast(I32), row(tok_row[1024:2048], 1024)),
                (nat3[:, 0, :].rearrange("p (c d) -> p c d", c=4), t["L3_ffn_w1"].rearrange("(c p) d -> p c d", p=P)),
                (nat3[:, 1, :], t["L3_ffn_w2"])])

            prog["pe"].append(lambda p: loaded(p, "layer2_attention"))
            turn([nat2[:, i, :] for i in range(4)], (wT2[:, :, :], flat(4)))
            kept_weights()
            prog["act"].append(lambda s: loaded(s, "layer2_attention"))
            prog["dve"].append(lambda s: loaded(s, "layer2_attention"))
            statistics(X, m.mv, m.rstd, 1e-5)

            def one(w, src):
                def f(p, bank, i, u):
                    return p.matmul(bank[:, 0:P], w, src[:, :], start=True, stop=True)
                return f

            def q_to_buffer(bias):
                def f(s, bank, i, u, own):
                    if bias is None:
                        return s.activation(QB[:, :], bank[:, 0:P], ACT.Copy)
                    return s.activation(QB[:, :], bank[:, 0:P], ACT.Identity, bias=bias)
                return f

            def k_to_buffer(bias):
                def f(s, bank, i, u, own):
                    if bias is None:
                        return s.activation(m.KT[:, 0, :], bank[:, 0:P], ACT.Copy)
                    return s.activation(m.KT[:, 0, :], bank[:, 0:P], ACT.Identity, bias=bias)
                return f

            def split_heads(g, i, u):
                g.wait_ge(ev["kept0"].sem, ev["kept0"].base + i + 1)
                g.tensor_tensor(m.QT[:, :, :], QB[:, :].unsqueeze(1).to_broadcast([P, 8, P]),
                                                     m.own_dims[:, :].unsqueeze(2).to_broadcast([P, 8, P]), ALU.mult).then_inc(ev["q_split"].sem, 1)

            def v2_piece(p, bank, i, u):
                for b in range(2):
                    for h in range(2):
                        ins = p.matmul(bank[64 * h:64 * h + 64, 64 * b:64 * b + 64], m.cT[:, 64 * b:64 * b + 64],
                                       wT2[:, 2, 64 * h:64 * h + 64], start=True, stop=True)
                return ins

            def v2_keep(v, bank, i, u, own):
                return v.tensor_tensor(m.V[:, u, :, 0:64], bank[:, 0:128].rearrange("p (b d) -> p b d", b=2),
                                       bv2[:, :].unsqueeze(1).to_broadcast([P, 2, 64]), ALU.add)
            run(Attention(heads="narrow", ctx="load", cx_base=next_ctx(), scale=float(1 / np.sqrt(np.float32(8))),
                     extra=["q_split"], pool_front=split_heads,
                     pieces=[dict(pe=one(wT2[:, 0, :], m.xT), act=q_to_buffer(bq2[:, :])),
                             dict(pe=one(wT2[:, 1, :], m.cT), act=k_to_buffer(bk2[:, :])),
                             dict(pe=v2_piece, dve=v2_keep)],
                     q_ready=["q_split", "kept1"], v_ready=["kept2"], w_out=wT2[:, 3:4, :],
                     normalise=normalise(X), finish=finish_biased(2, bo2)))
            barrier()
        if stop >= 7:
            again()
            statistics(X, m.mv, m.rstd, 1e-5)
            for eng in ("pe", "act", "dve", "pool"):
                prog[eng].append(lambda x: loaded(x, "layer2_ffn"))
            s_prep = sem("layer2_prepared")

            def prep2_dve(v):
                own = Own(v, m.own_dve)
                v.tensor_scalar(sw[:, :], sw[:, :], 0.5, 0.5, ALU.mult, ALU.add).then_inc(own.sem, own.one())
                v.wait_ge(own.sem, own.n)
                own.restart()

            def prep2_act(s):
                s.activation(sw[:, :], sw[:, :], ACT.Tanh, scale=0.5).then_inc(s_prep, 1)
                s.activation(wh2[0:32, :], wh2c[0:32, 0:1].to_broadcast([32, P]), ACT.Copy).then_inc(s_prep, 1)
                s.activation(bh2[:, :], bh2[:, :], ACT.Copy, scale=0.5).then_inc(s_prep, 1)
                s.activation(hb2[:, :], bs2[:, :], ACT.Copy, scale=0.5).then_inc(s_prep, 1)
            hb2 = sb("hb2", [P, 3])
            prog["act"].append(prep2_act)
            prog["dve"].append(lambda v: v.wait_ge(s_prep, 1))
            prog["dve"].append(prep2_dve)
            prog["pe"].append(lambda p: p.wait_ge(s_prep, 4))
            prog["act"].append(lambda s: s.wait_ge(s_prep, 4))
            routing(X, None, None, normalise(X), bias=br2[:, :], hidden=(wr1[:, :], br1c[0:32], hr[0:32, :], wr2[0:32, :]))
            softmax_and_ranks()
            top2_weights(True)
            WORK.again()
            m.XG = WORK.cut([P, GROUP, D])
            IT, VT = WORK.cut([P, GT]), WORK.cut([P, GT])
            HS, HG = WORK.cut([P, GT]), WORK.cut([P, 4, GT])
            OH, WH = WORK.cut([P, 2, GT]), WORK.cut([P, 2, GT])
            S4 = WORK.cut([P, 4, GROUP * E])
            ERR, XN, H1, TH = (WORK.cut([P, GT]) for _ in range(4))
            F1 = WORK.cut([P, 2, GT])
            RB.again()
            MK = RB.cut([P, 2, 4, GT])
            MH = RB.cut([P, 2, 4, GT])
            RA.at = LEFT_A
            WW, TA, TG = (RA.cut([P, 3, GT]) for _ in range(3))
            ZB, AB = (RA.cut([P, 3, GT]) for _ in range(2))
            per = dict(g_normed=1, g_turned=1, g_T=1, sel_ready=1, sel_turned=1, sel_T=1, spread=10, spread_kept=10,
                       hid=10, hid_gelu=10, masked0=8, masked1=8, steer=6, steer_kept=6, soft=2,
                       x_next=2, refine=6, refine_gelu=6, refined=2, halted=2, it_done=2, fin_turned=1, g_done=1)
            gs = {n: sem("update_" + n) for n in per}

            ahead = ("g_done", "g_turned", "sel_turned")

            def nth(name, g, k):
                return per[name] * g + k + (1 if name in ahead else 0)

            HB = [m.PTP[:, 0:512], m.PTP[:, 512:1024], m.OPS[:, :], m.TPS[:, :], m.RING[:, 0:512]]
            CB = [[m.RING[:, 0:512], m.RING[:, 512:1024], m.PS[:, 0:512]],
                  [m.PS[:, 512:1024], m.PTP[:, 0:512], m.PTP[:, 512:1024]]]

            def pe(p):
                def mm(out, l, r, start=True, stop=True):
                    return p.matmul(out, l, r, start=start, stop=stop)
                with p.Fori(0, NG) as g:
                    p.wait_ge(gs["g_normed"], nth("g_normed", g, 1))
                    p.wait_ge(gs["g_done"], nth("g_done", g, 0))
                    for i in range(GROUP):
                        ins = p.transpose(m.TPS[:, i * P:(i + 1) * P], m.XG[:, i, :], m.ident[:, :])
                    ins.then_inc(gs["g_turned"], 1)
                    p.wait_ge(gs["sel_ready"], nth("sel_ready", g, 1))
                    for k in range(4):
                        bank = (m.RING, m.PS)[k // 2]
                        for i in range(GROUP):
                            o = (k % 2) * 512 + i * P
                            ins = p.transpose(bank[0:E, o:o + P], S4[:, k, i * E:(i + 1) * E], m.ident[:, :])
                    ins.then_inc(gs["sel_turned"], 1)
                    p.wait_ge(gs["sel_T"], nth("sel_T", g, 1))
                    for j in range(10):
                        if j >= 2:
                            p.wait_ge(gs["spread_kept"], nth("spread_kept", g, j - 1))
                        bank = m.RING[:, (j % 2) * 512:(j % 2) * 512 + 512]
                        if j < 8:
                            ins = mm(bank, m.pick[:, (j % 4) * P:(j % 4 + 1) * P], OH[:, j // 4, :])
                        else:
                            ins = mm(bank, m.ones[:, :], WH[:, j - 8, :])
                        ins.then_inc(gs["spread"], 1)
                    p.wait_ge(gs["spread_kept"], nth("spread_kept", g, 10))
                    p.wait_ge(gs["g_T"], nth("g_T", g, 1))
                    for it in range(2):
                        if it:
                            p.wait_ge(gs["it_done"], nth("it_done", g, 1))
                        for j in range(5):
                            for k, c in enumerate((IT, VT)):
                                l = s1[:, k, :] if j == 0 else e1[:, k, (j - 1) * P:j * P]
                                o = HB[j][0:64, :] if j == 0 else HB[j]
                                ins = mm(o, l, c[:, :], start=(k == 0), stop=(k == 1))
                            ins.then_inc(gs["hid"], 1)
                        for r in range(3):
                            if r == 0:
                                p.wait_ge(gs["hid_gelu"], nth("hid_gelu", g, 5 * it + 5))
                            elif r == 1:
                                p.wait_ge(gs["masked0"], nth("masked0", g, 4 * it + 4))
                            else:
                                p.wait_ge(gs["steer_kept"], nth("steer_kept", g, 3 * it + 1))
                                p.wait_ge(gs["masked1"], nth("masked1", g, 4 * it + 4))
                            for j in range(3):
                                bank = CB[r % 2][j]
                                if r == 0:
                                    ins = mm(bank, s2[0:64, j * P:(j + 1) * P], HS[0:64, :])
                                else:
                                    for c in range(4):
                                        mm(bank, e2[:, c, j * P:(j + 1) * P], MH[:, r - 1, c, :], c == 0, False)
                                    ins = mm(bank, be2[:, j * P:(j + 1) * P], OH[:, r - 1, :], False, True)
                            ins.then_inc(gs["steer"], 1)
                        p.wait_ge(gs["x_next"], nth("x_next", g, it + 1))
                        for j in range(3):
                            o, l = (m.TPS[0:32, :], wh1[:, :]) if j == 0 else ((m.OPS, m.PTP)[j - 1][:, 0:512],
                                                                            f1[:, (j - 1) * P:j * P])
                            mm(o, l, XN[:, :]).then_inc(gs["refine"], 1)
                        p.wait_ge(gs["refine_gelu"], nth("refine_gelu", g, 3 * it + 3))
                        mm(m.RING[:, 0:512], wh2[0:32, :], H1[0:32, :])
                        for k in range(2):
                            ins = mm(m.RING[:, 512:1024], f2[:, k, :], F1[:, k, :], k == 0, k == 1)
                        ins.then_inc(gs["refined"], 1)
                    p.wait_ge(gs["it_done"], nth("it_done", g, 2))
                    for i in range(GROUP):
                        ins = p.transpose(m.TPS[:, i * P:(i + 1) * P], IT[:, i * P:(i + 1) * P], m.ident[:, :])
                    ins.then_inc(gs["fin_turned"], 1)

            def act(s):
                with s.Fori(0, NG) as g:
                    s.wait_ge(gs["g_turned"], nth("g_turned", g, 1))
                    s.activation(IT[:, :], m.TPS[:, :], ACT.Copy).then_inc(gs["g_T"], 1)
                    s.wait_ge(gs["sel_turned"], nth("sel_turned", g, 1))
                    s.activation(OH[0:E, :, :], m.RING[0:E, :].rearrange("p (k q) -> p k q", k=2), ACT.Copy)
                    s.activation(WH[0:E, :, :], m.PS[0:E, :].rearrange("p (k q) -> p k q", k=2), ACT.Copy)\
                        .then_inc(gs["sel_T"], 1)
                    for j in range(10):
                        s.wait_ge(gs["spread"], nth("spread", g, j + 1))
                        dst = MK[:, j // 4, j % 4, :] if j < 8 else WW[:, j - 7, :]
                        s.activation(dst, m.RING[:, (j % 2) * 512:(j % 2) * 512 + 512], ACT.Copy)\
                            .then_inc(gs["spread_kept"], 1)
                    for it in range(2):
                        for j in range(5):
                            s.wait_ge(gs["hid"], nth("hid", g, 5 * it + j + 1))
                            if j == 0:
                                ins = s.activation(HS[0:64, :], HB[0][0:64, :], ACT.Gelu, bias=bs1[0:64])
                            else:
                                ins = s.activation(HG[:, j - 1, :], HB[j], ACT.Gelu, bias=be1[:, j - 1:j])
                            ins.then_inc(gs["hid_gelu"], 1)
                        for r in range(3):
                            s.wait_ge(gs["steer"], nth("steer", g, 3 * it + r + 1))
                            a, b, c = CB[r % 2]
                            if r == 0:
                                s.activation(TA[:, r, :], a, ACT.Tanh, bias=hb2[:, 0:1], scale=0.5)
                                s.activation(TG[:, r, :], c, ACT.Tanh, bias=hb2[:, 2:3], scale=0.5)
                                ins = s.activation(ZB[:, r, :], b, ACT.Identity, bias=bs2[:, 1:2])
                            else:
                                s.activation(TA[:, r, :], a, ACT.Tanh, scale=0.5)
                                s.activation(TG[:, r, :], c, ACT.Tanh, scale=0.5)
                                ins = s.activation(ZB[:, r, :], b, ACT.Copy)
                            ins.then_inc(gs["steer_kept"], 1)
                        s.preload_act_table_set("natural_log_exp_and_others")
                        s.wait_ge(gs["steer_kept"], per["steer_kept"] * g + 3 * it + 3)
                        s.activation(AB[:, :, :], ZB[:, :, :], ACT.Abs).then_inc(m.own_act, 1)
                        s.wait_ge(m.own_act, 1)
                        s.activation(AB[:, :, :], AB[:, :, :], ACT.Exp, scale=-1.0).then_inc(m.own_act, 1)
                        s.wait_ge(m.own_act, 2)
                        s.activation(AB[:, :, :], AB[:, :, :], ACT.Ln, bias=1.0).then_inc(gs["soft"], 1)
                        s.sem_clear(m.own_act)
                        for j in range(3):
                            s.wait_ge(gs["refine"], nth("refine", g, 3 * it + j + 1))
                            if j == 0:
                                ins = s.activation(H1[0:32, :], m.TPS[0:32, :], ACT.Gelu, bias=bh1[0:32])
                            else:
                                ins = s.activation(F1[:, j - 1, :], (m.OPS, m.PTP)[j - 1][:, 0:512], ACT.Gelu,
                                                   bias=bf1[:, j - 1:j])
                            ins.then_inc(gs["refine_gelu"], 1)
                        s.wait_ge(gs["refined"], nth("refined", g, it + 1))
                        s.activation(TH[:, :], m.RING[:, 0:512], ACT.Tanh, bias=bh2[:, 0:1], scale=0.5)\
                            .then_inc(gs["halted"], 1)

            def dve(v):
                own = Own(v, m.own_dve)
                v.memset(OH[:, :, :], 0.0).then_inc(gs["g_done"], 1)
                v.memset(WH[:, :, :], 0.0).then_inc(gs["g_turned"], 1)
                v.memset(WW[:, 0, :], 0.0).then_inc(gs["sel_turned"], 1)
                for name in ahead:
                    v.wait_ge(gs[name], 1)
                v.tensor_scalar(WW[:, 0, :], WW[:, 0, :], sw[:, 0:1], None, ALU.add).then_inc(own.sem, own.one())
                own.restart()
                half = 0.5
                with v.Fori(0, NG) as g:
                    v.wait_ge(gs["g_turned"], nth("g_turned", g, 0))
                    for i in range(GROUP):
                        ins = norm_tile(v, m.XG[:, i, :], X, 4 * g + i, mv2, m.rstd)
                    ins.then_inc(gs["g_normed"], 1)
                    v.memset(VT[:, :], 0.0).then_inc(own.sem, own.one())
                    v.wait_ge(gs["sel_turned"], nth("sel_turned", g, 0))
                    for k in range(2):
                        sel = SEL[:, k, bass.ds(g * GROUP * E, GROUP * E)]
                        v.tensor_scalar(S4[:, k, :], sel, 1.0, None, ALU.mult)
                        ins = v.tensor_tensor(S4[:, 2 + k, :], sel, RW[:, bass.ds(g * GROUP * E, GROUP * E)], ALU.mult)
                    ins.then_inc(gs["sel_ready"], 1)
                    v.wait_ge(gs["spread_kept"], nth("spread_kept", g, 10))
                    v.tensor_tensor(TA[:, 1:3, :], WW[:, 1:3, :],
                                             sw[:, 0:1].unsqueeze(1).to_broadcast([P, 2, GT]), ALU.mult).then_inc(own.sem, own.one())
                    v.wait_ge(own.sem, own.n)
                    v.tensor_tensor(WW[:, 1:3, :], WW[:, 1:3, :], TA[:, 1:3, :], ALU.subtract).then_inc(own.sem, own.one())
                    v.wait_ge(own.sem, own.n)
                    own.restart()
                    for it in range(2):
                        for c in range(4):
                            v.wait_ge(gs["hid_gelu"], nth("hid_gelu", g, 5 * it + c + 2))
                            v.tensor_tensor(MH[:, 0, c, :], HG[:, c, :], MK[:, 0, c, :], ALU.mult).then_inc(gs["masked0"], 1)

                        def wide(x):
                            return x.unsqueeze(1).to_broadcast([P, 3, GT])
                        v.tensor_scalar(ERR[:, :], IT[:, :], mu[:, 0:1], None, ALU.subtract).then_inc(own.sem, own.one())
                        v.wait_ge(gs["steer_kept"], nth("steer_kept", g, 3 * it + 3))
                        v.tensor_scalar(TA[:, :, :], TA[:, :, :], half, half, ALU.mult, ALU.add).then_inc(own.sem, own.one())
                        v.tensor_scalar(TG[:, :, :], TG[:, :, :], 0.05, 0.05, ALU.mult, ALU.add).then_inc(own.sem, own.one())
                        v.wait_ge(own.sem, own.n)
                        v.tensor_tensor(TA[:, :, :], TA[:, :, :], wide(VT[:, :]), ALU.mult).then_inc(own.sem, own.one())
                        v.wait_ge(own.sem, own.n)
                        v.wait_ge(gs["soft"], nth("soft", g, it + 1))
                        z2 = ZB[:, :, :].rearrange("p r q -> p (r q)")
                        a2 = AB[:, :, :].rearrange("p r q -> p (r q)")
                        v.scalar_tensor_tensor(z2, z2, 0.0, a2, ALU.max, ALU.add).then_inc(own.sem, own.one())
                        v.wait_ge(own.sem, own.n)
                        v.tensor_tensor(ZB[:, :, :], ZB[:, :, :], wide(ERR[:, :]), ALU.mult).then_inc(own.sem, own.one())
                        v.wait_ge(own.sem, own.n)
                        v.tensor_tensor(TA[:, :, :], TA[:, :, :], ZB[:, :, :], ALU.subtract).then_inc(own.sem, own.one())
                        v.wait_ge(own.sem, own.n)
                        v.tensor_tensor(TG[:, :, :], TG[:, :, :], TA[:, :, :], ALU.mult).then_inc(own.sem, own.one())
                        v.wait_ge(own.sem, own.n)
                        v.tensor_tensor(TG[:, :, :], TG[:, :, :], wide(IT[:, :]), ALU.add).then_inc(own.sem, own.one())
                        v.wait_ge(own.sem, own.n)
                        v.tensor_tensor(TG[:, :, :], TG[:, :, :], WW[:, :, :], ALU.mult).then_inc(own.sem, own.one())
                        v.wait_ge(own.sem, own.n)
                        v.tensor_tensor(XN[:, :], TG[:, 0, :], TG[:, 1, :], ALU.add).then_inc(own.sem, own.one())
                        v.wait_ge(own.sem, own.n)
                        v.tensor_tensor(XN[:, :], XN[:, :], TG[:, 2, :], ALU.add).then_inc(gs["x_next"], 1)
                        v.tensor_tensor(TA[:, :, :], TA[:, :, :], WW[:, :, :], ALU.mult).then_inc(own.sem, own.one())
                        v.wait_ge(own.sem, own.n)
                        v.tensor_tensor(VT[:, :], TA[:, 0, :], TA[:, 1, :], ALU.add).then_inc(own.sem, own.one())
                        v.wait_ge(own.sem, own.n)
                        v.tensor_tensor(VT[:, :], VT[:, :], TA[:, 2, :], ALU.add).then_inc(own.sem, own.one())
                        v.wait_ge(own.sem, own.n)
                        v.wait_ge(gs["halted"], nth("halted", g, it + 1))
                        v.tensor_scalar(TH[:, :], TH[:, :], half, half, ALU.mult, ALU.add).then_inc(own.sem, own.one())
                        v.wait_ge(own.sem, own.n)
                        v.scalar_tensor_tensor(TH[:, :], m.RING[:, 512:1024], bf2[:, 0:1], TH[:, :], ALU.add, ALU.mult).then_inc(own.sem, own.one())
                        v.wait_ge(own.sem, own.n)
                        v.scalar_tensor_tensor(IT[:, :], TH[:, :], iw[:, 0:1], IT[:, :], ALU.mult, ALU.add)\
                            .then_inc(gs["it_done"], 1)
                        own.restart()
                        v.wait_ge(gs["it_done"], per["it_done"] * g + it + 1)
                    v.wait_ge(gs["fin_turned"], nth("fin_turned", g, 1))
                    v.scalar_tensor_tensor(tile_of(X, g, GT), m.TPS[:, :], m.tg[:, 6:7], tile_of(X, g, GT),
                                           ALU.mult, ALU.add).then_inc(gs["g_done"], 1)
                v.wait_ge(gs["g_done"], NG + 1)

            def pool(q):
                with q.Fori(0, NG) as g:
                    for it in range(2):
                        for c in range(4):
                            q.wait_ge(gs["hid_gelu"], nth("hid_gelu", g, 5 * it + c + 2))
                            q.tensor_tensor(MH[:, 1, c, :], HG[:, c, :], MK[:, 1, c, :], ALU.mult).then_inc(gs["masked1"], 1)
            for k, f in (("pe", pe), ("act", act), ("dve", dve), ("pool", pool)):
                prog[k].append(f)
            for k in prog:
                prog[k].append(lambda eng: eng.wait_ge(gs["g_done"], NG + 1))
        if stop >= 8:
            attention_buffers()
            RB.again()
            IWT1 = RB.cut([P, 256]).bitcast(BF16)
            IWT2 = RB.cut([P, 256]).bitcast(BF16)
            AW = RB.cut([P, 2, 512])
            sums3, s3, r3 = RB.cut([P, 2]), RB.cut([P, 2]), RB.cut([P, 2])
            s_abs, s_total = sem("magnitudes_summed"), sem("magnitudes_totalled")

            def prep3(v):
                loaded(v, "layer3")
                own = Own(v, m.own_dve)
                flat_cm = cmT[:, :, :].rearrange("p e q -> p (e q)")
                flat_pad = pad[:, :, :].rearrange("p t k -> p (t k)")
                v.tensor_copy(BK[:, 0:1024], flat_cm.bitcast(I32)).then_inc(own.sem, own.one())
                v.tensor_copy(BK[:, 1024:2048], flat_pad.bitcast(I32)).then_inc(own.sem, own.one())
                v.wait_ge(own.sem, own.n)
                v.tensor_copy(flat_pad, pad8.bitcast(U8)).then_inc(own.sem, own.one())
                v.tensor_tensor(kt3[:, :, :], qt3[:, :].unsqueeze(2).to_broadcast([P, NT, S]), kt3[:, :, :],
                                         ALU.subtract).then_inc(own.sem, own.one())
                v.wait_ge(own.sem, own.n)
                v.tensor_scalar(kt3[:, :, :], kt3[:, :, :], 0.0, None, ALU.is_lt).then_inc(own.sem, own.one())
                v.wait_ge(own.sem, own.n)
                v.tensor_tensor(kt3[:, :, :], kt3[:, :, :], pad[:, :, :], ALU.max).then_inc(own.sem, own.one())
                v.wait_ge(own.sem, own.n)
                v.tensor_scalar(kt3[:, :, :], kt3[:, :, :], -NEG, NEG, ALU.mult, ALU.add).then_inc(own.sem, own.one())
                v.wait_ge(own.sem, own.n)
                v.tensor_scalar(AW[:, :, :], nat3[:, :, :], -1.0, None, ALU.mult).then_inc(own.sem, own.one())
                v.wait_ge(own.sem, own.n)
                v.tensor_tensor(AW[:, :, :], AW[:, :, :], nat3[:, :, :], ALU.max).then_inc(own.sem, own.one())
                v.wait_ge(own.sem, own.n)
                v.tensor_reduce(sums3[:, :], AW[:, :, :], AX.X, ALU.add).then_inc(s_abs, 1)
                v.wait_ge(s_total, 1)
                v.tensor_scalar(s3[:, :], m.OPS[:, 0:2], 1.0 / (512 * D), 1e-5, ALU.mult, ALU.max).then_inc(own.sem, own.one())
                v.wait_ge(own.sem, own.n)
                v.reciprocal(r3[:, :], s3[:, :]).then_inc(own.sem, own.one())
                v.wait_ge(own.sem, own.n)
                v.tensor_tensor(nat3[:, :, :], nat3[:, :, :], r3[:, :].unsqueeze(2).to_broadcast([P, 2, 512]),
                                         ALU.mult).then_inc(own.sem, own.one())
                v.wait_ge(own.sem, own.n)
                v.tensor_scalar(nat3[:, :, :], nat3[:, :, :], MAGIC, MAGIC, ALU.add, ALU.subtract).then_inc(own.sem, own.one())
                v.wait_ge(own.sem, own.n)
                v.tensor_scalar(nat3[:, :, :], nat3[:, :, :], -1.0, 1.0, ALU.max, ALU.min).then_inc(own.sem, own.one())
                v.wait_ge(own.sem, own.n)
                v.tensor_scalar(s3[:, :], s3[:, :], 1.0 / 127.0, None, ALU.mult).then_inc(own.sem, own.one())
                v.wait_ge(own.sem, own.n)
                v.tensor_tensor(s3[:, 1:2], s3[:, 1:2], m.tg[:, 7:8], ALU.mult).then_inc(s_quant, 1)
                v.wait_ge(s_quant, n_q3)
                own.restart()

            def total3(p):
                loaded(p, "layer3")
                p.wait_ge(s_abs, 1)
                p.matmul(m.OPS[:, 0:2], m.ones[:, :], sums3[:, :], start=True, stop=True).then_inc(s_total, 1)
                p.wait_ge(s_quant, n_q3)
            n_q3 = m.n_quant = m.n_quant + 1
            prog["dve"].append(prep3)
            prog["pe"].append(total3)
            turn([nat3[:, 0, c * P:(c + 1) * P] for c in range(4)], (IWT1, lambda b: b))
            turn([nat3[:, 1, c * P:(c + 1) * P] for c in range(4)], (IWT2, lambda b: b))
            kept_weights()
            statistics(X, m.mv, m.rstd, 1e-5)

            def masked_context(v, own, i, u):
                v.wait_ge(ev["xT"].sem, ev["xT"].base + i + 1)
                for e in range(E):
                    ins = v.scalar_tensor_tensor(cmT[:, e, :], BK[:, bass.ds(i * P, P)], float(e), m.cT[:, :],
                                                 ALU.is_equal, ALU.mult)
                ins.then_inc(ev["masked_ctx"].sem, 1)

            def k3_piece(p, bank, i, u):
                for e in range(E):
                    ins = p.matmul(bank[:, 0:P], wk3[:, e, :], cmT[:, e, :], start=(e == 0), stop=(e == E - 1))
                return ins

            def v3_piece(p, bank, i, u):
                for b in range(2):
                    for h in range(2):
                        for e in range(E):
                            ins = p.matmul(bank[64 * h:64 * h + 64, 64 * b:64 * b + 64], cmT[:, e, 64 * b:64 * b + 64],
                                           wv3[:, e, 64 * h:64 * h + 64], start=(e == 0), stop=(e == E - 1))
                return ins

            def v3_keep(s, bank, i, u, own):
                return s.activation(m.V[:, u, :, 0:64], bank[:, 0:128].rearrange("p (b d) -> p b d", b=2), ACT.Copy)
            run(Attention(heads="narrow", ctx="load", cx_base=next_ctx(), scale=float(1 / np.sqrt(np.float32(8))),
                     extra=["q_split", "masked_ctx"], pool_front=split_heads, dve_front=masked_context,
                     mask=lambda i: kt3[:, bass.ds(i, 1), :].unsqueeze(1),
                     pieces=[dict(pe=one(wq3, m.xT), act=q_to_buffer(None)),
                             dict(pe=k3_piece, act=k_to_buffer(None), needs=["masked_ctx"]),
                             dict(pe=v3_piece, act=v3_keep)],
                     q_ready=["q_split", "kept1"], v_ready=["kept2"], w_out=wo3,
                     normalise=normalise(X), finish=finish_biased(3, bo3)))
            barrier()

        if stop >= 9:
            statistics(X, m.mv, m.rstd, 1e-5)
            bits = {n: sem("ternary_" + n) for n in ("rows_quantised", "rows_turned", "rows_kept", "up", "hidden",
                                                     "hidden_quantised", "hidden_turned", "hidden_kept", "down", "done")}
            XQ = RB.cut([P, 2, D])
            HQ = RB.cut([P, 2, 512])
            XQT = RB.cut([P, P // 2]).bitcast(BF16)
            HQT = RB.cut([P, 256]).bitcast(BF16)
            q3 = RB.cut([P, 2, 8])

            def eight_bits(v, own, x, u, col0, s):
                hi, lo, inv, sc = [q3[:, u, k:k + 1] for k in (4, 5, 6)] + [q3[:, u, col0:col0 + 1]]
                v.tensor_reduce(hi, x, AX.X, ALU.max).then_inc(own.sem, own.one())
                v.tensor_reduce(lo, x, AX.X, ALU.min).then_inc(own.sem, own.one())
                v.wait_ge(own.sem, own.n)
                v.scalar_tensor_tensor(hi, lo, -1.0, hi, ALU.mult, ALU.max).then_inc(own.sem, own.one())
                v.wait_ge(own.sem, own.n)
                v.tensor_scalar(hi, hi, 1e-5, None, ALU.max).then_inc(own.sem, own.one())
                v.wait_ge(own.sem, own.n)
                v.tensor_tensor(sc, hi, s, ALU.mult).then_inc(own.sem, own.one())
                v.reciprocal(inv, hi).then_inc(own.sem, own.one())
                v.wait_ge(own.sem, own.n)
                v.tensor_scalar(inv, inv, 127.0, None, ALU.mult).then_inc(own.sem, own.one())
                v.wait_ge(own.sem, own.n)
                v.tensor_scalar(x, x, inv, MAGIC, ALU.mult, ALU.add).then_inc(own.sem, own.one())
                v.wait_ge(own.sem, own.n)
                v.tensor_scalar(x, x, MAGIC, -128.0, ALU.subtract, ALU.max).then_inc(own.sem, own.one())
                v.wait_ge(own.sem, own.n)
                return v.tensor_scalar(x, x, 127.0, None, ALU.min)

            def pe(p):
                def step(n, u, on):
                    if on[1]:
                        t, w = n + 1, 1 - u
                        p.wait_ge(bits["rows_quantised"], t + 1)
                        if some(t):
                            p.wait_ge(bits["rows_kept"], t)
                        p.transpose(m.TPS[:, 0:P], XQ[:, w, :], m.ident[:, :]).then_inc(bits["rows_turned"], 1)
                    if on[0]:
                        t = n
                        p.wait_ge(bits["hidden_quantised"], t + 1)
                        if some(t):
                            p.wait_ge(bits["hidden_kept"], t)
                        for c in range(4):
                            ins = p.transpose(m.PS[:, c * P:(c + 1) * P], HQ[:, u, c * P:(c + 1) * P], m.ident[:, :])
                        ins.then_inc(bits["hidden_turned"], 1)
                    if on[1]:
                        t, w = n + 1, 1 - u
                        p.wait_ge(bits["rows_kept"], t + 1)
                        if some(t - 1):
                            p.wait_ge(bits["hidden"], t - 1)
                        p.matmul(m.RING[:, w * 512:w * 512 + 512], XQT, IWT1, start=True, stop=True).then_inc(bits["up"], 1)
                    if on[0]:
                        t = n
                        p.wait_ge(bits["hidden_kept"], t + 1)
                        if some(t):
                            p.wait_ge(bits["done"], t)
                        for c in range(4):
                            ins = p.matmul(m.OPS[:, 0:D], HQT[:, c * P:(c + 1) * P], IWT2[:, c * P:(c + 1) * P],
                                           start=(c == 0), stop=(c == 3))
                        ins.then_inc(bits["down"], 1)
                pipeline(p, None, step)

            def act(s):
                def step(n, u, on):
                    if on[1]:
                        if some(n + 2):
                            s.wait_ge(bits["rows_turned"], n + 2)
                        if some(n + 1):
                            s.wait_ge(bits["up"], n + 1)
                        s.activation(XQT, m.TPS[:, 0:P], ACT.Copy).then_inc(bits["rows_kept"], 1)
                    if on[0]:
                        if some(n + 1):
                            s.wait_ge(bits["hidden_turned"], n + 1)
                        if some(n):
                            s.wait_ge(bits["down"], n)
                        s.activation(HQT, m.PS[:, 0:512], ACT.Copy).then_inc(bits["hidden_kept"], 1)
                    if on[1]:
                        t, w = n + 1, 1 - u
                        s.wait_ge(bits["up"], t + 1)
                        if some(t - 1):
                            s.wait_ge(bits["hidden_turned"], t - 1)
                        s.activation(HQ[:, w, :], m.RING[:, w * 512:w * 512 + 512], ACT.Gelu, scale=q3[:, w, 0:1])\
                            .then_inc(bits["hidden"], 1)
                pipeline(s, None, step)

            def dve(v):
                own = Own(v, m.own_dve)

                def step(n, u, on):
                    if on[2]:
                        t = n + 2
                        if some(t - 1):
                            v.wait_ge(bits["rows_turned"], t - 1)
                        if some(t - 1):
                            v.wait_ge(bits["hidden"], t - 1)
                        norm_tile(v, XQ[:, u, :], X, t, mv2, m.rstd).then_inc(own.sem, own.one())
                        v.wait_ge(own.sem, own.n)
                        eight_bits(v, own, XQ[:, u, :], u, 0, s3[:, 0:1]).then_inc(bits["rows_quantised"], 1)
                    if on[0]:
                        t = n
                        v.wait_ge(bits["down"], t + 1)
                        v.scalar_tensor_tensor(tile_of(X, t), m.OPS[:, 0:D], q3[:, u, 1:2], tile_of(X, t),
                                               ALU.mult, ALU.add).then_inc(bits["done"], 1)
                    if on[1]:
                        t, w = n + 1, 1 - u
                        v.wait_ge(bits["hidden"], t + 1)
                        eight_bits(v, own, HQ[:, w, :], w, 1, s3[:, 1:2]).then_inc(bits["hidden_quantised"], 1)
                pipeline(v, own, step)
            for k, f in (("pe", pe), ("act", act), ("dve", dve)):
                prog[k].append(f)
            for k in prog:
                prog[k].append(lambda eng: eng.wait_ge(bits["done"], NT))
        src = XIN if stop in (0, 2) else X

        def store(q):
            q.dma_start(out.rearrange("(t b) s d -> (b s) t d", b=TILE_B), src[:, :].rearrange("p (t d) -> p t d", d=D))\
                .then_inc(s_stored, 16)
            q.wait_ge(s_stored, 16)
        prog["sp"].append(store)

        block = ctx.enter_context(nc.Block())

        @block.sync
        def _(eng):
            for f in prog["sp"]:
                f(eng)

        @block.scalar
        def _(eng):
            for f in prog["act"]:
                f(eng)

        @block.vector
        def _(eng):
            for f in prog["dve"]:
                f(eng)

        @block.gpsimd
        def _(eng):
            for f in prog["pool"]:
                f(eng)

        @block.tensor
        def _(eng):
            for f in prog["pe"]:
                f(eng)


def kernel(**inputs):
    import concourse.bacc as _bacc
    from concourse.bass_utils import run_bass_kernel_spmd as _run

    nc = _bacc.Bacc("TRN2", target_bir_lowering=False, num_devices=1)
    arrays, aps = {}, {}
    given = {name: np.ascontiguousarray(a) for name, a in inputs.items()}
    given.update({"const_" + name: a for name, a in CONST.items()})
    for name, a in given.items():
        if a.dtype == np.bool_:
            a = a.view(np.int32)
        if a.ndim == 0:
            a = a.reshape(1)
        arrays[f"in_{name}"] = a
        aps[name] = nc.dram_tensor(f"in_{name}", a.shape, mybir.dt.from_np(a.dtype), kind="ExternalInput").ap()
    out = nc.dram_tensor("out_x", (B, S, D), F32, kind="ExternalOutput").ap()
    program(nc, aps, out)
    r = _run(nc, [arrays], core_ids=[0])
    return r.results[0]["out_x"]
```

```python
from contextlib import ExitStack

import concourse.bass as bass
from concourse import mybir
import numpy as np

ALU = mybir.AluOpType
ACT = mybir.ActivationFunctionType
AX = mybir.AxisListType
F32 = mybir.dt.float32
BF16 = mybir.dt.bfloat16
I32 = mybir.dt.int32
U8 = mybir.dt.uint8

P = 128
D = 128
B, S = 32, 64
TILE_B = P // S
NT = B // TILE_B
H = 16
E = 8
NEG = -1.0e30
GROUP = 4
NG = NT // GROUP
GT = GROUP * P


def some(count):
    return not isinstance(count, int) or count > 0


class Own:

    def __init__(self, eng, sem):
        self.eng, self.sem, self.n = eng, sem, 0

    def one(self):
        self.n += 1
        return 1

    def restart(self):
        if self.n:
            self.eng.wait_ge(self.sem, self.n)
            self.eng.sem_clear(self.sem)
            self.n = 0


class Machine:
    pass


class Attention:

    def __init__(self, pieces, scale, w_out, normalise, finish, q_ready=(), v_ready=(), heads="pair", many_k=False,
                 ctx="none", cx_base=0, extra=(), x_gain=None, c_gain=None, mask=None, rowscale=None, dve_front=None,
                 pool_front=None, more_out=None):
        self.pieces, self.scale, self.q_ready, self.v_ready, self.w_out = pieces, scale, q_ready, v_ready, w_out
        self.normalise, self.finish, self.heads, self.many_k = normalise, finish, heads, many_k
        self.ctx, self.cx_base, self.extra, self.x_gain, self.c_gain = ctx, cx_base, extra, x_gain, c_gain
        self.mask, self.rowscale, self.dve_front, self.pool_front = mask, rowscale, dve_front, pool_front
        self.more_out = more_out


def pipeline(eng, own, step):
    def static(n):
        step(n, n % 2, [0 <= n + k < NT for k in range(3)])
        if own:
            own.restart()
    for n in range(-2, 2):
        static(n)
    with eng.Fori(1, NT // 2 - 1) as i:
        for u in range(2):
            step(2 * i + u, u, [True] * 3)
            if own:
                own.restart()
    for n in range(NT - 2, NT):
        static(n)


class Event:

    def __init__(self, sem):
        self.sem, self.base = sem, 0


def attention(m, a):
    ev = m.ev
    used = ["xn", "x_turned", "xT", "scores", "shifted", "exped", "rinv", "probs", "p_turned", "pT",
            "pv", "oT", "out", "done"]
    used += ["piece%d" % j for j in range(len(a.pieces))] + ["kept%d" % j for j in range(len(a.pieces))]
    used += list(a.extra)
    if a.heads == "narrow":
        used += ["o_turned", "onat"]
    npc = len(a.pieces)
    banks = [piece.get("bank", m.RING[:, (j % 2) * 512:(j % 2) * 512 + 512]) for j, piece in enumerate(a.pieces)]
    nb = 4 if a.heads == "wide" else 8
    nh = 2 * nb
    per = 1 if a.heads == "narrow" else 2
    PSv = (m.PS[:, 0:512].rearrange("q (c p k) -> q c p k", c=4, p=2) if a.heads == "wide"
           else m.PS[:, :].rearrange("q (p c k) -> q c p k", p=2, c=8))
    Pv = m.PROB[:, 0:nb * 128].rearrange("q (c p k) -> q c p k", c=nb, p=2)
    mx = m.mx[:, 0:nh].rearrange("q (c p) -> q c p", p=2)
    rs = m.rs[:, 0:nh].rearrange("q (c p) -> q c p", p=2)

    def bk(ap):
        return ap.unsqueeze(3).to_broadcast([128, nb, 2, S])

    def pe(p):
        def turn_input(t, v):
            p.wait_ge(ev["xn"].sem, ev["xn"].base + t + 1)
            if a.ctx == "load":
                p.wait_ge(m.cx_loaded[v], a.cx_base + 8 * t - 8 * v + 16)
            if some(t):
                p.wait_ge(ev["xT"].sem, ev["xT"].base + t)
            ins = p.transpose(m.TPS[:, 0:128], m.xn[:, v, :], m.ident[:, :])
            if a.ctx != "none":
                ins = p.transpose(m.TPS[:, 128:256], m.cx[:, v, :], m.ident[:, :])
            ins.then_inc(ev["x_turned"].sem, 1)

        def projections(t, v):
            p.wait_ge(ev["xT"].sem, ev["xT"].base + t + 1)
            if some(t - 1):
                p.wait_ge(ev["oT"].sem, ev["oT"].base + per * (t - 1))
                if a.heads == "narrow":
                    p.wait_ge(ev["onat"].sem, ev["onat"].base + t - 1)
            for j, piece in enumerate(a.pieces):
                before = piece.get("bank_after", j - 2)
                if before >= 0:
                    p.wait_ge(ev["kept%d" % before].sem, ev["kept%d" % before].base + t + 1)
                for w in piece.get("needs", []):
                    p.wait_ge(ev[w].sem, ev[w].base + t + 1)
                piece["pe"](p, banks[j], t, v).then_inc(ev["piece%d" % j].sem, 1)

        def turn_probs(t):
            p.wait_ge(ev["probs"].sem, ev["probs"].base + t + 1)
            if some(t):
                p.wait_ge(ev["pT"].sem, ev["pT"].base + t)
            for c in range(nb):
                ins = p.transpose(m.PTP[:, c * 128:(c + 1) * 128], m.PROB[:, c * 128:(c + 1) * 128], m.ident[:, :])
            ins.then_inc(ev["p_turned"].sem, 1)

        def turn_keys(t):
            p.wait_ge(ev["knat"].sem, ev["knat"].base + t + 1)
            if some(t):
                p.wait_ge(ev["kT"].sem, ev["kT"].base + t)
            for g in range(2):
                ins = p.transpose(m.PTP[:, 512 + g * 128:640 + g * 128], m.KN[:, g * 128:(g + 1) * 128], m.ident[:, :])
            ins.then_inc(ev["k_turned"].sem, 1)

        def scores(t):
            for w in a.q_ready:
                p.wait_ge(ev[w].sem, ev[w].base + t + 1)
            if some(t):
                p.wait_ge(ev["shifted"].sem, ev["shifted"].base + t)
            m.hold(p)
            for c in range(nb):
                if a.heads == "wide":
                    for b in range(2):
                        ins = p.matmul(m.PS[:, (2 * c + b) * 64:(2 * c + b) * 64 + 64],
                                       m.QW[:, (4 * b + c) * P:(4 * b + c + 1) * P],
                                       m.KT[:, c // 2, 64 * b:64 * b + 64], start=True, stop=True)
                else:
                    for h in range(2):
                        for b in range(2):
                            r = slice(64 * h, 64 * h + 64)
                            ins = p.matmul(m.PS[64 * b:64 * b + 64, h * 512 + c * 64:h * 512 + c * 64 + 64],
                                           m.QT[r, c, 64 * b:64 * b + 64],
                                           m.KT[r, c if a.many_k else 0, 64 * b:64 * b + 64], start=True, stop=True)
            ins.then_inc(ev["scores"].sem, 1)

        def values(t, u, next_too):
            p.wait_ge(ev["pT"].sem, ev["pT"].base + t + 1)
            ring = ["kept%d" % j for j in range(max(0, npc - 2), npc)] if next_too else []
            for w in ring:
                p.wait_ge(ev[w].sem, ev[w].base + t + 2)
            for w in a.v_ready:
                if w not in ring:
                    p.wait_ge(ev[w].sem, ev[w].base + t + 1)
            if some(t):
                if a.heads == "narrow":
                    p.wait_ge(ev["onat"].sem, ev["onat"].base + t)
                p.wait_ge(ev["oT"].sem, ev["oT"].base + per * t)
            m.hold(p)
            for k in range(per):
                if a.heads == "wide":
                    r = slice(64 * k, 64 * k + 64)
                    for g in range(2):
                        ins = p.matmul(m.RING[:, k * 512 + g * 256:k * 512 + g * 256 + 256], m.VW[r, u, g, :],
                                       m.PT[r, 2 * g:2 * g + 2, :], start=True, stop=True)
                elif a.heads == "pair" and not a.many_k:
                    bank = m.RING[:, k * 512:k * 512 + 512].rearrange("p (c q) -> p c q", c=4)
                    for b in range(2):
                        for h in range(2):
                            r = slice(64 * h, 64 * h + 64)
                            ins = p.matmul(bank[r, :, 64 * b:64 * b + 64], m.V[r, u, b, 0:64],
                                           m.PT[r, 4 * k:4 * k + 4, 64 * b:64 * b + 64], start=True, stop=True)
                elif a.heads == "pair":
                    for c in range(4 * k, 4 * k + 4):
                        for b in range(2):
                            for h in range(2):
                                r = slice(64 * h, 64 * h + 64)
                                ins = p.matmul(m.RING[r, c * 128 + 64 * b:c * 128 + 64 * b + 64],
                                               m.V[r, u, b, c * 64:c * 64 + 64], m.PT[r, c, 64 * b:64 * b + 64],
                                               start=True, stop=True)
                else:
                    for c in range(nb):
                        for h in range(2):
                            for b in range(2):
                                r = slice(64 * h, 64 * h + 64)
                                ins = p.matmul(m.RING[64 * b:64 * b + 64, h * 512 + c * 8:h * 512 + c * 8 + 8],
                                               m.PT[r, c, 64 * b:64 * b + 64], m.V[r, u, b, c * 8:c * 8 + 8],
                                               start=True, stop=True)
                ins.then_inc(ev["pv"].sem, 1)

        def turn_outputs(t):
            p.wait_ge(ev["onat"].sem, ev["onat"].base + t + 1)
            if some(t):
                p.wait_ge(ev["done"].sem, ev["done"].base + t)
            p.transpose(m.OPS[:, 128:256], m.ON[:, :], m.ident[:, :]).then_inc(ev["o_turned"].sem, 1)

        def output(t, u):
            if some(t):
                p.wait_ge(ev["done"].sem, ev["done"].base + t)
            mats = a.more_out(u) if a.more_out else []
            n_more = len(mats)
            n_out = 1 if a.heads == "narrow" else 8
            mats += [(m.OT[:, c, :], a.w_out[:, c, :]) for c in range(n_out)]
            for k, (l, r) in enumerate(mats):
                if a.heads == "pair" and k in (n_more, n_more + 4):
                    p.wait_ge(ev["oT"].sem, ev["oT"].base + 2 * t + 1 + (k - n_more) // 4)
                elif k == n_more:
                    p.wait_ge(ev["oT"].sem, ev["oT"].base + per * t + per)
                ins = p.matmul(m.OPS[:, 0:128], l, r, start=(k == 0), stop=(k == len(mats) - 1))
            ins.then_inc(ev["out"].sem, 1)

        def step(n, u, on):
            if on[1]:
                if a.heads != "wide":
                    turn_input(n + 1, 1 - u)
                projections(n + 1, 1 - u)
            if on[0]:
                turn_probs(n)
            if on[1] and a.heads == "pair":
                scores(n + 1)
            if on[0]:
                values(n, u, on[1])
            if on[1] and a.heads == "narrow":
                scores(n + 1)
            if on[0]:
                if a.heads == "narrow":
                    turn_outputs(n)
                output(n, u)
            if on[2] and a.heads == "wide":
                turn_input(n + 2, u)
            if on[1] and a.heads == "wide":
                turn_keys(n + 1)
                scores(n + 1)
        pipeline(p, None, step)

    def act(s):
        own = Own(s, m.own_act)

        def keep_input(t):
            s.wait_ge(ev["x_turned"].sem, ev["x_turned"].base + t + 1)
            if a.ctx != "none":
                s.activation(m.cT[:, :], m.TPS[:, 128:256], ACT.Copy if a.c_gain is None else ACT.Identity,
                             scale=1.0 if a.c_gain is None else a.c_gain)
            s.activation(m.xT[:, :], m.TPS[:, 0:128], ACT.Copy if a.x_gain is None else ACT.Identity,
                         scale=1.0 if a.x_gain is None else a.x_gain).then_inc(ev["xT"].sem, 1)

        def step(n, u, on):
            if on[1]:
                t, v = n + 1, 1 - u
                if a.heads != "wide":
                    keep_input(t)
                for j, piece in enumerate(a.pieces):
                    if "act" in piece:
                        s.wait_ge(ev["piece%d" % j].sem, ev["piece%d" % j].base + t + 1)
                        ins = piece["act"](s, banks[j], t, v, own)
                        ins.then_inc(ev[piece.get("raises", "kept%d" % j)].sem, 1)
            if on[0]:
                t = n
                s.wait_ge(ev["p_turned"].sem, ev["p_turned"].base + t + 1)
                s.activation(m.PT[:, 0:nb, :], m.PTP[:, 0:nb * 128].rearrange("p (c q) -> p c q", c=nb),
                                             ACT.Copy).then_inc(ev["pT"].sem, 1)
                for k in range(per):
                    s.wait_ge(ev["pv"].sem, ev["pv"].base + per * t + k + 1)
                    if a.heads == "pair":
                        s.activation(m.OT[:, 4 * k:4 * k + 4, :],
                                     m.RING[:, k * 512:k * 512 + 512].rearrange("p (c q) -> p c q", c=4), ACT.Copy)\
                            .then_inc(ev["oT"].sem, 1)
                    elif a.heads == "wide":
                        s.activation(m.OT[:, :, 64 * k:64 * k + 64],
                                     m.RING[:, k * 512:k * 512 + 512].rearrange("p (c q) -> p c q", c=8), ACT.Copy)\
                            .then_inc(ev["oT"].sem, 1)
                if a.heads == "narrow":
                    s.activation(m.ON[:, 0:64], m.RING[:, 0:64], ACT.Copy)
                    s.activation(m.ON[:, 64:128], m.RING[:, 512:576], ACT.Copy).then_inc(ev["onat"].sem, 1)
                    s.wait_ge(ev["o_turned"].sem, ev["o_turned"].base + t + 1)
                    s.activation(m.OT[:, 0, :], m.OPS[:, 128:256], ACT.Copy).then_inc(ev["oT"].sem, 1)
            if on[2] and a.heads == "wide":
                keep_input(n + 2)
            if on[1]:
                t = n + 1
                if a.heads == "wide":
                    s.wait_ge(ev["k_turned"].sem, ev["k_turned"].base + t + 1)
                    s.activation(m.KT[:, 0:2, :], m.PTP[:, 512:768].rearrange("p (g k) -> p g k", g=2),
                                                 ACT.Copy).then_inc(ev["kT"].sem, 1)
                s.wait_ge(ev["shifted"].sem, ev["shifted"].base + t + 1)
                s.activation(m.PROB[:, 0:nb * 128], m.PROB[:, 0:nb * 128], ACT.Exp, scale=a.scale).then_inc(ev["exped"].sem, 1)
        pipeline(s, own, step)

    def dve(v):
        own = Own(v, m.own_dve)

        def step(n, u, on):
            if on[2]:
                t = n + 2
                if some(t - 1):
                    v.wait_ge(ev["x_turned"].sem, ev["x_turned"].base + t - 1)
                a.normalise(v, own, t, u)
            if on[1]:
                t, w = n + 1, 1 - u
                if a.dve_front:
                    a.dve_front(v, own, t, w)
                order = sorted(range(npc), key=lambda j: "last" in a.pieces[j])
                for j, piece in [(j, a.pieces[j]) for j in order]:
                    if "dve" in piece:
                        v.wait_ge(ev["piece%d" % j].sem, ev["piece%d" % j].base + t + 1)
                        ins = piece["dve"](v, banks[j], t, w, own)
                        ins.then_inc(ev["kept%d" % j].sem, 1)
                        if "dve_after" in piece:
                            piece["dve_after"](v, t, own)
                v.wait_ge(ev["scores"].sem, ev["scores"].base + t + 1)
                if a.mask:
                    v.tensor_tensor(Pv, PSv, a.mask(t).to_broadcast([128, nb, 2, S]), ALU.add).then_inc(own.sem, own.one())
                    v.wait_ge(own.sem, own.n)
                    v.tensor_reduce(mx, Pv, AX.X, ALU.max).then_inc(own.sem, own.one())
                    v.wait_ge(own.sem, own.n)
                    ins = v.tensor_tensor(Pv, Pv, bk(mx), ALU.subtract)
                else:
                    v.tensor_reduce(mx, PSv, AX.X, ALU.max).then_inc(own.sem, own.one())
                    v.wait_ge(own.sem, own.n)
                    ins = v.tensor_tensor(Pv, PSv, bk(mx), ALU.subtract)
                ins.then_inc(ev["shifted"].sem, 1)
            if on[1]:
                t = n + 1
                v.wait_ge(ev["exped"].sem, ev["exped"].base + t + 1)
                v.tensor_reduce(rs, Pv, AX.X, ALU.add).then_inc(own.sem, own.one())
                v.wait_ge(own.sem, own.n)
                if a.rowscale:
                    v.reciprocal(rs, rs).then_inc(own.sem, own.one())
                    v.wait_ge(own.sem, own.n)
                    ins = v.tensor_scalar(rs, rs, a.rowscale(t), None, ALU.mult)
                else:
                    ins = v.reciprocal(rs, rs)
                ins.then_inc(ev["rinv"].sem, 1)
            if on[0]:
                if some(n + 1):
                    v.wait_ge(ev["out"].sem, ev["out"].base + n + 1)
                a.finish(v, own, n).then_inc(ev["done"].sem, 1)
        pipeline(v, own, step)

    def pool(g):
        def step(n, u, on):
            if on[1]:
                t = n + 1
                if a.pool_front:
                    a.pool_front(g, t, 1 - u)
                g.wait_ge(ev["rinv"].sem, ev["rinv"].base + t + 1)
                g.tensor_tensor(Pv, Pv, bk(rs), ALU.mult).then_inc(ev["probs"].sem, 1)
        pipeline(g, None, step)

    def sp(q):
        if a.ctx == "load":
            def step(n, u, on):
                if on[2]:
                    t = n + 2
                    if some(t - 1):
                        q.wait_ge(ev["x_turned"].sem, ev["x_turned"].base + t - 1)
                    src = m.ctx_tiles[bass.ds(t, 1), :, :].rearrange("a p d -> (a p) d")
                    q.dma_start(m.cx[:, u, :], src).then_inc(m.cx_loaded[u], 16)
            pipeline(q, None, step)

    programs = dict(pe=pe, act=act, dve=dve, pool=pool, sp=sp)
    counts = {n: NT * (per if n in ("pv", "oT") else 1) for n in used}
    return programs, counts


def narrow_attention(m, a):
    ev = m.ev
    used = ["xn", "x_turned", "xT", "piece0", "piece1", "piece2", "kept0", "kept1", "kept2", "heads_split",
            "scores", "shifted", "exped", "rinv", "probs", "p_turned", "pT", "pv", "oT", "out", "done"] + list(a.extra)
    q_bank, k_bank, v_bank = m.RING[:, 0:512], m.RING[:, 512:1024], m.TPS[:, 256:512]
    PSv = m.PS[:, :].rearrange("q (p c k) -> q c p k", p=2, c=8)
    mx = m.mx[:, 0:16].rearrange("q (c p) -> q c p", p=2)
    rs = m.rs[:, 0:16].rearrange("q (c p) -> q c p", p=2)
    OT = m.OT1[:, 0, :]

    def prob(v):
        return m.PROB2[:, v * 1024:v * 1024 + 1024].rearrange("q (c p k) -> q c p k", c=8, p=2)

    def wide(ap):
        return ap.unsqueeze(3).to_broadcast([128, 8, 2, S])

    def v_block(u, b, c):
        return m.VP[:, u * 2048 + b * 1024 + c * P:u * 2048 + b * 1024 + (c + 1) * P]

    def spread_v(put, bank, u):
        for b in range(2):
            for h in range(2):
                at = u * 2048 + b * 1024 + h * 64
                dst = m.VP[64 * h:64 * h + 64, at:at + 8 * (P + 8)].rearrange("p (c x) -> p c x", c=8)[:, :, 0:8]
                ins = put(dst, bank[64 * h:64 * h + 64, 64 * b:64 * b + 64].rearrange("p (c x) -> p c x", c=8), h)
        return ins

    def pe(p):
        def step(n, u, on):
            if on[1]:
                t = n + 1
                p.wait_ge(ev["kept0"].sem, ev["kept0"].base + t + 1)
                p.wait_ge(ev["heads_split"].sem, ev["heads_split"].base + t + 1)
                if some(t):
                    p.wait_ge(ev["shifted"].sem, ev["shifted"].base + t)
                m.hold(p)
                for h in range(2):
                    for b in range(2):
                        r = slice(64 * h, 64 * h + 64)
                        ins = p.matmul(m.PS[64 * b:64 * b + 64, h * 512:h * 512 + 512], m.QB[r, 64 * b:64 * b + 64],
                                       m.KT8[r, :, 64 * b:64 * b + 64], start=True, stop=True)
                ins.then_inc(ev["scores"].sem, 1)
            if on[2]:
                t = n + 2
                p.wait_ge(ev["xn"].sem, ev["xn"].base + t + 1)
                p.wait_ge(m.cx_loaded[u], a.cx_base + 8 * t - 8 * u + 16)
                if some(t):
                    p.wait_ge(ev["xT"].sem, ev["xT"].base + t)
                    p.wait_ge(ev["kept2"].sem, ev["kept2"].base + t)
                p.transpose(m.TPS[:, 0:128], m.xn[:, u, :], m.ident[:, :])
                p.transpose(m.TPS[:, 128:256], m.cx[:, u, :], m.ident[:, :]).then_inc(ev["x_turned"].sem, 1)
                p.wait_ge(ev["xT"].sem, ev["xT"].base + t + 1)
                if some(t - 2):
                    p.wait_ge(ev["oT"].sem, ev["oT"].base + t - 2)
                a.pieces[0]["pe"](p, q_bank, t, u).then_inc(ev["piece0"].sem, 1)
            if on[0]:
                p.wait_ge(ev["probs"].sem, ev["probs"].base + n + 1)
                if some(n):
                    p.wait_ge(ev["pT"].sem, ev["pT"].base + n)
                for c in range(8):
                    ins = p.transpose(m.PTP[:, c * P:(c + 1) * P],
                                      m.PROB2[:, u * 1024 + c * P:u * 1024 + (c + 1) * P], m.ident[:, :])
                ins.then_inc(ev["p_turned"].sem, 1)
            if on[2]:
                t = n + 2
                if some(t):
                    p.wait_ge(ev["kept1"].sem, ev["kept1"].base + t)
                for w in a.pieces[1].get("needs", []):
                    p.wait_ge(ev[w].sem, ev[w].base + t + 1)
                a.pieces[1]["pe"](p, k_bank, t, u).then_inc(ev["piece1"].sem, 1)
            if on[0]:
                p.wait_ge(ev["pT"].sem, ev["pT"].base + n + 1)
                p.wait_ge(ev["kept2"].sem, ev["kept2"].base + n + 1)
                if on[2]:
                    p.wait_ge(ev["kept0"].sem, ev["kept0"].base + n + 3)
                if some(n):
                    p.wait_ge(ev["oT"].sem, ev["oT"].base + n)
                for b in range(2):
                    for c in range(8):
                        ins = p.matmul(q_bank[:, 64 * b:64 * b + 64], v_block(u, b, c),
                                       m.PT8[:, c, 64 * b:64 * b + 64], start=(c == 0), stop=(c == 7))
                ins.then_inc(ev["pv"].sem, 1)
            if on[2]:
                a.pieces[2]["pe"](p, v_bank, n + 2, u).then_inc(ev["piece2"].sem, 1)
            if on[0]:
                p.wait_ge(ev["oT"].sem, ev["oT"].base + n + 1)
                if some(n):
                    p.wait_ge(ev["done"].sem, ev["done"].base + n)
                p.matmul(m.OPS[:, 0:128], OT, a.w_out[:, 0, :], start=True, stop=True).then_inc(ev["out"].sem, 1)
        pipeline(p, None, step)

    def act(s):
        def step(n, u, on):
            if on[2]:
                t = n + 2
                s.wait_ge(ev["x_turned"].sem, ev["x_turned"].base + t + 1)
                s.activation(m.cT[:, :], m.TPS[:, 128:256], ACT.Copy)
                s.activation(m.xT[:, :], m.TPS[:, 0:128], ACT.Copy).then_inc(ev["xT"].sem, 1)
                s.wait_ge(ev["piece0"].sem, ev["piece0"].base + t + 1)
                a.pieces[0]["act"](s, q_bank).then_inc(ev["kept0"].sem, 1)
            if on[1]:
                s.wait_ge(ev["shifted"].sem, ev["shifted"].base + n + 2)
                pr = m.PROB2[:, (1 - u) * 1024:(1 - u) * 1024 + 1024]
                s.activation(pr, pr, ACT.Exp, scale=a.scale).then_inc(ev["exped"].sem, 1)
            if on[0]:
                s.wait_ge(ev["p_turned"].sem, ev["p_turned"].base + n + 1)
                s.activation(m.PT8[:, :, :], m.PTP[:, :].rearrange("p (c q) -> p c q", c=8), ACT.Copy)\
                    .then_inc(ev["pT"].sem, 1)
            if on[2]:
                t = n + 2
                s.wait_ge(ev["piece1"].sem, ev["piece1"].base + t + 1)
                if some(t):
                    s.wait_ge(ev["heads_split"].sem, ev["heads_split"].base + t)
                a.pieces[1]["act"](s, k_bank).then_inc(ev["kept1"].sem, 1)
            if on[0]:
                s.wait_ge(ev["pv"].sem, ev["pv"].base + n + 1)
                s.activation(OT, q_bank[:, 0:P], ACT.Copy).then_inc(ev["oT"].sem, 1)
            if on[2] and "act" in a.pieces[2]:
                s.wait_ge(ev["piece2"].sem, ev["piece2"].base + n + 3)
                a.pieces[2]["act"](s, spread_v, v_bank, u).then_inc(ev["kept2"].sem, 1)
        pipeline(s, None, step)

    def dve(v):
        own = Own(v, m.own_dve)
        v.memset(m.VP[:, :], 0.0).then_inc(own.sem, own.one())
        own.restart()

        def step(n, u, on):
            if on[2]:
                t = n + 2
                if some(t - 1):
                    v.wait_ge(ev["x_turned"].sem, ev["x_turned"].base + t - 1)
                a.normalise(v, own, t, u)
            if on[1]:
                t, pr = n + 1, prob(1 - u)
                v.wait_ge(ev["scores"].sem, ev["scores"].base + t + 1)
                if some(t - 1):
                    v.wait_ge(ev["p_turned"].sem, ev["p_turned"].base + t - 1)
                if a.mask:
                    v.tensor_tensor(pr, PSv, a.mask(t).to_broadcast([128, 8, 2, S]), ALU.add).then_inc(own.sem, own.one())
                    v.wait_ge(own.sem, own.n)
                src = pr if a.mask else PSv
                v.tensor_reduce(mx, src, AX.X, ALU.max).then_inc(own.sem, own.one())
                v.wait_ge(own.sem, own.n)
                v.tensor_tensor(pr, src, wide(mx), ALU.subtract).then_inc(ev["shifted"].sem, 1)
            if on[2] and a.dve_front:
                a.dve_front(v, own, n + 2, u)
            if on[1]:
                t = n + 1
                v.wait_ge(ev["exped"].sem, ev["exped"].base + t + 1)
                if some(t):
                    v.wait_ge(ev["probs"].sem, ev["probs"].base + t)
                v.tensor_reduce(rs, prob(1 - u), AX.X, ALU.add).then_inc(own.sem, own.one())
                v.wait_ge(own.sem, own.n)
                v.reciprocal(rs, rs).then_inc(ev["rinv"].sem, 1)
            if on[2] and "dve" in a.pieces[2]:
                v.wait_ge(ev["piece2"].sem, ev["piece2"].base + n + 3)
                a.pieces[2]["dve"](v, spread_v, v_bank, u).then_inc(ev["kept2"].sem, 1)
            if on[0]:
                v.wait_ge(ev["out"].sem, ev["out"].base + n + 1)
                a.finish(v, own, n).then_inc(ev["done"].sem, 1)
        pipeline(v, own, step)

    def pool(g):
        def step(n, u, on):
            if on[2]:
                g.wait_ge(ev["kept1"].sem, ev["kept1"].base + n + 3)
                g.tensor_tensor(m.KT8[:, :, :], m.KB[:, :].unsqueeze(1).to_broadcast([P, 8, P]),
                                m.own_dims[:, :].unsqueeze(2).to_broadcast([P, 8, P]), ALU.mult)\
                    .then_inc(ev["heads_split"].sem, 1)
            if on[1]:
                g.wait_ge(ev["rinv"].sem, ev["rinv"].base + n + 2)
                g.tensor_tensor(prob(1 - u), prob(1 - u), wide(rs), ALU.mult).then_inc(ev["probs"].sem, 1)
        pipeline(g, None, step)

    def sp(q):
        def step(n, u, on):
            if on[2]:
                t = n + 2
                if some(t - 1):
                    q.wait_ge(ev["x_turned"].sem, ev["x_turned"].base + t - 1)
                src = m.ctx_tiles[bass.ds(t, 1), :, :].rearrange("a p d -> (a p) d")
                q.dma_start(m.cx[:, u, :], src).then_inc(m.cx_loaded[u], 16)
        pipeline(q, None, step)
    return dict(pe=pe, act=act, dve=dve, pool=pool, sp=sp), {n: NT for n in used}


def constants():
    q = np.arange(P)
    k = np.arange(S)
    pos = (q % S).astype(np.float32)
    inv = (1.0 / np.float32(1000000.0) ** (np.arange(0, D, 2, dtype=np.float32) / np.float32(D))).astype(np.float32)
    freqs = pos[:, None] * inv[None, :]
    emb = np.concatenate([freqs, freqs], 1).astype(np.float32)
    cos, sin = np.cos(emb).astype(np.float32), np.sin(emb).astype(np.float32)
    half = np.where(np.arange(D) < D // 2, -1.0, 1.0).astype(np.float32)
    e = np.arange(E)
    tie = (e[None, :] < e[:, None]).astype(np.float32).reshape(1, E * E).repeat(P, 0)
    return dict(
        ident=np.eye(P, dtype=np.float32),
        causal=np.where(k[None, :] > (q % S)[:, None], np.float32(NEG), np.float32(0)).astype(np.float32),
        before=(q[:, None] < q[None, :]).astype(np.float32),
        cosT=np.ascontiguousarray(cos.T), sinT=np.ascontiguousarray(sin.T),
        cosN=cos, sinN=(sin * half[None, :]).astype(np.float32),
        tie=tie,
        own_dims=((q[:, None] % 64) // 8 == np.arange(8)[None, :]).astype(np.float32),
        ones=np.ones((P, P), np.float32),
        zeros=np.zeros((P, 3 * P), np.float32),
        pick=(np.arange(P)[:, None] % E == (np.arange(512)[None, :] // 64)).astype(np.float32),
    )


CONST = constants()
ON_CHIP = [n for n in CONST if n != "zeros"]


def program(nc, t, out, stop=99):
    m = Machine()
    ctx = ExitStack()
    with ctx:
        def sb(name, shape, dt=F32, stack=ctx):
            return stack.enter_context(nc.sbuf_tensor(name, shape, dt))

        class Arena:

            def __init__(self, name, floats):
                self.buf, self.at, self.floats = sb(name, [P, floats]), 0, floats

            def cut(self, shape):
                n = int(np.prod(shape[1:]))
                assert self.at + n <= self.floats, (self.at, n)
                ap = self.buf[0:shape[0], self.at:self.at + n]
                self.at += n
                if len(shape) == 2:
                    return ap
                names = "abcd"[:len(shape) - 1]
                return ap.rearrange("p (%s) -> p %s" % (" ".join(names), " ".join(names)),
                                    **{k: v for k, v in zip(names, shape[1:])})

            def again(self):
                self.at = 0

        def ps(name, shape):
            return ctx.enter_context(nc.psum_tensor(name, shape, F32))

        def sem(name):
            return ctx.enter_context(nc.semaphore(name))

        X = m.X = sb("X", [P, NT * D])
        XIN = m.XIN = sb("XIN", [P, NT * D])
        table = {name: sb("table_" + name, [P, CONST[name].shape[1]]) for name in ON_CHIP}
        m.ident, m.causal, m.before, m.ones = table["ident"], table["causal"], table["before"], table["ones"]
        m.cosT, m.sinT, m.cosN, m.sinN = table["cosT"], table["sinT"], table["cosN"], table["sinN"]
        m.tie, m.own_dims, m.pick = table["tie"], table["own_dims"], table["pick"]
        m.g_all = sb("g_all", [P, 8])
        m.tg = sb("tg", [P, 8])
        m.gains = sb("gains", [P, 8])
        m.mhalf = sb("mhalf", [P, NT])
        m.st = sb("st", [P, NT, 6])
        m.mv = sb("mv", [P, NT, 2])
        m.rstd = sb("rstd", [P, NT])
        m.cmv = sb("cmv", [P, NT, 2])
        m.crstd = sb("crstd", [P, NT])
        m.anchor = sb("anchor", [P, 32], BF16)
        m.xn = sb("xn", [P, 2, D])
        m.cx = sb("cx", [P, 2, D])
        m.xT = sb("xT", [P, P])
        m.cT = sb("cT", [P, P])
        m.mx = sb("mx", [P, H])
        m.rs = sb("rs", [P, H])
        m.TPS = ps("TPS", [P, 512])
        m.RING = ps("RING", [P, 1024])
        m.PS = ps("PS", [P, 1024])
        m.PTP = ps("PTP", [P, 1024])
        m.OPS = ps("OPS", [P, 512])

        names = ["xn", "x_turned", "xT", "scores", "shifted", "exped", "rinv", "probs", "p_turned", "pT",
                 "pv", "oT", "out", "done", "o_turned", "onat", "kT", "knat", "k_turned", "gate_tanhed",
                 "q_turned_by_pos", "q_biased", "heads_split", "kv_biased", "masked_ctx"]
        names += ["piece%d" % j for j in range(6)] + ["kept%d" % j for j in range(6)]
        m.ev = {n: Event(sem(n)) for n in names}
        ev = m.ev
        m.own_act, m.own_dve, m.own_pool = sem("own_act"), sem("own_dve"), sem("own_pool")
        m.cx_loaded = [sem("even_context_loaded"), sem("odd_context_loaded")]
        s_const, s_x, s_ready = sem("constants_loaded"), sem("x_loaded"), sem("setup_done")
        s_var, s_rstd = sem("variance_ready"), sem("rstd_ready")
        s_stored = sem("stored")
        m.weights = {}
        prog = dict(pe=[], act=[], dve=[], pool=[], sp=[])
        m.nvar = 0

        def hold(p):
            p.ldweights(m.anchor[:, :], tile_position=(0, 0))
        m.hold = hold

        def load(group, pairs):
            s = sem("loaded_" + group)
            m.weights[group] = (s, 16 * len(pairs))

            def f(q):
                for dst, src in pairs:
                    q.dma_start(dst, src, allow_slow_non_contiguous=True).then_inc(s, 16)
            prog["sp"].append(f)

        def loaded(eng, group):
            s, n = m.weights[group]
            eng.wait_ge(s, n)
        m.loaded = loaded

        def row(ap, n):
            return ap.rearrange("(a n) -> a n", a=1).to_broadcast([P, n])

        def col(ap):
            return ap.rearrange("(p a) -> p a", a=1)

        def barrier():
            v = ev["done"].base
            for k in prog:
                prog[k].append(lambda eng, v=v: eng.wait_ge(ev["done"].sem, v))

        load("constants", [(table[n][:, :], t["const_" + n]) for n in ON_CHIP]
             + [(m.g_all[:, 0:4], row(t["g_xattn"], 4)), (m.g_all[:, 4:8], row(t["g_ffn"], 4))]
             + [(m.gains[:, i:i + 1], col(t[n])) for i, n in enumerate(
                 ["L0_xattn_ptb_gamma", "L0_xattn_ca_gamma", "L0_xattn_ca_ctx_gamma", "L0_ffn_g1", "L0_ffn_g2"])])
        load("x", [(X[:, :].rearrange("p (t d) -> p t d", d=D), t["x"].rearrange("(t b) s d -> (b s) t d", b=TILE_B))])
        m.ctx_tiles = t["ctx_1024"].rearrange("(t b) s d -> t (b s) d", b=TILE_B)

        def setup_dve(v):
            v.memset(m.mhalf[:, :], -0.5).then_inc(s_ready, 1)
            v.memset(m.anchor[:, :], 0.0).then_inc(s_ready, 1)
        prog["dve"].append(setup_dve)

        def setup_act(s):
            loaded(s, "constants")
            s.activation(m.tg[:, :], m.g_all[:, :], ACT.Tanh).then_inc(s_ready, 1)
        prog["act"].append(setup_act)
        for k in ("pe", "dve", "pool", "act"):
            prog[k].append(lambda eng: (loaded(eng, "constants"), eng.wait_ge(s_ready, 3)))

        def tile_of(buf, i, width=D):
            return buf[:, bass.ds(i * width, width)]
        m.tile_of = tile_of

        def statistics(src, mv, rstd, eps, rms=False):
            k = m.nvar = m.nvar + 1

            def dve(v):
                own = Own(v, m.own_dve)
                for i in range(NT):
                    v.bn_stats(m.st[:, i, :], src[:, i * D:(i + 1) * D]).then_inc(own.sem, own.one())
                v.wait_ge(own.sem, own.n)
                for i in range(NT):
                    v.bn_aggr(mv[:, i, :], m.st[:, i, :]).then_inc(own.sem, own.one())
                v.wait_ge(own.sem, own.n)
                if rms:
                    v.tensor_tensor(rstd[:, :], mv[:, :, 0], mv[:, :, 0], ALU.mult).then_inc(own.sem, own.one())
                    v.wait_ge(own.sem, own.n)
                    v.tensor_tensor(mv[:, :, 1], rstd[:, :], mv[:, :, 1], ALU.add).then_inc(own.sem, own.one())
                    v.wait_ge(own.sem, own.n)
                v.tensor_scalar(rstd[:, :], mv[:, :, 1], eps, None, ALU.add).then_inc(s_var, 1)
                own.restart()
                v.wait_ge(s_rstd, k)

            def pool(g):
                g.wait_ge(s_var, k)
                g.tensor_tensor(rstd[:, :], rstd[:, :], m.mhalf[:, :], ALU.pow).then_inc(s_rstd, 1)
            prog["dve"].append(dve)
            prog["pool"].append(pool)

        def norm_to_xin():
            def dve(v):
                own = Own(v, m.own_dve)
                x3 = X[:, :].rearrange("p (t d) -> p t d", d=D)
                y3 = XIN[:, :].rearrange("p (t d) -> p t d", d=D)
                v.tensor_tensor(y3, x3, m.mv[:, :, 0:1].to_broadcast([P, NT, D]), ALU.subtract).then_inc(own.sem, own.one())
                v.wait_ge(own.sem, own.n)
                v.tensor_tensor(y3, y3, m.rstd[:, :].unsqueeze(2).to_broadcast([P, NT, D]), ALU.mult).then_inc(own.sem, own.one())
                v.wait_ge(own.sem, own.n)
                own.restart()
            prog["dve"].append(dve)

        mv2 = m.mv[:, :, :].rearrange("p t s -> p (t s)")
        cmv2 = m.cmv[:, :, :].rearrange("p t s -> p (t s)")

        def norm_tile(v, dst, src, i, mvf, rstd):
            return v.tensor_scalar(dst, tile_of(src, i), mvf[:, bass.ds(2 * i, 1)], rstd[:, bass.ds(i, 1)],
                                   ALU.subtract, ALU.mult)

        def run(a):
            progs, used = narrow_attention(m, a) if a.heads == "narrow" else attention(m, a)
            for k in prog:
                def go(eng, f=progs[k], bases={n: ev[n].base for n in ev}):
                    for n, b in bases.items():
                        ev[n].base = b
                    f(eng)
                prog[k].append(go)
            for n, k in used.items():
                ev[n].base += k

        def q_piece(w, j, col0=0):
            def f(p, bank, i, u):
                for c in range(4):
                    ins = p.matmul(bank[:, c * P:(c + 1) * P], w[:, col0 + (4 * j + c) * P:col0 + (4 * j + c + 1) * P],
                                   m.xT[:, :], start=True, stop=True)
                return ins
            return f

        def q_keep(j):
            def f(s, bank, i, u, own):
                return s.activation(m.QT[:, 4 * j:4 * j + 4, :], bank.rearrange("p (c q) -> p c q", c=4), ACT.Copy)
            return f

        WORK, RB, RA = Arena("work_arena", 11904), Arena("arena_b", 8400), Arena("arena_a", 25000)
        Wf = RB.cut([P, 2176])
        Wao = RB.cut([P, 8, D])
        Wffo = RB.cut([P, 4, D])
        Wq0 = RB.cut([P, 1024])
        Wkv0 = RB.cut([P, 128])
        Wo0 = RB.cut([P, 8, D])
        m.QT = WORK.cut([P, 8, P])
        m.KT = WORK.cut([P, 8, P])
        m.V = WORK.cut([P, 2, 2, 512])
        m.VW = m.V[:, :, :, :].rearrange("p u b w -> p u (b w)")[:, :, 0:256].rearrange("p u (k d) -> p u k d", d=D)
        m.QW = m.QT[:, :, :].rearrange("p c q -> p (c q)")
        m.PROB = WORK.cut([P, 1024])
        m.PT = WORK.cut([P, 8, P])
        m.OT = WORK.cut([P, 8, P])
        m.ON = WORK.cut([P, P])
        m.KN = WORK.cut([P, 768])
        EG = WORK.cut([P, 512])
        UT = WORK.cut([P, 2, 4, P])
        m.CTX = WORK.cut([P, NT * D])
        load("layer0_fused", [(Wf[:, :], t["L0_xattn_W_fused"]),
                              (Wao[:, :, :], t["L0_xattn_W_attn_out"].rearrange("(c p) d -> p c d", p=P)),
                              (Wffo[:, :, :], t["L0_xattn_W_ff_out"].rearrange("(c p) d -> p c d", p=P))])
        load("layer0_cross", [(Wq0[:, :], t["L0_xattn_W_q"]), (Wkv0[:, :], t["L0_xattn_W_kv"]),
                              (Wo0[:, :, :], t["L0_xattn_W_out"].rearrange("(c p) d -> p c d", p=P)),
                              (m.CTX[:, :].rearrange("p (t d) -> p t d", d=D),
                               t["ctx_1024"].rearrange("(t b) s d -> (b s) t d", b=TILE_B))])
        prog["dve"].append(lambda v: loaded(v, "x"))
        statistics(X, m.mv, m.rstd, 1e-5)
        norm_to_xin()
        statistics(XIN, m.mv, m.rstd, 1e-5)
        prog["pe"].append(lambda p: loaded(p, "layer0_fused"))

        def mqa_kv(w, src, k0):
            def f(p, bank, i, u):
                for h in range(2):
                    p.matmul(bank[64 * h:64 * h + 64, 0:P], w[:, k0:k0 + 64], src[:, :], start=True, stop=True)
                for b in range(2):
                    for h in range(2):
                        ins = p.matmul(bank[64 * h:64 * h + 64, 128 + 64 * b:192 + 64 * b],
                                       src[:, 64 * b:64 * b + 64], w[:, k0 + 64:k0 + 128], start=True, stop=True)
                return ins
            return f

        def mqa_keep(s, bank, i, u, own):
            s.activation(m.KT[:, 0, :], bank[:, 0:P], ACT.Copy)
            return s.activation(m.V[:, u, :, 0:64], bank[:, 128:256].rearrange("p (b d) -> p b d", b=2), ACT.Copy)

        def gate_tanh(s, bank, i, u, own):
            return s.activation(EG[:, :], bank, ACT.Tanh, scale=0.5)

        def gate_times(v, bank, i, u, own):
            v.wait_ge(ev["gate_tanhed"].sem, ev["gate_tanhed"].base + i + 1)
            return v.scalar_tensor_tensor(EG[:, :], EG[:, :], 1.0, bank, ALU.add, ALU.mult)

        def up_times(v, bank, i, u, own):
            v.wait_ge(ev["kept3"].sem, ev["kept3"].base + i + 1)
            return v.scalar_tensor_tensor(UT[:, u, :, :].rearrange("p c q -> p (c q)"), EG[:, :], 0.5, bank,
                                          ALU.mult, ALU.mult)

        def finish_into_xin(v, own, i):
            return v.tensor_tensor(tile_of(XIN, i), m.OPS[:, 0:128], tile_of(XIN, i), ALU.add)

        def finish_into_x(gate):
            def f(v, own, i):
                return v.scalar_tensor_tensor(tile_of(X, i), m.OPS[:, 0:128], m.tg[:, gate:gate + 1], tile_of(X, i),
                                              ALU.mult, ALU.add)
            return f

        def normalise(src):
            def f(v, own, i, u):
                norm_tile(v, m.xn[:, u, :], src, i, mv2, m.rstd).then_inc(ev["xn"].sem, 1)
            return f

        def normalise_both(v, own, i, u):
            norm_tile(v, m.cx[:, u, :], m.CTX, i, cmv2, m.crstd)
            norm_tile(v, m.xn[:, u, :], XIN, i, mv2, m.rstd).then_inc(ev["xn"].sem, 1)

        def causal_mask(i):
            return m.causal[:, :].unsqueeze(1).unsqueeze(1)

        run(Attention(extra=["gate_tanhed"], x_gain=m.gains[:, 0:1], mask=causal_mask, scale=64 ** -0.5,
                 pieces=[dict(pe=q_piece(Wf, 0), act=q_keep(0)), dict(pe=q_piece(Wf, 1), act=q_keep(1)),
                         dict(pe=mqa_kv(Wf, m.xT, 1024), act=mqa_keep),
                         dict(pe=q_piece(Wf, 0, 1664), act=gate_tanh, raises="gate_tanhed", dve=gate_times),
                         dict(pe=q_piece(Wf, 0, 1152), dve=up_times)],
                 q_ready=["kept0", "kept1", "kept2"], v_ready=["kept2"], w_out=Wao,
                 more_out=lambda u: [(UT[:, u, c, :], Wffo[:, c, :]) for c in range(4)],
                 normalise=normalise(XIN), finish=finish_into_xin))
        barrier()
        if stop >= 1:
            prog["dve"].append(lambda v: loaded(v, "layer0_cross"))
            prog["pe"].append(lambda v: loaded(v, "layer0_cross"))
            statistics(m.CTX, m.cmv, m.crstd, 1e-5)
            statistics(XIN, m.mv, m.rstd, 1e-5)
            run(Attention(ctx="normed", x_gain=m.gains[:, 1:2], c_gain=m.gains[:, 2:3], scale=64 ** -0.5,
                     pieces=[dict(pe=q_piece(Wq0, 0), act=q_keep(0)), dict(pe=q_piece(Wq0, 1), act=q_keep(1)),
                             dict(pe=mqa_kv(Wkv0, m.cT, 0), act=mqa_keep)],
                     q_ready=["kept0", "kept1", "kept2"], v_ready=["kept2"], w_out=Wo0,
                     normalise=normalise_both, finish=finish_into_x(0)))
            barrier()
        wqT = RA.cut([P, 8 * P])
        wqrT = RA.cut([P, 8 * P])
        wkvT = RA.cut([P, 4 * P])
        woT = RA.cut([P, 8, D])
        KF, CF = 112, 4
        F0 = KF * CF
        w1T = RA.cut([P, E * F0])
        w3T = RA.cut([P, E * F0])
        w2T = RA.cut([P, E, CF, D])
        NGR = E * F0 // P
        small = RA.cut([P, 20, P])
        stage = [RA.cut([P, NGR, P]) for i in range(2)]
        wgT = sb("wgT", [P, 2, E])
        wg_n = sb("wg_n", [E, 2, D])
        qp = sb("qp", [P, 5, NGR])
        s_turned, s_kept_w, s_quant = sem("weights_turned"), sem("weights_kept"), sem("weights_quantised")
        s_stage, s_rotated = sem("staged_again"), sem("rotation_ready")
        m.n_turned = 0
        m.n_quant = 0

        def turn(sources, dst, rows=P, cols=P):
            n = m.n_turned = m.n_turned + 1
            bank = m.PTP[:, (n % 2) * 512:(n % 2) * 512 + 512]

            def pe(p):
                if some(n - 2):
                    p.wait_ge(s_kept_w, n - 2)
                for k, src in enumerate(sources):
                    ins = p.transpose(bank[0:cols, k * rows:(k + 1) * rows], src, m.ident[0:rows, 0:rows])
                ins.then_inc(s_turned, 1)

            def act(s):
                s.wait_ge(s_turned, n)
                s.activation(dst[0], dst[1](bank[0:cols, 0:rows * len(sources)]), ACT.Copy).then_inc(s_kept_w, 1)
            prog["pe"].append(pe)
            prog["act"].append(act)

        def kept_weights():
            n = m.n_turned
            prog["pe"].append(lambda p: p.wait_ge(s_kept_w, n))

        MAGIC = 12582912.0

        def quantise(v, own, w, g, prm=None):
            rows = w.shape[0]
            mx, mn, sc, ri, bs = [qp[0:rows, k, 0:g] for k in range(5)]

            def wide(x):
                return x.unsqueeze(2).to_broadcast([rows, g, P])
            v.tensor_reduce(mx, w, AX.X, ALU.max).then_inc(own.sem, own.one())
            v.wait_ge(own.sem, own.n)
            v.tensor_reduce(mn, w, AX.X, ALU.min).then_inc(own.sem, own.one())
            v.wait_ge(own.sem, own.n)
            v.tensor_tensor(sc, mx, mn, ALU.subtract).then_inc(own.sem, own.one())
            v.wait_ge(own.sem, own.n)
            v.tensor_scalar(sc, sc, 1e-5, 1.0 / 15.0, ALU.max, ALU.mult).then_inc(own.sem, own.one())
            v.wait_ge(own.sem, own.n)
            v.reciprocal(ri, sc).then_inc(own.sem, own.one())
            v.wait_ge(own.sem, own.n)
            v.tensor_tensor(bs, mn, ri, ALU.mult).then_inc(own.sem, own.one())
            v.wait_ge(own.sem, own.n)
            v.tensor_scalar(bs, bs, -1.0, MAGIC, ALU.mult, ALU.add).then_inc(own.sem, own.one())
            v.wait_ge(own.sem, own.n)
            v.tensor_scalar(bs, bs, MAGIC, 0.0, ALU.subtract, ALU.max).then_inc(own.sem, own.one())
            v.wait_ge(own.sem, own.n)
            v.tensor_scalar(bs, bs, 15.0, None, ALU.min).then_inc(own.sem, own.one())
            v.wait_ge(own.sem, own.n)
            v.tensor_tensor(w, w, wide(ri), ALU.mult).then_inc(own.sem, own.one())
            v.wait_ge(own.sem, own.n)
            v.tensor_scalar(w, w, MAGIC, MAGIC, ALU.add, ALU.subtract).then_inc(own.sem, own.one())
            v.wait_ge(own.sem, own.n)
            v.tensor_tensor(w, w, wide(bs), ALU.add).then_inc(own.sem, own.one())
            v.wait_ge(own.sem, own.n)
            v.tensor_scalar(w, w, 0.0, 15.0, ALU.max, ALU.min).then_inc(own.sem, own.one())
            v.wait_ge(own.sem, own.n)
            v.tensor_tensor(w, w, wide(bs), ALU.subtract).then_inc(own.sem, own.one())
            v.wait_ge(own.sem, own.n)
            return v.tensor_tensor(w, w, wide(sc), ALU.mult)

        def quantised(w, g, group, extra_wait=None):
            k = m.n_quant = m.n_quant + 1

            def dve(v):
                if group:
                    loaded(v, group)
                if extra_wait:
                    v.wait_ge(*extra_wait)
                own = Own(v, m.own_dve)
                quantise(v, own, w, g).then_inc(s_quant, 1)
                own.restart()
            prog["dve"].append(dve)
            prog["pe"].append(lambda p: p.wait_ge(s_quant, k))

        if stop >= 2:
            if stop >= 4:
                RB.again()
                Wq1 = RB.cut([P, 1024])
                Wkv1 = RB.cut([P, 2048])
                Wo1 = RB.cut([P, 8, D])
                WiE = RB.cut([P, E, 4 * P])
            load("layer0_small", [(small[:, 0:8, :], t["L0_ffn_w_q"].rearrange("(k p) d -> p k d", p=P)),
                                  (small[:, 8:10, :], t["L0_ffn_w_k"].rearrange("(k p) d -> p k d", p=P)),
                                  (small[:, 10:12, :], t["L0_ffn_w_v"].rearrange("(k p) d -> p k d", p=P)),
                                  (small[:, 12:20, :], t["L0_ffn_w_o"].rearrange("p (k d) -> p k d", k=8)),
                                  (wg_n[:, 0, :], t["L0_ffn_w_gate"]), (wg_n[:, 1, :], t["L1_ffn_W_router"])])
            rows = "e f d -> (e f) d"
            load("layer0_w1", [(stage[0][:, :, :], t["L0_ffn_w1"].rearrange(rows).rearrange("(k p) d -> p k d", p=P))])
            load("layer0_w3", [(stage[1][:, :, :], t["L0_ffn_w3"].rearrange(rows).rearrange("(k p) d -> p k d", p=P))])
            quantised(small[:, :, :], 20, "layer0_small")

            def flat(k):
                return lambda b: b.rearrange("p (k q) -> p k q", k=k)
            for k in range(0, 8, 4):
                turn([small[:, k + i, :] for i in range(4)], (wqT[:, k * P:(k + 4) * P], lambda b: b))
            turn([small[:, 8 + i, :] for i in range(4)], (wkvT[:, :], lambda b: b))
            for k in range(0, 8, 4):
                turn([small[:, 12 + k + i, :] for i in range(4)], (woT[:, k:k + 4, :], flat(4)))
            prog["pe"].append(lambda p: loaded(p, "layer0_small"))
            turn([wg_n[:, i, :] for i in range(2)], (wgT[:, :, :], flat(2)), rows=E)
            n_q = m.n_turned

            def rotate(s):
                s.wait_ge(s_kept_w, n_q)
                a4 = wqT[:, :].rearrange("p (h r d) -> p h r d", h=8, r=2)
                b4 = wqrT[:, :].rearrange("p (h r d) -> p h r d", h=8, r=2)
                s.activation(b4[:, :, 0, :], a4[:, :, 1, :], ACT.Copy, scale=-1.0).then_inc(s_rotated, 1)
                s.activation(b4[:, :, 1, :], a4[:, :, 0, :], ACT.Copy).then_inc(s_rotated, 1)
            prog["act"].append(rotate)
            prog["pe"].append(lambda p: p.wait_ge(s_rotated, 2))
            quantised(stage[0][:, :, :], NGR, "layer0_w1")
            for k in range(0, NGR, 4):
                turn([stage[0][:, k + i, :] for i in range(4)], (w1T[:, k * P:(k + 4) * P], lambda b: b))
            n_w1 = m.n_turned
            quantised(stage[1][:, :, :], NGR, "layer0_w3")
            for k in range(0, NGR, 4):
                turn([stage[1][:, k + i, :] for i in range(4)], (w3T[:, k * P:(k + 4) * P], lambda b: b))
            if stop >= 4:
                load("layer1_attention", [(Wq1[:, :], t["L1_xattn_Wq"]), (Wkv1[:, :], t["L1_xattn_Wkv"]),
                                          (Wo1[:, :, :], t["L1_xattn_Wo"].rearrange("(c p) d -> p c d", p=P))])
                load("layer1_experts", [(WiE[:, :, :], t["L1_ffn_experts_inter"].rearrange("e h i -> h e i"))])
            st2 = stage[0][:, :, :].rearrange("p (e g) q -> p e (g q)", e=4)

            def load_w2(q):
                q.wait_ge(s_turned, n_w1)
                for eh in range(2):
                    for el in range(4):
                        q.dma_start(st2[64 * eh:64 * eh + 64, el, :],
                                    t["L0_ffn_w2"][4 * eh + el].rearrange("(p r) f -> p (r f)", r=2))\
                            .then_inc(s_stage, 16)
            prog["sp"].append(load_w2)
            quantised(stage[0][:, :, :], NGR, None, (s_stage, 128))
            for el in range(4):
                for par in range(2):
                    dst = w2T[0:KF, :, :, :].rearrange("f (a e) c (q r) -> f a e c q r", a=2, r=2)[:, :, el, :, :, par]
                    turn([st2[:, el, par * F0 + c * KF:par * F0 + (c + 1) * KF] for c in range(CF)],
                         (dst.rearrange("f a c q -> f c a q"),
                          lambda b: b.rearrange("f (c a q) -> f c a q", c=CF, a=2)), cols=KF)
            kept_weights()

            statistics(X, m.mv, m.rstd, 1e-5)
            norm_to_xin()
            statistics(XIN, m.mv, m.rstd, 1e-5, rms=True)
            TR = UT[:, :, :, :].rearrange("p u c q -> p (u c q)")
            KR = EG[:, 0:256]
            KQ = m.KN[:, 256:768].rearrange("p (k d) -> p k d", d=D)

            def batch_head(buf, j):
                return buf.rearrange("p (b h q) -> p h b q", b=2, q=S)[:, 4 * j:4 * j + 4]

            def with_table(table, dst, j):
                def f(v, bank, i, u, own):
                    for b in range(2):
                        ins = v.tensor_tensor(batch_head(dst, j)[:, :, b, :],
                                              bank.rearrange("p (c b q) -> p c b q", c=4, b=2)[:, :, b, :],
                                              table[:, 64 * b:64 * b + 64].unsqueeze(1).to_broadcast([P, 4, S]), ALU.mult)
                    return ins
                return f

            def kv_piece(p, bank, i, u):
                return p.matmul(bank, m.xT[:, :], wkvT[:, :], start=True, stop=True)

            def kv_keep(v, bank, i, u, own):
                mx, mn, sc, ri, bs = [qp[:, k, 0:4] for k in range(5)]
                b3 = bank.rearrange("p (k d) -> p k d", d=D)
                v.tensor_reduce(mx, b3, AX.X, ALU.max).then_inc(own.sem, own.one())
                v.tensor_reduce(mn, b3, AX.X, ALU.min).then_inc(own.sem, own.one())
                v.wait_ge(own.sem, own.n)
                v.tensor_tensor(sc, mx, mn, ALU.subtract).then_inc(own.sem, own.one())
                v.wait_ge(own.sem, own.n)
                v.tensor_scalar(sc, sc, 1e-5, 1.0 / 15.0, ALU.max, ALU.mult).then_inc(own.sem, own.one())
                v.wait_ge(own.sem, own.n)
                v.reciprocal(ri, sc).then_inc(own.sem, own.one())
                v.wait_ge(own.sem, own.n)
                v.tensor_tensor(bs, mn, ri, ALU.mult).then_inc(own.sem, own.one())
                for k in range(4):
                    v.tensor_scalar(KQ[:, k, :], b3[:, k, :], ri[:, k:k + 1], MAGIC, ALU.mult, ALU.add)\
                        .then_inc(own.sem, own.one())
                v.wait_ge(own.sem, own.n)
                v.tensor_scalar(bs, bs, MAGIC, MAGIC, ALU.add, ALU.subtract).then_inc(own.sem, own.one())
                v.wait_ge(own.sem, own.n)
                v.tensor_scalar(bs, bs, 0.0, -15.0, ALU.min, ALU.max).then_inc(own.sem, own.one())
                v.wait_ge(own.sem, own.n)
                v.tensor_scalar(mx, bs, MAGIC, None, ALU.add).then_inc(own.sem, own.one())
                v.tensor_scalar(mn, bs, MAGIC + 15.0, None, ALU.add).then_inc(own.sem, own.one())
                v.wait_ge(own.sem, own.n)
                for k in range(4):
                    v.tensor_scalar(KQ[:, k, :], KQ[:, k, :], mx[:, k:k + 1], mn[:, k:k + 1], ALU.max, ALU.min)\
                        .then_inc(own.sem, own.one())
                v.wait_ge(own.sem, own.n)
                for k in range(4):
                    dst = m.KN[:, k * P:(k + 1) * P] if k < 2 else m.VW[:, u, k - 2, :]
                    ins = v.tensor_scalar(dst, KQ[:, k, :], MAGIC, sc[:, k:k + 1], ALU.subtract, ALU.mult)
                return ins

            def k_finish(v, i, own):
                v.wait_ge(ev["kept0"].sem, ev["kept0"].base + i + 1)
                k3 = m.KN[:, 0:256].rearrange("p (g d) -> p g d", g=2)
                r3 = KR.rearrange("p (g d) -> p g d", g=2)
                for h in range(2):
                    v.tensor_tensor(r3[:, :, 64 * h:64 * h + 64], k3[:, :, 64 - 64 * h:128 - 64 * h],
                                    m.sinN[:, 64 * h:64 * h + 64].unsqueeze(1).to_broadcast([P, 2, 64]),
                                    ALU.mult).then_inc(own.sem, own.one())
                v.wait_ge(own.sem, own.n)
                v.tensor_tensor(k3, k3, m.cosN[:, :].unsqueeze(1).to_broadcast([P, 2, P]), ALU.mult).then_inc(own.sem, own.one())
                v.wait_ge(own.sem, own.n)
                v.tensor_tensor(k3, k3, r3, ALU.add).then_inc(ev["knat"].sem, 1)

            def pool_rope(g, i, u):
                for j in range(2):
                    g.wait_ge(ev["kept%d" % (2 + 2 * j)].sem, ev["kept%d" % (2 + 2 * j)].base + i + 1)
                    q4 = m.QW.rearrange("p (b h q) -> p b (h q)", b=2, q=S)[:, :, 256 * j:256 * j + 256]
                    r4 = TR.rearrange("p (b h q) -> p b (h q)", b=2, q=S)[:, :, 256 * j:256 * j + 256]
                    ins = g.tensor_tensor(q4, q4, r4, ALU.add)
                ins.then_inc(ev["q_turned_by_pos"].sem, 1)

            def scaled(src):
                def f(v, own, i, u):
                    v.tensor_scalar(m.xn[:, u, :], tile_of(src, i), m.rstd[:, bass.ds(i, 1)], None,
                                                    ALU.mult).then_inc(ev["xn"].sem, 1)
                return f

            run(Attention(heads="wide", extra=["kT", "knat", "k_turned", "q_turned_by_pos"],
                     x_gain=m.gains[:, 3:4], mask=causal_mask, scale=float(1 / np.float32(np.sqrt(128))),
                     pieces=[dict(pe=kv_piece, dve=kv_keep, dve_after=k_finish, bank=m.PS[:, 512:1024], last=True),
                             dict(pe=q_piece(wqT, 0), dve=with_table(m.cosT, m.QW, 0), bank=m.RING[:, 0:512], bank_after=-1),
                             dict(pe=q_piece(wqrT, 0), dve=with_table(m.sinT, TR, 0), bank=m.RING[:, 512:1024], bank_after=-1),
                             dict(pe=q_piece(wqT, 1), dve=with_table(m.cosT, m.QW, 1), bank=m.RING[:, 0:512]),
                             dict(pe=q_piece(wqrT, 1), dve=with_table(m.sinT, TR, 1), bank=m.RING[:, 512:1024])],
                     q_ready=["q_turned_by_pos", "kT"], v_ready=["kept0"], w_out=woT, pool_front=pool_rope,
                     normalise=scaled(XIN), finish=finish_into_xin))
            barrier()
        LG = sb("LG", [P, NT * E])
        PR = sb("PR", [P, NT * E])
        RW = sb("RW", [P, NT * E])
        SEL = sb("SEL", [P, 2, NT * E])
        rt = sb("rt", [P, 4, NT])
        s_rt_ready, s_rt_exped = sem("logits_ready"), sem("logits_exped")
        m.n_rt = 0

        def by_tile(buf):
            return buf.rearrange("p (t e) -> p t e", e=E)

        def routing(x_src, w_router, gain, norm, bias=None, hidden=None):
            used = ["xn", "x_turned", "xT", "piece0", "kept0"] + (["piece1", "kept1"] if hidden else [])

            def pe(p):
                def step(n, u, on):
                    if on[1]:
                        t, v = n + 1, 1 - u
                        p.wait_ge(ev["xn"].sem, ev["xn"].base + t + 1)
                        if some(t):
                            p.wait_ge(ev["xT"].sem, ev["xT"].base + t)
                        p.transpose(m.TPS[:, 0:128], m.xn[:, v, :], m.ident[:, :]).then_inc(ev["x_turned"].sem, 1)
                        p.wait_ge(ev["xT"].sem, ev["xT"].base + t + 1)
                        if hidden:
                            if some(t):
                                p.wait_ge(ev["kept1"].sem, ev["kept1"].base + t)
                            p.matmul(m.PS[0:32, 0:128], hidden[0], m.xT[:, :], start=True, stop=True).then_inc(ev["piece1"].sem, 1)
                            p.wait_ge(ev["kept1"].sem, ev["kept1"].base + t + 1)
                        if some(t - 1):
                            p.wait_ge(ev["kept0"].sem, ev["kept0"].base + t - 1)
                        l, r = (hidden[2], hidden[3]) if hidden else (m.xT[:, :], w_router)
                        p.matmul(m.RING[:, v * 512:v * 512 + E], l, r, start=True, stop=True).then_inc(ev["piece0"].sem, 1)
                pipeline(p, None, step)

            def act(s):
                def step(n, u, on):
                    if on[1]:
                        t = n + 1
                        s.wait_ge(ev["x_turned"].sem, ev["x_turned"].base + t + 1)
                        s.activation(m.xT[:, :], m.TPS[:, 0:128], ACT.Copy if gain is None else
                                                     ACT.Identity, scale=1.0 if gain is None else gain).then_inc(ev["xT"].sem, 1)
                        if hidden:
                            s.wait_ge(ev["piece1"].sem, ev["piece1"].base + t + 1)
                            s.activation(hidden[2], m.PS[0:32, 0:128], ACT.Gelu, bias=hidden[1]).then_inc(ev["kept1"].sem, 1)
                pipeline(s, None, step)

            def dve(v):
                own = Own(v, m.own_dve)

                def step(n, u, on):
                    if on[2]:
                        if some(n + 1):
                            v.wait_ge(ev["x_turned"].sem, ev["x_turned"].base + n + 1)
                        norm(v, own, n + 2, u)
                    if on[0]:
                        if some(n + 1):
                            v.wait_ge(ev["piece0"].sem, ev["piece0"].base + n + 1)
                        ps = m.RING[:, u * 512:u * 512 + E]
                        dst = LG[:, bass.ds(n * E, E)]
                        if bias is not None:
                            v.tensor_tensor(dst, ps, bias, ALU.add).then_inc(ev["kept0"].sem, 1)
                        else:
                            v.tensor_scalar(dst, ps, 1.0, None, ALU.mult).then_inc(ev["kept0"].sem, 1)
                pipeline(v, own, step)
            bases = {n: ev[n].base for n in ev}
            for k, f in (("pe", pe), ("act", act), ("dve", dve)):
                def go(eng, f=f):
                    for n, b in bases.items():
                        ev[n].base = b
                    f(eng)
                prog[k].append(go)
            for n in used:
                ev[n].base += NT

        def softmax_and_ranks():
            k = m.n_rt = m.n_rt + 1
            lg, pr = by_tile(LG[:, :]), by_tile(PR[:, :])

            def wide(x):
                return x.unsqueeze(2).to_broadcast([P, NT, E])

            def dve(v):
                own = Own(v, m.own_dve)
                v.wait_ge(ev["kept0"].sem, kept)
                v.tensor_reduce(rt[:, 0, :], lg, AX.X, ALU.max).then_inc(own.sem, own.one())
                v.wait_ge(own.sem, own.n)
                v.tensor_tensor(lg, lg, wide(rt[:, 0, :]), ALU.subtract).then_inc(s_rt_ready, 1)
                v.wait_ge(s_rt_exped, k)
                v.tensor_reduce(rt[:, 1, :], lg, AX.X, ALU.add).then_inc(own.sem, own.one())
                v.wait_ge(own.sem, own.n)
                v.reciprocal(rt[:, 1, :], rt[:, 1, :]).then_inc(own.sem, own.one())
                v.wait_ge(own.sem, own.n)
                v.tensor_tensor(pr, lg, wide(rt[:, 1, :]), ALU.mult).then_inc(own.sem, own.one())
                v.wait_ge(own.sem, own.n)
                above, level = m.R1[:, :].rearrange("p (t e f) -> p t e f", e=E, f=E), \
                    m.R2[:, :].rearrange("p (t e f) -> p t e f", e=E, f=E)
                f_ = pr.unsqueeze(2).to_broadcast([P, NT, E, E])
                e_ = pr.unsqueeze(3).to_broadcast([P, NT, E, E])
                v.tensor_tensor(above, f_, e_, ALU.is_gt).then_inc(own.sem, own.one())
                v.tensor_tensor(level, f_, e_, ALU.is_equal).then_inc(own.sem, own.one())
                v.wait_ge(own.sem, own.n)
                tie = m.tie[:, :].unsqueeze(1).to_broadcast([P, NT, E * E])
                l3 = m.R2[:, :].rearrange("p (t g) -> p t g", g=E * E)
                v.tensor_tensor(l3, l3, tie, ALU.mult).then_inc(own.sem, own.one())
                v.wait_ge(own.sem, own.n)
                v.tensor_tensor(m.R1[:, :], m.R1[:, :], m.R2[:, :], ALU.add).then_inc(own.sem, own.one())
                v.wait_ge(own.sem, own.n)
                v.tensor_reduce(by_tile(RW[:, :]), above, AX.X, ALU.add).then_inc(own.sem, own.one())
                v.wait_ge(own.sem, own.n)
                v.tensor_scalar(SEL[:, 0, :], RW[:, :], 0.0, None, ALU.is_equal).then_inc(own.sem, own.one())
                v.tensor_scalar(SEL[:, 1, :], RW[:, :], 1.0, None, ALU.is_equal).then_inc(own.sem, own.one())
                v.wait_ge(own.sem, own.n)
                own.restart()
            kept = ev["kept0"].base

            def act(s):
                s.wait_ge(s_rt_ready, k)
                s.activation(LG[:, :], LG[:, :], ACT.Exp).then_inc(s_rt_exped, 1)
            prog["dve"].append(dve)
            prog["act"].append(act)

        def top2_weights(normed):
            def dve(v):
                own = Own(v, m.own_dve)
                v.tensor_tensor(RW[:, :], SEL[:, 0, :], SEL[:, 1, :], ALU.add).then_inc(own.sem, own.one())
                v.wait_ge(own.sem, own.n)
                v.tensor_tensor(RW[:, :], RW[:, :], PR[:, :], ALU.mult).then_inc(own.sem, own.one())
                v.wait_ge(own.sem, own.n)
                if normed:
                    v.tensor_reduce(rt[:, 2, :], by_tile(RW[:, :]), AX.X, ALU.add).then_inc(own.sem, own.one())
                    v.wait_ge(own.sem, own.n)
                    v.reciprocal(rt[:, 2, :], rt[:, 2, :]).then_inc(own.sem, own.one())
                    v.wait_ge(own.sem, own.n)
                    v.tensor_tensor(by_tile(RW[:, :]), by_tile(RW[:, :]),
                                             rt[:, 2, :].unsqueeze(2).to_broadcast([P, NT, E]), ALU.mult).then_inc(own.sem, own.one())
                    v.wait_ge(own.sem, own.n)
                own.restart()
            prog["dve"].append(dve)

        for n in ("group_normed", "group_turned", "group_T", "up", "silued", "hidden", "down", "summed", "group_done"):
            ev[n] = Event(sem(n))

        def one_ahead(v):
            v.memset(rt[:, 2, :], 0.0).then_inc(ev["group_done"].sem, 1)
            v.memset(rt[:, 3, :], 0.0).then_inc(ev["group_turned"].sem, 1)
            v.wait_ge(ev["group_done"].sem, 1)
            v.wait_ge(ev["group_turned"].sem, 1)
        prog["dve"].append(one_ahead)
        ev["group_done"].base = ev["group_turned"].base = 1

        def experts(kf, w_in, w_gate, w_out, gain, norm, gate, residual):
            base = {n: ev[n].base for n in ("group_normed", "group_turned", "group_T", "up", "silued", "hidden",
                                                     "down", "summed", "group_done", "done")}
            XG, XGT = m.XG, m.XGT

            def pe(p):
                def up(g, e):
                    for c in range(4):
                        j = 32 * g + 4 * e + c
                        if not (e == 0 and c < 2):
                            if w_gate is not None:
                                p.wait_ge(ev["silued"].sem, base["silued"] + j - 1)
                            p.wait_ge(ev["hidden"].sem, base["hidden"] + j - 1)
                        bank = (c % 2) * 512
                        ins = p.matmul(m.RING[0:kf, bank:bank + 512], w_in(e, c), XGT[:, :], start=True, stop=True)
                        if w_gate is not None:
                            ins = p.matmul(m.PS[0:kf, bank:bank + 512], w_gate(e, c), XGT[:, :], start=True, stop=True)
                        ins.then_inc(ev["up"].sem, 1)

                def down(g, e):
                    p.wait_ge(ev["hidden"].sem, base["hidden"] + 32 * g + 4 * e + 4)
                    if e >= 2:
                        p.wait_ge(ev["summed"].sem, base["summed"] + 8 * g + e - 1)
                    for i in range(GROUP):
                        for c in range(4):
                            ins = p.matmul(m.PTP[:, (e % 2) * 512 + i * P:(e % 2) * 512 + (i + 1) * P],
                                           m.UTE[0:kf, e % 2, c, i * P:(i + 1) * P], w_out(e, c),
                                           start=(c == 0), stop=(c == 3))
                    ins.then_inc(ev["down"].sem, 1)
                with p.Fori(0, NG) as g:
                    p.wait_ge(ev["group_normed"].sem, base["group_normed"] + g + 1)
                    p.wait_ge(ev["group_done"].sem, base["group_done"] + g)
                    for i in range(GROUP):
                        ins = p.transpose(m.TPS[:, i * P:(i + 1) * P], XG[:, i, :], m.ident[:, :])
                    ins.then_inc(ev["group_turned"].sem, 1)
                    p.wait_ge(ev["group_T"].sem, base["group_T"] + g + 1)
                    up(g, 0)
                    for e in range(E):
                        if e + 1 < E:
                            up(g, e + 1)
                        down(g, e)

            def act(s):
                with s.Fori(0, NG) as g:
                    s.wait_ge(ev["group_turned"].sem, base["group_turned"] + g + 1)
                    s.activation(XGT[:, :], m.TPS[:, :], ACT.Copy if gain is None else ACT.Identity,
                                 scale=1.0 if gain is None else gain).then_inc(ev["group_T"].sem, 1)
                    for e in range(E):
                        for c in range(4):
                            j = 32 * g + 4 * e + c
                            s.wait_ge(ev["up"].sem, base["up"] + j + 1)
                            src = m.RING[0:kf, (c % 2) * 512:(c % 2) * 512 + 512]
                            if w_gate is not None:
                                s.activation(m.SG[0:kf, c % 2, :], src, ACT.Silu).then_inc(ev["silued"].sem, 1)
                            else:
                                s.activation(m.UTE[0:kf, e % 2, c, :], src, ACT.Relu).then_inc(ev["hidden"].sem, 1)

            def dve(v):
                own = Own(v, m.own_dve)
                acc = m.ACC

                def add(g, e):
                    v.wait_ge(ev["down"].sem, base["down"] + 8 * g + e + 1)
                    for i in range(GROUP):
                        scalar = RW[:, bass.ds((4 * g + i) * E + e, 1)]
                        src = m.PTP[:, (e % 2) * 512 + i * P:(e % 2) * 512 + (i + 1) * P]
                        if e == 0:
                            ins = v.tensor_scalar(acc[:, i, :], src, scalar, None, ALU.mult)
                        else:
                            ins = v.scalar_tensor_tensor(acc[:, i, :], src, scalar, acc[:, i, :], ALU.mult, ALU.add)
                    ins.then_inc(ev["summed"].sem, 1)
                    v.wait_ge(ev["summed"].sem, base["summed"] + 8 * g + e + 1)
                with v.Fori(0, NG) as g:
                    v.wait_ge(ev["group_turned"].sem, base["group_turned"] + g)
                    for i in range(GROUP):
                        ins = norm(v, XG[:, i, :], 4 * g + i)
                    ins.then_inc(ev["group_normed"].sem, 1)
                    for e in range(E):
                        if w_gate is not None:
                            for c in range(4):
                                j = 32 * g + 4 * e + c
                                v.wait_ge(ev["silued"].sem, base["silued"] + j + 1)
                                v.tensor_tensor(m.UTE[0:kf, e % 2, c, :], m.PS[0:kf, (c % 2) * 512:(c % 2) * 512 + 512],
                                                m.SG[0:kf, c % 2, :], ALU.mult).then_inc(ev["hidden"].sem, 1)
                        if e:
                            add(g, e - 1)
                    add(g, E - 1)
                    a2 = acc.rearrange("p i d -> p (i d)")
                    if residual is not None:
                        v.tensor_tensor(a2, a2, tile_of(residual, g, GT), ALU.add).then_inc(own.sem, own.one())
                        v.wait_ge(own.sem, own.n)
                    v.scalar_tensor_tensor(tile_of(X, g, GT), a2, m.tg[:, gate:gate + 1], tile_of(X, g, GT),
                                           ALU.mult, ALU.add).then_inc(ev["group_done"].sem, 1)
                    own.restart()
                v.wait_ge(ev["group_done"].sem, base["group_done"] + NG)
            for k, f in (("pe", pe), ("act", act), ("dve", dve)):
                prog[k].append(f)
            per = dict(group_normed=NG, group_turned=NG, group_T=NG, up=32 * NG, hidden=32 * NG, down=E * NG, summed=E * NG,
                       group_done=NG, silued=32 * NG if w_gate is not None else 0)
            for n, k in per.items():
                ev[n].base += k

        def group_barrier():
            v = ev["group_done"].base
            for k in prog:
                prog[k].append(lambda eng, v=v: eng.wait_ge( ev["group_done"].sem, v))

        def again():
            WORK.again()
            m.XG = WORK.cut([P, GROUP, D])
            m.XGT = WORK.cut([P, GT])
            m.SG = WORK.cut([P, 2, GT])
            m.UTE = WORK.cut([P, 2, 4, GT])
            m.ACC = WORK.cut([P, GROUP, D])
            m.R1 = WORK.cut([P, NT * E * E])
            m.R2 = WORK.cut([P, NT * E * E])

        def attention_buffers():
            WORK.again()
            m.QT = WORK.cut([P, 8, P])
            m.KT = WORK.cut([P, 8, P])
            m.V = WORK.cut([P, 2, 2, 512])
            m.PROB = WORK.cut([P, 1024])
            m.PT = WORK.cut([P, 8, P])
            m.OT = WORK.cut([P, 8, P])

        def narrow_buffers():
            WORK.again()
            m.QB = WORK.cut([P, P])
            m.KB = WORK.cut([P, P])
            m.KT8 = WORK.cut([P, 8, P])
            m.VP = WORK.cut([P, 4 * 1024 + P])
            m.PROB2 = WORK.cut([P, 2 * 1024])
            m.PT8 = WORK.cut([P, 8, P])
            m.OT1 = WORK.cut([P, 1, P])

        if stop >= 3:
            again()
            statistics(XIN, m.mv, m.rstd, 1e-5, rms=True)
            routing(XIN, wgT[:, 0, :], m.gains[:, 4:5], scaled(XIN))
            softmax_and_ranks()
            top2_weights(True)
            experts(KF, lambda e, c: w1T[:, e * F0 + c * KF:e * F0 + (c + 1) * KF],
                    lambda e, c: w3T[:, e * F0 + c * KF:e * F0 + (c + 1) * KF],
                    lambda e, c: w2T[0:KF, e, c, :], m.gains[:, 4:5],
                    lambda v, dst, i: v.tensor_scalar(dst, tile_of(XIN, i), m.rstd[:, bass.ds(i, 1)], None, ALU.mult),
                    4, XIN)
            group_barrier()
        if stop >= 4:
            attention_buffers()
            RA.again()
            TMPO = RA.cut([P, D])
            WoE = RA.cut([P, E, 4, D])
            xm = RA.cut([P, NT])
            cm = RA.cut([P, NT, S])
            valid = RA.cut([P, NT])
            bo1 = RA.cut([P, D])
            br1 = RA.cut([P, E])
            NEXT_A = RA.at
            w_done = ev["group_done"].base
            halves = "(t b) s -> b t s"

            def of_keys(name, hb, words=S):
                return t[name].rearrange(halves, b=2)[hb].unsqueeze(0).to_broadcast([64, NT, words])

            def of_queries(name):
                return t[name].rearrange("(t b) s -> (b s) t", b=2)
            load("layer1_masks", [(xm[:, :], of_queries("mask_BxS2_fk1")),
                                  (cm[0:64], of_keys("mask_BxS2_fk1", 0)), (cm[64:128], of_keys("mask_BxS2_fk1", 1)),
                                  (bo1[:, :], row(t["L1_xattn_bo"], D)), (br1[:, :], row(t["L1_ffn_b_router"], E))])
            load("layer1_expert_out", [(WoE[:, e, :, :], t["L1_ffn_experts_out"][e].rearrange("(c p) h -> p c h", p=P))
                                       for e in range(E)])

            def mask1(v):
                loaded(v, "layer1_masks")
                own = Own(v, m.own_dve)
                v.tensor_tensor(cm[:, :, :], cm[:, :, :], xm[:, :].unsqueeze(2).to_broadcast([P, NT, S]), ALU.mult).then_inc(own.sem, own.one())
                v.wait_ge(own.sem, own.n)
                v.tensor_scalar(cm[:, :, :], cm[:, :, :], -1.0, 1.0, ALU.mult, ALU.add).then_inc(own.sem, own.one())
                v.wait_ge(own.sem, own.n)
                v.tensor_scalar(cm[:, :, :], cm[:, :, :], 1.0, None, ALU.subtract).then_inc(own.sem, own.one())
                v.wait_ge(own.sem, own.n)
                minus = m.PROB[:, :].rearrange("p (t k) -> p t k", k=S)
                v.tensor_scalar(minus, cm[:, :, :], -1.0, None, ALU.mult).then_inc(own.sem, own.one())
                v.wait_ge(own.sem, own.n)
                v.tensor_tensor(cm[:, :, :], cm[:, :, :], minus, ALU.max).then_inc(own.sem, own.one())
                v.wait_ge(own.sem, own.n)
                v.tensor_scalar(cm[:, :, :], cm[:, :, :], 1e-8 + 1e-5, NEG, ALU.is_le, ALU.mult).then_inc(own.sem, own.one())
                v.wait_ge(own.sem, own.n)
                v.tensor_reduce(valid[:, :], cm[:, :, :], AX.X, ALU.max).then_inc(own.sem, own.one())
                v.wait_ge(own.sem, own.n)
                v.tensor_scalar(valid[:, :], valid[:, :], NEG / 2, None, ALU.is_gt).then_inc(own.sem, own.one())
                v.wait_ge(own.sem, own.n)
                own.restart()
            prog["dve"].append(mask1)
            statistics(X, m.mv, m.rstd, 1e-5)
            prog["pe"].append(lambda p: loaded(p, "layer1_attention"))
            m.cx_phase = 0

            def kv1_piece(j):
                def f(p, bank, i, u):
                    for c in range(4):
                        ins = p.matmul(bank[:, c * P:(c + 1) * P], Wkv1[:, (4 * j + c) * P:(4 * j + c + 1) * P], m.cT[:, :],
                                       start=True, stop=True)
                    return ins
                return f

            def k1_keep(j):
                def f(s, bank, i, u, own):
                    return s.activation(m.KT[:, 4 * j:4 * j + 4, :], bank.rearrange("p (c q) -> p c q", c=4), ACT.Copy)
                return f

            def v1_piece(b):
                def f(p, bank, i, u):
                    w = Wkv1[:, 1024:2048].rearrange("p (c h d) -> p c h d", c=8, h=2)
                    for h in range(2):
                        ins = p.matmul(bank[64 * h:64 * h + 64, :].rearrange("p (c d) -> p c d", c=8),
                                       m.cT[:, 64 * b:64 * b + 64], w[:, :, h, :], start=True, stop=True)
                    return ins
                return f

            def v1_keep(b):
                def f(s, bank, i, u, own):
                    return s.activation(m.V[:, u, b, :], bank, ACT.Copy)
                return f

            def finish_biased(gate, bias):
                def f(v, own, i):
                    v.tensor_tensor(TMPO[:, :], m.OPS[:, 0:128], bias[:, :], ALU.add).then_inc(own.sem, own.one())
                    v.wait_ge(own.sem, own.n)
                    return v.scalar_tensor_tensor(tile_of(X, i), TMPO[:, :], m.tg[:, gate:gate + 1], tile_of(X, i),
                                                  ALU.mult, ALU.add)
                return f

            def next_ctx():
                k = m.cx_phase
                m.cx_phase += 1
                return k * 8 * NT

            run(Attention(ctx="load", cx_base=next_ctx(), many_k=True, scale=64 ** -0.5,
                     mask=lambda i: cm[:, bass.ds(i, 1), :].unsqueeze(1),
                     rowscale=lambda i: valid[:, bass.ds(i, 1)],
                     pieces=[dict(pe=q_piece(Wq1, 0), act=q_keep(0)), dict(pe=q_piece(Wq1, 1), act=q_keep(1)),
                             dict(pe=kv1_piece(0), act=k1_keep(0)), dict(pe=kv1_piece(1), act=k1_keep(1)),
                             dict(pe=v1_piece(0), act=v1_keep(0)), dict(pe=v1_piece(1), act=v1_keep(1))],
                     q_ready=["kept0", "kept1", "kept2", "kept3"], v_ready=["kept4", "kept5"], w_out=Wo1,
                     normalise=normalise(X), finish=finish_biased(1, bo1)))
            barrier()
        if stop >= 5:
            again()
            CAP = int(np.ceil(B * S / E * 1.25))
            statistics(X, m.mv, m.rstd, 1e-5)
            prog["dve"].append(lambda v: loaded(v, "layer1_masks"))
            routing(X, wgT[:, 1, :], None, normalise(X), bias=br1[:, :])
            softmax_and_ranks()
            top2_weights(False)
            s_chosen, s_counted = sem("chosen"), sem("counted")

            def chosen(v):
                own = Own(v, m.own_dve)
                v.tensor_scalar(SEL[:, 0, :], RW[:, :], 0.0, None, ALU.is_gt).then_inc(s_chosen, 1)
                v.wait_ge(s_counted, 1)
                cnt = m.PS[:, 512:640].rearrange("p (t e) -> p t e", e=E)
                a = [m.R1[:, 0:128].rearrange("p (t e) -> p t e", e=E), m.R2[:, 0:128].rearrange("p (t e) -> p t e", e=E)]
                v.tensor_copy(a[0], cnt).then_inc(own.sem, own.one())
                v.wait_ge(own.sem, own.n)
                for k, d in enumerate((1, 2, 4, 8)):
                    x, y = a[k % 2], a[1 - k % 2]
                    v.tensor_copy(y[:, 0:d, :], x[:, 0:d, :]).then_inc(own.sem, own.one())
                    v.tensor_tensor(y[:, d:NT, :], x[:, d:NT, :], x[:, 0:NT - d, :], ALU.add).then_inc(own.sem, own.one())
                    v.wait_ge(own.sem, own.n)
                v.tensor_tensor(a[0], a[0], cnt, ALU.subtract).then_inc(own.sem, own.one())
                v.wait_ge(own.sem, own.n)
                v.tensor_tensor(a[0], a[0], m.PS[:, 0:128].rearrange("p (t e) -> p t e", e=E), ALU.add).then_inc(own.sem, own.one())
                v.wait_ge(own.sem, own.n)
                v.tensor_scalar(m.R1[:, 0:128], m.R1[:, 0:128], float(CAP), None, ALU.is_lt).then_inc(own.sem, own.one())
                v.wait_ge(own.sem, own.n)
                v.tensor_tensor(RW[:, :], RW[:, :], m.R1[:, 0:128], ALU.mult).then_inc(own.sem, own.one())
                v.wait_ge(own.sem, own.n)
                own.restart()
            prog["dve"].append(chosen)

            def count(p):
                p.wait_ge(s_chosen, 1)
                p.matmul(m.PS[:, 0:128], m.before[:, :], SEL[:, 0, :], start=True, stop=True)
                p.matmul(m.PS[:, 512:640], m.ones[:, :], SEL[:, 0, :], start=True, stop=True).then_inc(s_counted, 1)
            prog["pe"].append(count)
            prog["pe"].append(lambda p: (loaded(p, "layer1_experts"), loaded(p, "layer1_expert_out")))
            experts(P, lambda e, c: WiE[:, e, c * P:(c + 1) * P], None, lambda e, c: WoE[:, e, c, :], None,
                    lambda v, dst, i: norm_tile(v, dst, X, i, mv2, m.rstd), 5, None)
            group_barrier()
        if stop >= 6:
            narrow_buffers()
            RB.again()
            RA.again()
            TMPO = RA.cut([P, D])
            nat2 = RA.cut([P, 4, D])
            wT2 = RA.cut([P, 4, D])
            bq2, bk2 = RA.cut([P, 1]), RA.cut([P, 1])
            bv2 = RA.cut([P, 64])
            bo2 = RA.cut([P, D])
            wr1, br1c, wr2, br2 = RA.cut([P, 32]), RA.cut([P, 1]), RA.cut([P, E]), RA.cut([P, E])
            hr = RA.cut([P, P])
            wh1, bh1, wh2c, wh2, bh2 = RA.cut([P, 32]), RA.cut([P, 1]), RA.cut([P, 1]), RA.cut([P, P]), RA.cut([P, 1])
            e1, be1 = RA.cut([P, 2, 512]), RA.cut([P, 4])
            e2, be2 = RA.cut([P, 4, 384]), RA.cut([P, 384])
            s1, bs1 = RA.cut([P, 2, 64]), RA.cut([P, 1])
            s2, bs2 = RA.cut([P, 384]), RA.cut([P, 3])
            f1, bf1, f2, bf2 = RA.cut([P, 256]), RA.cut([P, 2]), RA.cut([P, 2, D]), RA.cut([P, 1])
            iw, mu, sw = RA.cut([P, 1]), RA.cut([P, 1]), RA.cut([P, 1])
            wq3, wk3, wv3, wo3, bo3 = (RA.cut([P, D]), RA.cut([P, E, D]), RA.cut([P, E, D]), RA.cut([P, 1, D]),
                                       RA.cut([P, D]))
            kt3, qt3 = RA.cut([P, NT, S]), RA.cut([P, NT])
            pad = RA.cut([P, NT, S])
            BK = RA.cut([P, NT * P])
            cmT = RA.cut([P, E, P])
            nat3 = RA.cut([P, 2, 512])
            pad8 = RA.cut([P, NT * S // 4])
            LEFT_A = RA.at
            tok_row = t["itok_BxS2_0_7"].rearrange("b s -> (b s)")
            load("layer2_attention", [(nat2[:, i, :], t["L2_xattn_W" + n]) for i, n in enumerate("qkvo")]
                 + [(bq2[:, :], col(t["L2_xattn_bq"])), (bk2[:, :], col(t["L2_xattn_bk"])),
                    (bv2[0:64], row(t["L2_xattn_bv"][0:64], 64)[0:64]), (bv2[64:128], row(t["L2_xattn_bv"][64:128], 64)[0:64]),
                    (bo2[:, :], row(t["L2_xattn_bo"], D))])
            A2 = "L2_ffn_"
            load("layer2_ffn", [
                (wr1[:, :], t[A2 + "w_r1"]), (br1c[0:32], col(t[A2 + "b_r1"])), (wr2[0:32], t[A2 + "w_r2"]),
                (br2[:, :], row(t[A2 + "b_r2"], E)), (wh1[:, :], t[A2 + "w_h1"]), (bh1[0:32], col(t[A2 + "b_h1"])),
                (wh2c[0:32], t[A2 + "w_h2"]), (bh2[:, :], row(t[A2 + "b_h2"], 1))]
                + [(e1[:, k, :].rearrange("p (e h) -> p e h", e=E), t[A2 + "expert_w1"].rearrange("e (k p) h -> k p e h", k=2)[k])
                   for k in range(2)]
                + [(be1[:, :], t[A2 + "expert_b1"].rearrange("(c a) h -> (a h) c", a=2)),
                   (e2[:, :, :], t[A2 + "expert_w2"].rearrange("(c a) h o -> (a h) c o", a=2)),
                   (be2[0:E], t[A2 + "expert_b2"]), (be2[E:P], t["const_zeros"][E:P]),
                   (s1[:, :, :], t[A2 + "w_s1"].rearrange("(k p) h -> p k h", p=P)), (bs1[0:64], col(t[A2 + "b_s1"])),
                   (s2[0:64], t[A2 + "w_s2"]), (bs2[:, :], t[A2 + "b_s2"].rearrange("(j p) -> p j", p=P)),
                   (f1[:, :], t[A2 + "w_f1"]), (bf1[:, :], t[A2 + "b_f1"].rearrange("(j p) -> p j", p=P)),
                   (f2[:, :, :], t[A2 + "w_f2"].rearrange("(k p) d -> p k d", p=P)), (bf2[:, :], col(t[A2 + "b_f2"])),
                   (iw[:, :], col(t[A2 + "integration_weight"])), (mu[:, :], col(t[A2 + "mu"])),
                   (sw[:, :], row(t[A2 + "shared_weight"], 1))])
            load("layer3", [
                (wq3[:, :], t["L3_xattn_Wq"]), (wk3[:, :, :], t["L3_xattn_Wk_b"].rearrange("e d k -> d e k")),
                (wv3[:, :, :], t["L3_xattn_Wv_b"].rearrange("e d k -> d e k")), (wo3[:, 0, :], t["L3_xattn_Wo"]),
                (bo3[:, :], row(t["L3_xattn_bo"], D)), (qt3[:, :], of_queries("fside_BxS2_0")),
                (kt3[0:64], of_keys("fside_BxS2_0", 0)), (kt3[64:128], of_keys("fside_BxS2_0", 1)),
                (pad8.bitcast(I32)[0:64].rearrange("p (t k) -> p t k", t=NT), of_keys("mask_BxS2_bf0", 0, S // 4)),
                (pad8.bitcast(I32)[64:128].rearrange("p (t k) -> p t k", t=NT), of_keys("mask_BxS2_bf0", 1, S // 4)),
                (cmT[:, :, :].rearrange("p e q -> p (e q)").bitcast(I32), row(tok_row[0:1024], 1024)),
                (pad[:, :, :].rearrange("p t k -> p (t k)").bitcast(I32), row(tok_row[1024:2048], 1024)),
                (nat3[:, 0, :].rearrange("p (c d) -> p c d", c=4), t["L3_ffn_w1"].rearrange("(c p) d -> p c d", p=P)),
                (nat3[:, 1, :], t["L3_ffn_w2"])])

            prog["pe"].append(lambda p: loaded(p, "layer2_attention"))
            turn([nat2[:, i, :] for i in range(4)], (wT2[:, :, :], flat(4)))
            kept_weights()
            prog["act"].append(lambda s: loaded(s, "layer2_attention"))
            prog["dve"].append(lambda s: loaded(s, "layer2_attention"))
            statistics(X, m.mv, m.rstd, 1e-5)

            def one(w, src):
                def f(p, bank, i, u):
                    return p.matmul(bank[:, 0:P], w, src[:, :], start=True, stop=True)
                return f

            def to_buffer(dst, bias=None):
                def f(s, bank):
                    if bias is None:
                        return s.activation(dst, bank[:, 0:P], ACT.Copy)
                    return s.activation(dst, bank[:, 0:P], ACT.Identity, bias=bias)
                return f

            def v2_piece(p, bank, i, u):
                for b in range(2):
                    for h in range(2):
                        ins = p.matmul(bank[64 * h:64 * h + 64, 64 * b:64 * b + 64], m.cT[:, 64 * b:64 * b + 64],
                                       wT2[:, 2, 64 * h:64 * h + 64], start=True, stop=True)
                return ins

            def v2_keep(v, spread_v, bank, u):
                def put(dst, src, h):
                    bias = bv2[64 * h:64 * h + 64, :].rearrange("p (c x) -> p c x", c=8)
                    return v.tensor_tensor(dst, src, bias, ALU.add)
                return spread_v(put, bank, u)
            run(Attention(heads="narrow", ctx="load", cx_base=next_ctx(), scale=float(1 / np.sqrt(np.float32(8))),
                          pieces=[dict(pe=one(wT2[:, 0, :], m.xT), act=to_buffer(m.QB[:, :], bq2[:, :])),
                                  dict(pe=one(wT2[:, 1, :], m.cT), act=to_buffer(m.KB[:, :], bk2[:, :])),
                                  dict(pe=v2_piece, dve=v2_keep)],
                          w_out=wT2[:, 3:4, :], normalise=normalise(X), finish=finish_biased(2, bo2)))
            barrier()
        if stop >= 7:
            again()
            statistics(X, m.mv, m.rstd, 1e-5)
            for eng in ("pe", "act", "dve", "pool"):
                prog[eng].append(lambda x: loaded(x, "layer2_ffn"))
            s_prep = sem("layer2_prepared")

            def prep2_dve(v):
                own = Own(v, m.own_dve)
                v.tensor_scalar(sw[:, :], sw[:, :], 0.5, 0.5, ALU.mult, ALU.add).then_inc(own.sem, own.one())
                v.wait_ge(own.sem, own.n)
                own.restart()

            def prep2_act(s):
                s.activation(sw[:, :], sw[:, :], ACT.Tanh, scale=0.5).then_inc(s_prep, 1)
                s.activation(wh2[0:32, :], wh2c[0:32, 0:1].to_broadcast([32, P]), ACT.Copy).then_inc(s_prep, 1)
                s.activation(bh2[:, :], bh2[:, :], ACT.Copy, scale=0.5).then_inc(s_prep, 1)
                s.activation(hb2[:, :], bs2[:, :], ACT.Copy, scale=0.5).then_inc(s_prep, 1)
            hb2 = sb("hb2", [P, 3])
            prog["act"].append(prep2_act)
            prog["dve"].append(lambda v: v.wait_ge(s_prep, 1))
            prog["dve"].append(prep2_dve)
            prog["pe"].append(lambda p: p.wait_ge(s_prep, 4))
            prog["act"].append(lambda s: s.wait_ge(s_prep, 4))
            routing(X, None, None, normalise(X), bias=br2[:, :], hidden=(wr1[:, :], br1c[0:32], hr[0:32, :], wr2[0:32, :]))
            softmax_and_ranks()
            top2_weights(True)
            WORK.again()
            m.XG = WORK.cut([P, GROUP, D])
            IT, VT = WORK.cut([P, GT]), WORK.cut([P, GT])
            HS, HG = WORK.cut([P, GT]), WORK.cut([P, 4, GT])
            OH, WH = WORK.cut([P, 2, GT]), WORK.cut([P, 2, GT])
            S4 = WORK.cut([P, 4, GROUP * E])
            ERR, XN, H1, TH = (WORK.cut([P, GT]) for _ in range(4))
            F1 = WORK.cut([P, 2, GT])
            RB.again()
            MK = RB.cut([P, 2, 4, GT])
            MH = RB.cut([P, 2, 4, GT])
            RA.at = LEFT_A
            WW, TA, TG = (RA.cut([P, 3, GT]) for _ in range(3))
            ZB, AB = (RA.cut([P, 3, GT]) for _ in range(2))
            per = dict(g_normed=1, g_turned=1, g_T=1, sel_ready=1, sel_turned=1, sel_T=1, spread=10, spread_kept=10,
                       hid=10, hid_gelu=10, masked0=8, masked1=8, steer=6, steer_kept=6, soft=2,
                       x_next=2, refine=6, refine_gelu=6, refined=2, halted=2, it_done=2, fin_turned=1, g_done=1)
            gs = {n: sem("update_" + n) for n in per}

            ahead = ("g_done", "g_turned", "sel_turned")

            def nth(name, g, k):
                return per[name] * g + k + (1 if name in ahead else 0)

            HB = [m.PTP[:, 0:512], m.PTP[:, 512:1024], m.OPS[:, :], m.TPS[:, :], m.RING[:, 0:512]]
            CB = [[m.RING[:, 0:512], m.RING[:, 512:1024], m.PS[:, 0:512]],
                  [m.PS[:, 512:1024], m.PTP[:, 0:512], m.PTP[:, 512:1024]]]

            def pe(p):
                def mm(out, l, r, start=True, stop=True):
                    return p.matmul(out, l, r, start=start, stop=stop)
                with p.Fori(0, NG) as g:
                    p.wait_ge(gs["g_normed"], nth("g_normed", g, 1))
                    p.wait_ge(gs["g_done"], nth("g_done", g, 0))
                    for i in range(GROUP):
                        ins = p.transpose(m.TPS[:, i * P:(i + 1) * P], m.XG[:, i, :], m.ident[:, :])
                    ins.then_inc(gs["g_turned"], 1)
                    p.wait_ge(gs["sel_ready"], nth("sel_ready", g, 1))
                    for k in range(4):
                        bank = (m.RING, m.PS)[k // 2]
                        for i in range(GROUP):
                            o = (k % 2) * 512 + i * P
                            ins = p.transpose(bank[0:E, o:o + P], S4[:, k, i * E:(i + 1) * E], m.ident[:, :])
                    ins.then_inc(gs["sel_turned"], 1)
                    p.wait_ge(gs["sel_T"], nth("sel_T", g, 1))
                    for j in range(10):
                        if j >= 2:
                            p.wait_ge(gs["spread_kept"], nth("spread_kept", g, j - 1))
                        bank = m.RING[:, (j % 2) * 512:(j % 2) * 512 + 512]
                        if j < 8:
                            ins = mm(bank, m.pick[:, (j % 4) * P:(j % 4 + 1) * P], OH[:, j // 4, :])
                        else:
                            ins = mm(bank, m.ones[:, :], WH[:, j - 8, :])
                        ins.then_inc(gs["spread"], 1)
                    p.wait_ge(gs["spread_kept"], nth("spread_kept", g, 10))
                    p.wait_ge(gs["g_T"], nth("g_T", g, 1))
                    for it in range(2):
                        if it:
                            p.wait_ge(gs["it_done"], nth("it_done", g, 1))
                        for j in range(5):
                            for k, c in enumerate((IT, VT)):
                                l = s1[:, k, :] if j == 0 else e1[:, k, (j - 1) * P:j * P]
                                o = HB[j][0:64, :] if j == 0 else HB[j]
                                ins = mm(o, l, c[:, :], start=(k == 0), stop=(k == 1))
                            ins.then_inc(gs["hid"], 1)
                        for r in range(3):
                            if r == 0:
                                p.wait_ge(gs["hid_gelu"], nth("hid_gelu", g, 5 * it + 5))
                            elif r == 1:
                                p.wait_ge(gs["masked0"], nth("masked0", g, 4 * it + 4))
                            else:
                                p.wait_ge(gs["steer_kept"], nth("steer_kept", g, 3 * it + 1))
                                p.wait_ge(gs["masked1"], nth("masked1", g, 4 * it + 4))
                            for j in range(3):
                                bank = CB[r % 2][j]
                                if r == 0:
                                    ins = mm(bank, s2[0:64, j * P:(j + 1) * P], HS[0:64, :])
                                else:
                                    for c in range(4):
                                        mm(bank, e2[:, c, j * P:(j + 1) * P], MH[:, r - 1, c, :], c == 0, False)
                                    ins = mm(bank, be2[:, j * P:(j + 1) * P], OH[:, r - 1, :], False, True)
                            ins.then_inc(gs["steer"], 1)
                        p.wait_ge(gs["x_next"], nth("x_next", g, it + 1))
                        for j in range(3):
                            o, l = (m.TPS[0:32, :], wh1[:, :]) if j == 0 else ((m.OPS, m.PTP)[j - 1][:, 0:512],
                                                                            f1[:, (j - 1) * P:j * P])
                            mm(o, l, XN[:, :]).then_inc(gs["refine"], 1)
                        p.wait_ge(gs["refine_gelu"], nth("refine_gelu", g, 3 * it + 3))
                        mm(m.RING[:, 0:512], wh2[0:32, :], H1[0:32, :])
                        for k in range(2):
                            ins = mm(m.RING[:, 512:1024], f2[:, k, :], F1[:, k, :], k == 0, k == 1)
                        ins.then_inc(gs["refined"], 1)
                    p.wait_ge(gs["it_done"], nth("it_done", g, 2))
                    for i in range(GROUP):
                        ins = p.transpose(m.TPS[:, i * P:(i + 1) * P], IT[:, i * P:(i + 1) * P], m.ident[:, :])
                    ins.then_inc(gs["fin_turned"], 1)

            def act(s):
                with s.Fori(0, NG) as g:
                    s.wait_ge(gs["g_turned"], nth("g_turned", g, 1))
                    s.activation(IT[:, :], m.TPS[:, :], ACT.Copy).then_inc(gs["g_T"], 1)
                    s.wait_ge(gs["sel_turned"], nth("sel_turned", g, 1))
                    s.activation(OH[0:E, :, :], m.RING[0:E, :].rearrange("p (k q) -> p k q", k=2), ACT.Copy)
                    s.activation(WH[0:E, :, :], m.PS[0:E, :].rearrange("p (k q) -> p k q", k=2), ACT.Copy)\
                        .then_inc(gs["sel_T"], 1)
                    for j in range(10):
                        s.wait_ge(gs["spread"], nth("spread", g, j + 1))
                        dst = MK[:, j // 4, j % 4, :] if j < 8 else WW[:, j - 7, :]
                        s.activation(dst, m.RING[:, (j % 2) * 512:(j % 2) * 512 + 512], ACT.Copy)\
                            .then_inc(gs["spread_kept"], 1)
                    for it in range(2):
                        for j in range(5):
                            s.wait_ge(gs["hid"], nth("hid", g, 5 * it + j + 1))
                            if j == 0:
                                ins = s.activation(HS[0:64, :], HB[0][0:64, :], ACT.Gelu, bias=bs1[0:64])
                            else:
                                ins = s.activation(HG[:, j - 1, :], HB[j], ACT.Gelu, bias=be1[:, j - 1:j])
                            ins.then_inc(gs["hid_gelu"], 1)
                        for r in range(3):
                            s.wait_ge(gs["steer"], nth("steer", g, 3 * it + r + 1))
                            a, b, c = CB[r % 2]
                            if r == 0:
                                s.activation(TA[:, r, :], a, ACT.Tanh, bias=hb2[:, 0:1], scale=0.5)
                                s.activation(TG[:, r, :], c, ACT.Tanh, bias=hb2[:, 2:3], scale=0.5)
                                ins = s.activation(ZB[:, r, :], b, ACT.Identity, bias=bs2[:, 1:2])
                            else:
                                s.activation(TA[:, r, :], a, ACT.Tanh, scale=0.5)
                                s.activation(TG[:, r, :], c, ACT.Tanh, scale=0.5)
                                ins = s.activation(ZB[:, r, :], b, ACT.Copy)
                            ins.then_inc(gs["steer_kept"], 1)
                        s.preload_act_table_set("natural_log_exp_and_others")
                        s.wait_ge(gs["steer_kept"], per["steer_kept"] * g + 3 * it + 3)
                        s.activation(AB[:, :, :], ZB[:, :, :], ACT.Abs).then_inc(m.own_act, 1)
                        s.wait_ge(m.own_act, 1)
                        s.activation(AB[:, :, :], AB[:, :, :], ACT.Exp, scale=-1.0).then_inc(m.own_act, 1)
                        s.wait_ge(m.own_act, 2)
                        s.activation(AB[:, :, :], AB[:, :, :], ACT.Ln, bias=1.0).then_inc(gs["soft"], 1)
                        s.sem_clear(m.own_act)
                        for j in range(3):
                            s.wait_ge(gs["refine"], nth("refine", g, 3 * it + j + 1))
                            if j == 0:
                                ins = s.activation(H1[0:32, :], m.TPS[0:32, :], ACT.Gelu, bias=bh1[0:32])
                            else:
                                ins = s.activation(F1[:, j - 1, :], (m.OPS, m.PTP)[j - 1][:, 0:512], ACT.Gelu,
                                                   bias=bf1[:, j - 1:j])
                            ins.then_inc(gs["refine_gelu"], 1)
                        s.wait_ge(gs["refined"], nth("refined", g, it + 1))
                        s.activation(TH[:, :], m.RING[:, 0:512], ACT.Tanh, bias=bh2[:, 0:1], scale=0.5)\
                            .then_inc(gs["halted"], 1)

            def dve(v):
                own = Own(v, m.own_dve)
                v.memset(OH[:, :, :], 0.0).then_inc(gs["g_done"], 1)
                v.memset(WH[:, :, :], 0.0).then_inc(gs["g_turned"], 1)
                v.memset(WW[:, 0, :], 0.0).then_inc(gs["sel_turned"], 1)
                for name in ahead:
                    v.wait_ge(gs[name], 1)
                v.tensor_scalar(WW[:, 0, :], WW[:, 0, :], sw[:, 0:1], None, ALU.add).then_inc(own.sem, own.one())
                own.restart()
                half = 0.5
                with v.Fori(0, NG) as g:
                    v.wait_ge(gs["g_turned"], nth("g_turned", g, 0))
                    for i in range(GROUP):
                        ins = norm_tile(v, m.XG[:, i, :], X, 4 * g + i, mv2, m.rstd)
                    ins.then_inc(gs["g_normed"], 1)
                    v.memset(VT[:, :], 0.0).then_inc(own.sem, own.one())
                    v.wait_ge(gs["sel_turned"], nth("sel_turned", g, 0))
                    for k in range(2):
                        sel = SEL[:, k, bass.ds(g * GROUP * E, GROUP * E)]
                        v.tensor_scalar(S4[:, k, :], sel, 1.0, None, ALU.mult)
                        ins = v.tensor_tensor(S4[:, 2 + k, :], sel, RW[:, bass.ds(g * GROUP * E, GROUP * E)], ALU.mult)
                    ins.then_inc(gs["sel_ready"], 1)
                    v.wait_ge(gs["spread_kept"], nth("spread_kept", g, 10))
                    v.tensor_tensor(TA[:, 1:3, :], WW[:, 1:3, :],
                                             sw[:, 0:1].unsqueeze(1).to_broadcast([P, 2, GT]), ALU.mult).then_inc(own.sem, own.one())
                    v.wait_ge(own.sem, own.n)
                    v.tensor_tensor(WW[:, 1:3, :], WW[:, 1:3, :], TA[:, 1:3, :], ALU.subtract).then_inc(own.sem, own.one())
                    v.wait_ge(own.sem, own.n)
                    own.restart()
                    for it in range(2):
                        for c in range(4):
                            v.wait_ge(gs["hid_gelu"], nth("hid_gelu", g, 5 * it + c + 2))
                            v.tensor_tensor(MH[:, 0, c, :], HG[:, c, :], MK[:, 0, c, :], ALU.mult).then_inc(gs["masked0"], 1)

                        def wide(x):
                            return x.unsqueeze(1).to_broadcast([P, 3, GT])
                        v.tensor_scalar(ERR[:, :], IT[:, :], mu[:, 0:1], None, ALU.subtract).then_inc(own.sem, own.one())
                        v.wait_ge(gs["steer_kept"], nth("steer_kept", g, 3 * it + 3))
                        v.tensor_scalar(TA[:, :, :], TA[:, :, :], half, half, ALU.mult, ALU.add).then_inc(own.sem, own.one())
                        v.tensor_scalar(TG[:, :, :], TG[:, :, :], 0.05, 0.05, ALU.mult, ALU.add).then_inc(own.sem, own.one())
                        v.wait_ge(own.sem, own.n)
                        v.tensor_tensor(TA[:, :, :], TA[:, :, :], wide(VT[:, :]), ALU.mult).then_inc(own.sem, own.one())
                        v.wait_ge(own.sem, own.n)
                        v.wait_ge(gs["soft"], nth("soft", g, it + 1))
                        z2 = ZB[:, :, :].rearrange("p r q -> p (r q)")
                        a2 = AB[:, :, :].rearrange("p r q -> p (r q)")
                        v.scalar_tensor_tensor(z2, z2, 0.0, a2, ALU.max, ALU.add).then_inc(own.sem, own.one())
                        v.wait_ge(own.sem, own.n)
                        v.tensor_tensor(ZB[:, :, :], ZB[:, :, :], wide(ERR[:, :]), ALU.mult).then_inc(own.sem, own.one())
                        v.wait_ge(own.sem, own.n)
                        v.tensor_tensor(TA[:, :, :], TA[:, :, :], ZB[:, :, :], ALU.subtract).then_inc(own.sem, own.one())
                        v.wait_ge(own.sem, own.n)
                        v.tensor_tensor(TG[:, :, :], TG[:, :, :], TA[:, :, :], ALU.mult).then_inc(own.sem, own.one())
                        v.wait_ge(own.sem, own.n)
                        v.tensor_tensor(TG[:, :, :], TG[:, :, :], wide(IT[:, :]), ALU.add).then_inc(own.sem, own.one())
                        v.wait_ge(own.sem, own.n)
                        v.tensor_tensor(TG[:, :, :], TG[:, :, :], WW[:, :, :], ALU.mult).then_inc(own.sem, own.one())
                        v.wait_ge(own.sem, own.n)
                        v.tensor_tensor(XN[:, :], TG[:, 0, :], TG[:, 1, :], ALU.add).then_inc(own.sem, own.one())
                        v.wait_ge(own.sem, own.n)
                        v.tensor_tensor(XN[:, :], XN[:, :], TG[:, 2, :], ALU.add).then_inc(gs["x_next"], 1)
                        v.tensor_tensor(TA[:, :, :], TA[:, :, :], WW[:, :, :], ALU.mult).then_inc(own.sem, own.one())
                        v.wait_ge(own.sem, own.n)
                        v.tensor_tensor(VT[:, :], TA[:, 0, :], TA[:, 1, :], ALU.add).then_inc(own.sem, own.one())
                        v.wait_ge(own.sem, own.n)
                        v.tensor_tensor(VT[:, :], VT[:, :], TA[:, 2, :], ALU.add).then_inc(own.sem, own.one())
                        v.wait_ge(own.sem, own.n)
                        v.wait_ge(gs["halted"], nth("halted", g, it + 1))
                        v.tensor_scalar(TH[:, :], TH[:, :], half, half, ALU.mult, ALU.add).then_inc(own.sem, own.one())
                        v.wait_ge(own.sem, own.n)
                        v.scalar_tensor_tensor(TH[:, :], m.RING[:, 512:1024], bf2[:, 0:1], TH[:, :], ALU.add, ALU.mult).then_inc(own.sem, own.one())
                        v.wait_ge(own.sem, own.n)
                        v.scalar_tensor_tensor(IT[:, :], TH[:, :], iw[:, 0:1], IT[:, :], ALU.mult, ALU.add)\
                            .then_inc(gs["it_done"], 1)
                        own.restart()
                        v.wait_ge(gs["it_done"], per["it_done"] * g + it + 1)
                    v.wait_ge(gs["fin_turned"], nth("fin_turned", g, 1))
                    v.scalar_tensor_tensor(tile_of(X, g, GT), m.TPS[:, :], m.tg[:, 6:7], tile_of(X, g, GT),
                                           ALU.mult, ALU.add).then_inc(gs["g_done"], 1)
                v.wait_ge(gs["g_done"], NG + 1)

            def pool(q):
                with q.Fori(0, NG) as g:
                    for it in range(2):
                        for c in range(4):
                            q.wait_ge(gs["hid_gelu"], nth("hid_gelu", g, 5 * it + c + 2))
                            q.tensor_tensor(MH[:, 1, c, :], HG[:, c, :], MK[:, 1, c, :], ALU.mult).then_inc(gs["masked1"], 1)
            for k, f in (("pe", pe), ("act", act), ("dve", dve), ("pool", pool)):
                prog[k].append(f)
            for k in prog:
                prog[k].append(lambda eng: eng.wait_ge(gs["g_done"], NG + 1))
        if stop >= 8:
            narrow_buffers()
            RB.again()
            IWT1 = RB.cut([P, 256]).bitcast(BF16)
            IWT2 = RB.cut([P, 256]).bitcast(BF16)
            AW = RB.cut([P, 2, 512])
            sums3, s3, r3 = RB.cut([P, 2]), RB.cut([P, 2]), RB.cut([P, 2])
            s_abs, s_total = sem("magnitudes_summed"), sem("magnitudes_totalled")

            def prep3(v):
                loaded(v, "layer3")
                own = Own(v, m.own_dve)
                flat_cm = cmT[:, :, :].rearrange("p e q -> p (e q)")
                flat_pad = pad[:, :, :].rearrange("p t k -> p (t k)")
                v.tensor_copy(BK[:, 0:1024], flat_cm.bitcast(I32)).then_inc(own.sem, own.one())
                v.tensor_copy(BK[:, 1024:2048], flat_pad.bitcast(I32)).then_inc(own.sem, own.one())
                v.wait_ge(own.sem, own.n)
                v.tensor_copy(flat_pad, pad8.bitcast(U8)).then_inc(own.sem, own.one())
                v.tensor_tensor(kt3[:, :, :], qt3[:, :].unsqueeze(2).to_broadcast([P, NT, S]), kt3[:, :, :],
                                         ALU.subtract).then_inc(own.sem, own.one())
                v.wait_ge(own.sem, own.n)
                v.tensor_scalar(kt3[:, :, :], kt3[:, :, :], 0.0, None, ALU.is_lt).then_inc(own.sem, own.one())
                v.wait_ge(own.sem, own.n)
                v.tensor_tensor(kt3[:, :, :], kt3[:, :, :], pad[:, :, :], ALU.max).then_inc(own.sem, own.one())
                v.wait_ge(own.sem, own.n)
                v.tensor_scalar(kt3[:, :, :], kt3[:, :, :], -NEG, NEG, ALU.mult, ALU.add).then_inc(own.sem, own.one())
                v.wait_ge(own.sem, own.n)
                v.tensor_scalar(AW[:, :, :], nat3[:, :, :], -1.0, None, ALU.mult).then_inc(own.sem, own.one())
                v.wait_ge(own.sem, own.n)
                v.tensor_tensor(AW[:, :, :], AW[:, :, :], nat3[:, :, :], ALU.max).then_inc(own.sem, own.one())
                v.wait_ge(own.sem, own.n)
                v.tensor_reduce(sums3[:, :], AW[:, :, :], AX.X, ALU.add).then_inc(s_abs, 1)
                v.wait_ge(s_total, 1)
                v.tensor_scalar(s3[:, :], m.OPS[:, 0:2], 1.0 / (512 * D), 1e-5, ALU.mult, ALU.max).then_inc(own.sem, own.one())
                v.wait_ge(own.sem, own.n)
                v.reciprocal(r3[:, :], s3[:, :]).then_inc(own.sem, own.one())
                v.wait_ge(own.sem, own.n)
                v.tensor_tensor(nat3[:, :, :], nat3[:, :, :], r3[:, :].unsqueeze(2).to_broadcast([P, 2, 512]),
                                         ALU.mult).then_inc(own.sem, own.one())
                v.wait_ge(own.sem, own.n)
                v.tensor_scalar(nat3[:, :, :], nat3[:, :, :], MAGIC, MAGIC, ALU.add, ALU.subtract).then_inc(own.sem, own.one())
                v.wait_ge(own.sem, own.n)
                v.tensor_scalar(nat3[:, :, :], nat3[:, :, :], -1.0, 1.0, ALU.max, ALU.min).then_inc(own.sem, own.one())
                v.wait_ge(own.sem, own.n)
                v.tensor_scalar(s3[:, :], s3[:, :], 1.0 / 127.0, None, ALU.mult).then_inc(own.sem, own.one())
                v.wait_ge(own.sem, own.n)
                v.tensor_tensor(s3[:, 1:2], s3[:, 1:2], m.tg[:, 7:8], ALU.mult).then_inc(s_quant, 1)
                v.wait_ge(s_quant, n_q3)
                own.restart()

            def total3(p):
                loaded(p, "layer3")
                p.wait_ge(s_abs, 1)
                p.matmul(m.OPS[:, 0:2], m.ones[:, :], sums3[:, :], start=True, stop=True).then_inc(s_total, 1)
                p.wait_ge(s_quant, n_q3)
            n_q3 = m.n_quant = m.n_quant + 1
            prog["dve"].append(prep3)
            prog["pe"].append(total3)
            turn([nat3[:, 0, c * P:(c + 1) * P] for c in range(4)], (IWT1, lambda b: b))
            turn([nat3[:, 1, c * P:(c + 1) * P] for c in range(4)], (IWT2, lambda b: b))
            kept_weights()
            statistics(X, m.mv, m.rstd, 1e-5)

            def masked_context(v, own, i, u):
                v.wait_ge(ev["xT"].sem, ev["xT"].base + i + 1)
                for e in range(E):
                    ins = v.scalar_tensor_tensor(cmT[:, e, :], BK[:, bass.ds(i * P, P)], float(e), m.cT[:, :],
                                                 ALU.is_equal, ALU.mult)
                ins.then_inc(ev["masked_ctx"].sem, 1)

            def k3_piece(p, bank, i, u):
                for e in range(E):
                    ins = p.matmul(bank[:, 0:P], wk3[:, e, :], cmT[:, e, :], start=(e == 0), stop=(e == E - 1))
                return ins

            def v3_piece(p, bank, i, u):
                for b in range(2):
                    for h in range(2):
                        for e in range(E):
                            ins = p.matmul(bank[64 * h:64 * h + 64, 64 * b:64 * b + 64], cmT[:, e, 64 * b:64 * b + 64],
                                           wv3[:, e, 64 * h:64 * h + 64], start=(e == 0), stop=(e == E - 1))
                return ins

            def v3_keep(s, spread_v, bank, u):
                return spread_v(lambda dst, src, h: s.activation(dst, src, ACT.Copy), bank, u)
            run(Attention(heads="narrow", ctx="load", cx_base=next_ctx(), scale=float(1 / np.sqrt(np.float32(8))),
                          extra=["masked_ctx"], dve_front=masked_context,
                          mask=lambda i: kt3[:, bass.ds(i, 1), :].unsqueeze(1),
                          pieces=[dict(pe=one(wq3, m.xT), act=to_buffer(m.QB[:, :])),
                                  dict(pe=k3_piece, act=to_buffer(m.KB[:, :]), needs=["masked_ctx"]),
                                  dict(pe=v3_piece, act=v3_keep)],
                          w_out=wo3, normalise=normalise(X), finish=finish_biased(3, bo3)))
            barrier()

        if stop >= 9:
            statistics(X, m.mv, m.rstd, 1e-5)
            bits = {n: sem("ternary_" + n) for n in ("rows_quantised", "rows_turned", "rows_kept", "up", "hidden",
                                                     "hidden_quantised", "hidden_turned", "hidden_kept", "down", "done")}
            XQ = RB.cut([P, 2, D])
            HQ = RB.cut([P, 2, 512])
            XQT = RB.cut([P, P // 2]).bitcast(BF16)
            HQT = RB.cut([P, 256]).bitcast(BF16)
            q3 = RB.cut([P, 2, 8])

            def eight_bits(v, own, x, u, col0, s):
                hi, lo, inv, sc = [q3[:, u, k:k + 1] for k in (4, 5, 6)] + [q3[:, u, col0:col0 + 1]]
                v.tensor_reduce(hi, x, AX.X, ALU.max).then_inc(own.sem, own.one())
                v.tensor_reduce(lo, x, AX.X, ALU.min).then_inc(own.sem, own.one())
                v.wait_ge(own.sem, own.n)
                v.scalar_tensor_tensor(hi, lo, -1.0, hi, ALU.mult, ALU.max).then_inc(own.sem, own.one())
                v.wait_ge(own.sem, own.n)
                v.tensor_scalar(hi, hi, 1e-5, None, ALU.max).then_inc(own.sem, own.one())
                v.wait_ge(own.sem, own.n)
                v.tensor_tensor(sc, hi, s, ALU.mult).then_inc(own.sem, own.one())
                v.reciprocal(inv, hi).then_inc(own.sem, own.one())
                v.wait_ge(own.sem, own.n)
                v.tensor_scalar(inv, inv, 127.0, None, ALU.mult).then_inc(own.sem, own.one())
                v.wait_ge(own.sem, own.n)
                v.tensor_scalar(x, x, inv, MAGIC, ALU.mult, ALU.add).then_inc(own.sem, own.one())
                v.wait_ge(own.sem, own.n)
                v.tensor_scalar(x, x, MAGIC, -128.0, ALU.subtract, ALU.max).then_inc(own.sem, own.one())
                v.wait_ge(own.sem, own.n)
                return v.tensor_scalar(x, x, 127.0, None, ALU.min)

            def pe(p):
                def step(n, u, on):
                    if on[1]:
                        t, w = n + 1, 1 - u
                        p.wait_ge(bits["rows_quantised"], t + 1)
                        if some(t):
                            p.wait_ge(bits["rows_kept"], t)
                        p.transpose(m.TPS[:, 0:P], XQ[:, w, :], m.ident[:, :]).then_inc(bits["rows_turned"], 1)
                    if on[0]:
                        t = n
                        p.wait_ge(bits["hidden_quantised"], t + 1)
                        if some(t):
                            p.wait_ge(bits["hidden_kept"], t)
                        for c in range(4):
                            ins = p.transpose(m.PS[:, c * P:(c + 1) * P], HQ[:, u, c * P:(c + 1) * P], m.ident[:, :])
                        ins.then_inc(bits["hidden_turned"], 1)
                    if on[1]:
                        t, w = n + 1, 1 - u
                        p.wait_ge(bits["rows_kept"], t + 1)
                        if some(t - 1):
                            p.wait_ge(bits["hidden"], t - 1)
                        p.matmul(m.RING[:, w * 512:w * 512 + 512], XQT, IWT1, start=True, stop=True).then_inc(bits["up"], 1)
                    if on[0]:
                        t = n
                        p.wait_ge(bits["hidden_kept"], t + 1)
                        if some(t):
                            p.wait_ge(bits["done"], t)
                        for c in range(4):
                            ins = p.matmul(m.OPS[:, 0:D], HQT[:, c * P:(c + 1) * P], IWT2[:, c * P:(c + 1) * P],
                                           start=(c == 0), stop=(c == 3))
                        ins.then_inc(bits["down"], 1)
                pipeline(p, None, step)

            def act(s):
                def step(n, u, on):
                    if on[1]:
                        if some(n + 2):
                            s.wait_ge(bits["rows_turned"], n + 2)
                        if some(n + 1):
                            s.wait_ge(bits["up"], n + 1)
                        s.activation(XQT, m.TPS[:, 0:P], ACT.Copy).then_inc(bits["rows_kept"], 1)
                    if on[0]:
                        if some(n + 1):
                            s.wait_ge(bits["hidden_turned"], n + 1)
                        if some(n):
                            s.wait_ge(bits["down"], n)
                        s.activation(HQT, m.PS[:, 0:512], ACT.Copy).then_inc(bits["hidden_kept"], 1)
                    if on[1]:
                        t, w = n + 1, 1 - u
                        s.wait_ge(bits["up"], t + 1)
                        if some(t - 1):
                            s.wait_ge(bits["hidden_turned"], t - 1)
                        s.activation(HQ[:, w, :], m.RING[:, w * 512:w * 512 + 512], ACT.Gelu, scale=q3[:, w, 0:1])\
                            .then_inc(bits["hidden"], 1)
                pipeline(s, None, step)

            def dve(v):
                own = Own(v, m.own_dve)

                def step(n, u, on):
                    if on[2]:
                        t = n + 2
                        if some(t - 1):
                            v.wait_ge(bits["rows_turned"], t - 1)
                        if some(t - 1):
                            v.wait_ge(bits["hidden"], t - 1)
                        norm_tile(v, XQ[:, u, :], X, t, mv2, m.rstd).then_inc(own.sem, own.one())
                        v.wait_ge(own.sem, own.n)
                        eight_bits(v, own, XQ[:, u, :], u, 0, s3[:, 0:1]).then_inc(bits["rows_quantised"], 1)
                    if on[0]:
                        t = n
                        v.wait_ge(bits["down"], t + 1)
                        v.scalar_tensor_tensor(tile_of(X, t), m.OPS[:, 0:D], q3[:, u, 1:2], tile_of(X, t),
                                               ALU.mult, ALU.add).then_inc(bits["done"], 1)
                    if on[1]:
                        t, w = n + 1, 1 - u
                        v.wait_ge(bits["hidden"], t + 1)
                        eight_bits(v, own, HQ[:, w, :], w, 1, s3[:, 1:2]).then_inc(bits["hidden_quantised"], 1)
                pipeline(v, own, step)
            for k, f in (("pe", pe), ("act", act), ("dve", dve)):
                prog[k].append(f)
            for k in prog:
                prog[k].append(lambda eng: eng.wait_ge(bits["done"], NT))
        src = XIN if stop in (0, 2) else X

        def store(q):
            q.dma_start(out.rearrange("(t b) s d -> (b s) t d", b=TILE_B), src[:, :].rearrange("p (t d) -> p t d", d=D))\
                .then_inc(s_stored, 16)
            q.wait_ge(s_stored, 16)
        prog["sp"].append(store)

        block = ctx.enter_context(nc.Block())

        @block.sync
        def _(eng):
            for f in prog["sp"]:
                f(eng)

        @block.scalar
        def _(eng):
            for f in prog["act"]:
                f(eng)

        @block.vector
        def _(eng):
            for f in prog["dve"]:
                f(eng)

        @block.gpsimd
        def _(eng):
            for f in prog["pool"]:
                f(eng)

        @block.tensor
        def _(eng):
            for f in prog["pe"]:
                f(eng)


def kernel(**inputs):
    import concourse.bacc as _bacc
    from concourse.bass_utils import run_bass_kernel_spmd as _run

    nc = _bacc.Bacc("TRN2", target_bir_lowering=False, num_devices=1)
    arrays, aps = {}, {}
    given = {name: np.ascontiguousarray(a) for name, a in inputs.items()}
    given.update({"const_" + name: a for name, a in CONST.items()})
    for name, a in given.items():
        if a.dtype == np.bool_:
            a = a.view(np.int32)
        if a.ndim == 0:
            a = a.reshape(1)
        arrays[f"in_{name}"] = a
        aps[name] = nc.dram_tensor(f"in_{name}", a.shape, mybir.dt.from_np(a.dtype), kind="ExternalInput").ap()
    out = nc.dram_tensor("out_x", (B, S, D), F32, kind="ExternalOutput").ap()
    program(nc, aps, out)
    r = _run(nc, [arrays], core_ids=[0])
    return r.results[0]["out_x"]
```

```python
from contextlib import ExitStack

import concourse.bass as bass
from concourse import mybir
import numpy as np

ALU = mybir.AluOpType
ACT = mybir.ActivationFunctionType
AX = mybir.AxisListType
F32 = mybir.dt.float32
BF16 = mybir.dt.bfloat16
I32 = mybir.dt.int32
U8 = mybir.dt.uint8

P = 128
D = 128
B, S = 32, 64
TILE_B = P // S
NT = B // TILE_B
H = 16
E = 8
NEG = -1.0e30
GROUP = 4
NG = NT // GROUP
GT = GROUP * P


def some(count):
    return not isinstance(count, int) or count > 0


class Own:

    def __init__(self, eng, sem):
        self.eng, self.sem, self.n = eng, sem, 0

    def one(self):
        self.n += 1
        return 1

    def restart(self):
        if self.n:
            self.eng.wait_ge(self.sem, self.n)
            self.eng.sem_clear(self.sem)
            self.n = 0


class Machine:
    pass


class Attention:

    def __init__(self, pieces, scale, w_out, normalise, finish, out, q_ready=(), v_ready=(), heads="pair", many_k=False,
                 ctx="none", cx_base=0, extra=(), x_gain=None, c_gain=None, mask=None, rowscale=None, dve_front=None,
                 pool_front=None, more_out=None, dve_extra=None):
        self.pieces, self.scale, self.q_ready, self.v_ready, self.w_out = pieces, scale, q_ready, v_ready, w_out
        self.out = out
        self.normalise, self.finish, self.heads, self.many_k = normalise, finish, heads, many_k
        self.ctx, self.cx_base, self.extra, self.x_gain, self.c_gain = ctx, cx_base, extra, x_gain, c_gain
        self.mask, self.rowscale, self.dve_front, self.pool_front = mask, rowscale, dve_front, pool_front
        self.more_out, self.dve_extra = more_out, dve_extra


def pipeline(eng, own, step, count=NT):
    def static(n):
        step(n, n % 2, [0 <= n + k < count for k in range(3)])
        if own:
            own.restart()
    for n in range(-2, 2):
        static(n)
    with eng.Fori(1, count // 2 - 1) as i:
        for u in range(2):
            step(2 * i + u, u, [True] * 3)
            if own:
                own.restart()
    for n in range(count - 2, count):
        static(n)


class Event:

    def __init__(self, sem):
        self.sem, self.base = sem, 0


def attention(m, a):
    ev = m.ev
    used = ["xn", "x_turned", "xT", "scores", "shifted", "exped", "rinv", "probs", "p_turned", "pT",
            "pv", "oT", "out", "done"]
    used += ["piece%d" % j for j in range(len(a.pieces))] + ["kept%d" % j for j in range(len(a.pieces))]
    used += list(a.extra)
    npc = len(a.pieces)
    banks = [piece.get("bank", m.RING[:, (j % 2) * 512:(j % 2) * 512 + 512]) for j, piece in enumerate(a.pieces)]
    nb = 4 if a.heads == "wide" else 8
    nh = 2 * nb
    per = 2
    PSv = (m.PS[:, 0:512].rearrange("q (c p k) -> q c p k", c=4, p=2) if a.heads == "wide"
           else m.PS[:, :].rearrange("q (p c k) -> q c p k", p=2, c=8))
    Pv = m.PROB[:, 0:nb * 128].rearrange("q (c p k) -> q c p k", c=nb, p=2)
    mx = m.mx[:, 0:nh].rearrange("q (c p) -> q c p", p=2)
    rs = m.rs[:, 0:nh].rearrange("q (c p) -> q c p", p=2)

    def bk(ap):
        return ap.unsqueeze(3).to_broadcast([128, nb, 2, S])

    def pe(p):
        def turn_input(t, v):
            p.wait_ge(ev["xn"].sem, ev["xn"].base + t + 1)
            if a.ctx == "load":
                p.wait_ge(m.cx_loaded[v], a.cx_base + 8 * t - 8 * v + 16)
            if some(t):
                p.wait_ge(ev["xT"].sem, ev["xT"].base + t)
            ins = p.transpose(m.TPS[:, 0:128], m.xn[:, v, :], m.ident[:, :])
            if a.ctx != "none":
                ins = p.transpose(m.TPS[:, 128:256], m.cx[:, v, :], m.ident[:, :])
            ins.then_inc(ev["x_turned"].sem, 1)

        def projections(t, v):
            p.wait_ge(ev["xT"].sem, ev["xT"].base + t + 1)
            if some(t - 1):
                p.wait_ge(ev["oT"].sem, ev["oT"].base + per * (t - 1))
            for j, piece in enumerate(a.pieces):
                before = piece.get("bank_after", j - 2)
                if before >= 0:
                    p.wait_ge(ev["kept%d" % before].sem, ev["kept%d" % before].base + t + 1)
                for w in piece.get("needs", []):
                    p.wait_ge(ev[w].sem, ev[w].base + t + 1)
                piece["pe"](p, banks[j], t, v).then_inc(ev["piece%d" % j].sem, 1)

        def turn_probs(t):
            p.wait_ge(ev["probs"].sem, ev["probs"].base + t + 1)
            if some(t):
                p.wait_ge(ev["pT"].sem, ev["pT"].base + t)
            for c in range(nb):
                ins = p.transpose(m.PTP[:, c * 128:(c + 1) * 128], m.PROB[:, c * 128:(c + 1) * 128], m.ident[:, :])
            ins.then_inc(ev["p_turned"].sem, 1)

        def turn_keys(t):
            p.wait_ge(ev["knat"].sem, ev["knat"].base + t + 1)
            if some(t):
                p.wait_ge(ev["kT"].sem, ev["kT"].base + t)
            for g in range(2):
                ins = p.transpose(m.PTP[:, 512 + g * 128:640 + g * 128], m.KN[:, g * 128:(g + 1) * 128], m.ident[:, :])
            ins.then_inc(ev["k_turned"].sem, 1)

        def scores(t):
            for w in a.q_ready:
                p.wait_ge(ev[w].sem, ev[w].base + t + 1)
            if some(t):
                p.wait_ge(ev["shifted"].sem, ev["shifted"].base + t)
            m.hold(p)
            for c in range(nb):
                if a.heads == "wide":
                    for b in range(2):
                        ins = p.matmul(m.PS[:, (2 * c + b) * 64:(2 * c + b) * 64 + 64],
                                       m.QW[:, (4 * b + c) * P:(4 * b + c + 1) * P],
                                       m.KT[:, c // 2, 64 * b:64 * b + 64], start=True, stop=True)
                else:
                    for h in range(2):
                        for b in range(2):
                            r = slice(64 * h, 64 * h + 64)
                            ins = p.matmul(m.PS[64 * b:64 * b + 64, h * 512 + c * 64:h * 512 + c * 64 + 64],
                                           m.QT[r, c, 64 * b:64 * b + 64],
                                           m.KT[r, c if a.many_k else 0, 64 * b:64 * b + 64], start=True, stop=True)
            ins.then_inc(ev["scores"].sem, 1)

        def values(t, u, next_too):
            p.wait_ge(ev["pT"].sem, ev["pT"].base + t + 1)
            ring = ["kept%d" % j for j in range(max(0, npc - 2), npc)] if next_too else []
            for w in ring:
                p.wait_ge(ev[w].sem, ev[w].base + t + 2)
            for w in a.v_ready:
                if w not in ring:
                    p.wait_ge(ev[w].sem, ev[w].base + t + 1)
            if some(t):
                p.wait_ge(ev["oT"].sem, ev["oT"].base + per * t)
            m.hold(p)
            for k in range(per):
                if a.heads == "wide":
                    r = slice(64 * k, 64 * k + 64)
                    for g in range(2):
                        ins = p.matmul(m.RING[:, k * 512 + g * 256:k * 512 + g * 256 + 256], m.VW[r, u, g, :],
                                       m.PT[r, 2 * g:2 * g + 2, :], start=True, stop=True)
                elif a.heads == "pair" and not a.many_k:
                    bank = m.RING[:, k * 512:k * 512 + 512].rearrange("p (c q) -> p c q", c=4)
                    for b in range(2):
                        for h in range(2):
                            r = slice(64 * h, 64 * h + 64)
                            ins = p.matmul(bank[r, :, 64 * b:64 * b + 64], m.V[r, u, b, 0:64],
                                           m.PT[r, 4 * k:4 * k + 4, 64 * b:64 * b + 64], start=True, stop=True)
                else:
                    for c in range(4 * k, 4 * k + 4):
                        for b in range(2):
                            for h in range(2):
                                r = slice(64 * h, 64 * h + 64)
                                ins = p.matmul(m.RING[r, c * 128 + 64 * b:c * 128 + 64 * b + 64],
                                               m.V[r, u, b, c * 64:c * 64 + 64], m.PT[r, c, 64 * b:64 * b + 64],
                                               start=True, stop=True)
                ins.then_inc(ev["pv"].sem, 1)

        def output(t, u):
            if some(t):
                p.wait_ge(ev["done"].sem, ev["done"].base + t)
            mats = a.more_out(u) if a.more_out else []
            n_more = len(mats)
            mats += [(m.OT[:, c, :], a.w_out[:, c, :]) for c in range(8)]
            for k, (l, r) in enumerate(mats):
                if a.heads == "pair" and k in (n_more, n_more + 4):
                    p.wait_ge(ev["oT"].sem, ev["oT"].base + 2 * t + 1 + (k - n_more) // 4)
                elif k == n_more:
                    p.wait_ge(ev["oT"].sem, ev["oT"].base + per * t + per)
                ins = p.matmul(m.OPS[:, 0:128], l, r, start=(k == 0), stop=(k == len(mats) - 1))
            ins.then_inc(ev["out"].sem, 1)

        def step(n, u, on):
            if on[1]:
                if a.heads != "wide":
                    turn_input(n + 1, 1 - u)
                projections(n + 1, 1 - u)
            if on[0]:
                turn_probs(n)
            if on[1] and a.heads == "pair":
                scores(n + 1)
            if on[0]:
                values(n, u, on[1])
            if on[0]:
                output(n, u)
            if on[2] and a.heads == "wide":
                turn_input(n + 2, u)
            if on[1] and a.heads == "wide":
                turn_keys(n + 1)
                scores(n + 1)
        pipeline(p, None, step)

    def act(s):
        own = Own(s, m.own_act)

        def keep_input(t):
            s.wait_ge(ev["x_turned"].sem, ev["x_turned"].base + t + 1)
            if a.ctx != "none":
                s.activation(m.cT[:, :], m.TPS[:, 128:256], ACT.Copy if a.c_gain is None else ACT.Identity,
                             scale=1.0 if a.c_gain is None else a.c_gain)
            s.activation(m.xT[:, :], m.TPS[:, 0:128], ACT.Copy if a.x_gain is None else ACT.Identity,
                         scale=1.0 if a.x_gain is None else a.x_gain).then_inc(ev["xT"].sem, 1)

        def step(n, u, on):
            if on[1]:
                t, v = n + 1, 1 - u
                if a.heads != "wide":
                    keep_input(t)
                for j, piece in enumerate(a.pieces):
                    if "act" in piece:
                        s.wait_ge(ev["piece%d" % j].sem, ev["piece%d" % j].base + t + 1)
                        ins = piece["act"](s, banks[j], t, v, own)
                        ins.then_inc(ev[piece.get("raises", "kept%d" % j)].sem, 1)
            if on[0]:
                t = n
                s.wait_ge(ev["p_turned"].sem, ev["p_turned"].base + t + 1)
                s.activation(m.PT[:, 0:nb, :], m.PTP[:, 0:nb * 128].rearrange("p (c q) -> p c q", c=nb),
                                             ACT.Copy).then_inc(ev["pT"].sem, 1)
                for k in range(per):
                    s.wait_ge(ev["pv"].sem, ev["pv"].base + per * t + k + 1)
                    if a.heads == "pair":
                        s.activation(m.OT[:, 4 * k:4 * k + 4, :],
                                     m.RING[:, k * 512:k * 512 + 512].rearrange("p (c q) -> p c q", c=4), ACT.Copy)\
                            .then_inc(ev["oT"].sem, 1)
                    elif a.heads == "wide":
                        s.activation(m.OT[:, :, 64 * k:64 * k + 64],
                                     m.RING[:, k * 512:k * 512 + 512].rearrange("p (c q) -> p c q", c=8), ACT.Copy)\
                            .then_inc(ev["oT"].sem, 1)
            if on[2] and a.heads == "wide":
                keep_input(n + 2)
            if on[1]:
                t = n + 1
                if a.heads == "wide":
                    s.wait_ge(ev["k_turned"].sem, ev["k_turned"].base + t + 1)
                    s.activation(m.KT[:, 0:2, :], m.PTP[:, 512:768].rearrange("p (g k) -> p g k", g=2),
                                                 ACT.Copy).then_inc(ev["kT"].sem, 1)
                s.wait_ge(ev["shifted"].sem, ev["shifted"].base + t + 1)
                s.activation(m.PROB[:, 0:nb * 128], m.PROB[:, 0:nb * 128], ACT.Exp, scale=a.scale).then_inc(ev["exped"].sem, 1)
        pipeline(s, own, step)

    def dve(v):
        own = Own(v, m.own_dve)

        def step(n, u, on):
            if on[2]:
                t = n + 2
                if some(t - 1):
                    v.wait_ge(ev["x_turned"].sem, ev["x_turned"].base + t - 1)
                a.normalise(v, own, t, u)
            if on[1]:
                t, w = n + 1, 1 - u
                if a.dve_front:
                    a.dve_front(v, own, t, w)
                order = sorted(range(npc), key=lambda j: "last" in a.pieces[j])
                for j, piece in [(j, a.pieces[j]) for j in order]:
                    if "dve" in piece:
                        v.wait_ge(ev["piece%d" % j].sem, ev["piece%d" % j].base + t + 1)
                        ins = piece["dve"](v, banks[j], t, w, own)
                        ins.then_inc(ev["kept%d" % j].sem, 1)
                        if "dve_after" in piece:
                            piece["dve_after"](v, t, own)
                v.wait_ge(ev["scores"].sem, ev["scores"].base + t + 1)
                if a.mask:
                    v.tensor_tensor(Pv, PSv, a.mask(t).to_broadcast([128, nb, 2, S]), ALU.add).then_inc(own.sem, own.one())
                    v.wait_ge(own.sem, own.n)
                    v.tensor_reduce(mx, Pv, AX.X, ALU.max).then_inc(own.sem, own.one())
                    v.wait_ge(own.sem, own.n)
                    ins = v.tensor_tensor(Pv, Pv, bk(mx), ALU.subtract)
                else:
                    v.tensor_reduce(mx, PSv, AX.X, ALU.max).then_inc(own.sem, own.one())
                    v.wait_ge(own.sem, own.n)
                    ins = v.tensor_tensor(Pv, PSv, bk(mx), ALU.subtract)
                ins.then_inc(ev["shifted"].sem, 1)
            if on[1]:
                t = n + 1
                v.wait_ge(ev["exped"].sem, ev["exped"].base + t + 1)
                v.tensor_reduce(rs, Pv, AX.X, ALU.add).then_inc(own.sem, own.one())
                v.wait_ge(own.sem, own.n)
                if a.rowscale:
                    v.reciprocal(rs, rs).then_inc(own.sem, own.one())
                    v.wait_ge(own.sem, own.n)
                    ins = v.tensor_scalar(rs, rs, a.rowscale(t), None, ALU.mult)
                else:
                    ins = v.reciprocal(rs, rs)
                ins.then_inc(ev["rinv"].sem, 1)
            if on[1] and a.dve_extra:
                a.dve_extra(v, own, n + 1)
            if on[0]:
                if some(n + 1):
                    v.wait_ge(ev["out"].sem, ev["out"].base + n + 1)
                a.finish(v, own, n).then_inc(ev["done"].sem, 1)
                if some(n):
                    v.bn_stats(m.st[:, bass.ds(n - 1, 1), :].rearrange("p a s -> p (a s)"),
                               a.out[:, bass.ds((n - 1) * D, D)]).then_inc(own.sem, own.one())
        pipeline(v, own, step)
        v.wait_ge(ev["done"].sem, ev["done"].base + NT)
        v.bn_stats(m.st[:, NT - 1, :], a.out[:, (NT - 1) * D:NT * D]).then_inc(own.sem, own.one())
        own.restart()

    def pool(g):
        def step(n, u, on):
            if on[1]:
                t = n + 1
                if a.pool_front:
                    a.pool_front(g, t, 1 - u)
                g.wait_ge(ev["rinv"].sem, ev["rinv"].base + t + 1)
                g.tensor_tensor(Pv, Pv, bk(rs), ALU.mult).then_inc(ev["probs"].sem, 1)
        pipeline(g, None, step)

    def sp(q):
        if a.ctx == "load":
            def step(n, u, on):
                if on[2]:
                    t = n + 2
                    if some(t - 1):
                        q.wait_ge(ev["x_turned"].sem, ev["x_turned"].base + t - 1)
                    src = m.ctx_tiles[bass.ds(t, 1), :, :].rearrange("a p d -> (a p) d")
                    q.dma_start(m.cx[:, u, :], src).then_inc(m.cx_loaded[u], 16)
            pipeline(q, None, step)

    programs = dict(pe=pe, act=act, dve=dve, pool=pool, sp=sp)
    counts = {n: NT * (per if n in ("pv", "oT") else 1) for n in used}
    return programs, counts


def narrow_attention(m, a):
    ev = m.ev
    used = ["xn", "x_turned", "xT", "piece0", "piece1", "piece2", "kept0", "kept1", "kept2", "heads_split",
            "scores", "shifted", "exped", "rinv", "probs", "p_turned", "pT", "pv", "oT", "out", "done"] + list(a.extra)
    q_bank, k_bank, v_bank = m.RING[:, 0:512], m.RING[:, 512:1024], m.TPS[:, 256:512]
    PSv = m.PS[:, :].rearrange("q (p c k) -> q c p k", p=2, c=8)
    mx = m.mx[:, 0:16].rearrange("q (c p) -> q c p", p=2)
    rs = m.rs[:, 0:16].rearrange("q (c p) -> q c p", p=2)
    OT = m.OT1[:, :, :]

    def prob(v):
        return m.PROB2[:, v * 1024:v * 1024 + 1024].rearrange("q (c p k) -> q c p k", c=8, p=2)

    def wide(ap):
        return ap.unsqueeze(3).to_broadcast([128, 8, 2, S])

    def v_block(u, b, c):
        at = ((2 * u + b) * 8 + c) * 32
        return m.VP[:, at:at + 32]

    def spread_v(put, bank, u):
        for b in range(2):
            for h in range(2):
                at = (2 * u + b) * 256 + 8 * h
                dst = m.VP[64 * h:64 * h + 64, at:at + 256].rearrange("p (c x) -> p c x", c=8)[:, :, 0:8]
                ins = put(dst, bank[64 * b:64 * b + 64, 64 * h:64 * h + 64].rearrange("p (c x) -> p c x", c=8), h, b)
        return ins

    def pe(p):
        def step(n, u, on):
            if on[1]:
                t = n + 1
                p.wait_ge(ev["kept0"].sem, ev["kept0"].base + t + 1)
                p.wait_ge(ev["heads_split"].sem, ev["heads_split"].base + t + 1)
                if some(t):
                    p.wait_ge(ev["shifted"].sem, ev["shifted"].base + t)
                m.hold(p)
                for h in range(2):
                    for b in range(2):
                        r = slice(64 * h, 64 * h + 64)
                        ins = p.matmul(m.PS[64 * b:64 * b + 64, h * 512:h * 512 + 512], m.QB[r, 64 * b:64 * b + 64],
                                       m.KT8[r, :, 64 * b:64 * b + 64], start=True, stop=True)
                ins.then_inc(ev["scores"].sem, 1)
            if on[2]:
                t = n + 2
                p.wait_ge(ev["xn"].sem, ev["xn"].base + t + 1)
                p.wait_ge(m.cx_loaded[u], a.cx_base + 8 * t - 8 * u + 16)
                if some(t):
                    p.wait_ge(ev["xT"].sem, ev["xT"].base + t)
                    p.wait_ge(ev["kept2"].sem, ev["kept2"].base + t)
                p.transpose(m.TPS[:, 0:128], m.xn[:, u, :], m.ident[:, :])
                p.transpose(m.TPS[:, 128:256], m.cx[:, u, :], m.ident[:, :]).then_inc(ev["x_turned"].sem, 1)
                p.wait_ge(ev["xT"].sem, ev["xT"].base + t + 1)
                if some(t - 2):
                    p.wait_ge(ev["oT"].sem, ev["oT"].base + t - 2)
                a.pieces[0]["pe"](p, q_bank, t, u).then_inc(ev["piece0"].sem, 1)
            if on[0]:
                p.wait_ge(ev["probs"].sem, ev["probs"].base + n + 1)
                if some(n):
                    p.wait_ge(ev["pT"].sem, ev["pT"].base + n)
                for c in range(8):
                    ins = p.transpose(m.PTP[:, c * P:(c + 1) * P],
                                      m.PROB2[:, u * 1024 + c * P:u * 1024 + (c + 1) * P], m.ident[:, :])
                ins.then_inc(ev["p_turned"].sem, 1)
            if on[2]:
                t = n + 2
                if some(t):
                    p.wait_ge(ev["kept1"].sem, ev["kept1"].base + t)
                for w in a.pieces[1].get("needs", []):
                    p.wait_ge(ev[w].sem, ev[w].base + t + 1)
                a.pieces[1]["pe"](p, k_bank, t, u).then_inc(ev["piece1"].sem, 1)
            if on[0]:
                p.wait_ge(ev["pT"].sem, ev["pT"].base + n + 1)
                p.wait_ge(ev["kept2"].sem, ev["kept2"].base + n + 1)
                if on[2]:
                    p.wait_ge(ev["kept0"].sem, ev["kept0"].base + n + 3)
                if some(n):
                    p.wait_ge(ev["oT"].sem, ev["oT"].base + n)
                for g in range(2):
                    for b in range(2):
                        for c in range(4):
                            at = g * P + 64 * b
                            ins = p.matmul(q_bank[32 * c:32 * c + 32, at:at + 64], v_block(u, b, 4 * g + c),
                                           m.PT8[:, 4 * g + c, 64 * b:64 * b + 64], start=True, stop=True,
                                           tile_position=(0, 32 * c))
                ins.then_inc(ev["pv"].sem, 1)
            if on[2]:
                a.pieces[2]["pe"](p, v_bank, n + 2, u).then_inc(ev["piece2"].sem, 1)
            if on[0]:
                p.wait_ge(ev["oT"].sem, ev["oT"].base + n + 1)
                if some(n):
                    p.wait_ge(ev["done"].sem, ev["done"].base + n)
                for g in range(2):
                    ins = p.matmul(m.OPS[:, 0:128], OT[:, g, :], a.w_out[:, g, :], start=(g == 0), stop=(g == 1))
                ins.then_inc(ev["out"].sem, 1)
        pipeline(p, None, step)

    def act(s):
        def step(n, u, on):
            if on[2]:
                t = n + 2
                s.wait_ge(ev["x_turned"].sem, ev["x_turned"].base + t + 1)
                s.activation(m.cT[:, :], m.TPS[:, 128:256], ACT.Copy)
                s.activation(m.xT[:, :], m.TPS[:, 0:128], ACT.Copy).then_inc(ev["xT"].sem, 1)
                s.wait_ge(ev["piece0"].sem, ev["piece0"].base + t + 1)
                a.pieces[0]["act"](s, q_bank).then_inc(ev["kept0"].sem, 1)
            if on[1]:
                s.wait_ge(ev["shifted"].sem, ev["shifted"].base + n + 2)
                pr = m.PROB2[:, (1 - u) * 1024:(1 - u) * 1024 + 1024]
                s.activation(pr, pr, ACT.Exp, scale=a.scale).then_inc(ev["exped"].sem, 1)
            if on[0]:
                s.wait_ge(ev["p_turned"].sem, ev["p_turned"].base + n + 1)
                s.activation(m.PT8[:, :, :], m.PTP[:, :].rearrange("p (c q) -> p c q", c=8), ACT.Copy)\
                    .then_inc(ev["pT"].sem, 1)
            if on[2]:
                t = n + 2
                s.wait_ge(ev["piece1"].sem, ev["piece1"].base + t + 1)
                if some(t):
                    s.wait_ge(ev["heads_split"].sem, ev["heads_split"].base + t)
                a.pieces[1]["act"](s, k_bank).then_inc(ev["kept1"].sem, 1)
            if on[0]:
                s.wait_ge(ev["pv"].sem, ev["pv"].base + n + 1)
                s.activation(OT, q_bank[:, 0:2 * P].rearrange("p (g q) -> p g q", g=2), ACT.Copy).then_inc(ev["oT"].sem, 1)
            if on[2] and "act" in a.pieces[2]:
                s.wait_ge(ev["piece2"].sem, ev["piece2"].base + n + 3)
                a.pieces[2]["act"](s, spread_v, v_bank, u).then_inc(ev["kept2"].sem, 1)
        pipeline(s, None, step)

    def dve(v):
        own = Own(v, m.own_dve)
        v.memset(m.VP[:, :], 0.0).then_inc(own.sem, own.one())
        own.restart()

        def step(n, u, on):
            if on[2]:
                t = n + 2
                if some(t - 1):
                    v.wait_ge(ev["x_turned"].sem, ev["x_turned"].base + t - 1)
                a.normalise(v, own, t, u)
            if on[1]:
                t, pr = n + 1, prob(1 - u)
                v.wait_ge(ev["scores"].sem, ev["scores"].base + t + 1)
                if some(t - 1):
                    v.wait_ge(ev["p_turned"].sem, ev["p_turned"].base + t - 1)
                if a.mask:
                    v.tensor_tensor(pr, PSv, a.mask(t).to_broadcast([128, 8, 2, S]), ALU.add).then_inc(own.sem, own.one())
                    v.wait_ge(own.sem, own.n)
                src = pr if a.mask else PSv
                v.tensor_reduce(mx, src, AX.X, ALU.max).then_inc(own.sem, own.one())
                v.wait_ge(own.sem, own.n)
                v.tensor_tensor(pr, src, wide(mx), ALU.subtract).then_inc(ev["shifted"].sem, 1)
            if on[2] and a.dve_front:
                a.dve_front(v, own, n + 2, u)
            if on[1]:
                t = n + 1
                v.wait_ge(ev["exped"].sem, ev["exped"].base + t + 1)
                if some(t):
                    v.wait_ge(ev["probs"].sem, ev["probs"].base + t)
                v.tensor_reduce(rs, prob(1 - u), AX.X, ALU.add).then_inc(own.sem, own.one())
                v.wait_ge(own.sem, own.n)
                v.reciprocal(rs, rs).then_inc(ev["rinv"].sem, 1)
            if on[2] and "dve" in a.pieces[2]:
                v.wait_ge(ev["piece2"].sem, ev["piece2"].base + n + 3)
                a.pieces[2]["dve"](v, spread_v, v_bank, u).then_inc(ev["kept2"].sem, 1)
            if on[0]:
                v.wait_ge(ev["out"].sem, ev["out"].base + n + 1)
                a.finish(v, own, n).then_inc(ev["done"].sem, 1)
                if some(n):
                    v.bn_stats(m.st[:, bass.ds(n - 1, 1), :].rearrange("p a s -> p (a s)"),
                               a.out[:, bass.ds((n - 1) * D, D)]).then_inc(own.sem, own.one())
        pipeline(v, own, step)
        v.wait_ge(ev["done"].sem, ev["done"].base + NT)
        v.bn_stats(m.st[:, NT - 1, :], a.out[:, (NT - 1) * D:NT * D]).then_inc(own.sem, own.one())
        own.restart()

    def pool(g):
        def step(n, u, on):
            if on[2]:
                g.wait_ge(ev["kept1"].sem, ev["kept1"].base + n + 3)
                g.tensor_tensor(m.KT8[:, :, :], m.KB[:, :].unsqueeze(1).to_broadcast([P, 8, P]),
                                m.own_dims[:, :].unsqueeze(2).to_broadcast([P, 8, P]), ALU.mult)\
                    .then_inc(ev["heads_split"].sem, 1)
            if on[1]:
                g.wait_ge(ev["rinv"].sem, ev["rinv"].base + n + 2)
                g.tensor_tensor(prob(1 - u), prob(1 - u), wide(rs), ALU.mult).then_inc(ev["probs"].sem, 1)
        pipeline(g, None, step)

    def sp(q):
        def step(n, u, on):
            if on[2]:
                t = n + 2
                if some(t - 1):
                    q.wait_ge(ev["x_turned"].sem, ev["x_turned"].base + t - 1)
                src = m.ctx_tiles[bass.ds(t, 1), :, :].rearrange("a p d -> (a p) d")
                q.dma_start(m.cx[:, u, :], src).then_inc(m.cx_loaded[u], 16)
        pipeline(q, None, step)
    return dict(pe=pe, act=act, dve=dve, pool=pool, sp=sp), {n: NT for n in used}


def constants():
    q = np.arange(P)
    k = np.arange(S)
    pos = (q % S).astype(np.float32)
    inv = (1.0 / np.float32(1000000.0) ** (np.arange(0, D, 2, dtype=np.float32) / np.float32(D))).astype(np.float32)
    freqs = pos[:, None] * inv[None, :]
    emb = np.concatenate([freqs, freqs], 1).astype(np.float32)
    cos, sin = np.cos(emb).astype(np.float32), np.sin(emb).astype(np.float32)
    half = np.where(np.arange(D) < D // 2, -1.0, 1.0).astype(np.float32)
    e = np.arange(E)
    tie = (e[None, :] < e[:, None]).astype(np.float32).reshape(1, E * E).repeat(P, 0)
    return dict(
        ident=np.eye(P, dtype=np.float32),
        causal=np.where(k[None, :] > (q % S)[:, None], np.float32(NEG), np.float32(0)).astype(np.float32),
        before=(q[:, None] < q[None, :]).astype(np.float32),
        cosT=np.ascontiguousarray(cos.T), sinT=np.ascontiguousarray(sin.T),
        cosN=cos, sinN=(sin * half[None, :]).astype(np.float32),
        tie=tie,
        own_dims=((q[:, None] % 64) // 8 == np.arange(8)[None, :]).astype(np.float32),
        ones=np.ones((P, P), np.float32),
        zeros=np.zeros((P, 3 * P), np.float32),
        pick=(np.arange(P)[:, None] % E == (np.arange(512)[None, :] // 64)).astype(np.float32),
    )


CONST = constants()
ON_CHIP = [n for n in CONST if n != "zeros"]


def program(nc, t, out):
    m = Machine()
    ctx = ExitStack()
    with ctx:
        def sb(name, shape, dt=F32, stack=ctx):
            return stack.enter_context(nc.sbuf_tensor(name, shape, dt))

        class Arena:

            def __init__(self, name, floats):
                self.buf, self.at, self.floats = sb(name, [P, floats]), 0, floats

            def cut(self, shape):
                n = int(np.prod(shape[1:]))
                assert self.at + n <= self.floats, (self.at, n)
                ap = self.buf[0:shape[0], self.at:self.at + n]
                self.at += n
                if len(shape) == 2:
                    return ap
                names = "abcd"[:len(shape) - 1]
                return ap.rearrange("p (%s) -> p %s" % (" ".join(names), " ".join(names)),
                                    **{k: v for k, v in zip(names, shape[1:])})

            def again(self):
                self.at = 0

        def ps(name, shape):
            return ctx.enter_context(nc.psum_tensor(name, shape, F32))

        def sem(name):
            return ctx.enter_context(nc.semaphore(name))

        X = m.X = sb("X", [P, NT * D])
        XIN = m.XIN = sb("XIN", [P, NT * D])
        table = {name: sb("table_" + name, [P, CONST[name].shape[1]]) for name in ON_CHIP}
        m.ident, m.causal, m.before, m.ones = table["ident"], table["causal"], table["before"], table["ones"]
        m.cosT, m.sinT, m.cosN, m.sinN = table["cosT"], table["sinT"], table["cosN"], table["sinN"]
        m.tie, m.own_dims, m.pick = table["tie"], table["own_dims"], table["pick"]
        m.g_all = sb("g_all", [P, 8])
        m.tg = sb("tg", [P, 8])
        m.gains = sb("gains", [P, 8])
        m.mhalf = sb("mhalf", [P, NT])
        m.st = sb("st", [P, NT, 6])
        st_ctx = sb("st_ctx", [P, NT, 6])
        m.mv = sb("mv", [P, NT, 2])
        m.rstd = sb("rstd", [P, NT])
        m.cmv = sb("cmv", [P, NT, 2])
        m.crstd = sb("crstd", [P, NT])
        m.anchor = sb("anchor", [P, 32], BF16)
        m.xn = sb("xn", [P, 2, D])
        m.cx = sb("cx", [P, 2, D])
        m.xT = sb("xT", [P, P])
        m.cT = sb("cT", [P, P])
        m.mx = sb("mx", [P, H])
        m.rs = sb("rs", [P, H])
        m.TPS = ps("TPS", [P, 512])
        m.RING = ps("RING", [P, 1024])
        m.PS = ps("PS", [P, 1024])
        m.PTP = ps("PTP", [P, 1024])
        m.OPS = ps("OPS", [P, 512])

        names = ["xn", "x_turned", "xT", "scores", "shifted", "exped", "rinv", "probs", "p_turned", "pT",
                 "pv", "oT", "out", "done", "kT", "knat", "k_turned", "gate_tanhed", "q_turned_by_pos",
                 "heads_split", "masked_ctx"]
        names += ["piece%d" % j for j in range(6)] + ["kept%d" % j for j in range(6)]
        m.ev = {n: Event(sem(n)) for n in names}
        ev = m.ev
        m.own_act, m.own_dve = sem("own_act"), sem("own_dve")
        m.cx_loaded = [sem("even_context_loaded"), sem("odd_context_loaded")]
        s_ready = sem("setup_done")
        s_var, s_rstd = sem("variance_ready"), sem("rstd_ready")
        s_stored = sem("stored")
        m.weights = {}
        prog = dict(pe=[], act=[], dve=[], pool=[], sp=[])
        m.nvar = 0

        def hold(p):
            p.ldweights(m.anchor[:, :], tile_position=(0, 0))
        m.hold = hold

        def load(group, pairs):
            s = sem("loaded_" + group)
            m.weights[group] = (s, 16 * len(pairs))

            def f(q):
                for dst, src in pairs:
                    q.dma_start(dst, src, allow_slow_non_contiguous=True).then_inc(s, 16)
            prog["sp"].append(f)

        def loaded(eng, group):
            s, n = m.weights[group]
            eng.wait_ge(s, n)
        m.loaded = loaded

        def row(ap, n):
            return ap.rearrange("(a n) -> a n", a=1).to_broadcast([P, n])

        def col(ap):
            return ap.rearrange("(p a) -> p a", a=1)

        def barrier():
            v = ev["done"].base
            for k in prog:
                prog[k].append(lambda eng, v=v: eng.wait_ge(ev["done"].sem, v))

        load("x", [(X[:, :].rearrange("p (t d) -> p t d", d=D), t["x"].rearrange("(t b) s d -> (b s) t d", b=TILE_B))])
        load("constants", [(table[n][:, :], t["const_" + n]) for n in ON_CHIP]
             + [(m.g_all[:, 0:4], row(t["g_xattn"], 4)), (m.g_all[:, 4:8], row(t["g_ffn"], 4))]
             + [(m.gains[:, i:i + 1], col(t[n])) for i, n in enumerate(
                 ["L0_xattn_ptb_gamma", "L0_xattn_ca_gamma", "L0_xattn_ca_ctx_gamma", "L0_ffn_g1", "L0_ffn_g2"])])
        m.ctx_tiles = t["ctx_1024"].rearrange("(t b) s d -> t (b s) d", b=TILE_B)

        def setup_dve(v):
            v.memset(m.mhalf[:, :], -0.5).then_inc(s_ready, 1)
            v.memset(m.anchor[:, :], 0.0).then_inc(s_ready, 1)
        prog["dve"].append(setup_dve)

        def setup_act(s):
            loaded(s, "constants")
            s.activation(m.tg[:, :], m.g_all[:, :], ACT.Tanh).then_inc(s_ready, 1)
        prog["act"].append(setup_act)
        for k in ("pe", "dve", "pool", "act"):
            prog[k].append(lambda eng: (loaded(eng, "constants"), eng.wait_ge(s_ready, 3)))

        def tile_of(buf, i, width=D):
            return buf[:, bass.ds(i * width, width)]
        m.tile_of = tile_of

        def statistics(src, mv, rstd, eps, rms=False, ready=False, st=None):
            st = m.st if st is None else st
            k = m.nvar = m.nvar + 1

            def dve(v):
                own = Own(v, m.own_dve)
                if not ready:
                    for i in range(NT):
                        v.bn_stats(st[:, i, :], src[:, i * D:(i + 1) * D]).then_inc(own.sem, own.one())
                    v.wait_ge(own.sem, own.n)
                for i in range(NT):
                    v.bn_aggr(mv[:, i, :], st[:, i, :]).then_inc(own.sem, own.one())
                v.wait_ge(own.sem, own.n)
                if rms:
                    v.tensor_tensor(rstd[:, :], mv[:, :, 0], mv[:, :, 0], ALU.mult).then_inc(own.sem, own.one())
                    v.wait_ge(own.sem, own.n)
                    v.tensor_tensor(mv[:, :, 1], rstd[:, :], mv[:, :, 1], ALU.add).then_inc(own.sem, own.one())
                    v.wait_ge(own.sem, own.n)
                v.tensor_scalar(rstd[:, :], mv[:, :, 1], eps, None, ALU.add).then_inc(s_var, 1)
                own.restart()
                v.wait_ge(s_rstd, k)

            def pool(g):
                g.wait_ge(s_var, k)
                g.tensor_tensor(rstd[:, :], rstd[:, :], m.mhalf[:, :], ALU.pow).then_inc(s_rstd, 1)
            prog["dve"].append(dve)
            prog["pool"].append(pool)

        def norm_to_xin():
            def dve(v):
                own = Own(v, m.own_dve)
                x3 = X[:, :].rearrange("p (t d) -> p t d", d=D)
                y3 = XIN[:, :].rearrange("p (t d) -> p t d", d=D)
                v.tensor_tensor(y3, x3, m.mv[:, :, 0:1].to_broadcast([P, NT, D]), ALU.subtract).then_inc(own.sem, own.one())
                v.wait_ge(own.sem, own.n)
                v.tensor_tensor(y3, y3, m.rstd[:, :].unsqueeze(2).to_broadcast([P, NT, D]), ALU.mult).then_inc(own.sem, own.one())
                v.wait_ge(own.sem, own.n)
                own.restart()
            prog["dve"].append(dve)

        mv2 = m.mv[:, :, :].rearrange("p t s -> p (t s)")
        cmv2 = m.cmv[:, :, :].rearrange("p t s -> p (t s)")

        def norm_tile(v, dst, src, i, mvf, rstd):
            return v.tensor_scalar(dst, tile_of(src, i), mvf[:, bass.ds(2 * i, 1)], rstd[:, bass.ds(i, 1)],
                                   ALU.subtract, ALU.mult)

        def run(a):
            progs, used = narrow_attention(m, a) if a.heads == "narrow" else attention(m, a)
            for k in prog:
                def go(eng, f=progs[k], bases={n: ev[n].base for n in ev}):
                    for n, b in bases.items():
                        ev[n].base = b
                    f(eng)
                prog[k].append(go)
            for n, k in used.items():
                ev[n].base += k

        def q_piece(w, j, col0=0):
            def f(p, bank, i, u):
                for c in range(4):
                    ins = p.matmul(bank[:, c * P:(c + 1) * P], w[:, col0 + (4 * j + c) * P:col0 + (4 * j + c + 1) * P],
                                   m.xT[:, :], start=True, stop=True)
                return ins
            return f

        def q_keep(j):
            def f(s, bank, i, u, own):
                return s.activation(m.QT[:, 4 * j:4 * j + 4, :], bank.rearrange("p (c q) -> p c q", c=4), ACT.Copy)
            return f

        WORK, RB, RA = Arena("work_arena", 11008), Arena("arena_b", 8400), Arena("arena_a", 25700)
        Wf = RB.cut([P, 2176])
        Wao = RB.cut([P, 8, D])
        Wffo = RB.cut([P, 4, D])
        Wq0 = RB.cut([P, 1024])
        Wkv0 = RB.cut([P, 128])
        Wo0 = RB.cut([P, 8, D])
        m.QT = WORK.cut([P, 8, P])
        m.KT = WORK.cut([P, 8, P])
        m.V = WORK.cut([P, 2, 2, 512])
        m.VW = m.V[:, :, :, :].rearrange("p u b w -> p u (b w)")[:, :, 0:256].rearrange("p u (k d) -> p u k d", d=D)
        m.QW = m.QT[:, :, :].rearrange("p c q -> p (c q)")
        m.PROB = WORK.cut([P, 1024])
        m.PT = WORK.cut([P, 8, P])
        m.OT = WORK.cut([P, 8, P])
        EG = WORK.cut([P, 512])
        UT = WORK.cut([P, 2, 4, P])
        m.CTX = WORK.cut([P, NT * D])
        m.KN = m.CTX[:, 0:768]
        load("layer0_fused", [(Wf[:, :], t["L0_xattn_W_fused"]),
                              (Wao[:, :, :], t["L0_xattn_W_attn_out"].rearrange("(c p) d -> p c d", p=P)),
                              (Wffo[:, :, :], t["L0_xattn_W_ff_out"].rearrange("(c p) d -> p c d", p=P))])
        load("layer0_cross", [(Wq0[:, :], t["L0_xattn_W_q"]), (Wkv0[:, :], t["L0_xattn_W_kv"]),
                              (Wo0[:, :, :], t["L0_xattn_W_out"].rearrange("(c p) d -> p c d", p=P)),
                              (m.CTX[:, :].rearrange("p (t d) -> p t d", d=D),
                               t["ctx_1024"].rearrange("(t b) s d -> (b s) t d", b=TILE_B))])
        KF, CF = 112, 4
        F0 = KF * CF
        NGR = E * F0 // P
        wqT = RA.cut([P, 8 * P])
        wqrT = RA.cut([P, 8 * P])
        wkvT = RA.cut([P, 4 * P])
        woT = RA.cut([P, 8, D])
        w1T = RA.cut([P, E * F0 // 2]).bitcast(BF16)
        w3T = RA.cut([P, E * F0 // 2]).bitcast(BF16)
        w2T = RA.cut([P, E, CF, D])
        AT_W1, AT_W3, AT_W2, AT_SMALL = 0, E * CF, 2 * E * CF, 2 * E * CF + NGR
        QALL = RA.cut([P, AT_SMALL + 20, P])
        QN = (AT_SMALL + 20) // NT
        QS = sb("QS", [P, AT_SMALL + 20])
        qp = sb("qp", [P, 5, 8])
        wgT = sb("wgT", [P, 2, E])
        wg_n = sb("wg_n", [E, 2, D])
        MAGIC = 12582912.0
        s_cleared, s_w0 = sem("unused_rows_cleared"), sem("loaded_layer0_ffn")

        def clear_rows(v):
            v.memset(QALL[96:128, AT_W1:AT_W2, :], 0.0).then_inc(s_cleared, 1)
        prog["dve"].insert(0, clear_rows)

        def load_blocks(q):
            q.wait_ge(s_cleared, 1)
            for first, name in ((AT_W1, "L0_ffn_w1"), (AT_W3, "L0_ffn_w3")):
                q.dma_start(QALL[0:KF, first:first + E * CF, :],
                            t[name].rearrange("e f d -> (e f) d").rearrange("(k p) d -> p k d", p=KF)).then_inc(s_w0, 16)
            st2 = QALL[:, AT_W2:AT_W2 + NGR, :].rearrange("p (e g) q -> p e (g q)", e=4)
            for eh in range(2):
                for el in range(4):
                    q.dma_start(st2[64 * eh:64 * eh + 64, el, :],
                                t["L0_ffn_w2"][4 * eh + el].rearrange("(p r) f -> p (r f)", r=2)).then_inc(s_w0, 16)
            small = QALL[:, AT_SMALL:AT_SMALL + 20, :]
            for at, n, name in ((0, 8, "w_q"), (8, 2, "w_k"), (10, 2, "w_v")):
                q.dma_start(small[:, at:at + n, :], t["L0_ffn_" + name].rearrange("(k p) d -> p k d", p=P)).then_inc(s_w0, 16)
            q.dma_start(small[:, 12:20, :], t["L0_ffn_w_o"].rearrange("p (k d) -> p k d", k=8)).then_inc(s_w0, 16)
        prog["sp"].append(load_blocks)
        load("routers", [(wg_n[:, 0, :], t["L0_ffn_w_gate"]), (wg_n[:, 1, :], t["L1_ffn_W_router"])])

        def quantise_blocks(v, own, i):
            mx, mn, ri, bs = [qp[:, k, 0:QN] for k in range(4)]
            blocks, sc = QALL[:, bass.ds(QN * i, QN), :], QS[:, bass.ds(QN * i, QN)]

            def then(ins):
                ins.then_inc(own.sem, own.one())
                v.wait_ge(own.sem, own.n)
            v.tensor_reduce(mx, blocks, AX.X, ALU.max).then_inc(own.sem, own.one())
            then(v.tensor_reduce(mn, blocks, AX.X, ALU.min))
            then(v.tensor_tensor(sc, mx, mn, ALU.subtract))
            then(v.tensor_scalar(sc, sc, 1e-5, 1.0 / 15.0, ALU.max, ALU.mult))
            then(v.reciprocal(ri, sc))
            v.tensor_tensor(bs, mn, ri, ALU.mult).then_inc(own.sem, own.one())
            for k in range(QN):
                b = QALL[:, bass.ds(QN * i + k, 1), :].rearrange("p a q -> p (a q)")
                v.tensor_scalar(b, b, ri[:, k:k + 1], MAGIC, ALU.mult, ALU.add).then_inc(own.sem, own.one())
            v.wait_ge(own.sem, own.n)
            then(v.tensor_scalar(bs, bs, MAGIC, MAGIC, ALU.add, ALU.subtract))
            then(v.tensor_scalar(bs, bs, 0.0, -15.0, ALU.min, ALU.max))
            v.tensor_scalar(mx, bs, MAGIC, None, ALU.add).then_inc(own.sem, own.one())
            then(v.tensor_scalar(mn, bs, MAGIC + 15.0, None, ALU.add))
            for k in range(QN):
                b = QALL[:, bass.ds(QN * i + k, 1), :].rearrange("p a q -> p (a q)")
                v.tensor_scalar(b, b, mx[:, k:k + 1], mn[:, k:k + 1], ALU.max, ALU.min).then_inc(own.sem, own.one())
            v.wait_ge(own.sem, own.n)
            then(v.tensor_scalar(blocks, blocks, MAGIC, None, ALU.subtract))
        prog["dve"].append(lambda v: loaded(v, "x"))
        statistics(X, m.mv, m.rstd, 1e-5)
        norm_to_xin()
        statistics(XIN, m.mv, m.rstd, 1e-5)
        prog["pe"].append(lambda p: loaded(p, "layer0_fused"))

        def mqa_kv(w, src, k0):
            def f(p, bank, i, u):
                for h in range(2):
                    p.matmul(bank[64 * h:64 * h + 64, 0:P], w[:, k0:k0 + 64], src[:, :], start=True, stop=True)
                for b in range(2):
                    for h in range(2):
                        ins = p.matmul(bank[64 * h:64 * h + 64, 128 + 64 * b:192 + 64 * b],
                                       src[:, 64 * b:64 * b + 64], w[:, k0 + 64:k0 + 128], start=True, stop=True)
                return ins
            return f

        def mqa_keep(s, bank, i, u, own):
            s.activation(m.KT[:, 0, :], bank[:, 0:P], ACT.Copy)
            return s.activation(m.V[:, u, :, 0:64], bank[:, 128:256].rearrange("p (b d) -> p b d", b=2), ACT.Copy)

        def gate_tanh(s, bank, i, u, own):
            return s.activation(EG[:, :], bank, ACT.Tanh, scale=0.5)

        def gate_times(v, bank, i, u, own):
            v.wait_ge(ev["gate_tanhed"].sem, ev["gate_tanhed"].base + i + 1)
            return v.scalar_tensor_tensor(EG[:, :], EG[:, :], 1.0, bank, ALU.add, ALU.mult)

        def up_times(v, bank, i, u, own):
            v.wait_ge(ev["kept3"].sem, ev["kept3"].base + i + 1)
            return v.scalar_tensor_tensor(UT[:, u, :, :].rearrange("p c q -> p (c q)"), EG[:, :], 0.5, bank,
                                          ALU.mult, ALU.mult)

        def finish_into_xin(v, own, i):
            return v.tensor_tensor(tile_of(XIN, i), m.OPS[:, 0:128], tile_of(XIN, i), ALU.add)

        def finish_into_x(gate):
            def f(v, own, i):
                return v.scalar_tensor_tensor(tile_of(X, i), m.OPS[:, 0:128], m.tg[:, gate:gate + 1], tile_of(X, i),
                                              ALU.mult, ALU.add)
            return f

        def normalise(src):
            def f(v, own, i, u):
                norm_tile(v, m.xn[:, u, :], src, i, mv2, m.rstd).then_inc(ev["xn"].sem, 1)
            return f

        def normalise_both(v, own, i, u):
            norm_tile(v, m.cx[:, u, :], m.CTX, i, cmv2, m.crstd)
            norm_tile(v, m.xn[:, u, :], XIN, i, mv2, m.rstd).then_inc(ev["xn"].sem, 1)

        def causal_mask(i):
            return m.causal[:, :].unsqueeze(1).unsqueeze(1)

        run(Attention(extra=["gate_tanhed"], x_gain=m.gains[:, 0:1], mask=causal_mask, scale=64 ** -0.5,
                 pieces=[dict(pe=q_piece(Wf, 0), act=q_keep(0)), dict(pe=q_piece(Wf, 1), act=q_keep(1)),
                         dict(pe=mqa_kv(Wf, m.xT, 1024), act=mqa_keep),
                         dict(pe=q_piece(Wf, 0, 1664), act=gate_tanh, raises="gate_tanhed", dve=gate_times),
                         dict(pe=q_piece(Wf, 0, 1152), dve=up_times)],
                 q_ready=["kept0", "kept1", "kept2"], v_ready=["kept2"], w_out=Wao,
                 more_out=lambda u: [(UT[:, u, c, :], Wffo[:, c, :]) for c in range(4)],
                 normalise=normalise(XIN), finish=finish_into_xin, out=XIN))
        barrier()
        prog["dve"].append(lambda v: (loaded(v, "layer0_cross"), v.wait_ge(s_w0, 16 * 14)))
        prog["pe"].append(lambda v: loaded(v, "layer0_cross"))
        statistics(m.CTX, m.cmv, m.crstd, 1e-5, st=st_ctx)
        statistics(XIN, m.mv, m.rstd, 1e-5, ready=True)
        run(Attention(ctx="normed", x_gain=m.gains[:, 1:2], c_gain=m.gains[:, 2:3], scale=64 ** -0.5,
                 pieces=[dict(pe=q_piece(Wq0, 0), act=q_keep(0)), dict(pe=q_piece(Wq0, 1), act=q_keep(1)),
                         dict(pe=mqa_kv(Wkv0, m.cT, 0), act=mqa_keep)],
                 q_ready=["kept0", "kept1", "kept2"], v_ready=["kept2"], w_out=Wo0,
                 normalise=normalise_both, finish=finish_into_x(0), out=X, dve_extra=quantise_blocks))
        barrier()
        s_turned, s_kept_w, s_quant = sem("weights_turned"), sem("weights_kept"), sem("weights_quantised")
        s_rotated = sem("rotation_ready")
        m.n_turned = 0
        m.n_quant = 0

        def turn(sources, dst, rows=P, cols=P):
            n = m.n_turned = m.n_turned + 1
            bank = m.PTP[:, (n % 2) * 512:(n % 2) * 512 + 512]

            def pe(p):
                if some(n - 2):
                    p.wait_ge(s_kept_w, n - 2)
                for k, src in enumerate(sources):
                    ins = p.transpose(bank[0:cols, k * rows:(k + 1) * rows], src, m.ident[0:rows, 0:rows])
                ins.then_inc(s_turned, 1)

            def act(s):
                s.wait_ge(s_turned, n)
                s.activation(dst[0], dst[1](bank[0:cols, 0:rows * len(sources)]), ACT.Copy).then_inc(s_kept_w, 1)
            prog["pe"].append(pe)
            prog["act"].append(act)

        def kept_weights():
            n = m.n_turned
            prog["pe"].append(lambda p: p.wait_ge(s_kept_w, n))

        def scaled_weights(first, count):
            k = m.n_quant = m.n_quant + 1

            def dve(v):
                w = QALL[:, first:first + count, :]
                v.tensor_tensor(w, w, QS[:, first:first + count].unsqueeze(2).to_broadcast([P, count, P]), ALU.mult)\
                    .then_inc(s_quant, 1)
                v.wait_ge(s_quant, k)
            prog["dve"].append(dve)
            prog["pe"].append(lambda p: p.wait_ge(s_quant, k))

        RB.again()
        Wq1 = RB.cut([P, 1024])
        Wkv1 = RB.cut([P, 2048])
        Wo1 = RB.cut([P, 8, D])
        WiE = RB.cut([P, E, 4 * P])
        small = QALL[:, AT_SMALL:AT_SMALL + 20, :]
        scaled_weights(AT_SMALL, 20)

        def flat(k):
            return lambda b: b.rearrange("p (k q) -> p k q", k=k)
        for k in range(0, 8, 4):
            turn([small[:, k + i, :] for i in range(4)], (wqT[:, k * P:(k + 4) * P], lambda b: b))
        turn([small[:, 8 + i, :] for i in range(4)], (wkvT[:, :], lambda b: b))
        for k in range(0, 8, 4):
            turn([small[:, 12 + k + i, :] for i in range(4)], (woT[:, k:k + 4, :], flat(4)))
        prog["pe"].append(lambda p: loaded(p, "routers"))
        turn([wg_n[:, i, :] for i in range(2)], (wgT[:, :, :], flat(2)), rows=E)
        n_q = m.n_turned

        def rotate(s):
            s.wait_ge(s_kept_w, n_q)
            a4 = wqT[:, :].rearrange("p (h r d) -> p h r d", h=8, r=2)
            b4 = wqrT[:, :].rearrange("p (h r d) -> p h r d", h=8, r=2)
            s.activation(b4[:, :, 0, :], a4[:, :, 1, :], ACT.Copy, scale=-1.0).then_inc(s_rotated, 1)
            s.activation(b4[:, :, 1, :], a4[:, :, 0, :], ACT.Copy).then_inc(s_rotated, 1)
        prog["act"].append(rotate)
        prog["pe"].append(lambda p: p.wait_ge(s_rotated, 2))
        for first, dst in ((AT_W1, w1T), (AT_W3, w3T)):
            for e in range(E):
                turn([QALL[0:KF, first + CF * e + c, :] for c in range(CF)], (dst[:, e * F0:(e + 1) * F0], lambda b: b),
                     rows=KF)
        load("layer1_attention", [(Wq1[:, :], t["L1_xattn_Wq"]), (Wkv1[:, :], t["L1_xattn_Wkv"]),
                                  (Wo1[:, :, :], t["L1_xattn_Wo"].rearrange("(c p) d -> p c d", p=P))])
        load("layer1_experts", [(WiE[:, :, :], t["L1_ffn_experts_inter"].rearrange("e h i -> h e i"))])
        scaled_weights(AT_W2, NGR)
        st2 = QALL[:, AT_W2:AT_W2 + NGR, :].rearrange("p (e g) q -> p e (g q)", e=4)
        for el in range(4):
            for par in range(2):
                dst = w2T[0:KF, :, :, :].rearrange("f (a e) c (q r) -> f a e c q r", a=2, r=2)[:, :, el, :, :, par]
                turn([st2[:, el, par * F0 + c * KF:par * F0 + (c + 1) * KF] for c in range(CF)],
                     (dst.rearrange("f a c q -> f c a q"),
                      lambda b: b.rearrange("f (c a q) -> f c a q", c=CF, a=2)), cols=KF)
        kept_weights()

        statistics(X, m.mv, m.rstd, 1e-5, ready=True)
        norm_to_xin()
        statistics(XIN, m.mv, m.rstd, 1e-5, rms=True)
        TR = UT[:, :, :, :].rearrange("p u c q -> p (u c q)")
        KR = EG[:, 0:256]
        KQ = m.KN[:, 256:768].rearrange("p (k d) -> p k d", d=D)

        def batch_head(buf, j):
            return buf.rearrange("p (b h q) -> p h b q", b=2, q=S)[:, 4 * j:4 * j + 4]

        def with_table(table, dst, j):
            def f(v, bank, i, u, own):
                for b in range(2):
                    ins = v.tensor_tensor(batch_head(dst, j)[:, :, b, :],
                                          bank.rearrange("p (c b q) -> p c b q", c=4, b=2)[:, :, b, :],
                                          table[:, 64 * b:64 * b + 64].unsqueeze(1).to_broadcast([P, 4, S]), ALU.mult)
                return ins
            return f

        def kv_piece(p, bank, i, u):
            return p.matmul(bank, m.xT[:, :], wkvT[:, :], start=True, stop=True)

        def kv_keep(v, bank, i, u, own):
            mx, mn, sc, ri, bs = [qp[:, k, 0:4] for k in range(5)]
            b3 = bank.rearrange("p (k d) -> p k d", d=D)
            v.tensor_reduce(mx, b3, AX.X, ALU.max).then_inc(own.sem, own.one())
            v.tensor_reduce(mn, b3, AX.X, ALU.min).then_inc(own.sem, own.one())
            v.wait_ge(own.sem, own.n)
            v.tensor_tensor(sc, mx, mn, ALU.subtract).then_inc(own.sem, own.one())
            v.wait_ge(own.sem, own.n)
            v.tensor_scalar(sc, sc, 1e-5, 1.0 / 15.0, ALU.max, ALU.mult).then_inc(own.sem, own.one())
            v.wait_ge(own.sem, own.n)
            v.reciprocal(ri, sc).then_inc(own.sem, own.one())
            v.wait_ge(own.sem, own.n)
            v.tensor_tensor(bs, mn, ri, ALU.mult).then_inc(own.sem, own.one())
            for k in range(4):
                v.tensor_scalar(KQ[:, k, :], b3[:, k, :], ri[:, k:k + 1], MAGIC, ALU.mult, ALU.add)\
                    .then_inc(own.sem, own.one())
            v.wait_ge(own.sem, own.n)
            v.tensor_scalar(bs, bs, MAGIC, MAGIC, ALU.add, ALU.subtract).then_inc(own.sem, own.one())
            v.wait_ge(own.sem, own.n)
            v.tensor_scalar(bs, bs, 0.0, -15.0, ALU.min, ALU.max).then_inc(own.sem, own.one())
            v.wait_ge(own.sem, own.n)
            v.tensor_scalar(mx, bs, MAGIC, None, ALU.add).then_inc(own.sem, own.one())
            v.tensor_scalar(mn, bs, MAGIC + 15.0, None, ALU.add).then_inc(own.sem, own.one())
            v.wait_ge(own.sem, own.n)
            for k in range(4):
                v.tensor_scalar(KQ[:, k, :], KQ[:, k, :], mx[:, k:k + 1], mn[:, k:k + 1], ALU.max, ALU.min)\
                    .then_inc(own.sem, own.one())
            v.wait_ge(own.sem, own.n)
            for k in range(4):
                dst = m.KN[:, k * P:(k + 1) * P] if k < 2 else m.VW[:, u, k - 2, :]
                ins = v.tensor_scalar(dst, KQ[:, k, :], MAGIC, sc[:, k:k + 1], ALU.subtract, ALU.mult)
            return ins

        def k_finish(v, i, own):
            v.wait_ge(ev["kept0"].sem, ev["kept0"].base + i + 1)
            k3 = m.KN[:, 0:256].rearrange("p (g d) -> p g d", g=2)
            r3 = KR.rearrange("p (g d) -> p g d", g=2)
            for h in range(2):
                v.tensor_tensor(r3[:, :, 64 * h:64 * h + 64], k3[:, :, 64 - 64 * h:128 - 64 * h],
                                m.sinN[:, 64 * h:64 * h + 64].unsqueeze(1).to_broadcast([P, 2, 64]),
                                ALU.mult).then_inc(own.sem, own.one())
            v.wait_ge(own.sem, own.n)
            v.tensor_tensor(k3, k3, m.cosN[:, :].unsqueeze(1).to_broadcast([P, 2, P]), ALU.mult).then_inc(own.sem, own.one())
            v.wait_ge(own.sem, own.n)
            v.tensor_tensor(k3, k3, r3, ALU.add).then_inc(ev["knat"].sem, 1)

        def pool_rope(g, i, u):
            for j in range(2):
                g.wait_ge(ev["kept%d" % (2 + 2 * j)].sem, ev["kept%d" % (2 + 2 * j)].base + i + 1)
                q4 = m.QW.rearrange("p (b h q) -> p b (h q)", b=2, q=S)[:, :, 256 * j:256 * j + 256]
                r4 = TR.rearrange("p (b h q) -> p b (h q)", b=2, q=S)[:, :, 256 * j:256 * j + 256]
                ins = g.tensor_tensor(q4, q4, r4, ALU.add)
            ins.then_inc(ev["q_turned_by_pos"].sem, 1)

        def scaled(src):
            def f(v, own, i, u):
                v.tensor_scalar(m.xn[:, u, :], tile_of(src, i), m.rstd[:, bass.ds(i, 1)], None,
                                                ALU.mult).then_inc(ev["xn"].sem, 1)
            return f

        run(Attention(heads="wide", extra=["kT", "knat", "k_turned", "q_turned_by_pos"],
                 x_gain=m.gains[:, 3:4], mask=causal_mask, scale=float(1 / np.float32(np.sqrt(128))),
                 pieces=[dict(pe=kv_piece, dve=kv_keep, dve_after=k_finish, bank=m.PS[:, 512:1024], last=True),
                         dict(pe=q_piece(wqT, 0), dve=with_table(m.cosT, m.QW, 0), bank=m.RING[:, 0:512], bank_after=-1),
                         dict(pe=q_piece(wqrT, 0), dve=with_table(m.sinT, TR, 0), bank=m.RING[:, 512:1024], bank_after=-1),
                         dict(pe=q_piece(wqT, 1), dve=with_table(m.cosT, m.QW, 1), bank=m.RING[:, 0:512]),
                         dict(pe=q_piece(wqrT, 1), dve=with_table(m.sinT, TR, 1), bank=m.RING[:, 512:1024])],
                 q_ready=["q_turned_by_pos", "kT"], v_ready=["kept0"], w_out=woT, pool_front=pool_rope,
                 normalise=scaled(XIN), finish=finish_into_xin, out=XIN))
        barrier()
        LG = sb("LG", [P, NT * E])
        PR = sb("PR", [P, NT * E])
        RW = sb("RW", [P, NT * E])
        SEL = sb("SEL", [P, 2, NT * E])
        rt = sb("rt", [P, 4, NT])
        s_rt_ready, s_rt_exped = sem("logits_ready"), sem("logits_exped")
        m.n_rt = 0

        def by_tile(buf):
            return buf.rearrange("p (t e) -> p t e", e=E)

        s_r = {n: sem("routing_" + n) for n in ("normed", "turned", "T", "hidden", "hidden_gelu", "logits", "kept")}
        m.n_route = 0

        def routing(w_router, gain, norm, bias=None, hidden=None):
            base = NG * m.n_route
            m.n_route += 1
            XN, XT, HR = m.ROUTE_XN, m.ROUTE_XT, m.ROUTE_H
            banks = [m.PS[:, 0:512], m.PS[:, 512:1024], m.PTP[:, 0:512], m.PTP[:, 512:1024]]

            def pe(p):
                for g in range(NG):
                    p.wait_ge(s_r["normed"], base + g + 1)
                    for i in range(GROUP):
                        t = GROUP * g + i
                        ins = p.transpose(banks[g][:, i * P:(i + 1) * P], XN[:, t * D:(t + 1) * D], m.ident[:, :])
                    ins.then_inc(s_r["turned"], 1)
                if hidden:
                    for g in range(NG):
                        p.wait_ge(s_r["T"], base + g + 1)
                        p.matmul(banks[g][0:32, :], hidden[0], XT[:, g * GT:(g + 1) * GT], start=True, stop=True)\
                            .then_inc(s_r["hidden"], 1)
                for g in range(NG):
                    if hidden:
                        p.wait_ge(s_r["hidden_gelu"], g + 1)
                    else:
                        p.wait_ge(s_r["T"], base + g + 1)
                    for i in range(GROUP):
                        t = GROUP * g + i
                        l = (HR[0:32, t * P:(t + 1) * P] if hidden else XT[:, t * P:(t + 1) * P])
                        ins = p.matmul(m.OPS[:, t * E:(t + 1) * E], l, w_router, start=True, stop=True)
                ins.then_inc(s_r["logits"], 1)

            def act(s):
                for g in range(NG):
                    s.wait_ge(s_r["turned"], base + g + 1)
                    s.activation(XT[:, g * GT:(g + 1) * GT], banks[g], ACT.Copy if gain is None else ACT.Identity,
                                 scale=1.0 if gain is None else gain).then_inc(s_r["T"], 1)
                if hidden:
                    for g in range(NG):
                        s.wait_ge(s_r["hidden"], g + 1)
                        s.activation(HR[0:32, g * GT:(g + 1) * GT], banks[g][0:32, :], ACT.Gelu, bias=hidden[1])\
                            .then_inc(s_r["hidden_gelu"], 1)

            def dve(v):
                for g in range(NG):
                    for i in range(GROUP):
                        t = GROUP * g + i
                        ins = norm(v, XN[:, t * D:(t + 1) * D], t)
                    ins.then_inc(s_r["normed"], 1)
                v.wait_ge(s_r["logits"], base // NG + 1)
                if bias is not None:
                    ins = v.tensor_tensor(by_tile(LG[:, :]), by_tile(m.OPS[:, 0:NT * E]),
                                          bias.unsqueeze(1).to_broadcast([P, NT, E]), ALU.add)
                else:
                    ins = v.tensor_scalar(LG[:, :], m.OPS[:, 0:NT * E], 1.0, None, ALU.mult)
                ins.then_inc(s_r["kept"], 1)
                v.wait_ge(s_r["kept"], base // NG + 1)
            for k, f in (("pe", pe), ("act", act), ("dve", dve)):
                prog[k].append(f)

        def norm_rms(v, dst, i):
            return v.tensor_scalar(dst, tile_of(XIN, i), m.rstd[:, bass.ds(i, 1)], None, ALU.mult)

        def norm_x(v, dst, i):
            return norm_tile(v, dst, X, i, mv2, m.rstd)

        def softmax_and_ranks():
            k = m.n_rt = m.n_rt + 1
            lg, pr = by_tile(LG[:, :]), by_tile(PR[:, :])

            def wide(x):
                return x.unsqueeze(2).to_broadcast([P, NT, E])

            def dve(v):
                own = Own(v, m.own_dve)
                v.tensor_reduce(rt[:, 0, :], lg, AX.X, ALU.max).then_inc(own.sem, own.one())
                v.wait_ge(own.sem, own.n)
                v.tensor_tensor(lg, lg, wide(rt[:, 0, :]), ALU.subtract).then_inc(s_rt_ready, 1)
                v.wait_ge(s_rt_exped, k)
                v.tensor_reduce(rt[:, 1, :], lg, AX.X, ALU.add).then_inc(own.sem, own.one())
                v.wait_ge(own.sem, own.n)
                v.reciprocal(rt[:, 1, :], rt[:, 1, :]).then_inc(own.sem, own.one())
                v.wait_ge(own.sem, own.n)
                v.tensor_tensor(pr, lg, wide(rt[:, 1, :]), ALU.mult).then_inc(own.sem, own.one())
                v.wait_ge(own.sem, own.n)
                above, level = m.R1[:, :].rearrange("p (t e f) -> p t e f", e=E, f=E), \
                    m.R2[:, :].rearrange("p (t e f) -> p t e f", e=E, f=E)
                f_ = pr.unsqueeze(2).to_broadcast([P, NT, E, E])
                e_ = pr.unsqueeze(3).to_broadcast([P, NT, E, E])
                v.tensor_tensor(above, f_, e_, ALU.is_gt).then_inc(own.sem, own.one())
                v.tensor_tensor(level, f_, e_, ALU.is_equal).then_inc(own.sem, own.one())
                v.wait_ge(own.sem, own.n)
                tie = m.tie[:, :].unsqueeze(1).to_broadcast([P, NT, E * E])
                l3 = m.R2[:, :].rearrange("p (t g) -> p t g", g=E * E)
                v.tensor_tensor(l3, l3, tie, ALU.mult).then_inc(own.sem, own.one())
                v.wait_ge(own.sem, own.n)
                v.tensor_tensor(m.R1[:, :], m.R1[:, :], m.R2[:, :], ALU.add).then_inc(own.sem, own.one())
                v.wait_ge(own.sem, own.n)
                v.tensor_reduce(by_tile(RW[:, :]), above, AX.X, ALU.add).then_inc(own.sem, own.one())
                v.wait_ge(own.sem, own.n)
                v.tensor_scalar(SEL[:, 0, :], RW[:, :], 0.0, None, ALU.is_equal).then_inc(own.sem, own.one())
                v.tensor_scalar(SEL[:, 1, :], RW[:, :], 1.0, None, ALU.is_equal).then_inc(own.sem, own.one())
                v.wait_ge(own.sem, own.n)
                own.restart()

            def act(s):
                s.wait_ge(s_rt_ready, k)
                s.activation(LG[:, :], LG[:, :], ACT.Exp).then_inc(s_rt_exped, 1)
            m.before_ranks = len(prog["dve"])
            prog["dve"].append(dve)
            prog["act"].append(act)

        def top2_weights(normed):
            def dve(v):
                own = Own(v, m.own_dve)
                v.tensor_tensor(RW[:, :], SEL[:, 0, :], SEL[:, 1, :], ALU.add).then_inc(own.sem, own.one())
                v.wait_ge(own.sem, own.n)
                v.tensor_tensor(RW[:, :], RW[:, :], PR[:, :], ALU.mult).then_inc(own.sem, own.one())
                v.wait_ge(own.sem, own.n)
                if normed:
                    v.tensor_reduce(rt[:, 2, :], by_tile(RW[:, :]), AX.X, ALU.add).then_inc(own.sem, own.one())
                    v.wait_ge(own.sem, own.n)
                    v.reciprocal(rt[:, 2, :], rt[:, 2, :]).then_inc(own.sem, own.one())
                    v.wait_ge(own.sem, own.n)
                    v.tensor_tensor(by_tile(RW[:, :]), by_tile(RW[:, :]),
                                             rt[:, 2, :].unsqueeze(2).to_broadcast([P, NT, E]), ALU.mult).then_inc(own.sem, own.one())
                    v.wait_ge(own.sem, own.n)
                own.restart()
            prog["dve"].append(dve)

        s_whole, s_part = sem("group_whole"), sem("parts_ready")
        for n in ("group_normed", "group_turned", "group_T", "up", "silued", "hidden", "down", "summed", "group_done"):
            ev[n] = Event(sem(n))

        def one_ahead(v):
            v.memset(rt[:, 2, :], 0.0).then_inc(ev["group_done"].sem, 1)
            v.memset(rt[:, 3, :], 0.0).then_inc(ev["group_turned"].sem, 1)
            v.wait_ge(ev["group_done"].sem, 1)
            v.wait_ge(ev["group_turned"].sem, 1)
        prog["dve"].append(one_ahead)
        ev["group_done"].base = ev["group_turned"].base = 1

        def experts(kf, w_in, w_gate, w_out, gain, norm, gate, residual, scales=None):
            base = {n: ev[n].base for n in ("group_normed", "group_turned", "group_T", "up", "silued", "hidden",
                                                     "down", "summed", "group_done", "done")}
            XG, XGT = m.XG, m.XGT
            parts = [m.X3[:, k, :] for k in range(3)] if scales else [XGT[:, :]]

            def pe(p):
                def up(g, e):
                    for c in range(4):
                        j = 32 * g + 4 * e + c
                        if not (e == 0 and c < 2):
                            if w_gate is not None:
                                p.wait_ge(ev["silued"].sem, base["silued"] + j - 1)
                            p.wait_ge(ev["hidden"].sem, base["hidden"] + j - 1)
                        bank = (c % 2) * 512
                        for k in range(len(parts)):
                            ins = p.matmul(m.RING[0:kf, bank:bank + 512], w_in(e, c), parts[k],
                                           start=(k == 0), stop=(k == len(parts) - 1))
                        if w_gate is not None:
                            for k in range(len(parts)):
                                ins = p.matmul(m.PS[0:kf, bank:bank + 512], w_gate(e, c), parts[k],
                                               start=(k == 0), stop=(k == len(parts) - 1))
                        ins.then_inc(ev["up"].sem, 1)

                def down(g, e):
                    p.wait_ge(ev["hidden"].sem, base["hidden"] + 32 * g + 4 * e + 4)
                    if e == 0:
                        p.wait_ge(ev["group_done"].sem, base["group_done"] + g)
                    if e >= 2:
                        p.wait_ge(ev["summed"].sem, base["summed"] + 8 * g + e - 1)
                    for i in range(GROUP):
                        for c in range(4):
                            ins = p.matmul(m.PTP[:, (e % 2) * 512 + i * P:(e % 2) * 512 + (i + 1) * P],
                                           m.UTE[0:kf, e % 2, c, i * P:(i + 1) * P], w_out(e, c),
                                           start=(c == 0), stop=(c == 3))
                    ins.then_inc(ev["down"].sem, 1)
                def turn(g):
                    p.wait_ge(ev["group_normed"].sem, base["group_normed"] + g + 1)
                    for i in range(GROUP):
                        ins = p.transpose(m.TPS[:, i * P:(i + 1) * P], XG[:, i, :], m.ident[:, :])
                    ins.then_inc(ev["group_turned"].sem, 1)

                def group(g, last=False):
                    p.wait_ge(ev["group_T"].sem, base["group_T"] + g + 1)
                    up(g, 0)
                    for e in range(E):
                        if e + 1 < E:
                            up(g, e + 1)
                        if e == E - 2 and not last:
                            turn(g + 1)
                        down(g, e)
                turn(0)
                with p.Fori(0, NG - 1) as g:
                    group(g)
                group(NG - 1, True)

            def act(s):
                def keep_turned(g):
                    s.wait_ge(ev["group_turned"].sem, base["group_turned"] + g + 1)
                    s.activation(XGT[:, :], m.TPS[:, :], ACT.Copy if gain is None else ACT.Identity,
                                 scale=1.0 if gain is None else gain).then_inc(s_whole if scales else ev["group_T"].sem, 1)

                def group(g, last=False):
                    for e in range(E):
                        for c in range(4):
                            j = 32 * g + 4 * e + c
                            s.wait_ge(ev["up"].sem, base["up"] + j + 1)
                            src = m.RING[0:kf, (c % 2) * 512:(c % 2) * 512 + 512]
                            if w_gate is not None:
                                s.activation(m.SG[0:kf, c % 2, :], src, ACT.Silu, scale=scales[0][0:kf, 4 * e + c:4 * e + c + 1])\
                                    .then_inc(ev["silued"].sem, 1)
                            else:
                                s.activation(m.UTE[0:kf, e % 2, c, :], src, ACT.Relu).then_inc(ev["hidden"].sem, 1)
                    if not last:
                        keep_turned(g + 1)
                keep_turned(0)
                with s.Fori(0, NG - 1) as g:
                    group(g)
                group(NG - 1, True)

            def dve(v):
                own = Own(v, m.own_dve)
                acc = m.ACC

                def add(g, e):
                    v.wait_ge(ev["down"].sem, base["down"] + 8 * g + e + 1)
                    for i in range(GROUP):
                        scalar = RW[:, bass.ds((4 * g + i) * E + e, 1)]
                        src = m.PTP[:, (e % 2) * 512 + i * P:(e % 2) * 512 + (i + 1) * P]
                        if e == 0:
                            ins = v.tensor_scalar(acc[:, i, :], src, scalar, None, ALU.mult)
                        else:
                            ins = v.scalar_tensor_tensor(acc[:, i, :], src, scalar, acc[:, i, :], ALU.mult, ALU.add)
                    ins.then_inc(ev["summed"].sem, 1)
                    v.wait_ge(ev["summed"].sem, base["summed"] + 8 * g + e + 1)
                def normalise_group(g):
                    for i in range(GROUP):
                        ins = norm(v, XG[:, i, :], 4 * g + i)
                    ins.then_inc(ev["group_normed"].sem, 1)

                def group(g, last=False):
                    for e in range(E):
                        if w_gate is not None:
                            for c in range(4):
                                j = 32 * g + 4 * e + c
                                v.wait_ge(ev["silued"].sem, base["silued"] + j + 1)
                                v.scalar_tensor_tensor(m.UTE[0:kf, e % 2, c, :],
                                                       m.PS[0:kf, (c % 2) * 512:(c % 2) * 512 + 512],
                                                       scales[1][0:kf, 4 * e + c:4 * e + c + 1], m.SG[0:kf, c % 2, :],
                                                       ALU.mult, ALU.mult).then_inc(ev["hidden"].sem, 1)
                        if e:
                            add(g, e - 1)
                        if e == 2 and not last:
                            v.wait_ge(ev["group_turned"].sem, base["group_turned"] + g + 1)
                            normalise_group(g + 1)
                    add(g, E - 1)
                    a2 = acc.rearrange("p i d -> p (i d)")
                    if residual is not None:
                        v.tensor_tensor(a2, a2, tile_of(residual, g, GT), ALU.add).then_inc(own.sem, own.one())
                        v.wait_ge(own.sem, own.n)
                    v.scalar_tensor_tensor(tile_of(X, g, GT), a2, m.tg[:, gate:gate + 1], tile_of(X, g, GT),
                                           ALU.mult, ALU.add).then_inc(own.sem, own.one())
                    own.restart()
                    for i in range(GROUP):
                        ins = v.bn_stats(m.st[:, bass.ds(4 * g + i, 1), :].rearrange("p a s -> p (a s)"),
                                         X[:, bass.ds((4 * g + i) * D, D)])
                    ins.then_inc(ev["group_done"].sem, 1)
                with v.Fori(0, NG - 1) as g:
                    group(g)
                group(NG - 1, True)

            def dve_first(v):
                for i in range(GROUP):
                    ins = norm(v, XG[:, i, :], i)
                ins.then_inc(ev["group_normed"].sem, 1)
            prog["dve"].insert(m.before_ranks, dve_first)

            def pool(q):
                def group(g):
                    q.wait_ge(s_whole, g + 1)
                    q.tensor_copy(m.X3[:, 0, :], XGT[:, :]).then_inc(s_part, 1)
                    q.wait_ge(s_part, 1)
                    q.tensor_tensor(XGT[:, :], XGT[:, :], m.X3[:, 0, :], ALU.subtract).then_inc(s_part, 1)
                    q.wait_ge(s_part, 2)
                    q.tensor_copy(m.X3[:, 1, :], XGT[:, :]).then_inc(s_part, 1)
                    q.wait_ge(s_part, 3)
                    q.tensor_tensor(XGT[:, :], XGT[:, :], m.X3[:, 1, :], ALU.subtract).then_inc(s_part, 1)
                    q.wait_ge(s_part, 4)
                    q.sem_clear(s_part)
                    q.tensor_copy(m.X3[:, 2, :], XGT[:, :]).then_inc(ev["group_T"].sem, 1)
                    q.wait_ge(ev["group_T"].sem, base["group_T"] + g + 1)
                for g in range(NG):
                    group(g)
            if scales:
                prog["pool"].append(pool)
            for k, f in (("pe", pe), ("act", act), ("dve", dve)):
                prog[k].append(f)
            per = dict(group_normed=NG, group_turned=NG, group_T=NG, up=32 * NG, hidden=32 * NG, down=E * NG, summed=E * NG,
                       group_done=NG, silued=32 * NG if w_gate is not None else 0)
            for n, k in per.items():
                ev[n].base += k

        def group_barrier():
            v = ev["group_done"].base
            for k in prog:
                prog[k].append(lambda eng, v=v: eng.wait_ge( ev["group_done"].sem, v))

        def again():
            WORK.again()
            m.XG = WORK.cut([P, GROUP, D])
            m.XGT = WORK.cut([P, GT])
            m.SG = WORK.cut([P, 2, GT])
            m.UTE = WORK.cut([P, 2, 4, GT])
            m.ACC = WORK.cut([P, GROUP, D])
            m.r_at = WORK.at
            m.R1 = WORK.cut([P, NT * E * E])
            m.R2 = WORK.cut([P, NT * E * E])
            flat = m.UTE.rearrange("p a c q -> p (a c q)")
            m.ROUTE_XN, m.ROUTE_H = flat[:, 0:NT * D], flat[:, NT * D:2 * NT * D]
            m.ROUTE_XT = WORK.buf[:, m.r_at:m.r_at + NT * D]

        def attention_buffers():
            WORK.again()
            m.QT = WORK.cut([P, 8, P])
            m.KT = WORK.cut([P, 8, P])
            m.V = WORK.cut([P, 2, 2, 512])
            m.PROB = WORK.cut([P, 1024])
            m.PT = WORK.cut([P, 8, P])
            m.OT = WORK.cut([P, 8, P])

        def narrow_buffers():
            WORK.again()
            m.QB = WORK.cut([P, P])
            m.KB = WORK.cut([P, P])
            m.KT8 = WORK.cut([P, 8, P])
            m.VP = WORK.cut([P, 4 * 256 + 8])
            m.PROB2 = WORK.cut([P, 2 * 1024])
            m.PT8 = WORK.cut([P, 8, P])
            m.OT1 = WORK.cut([P, 2, P])

        again()
        m.X3 = WORK.cut([P, 3 * GT // 2]).bitcast(BF16).rearrange("p (k q) -> p k q", k=3)
        near = QALL[:, 0:8, :].rearrange("p a (b s) -> p (a b) s", s=S)
        WORK.at = WORK.floats - 1220
        xm = WORK.cut([P, NT])
        cm = WORK.cut([P, NT, S])
        valid = WORK.cut([P, NT])
        bo1 = WORK.cut([P, D])
        br1 = WORK.cut([P, E])
        halves = "(t b) s -> b t s"

        def of_keys(name, hb, words=S):
            return t[name].rearrange(halves, b=2)[hb].unsqueeze(0).to_broadcast([64, NT, words])

        def of_queries(name):
            return t[name].rearrange("(t b) s -> (b s) t", b=2)
        load("layer1_masks", [(xm[:, :], of_queries("mask_BxS2_fk1")),
                              (cm[0:64], of_keys("mask_BxS2_fk1", 0)), (cm[64:128], of_keys("mask_BxS2_fk1", 1)),
                              (bo1[:, :], row(t["L1_xattn_bo"], D)), (br1[:, :], row(t["L1_ffn_b_router"], E))])
        s_masks = sem("masks_prepared")

        def masks_pool(g):
            loaded(g, "layer1_masks")
            g.tensor_tensor(cm[:, :, :], cm[:, :, :], xm[:, :].unsqueeze(2).to_broadcast([P, NT, S]), ALU.mult)\
                .then_inc(s_masks, 1)
            g.wait_ge(s_masks, 1)
            g.tensor_scalar(cm[:, :, :], cm[:, :, :], -1.0, 1.0, ALU.mult, ALU.add).then_inc(s_masks, 1)
            g.wait_ge(s_masks, 2)
            g.tensor_scalar(cm[:, :, :], cm[:, :, :], 1.0, None, ALU.subtract).then_inc(s_masks, 1)
            g.wait_ge(s_masks, 3)
            g.tensor_scalar(near[:, :, :], cm[:, :, :], -(1e-8 + 1e-5), NEG, ALU.is_ge, ALU.mult).then_inc(s_masks, 1)
            g.wait_ge(s_masks, 4)
            g.tensor_scalar(cm[:, :, :], cm[:, :, :], 1e-8 + 1e-5, None, ALU.is_le).then_inc(s_masks, 1)
            g.wait_ge(s_masks, 5)
            g.tensor_tensor(cm[:, :, :], cm[:, :, :], near[:, :, :], ALU.mult).then_inc(s_masks, 1)
        statistics(XIN, m.mv, m.rstd, 1e-5, rms=True, ready=True)
        routing(wgT[:, 0, :], m.gains[:, 4:5], norm_rms)
        softmax_and_ranks()
        top2_weights(True)
        experts(KF, lambda e, c: w1T[:, e * F0 + c * KF:e * F0 + (c + 1) * KF],
                lambda e, c: w3T[:, e * F0 + c * KF:e * F0 + (c + 1) * KF],
                lambda e, c: w2T[0:KF, e, c, :], m.gains[:, 4:5],
                norm_rms, 4, XIN, scales=(QS[:, AT_W1:AT_W3], QS[:, AT_W3:AT_W2]))
        prog["pool"].append(masks_pool)
        group_barrier()
        attention_buffers()
        RA.again()
        TMPO = RA.cut([P, D])
        WoE = RA.cut([P, E, 4, D])
        NEXT_A = RA.at
        w_done = ev["group_done"].base
        load("layer1_expert_out", [(WoE[:, e, :, :], t["L1_ffn_experts_out"][e].rearrange("(c p) h -> p c h", p=P))
                                   for e in range(E)])

        def mask1(v):
            v.wait_ge(s_masks, 6)
            own = Own(v, m.own_dve)
            v.tensor_reduce(valid[:, :], cm[:, :, :], AX.X, ALU.max).then_inc(own.sem, own.one())
            v.wait_ge(own.sem, own.n)
            v.tensor_scalar(valid[:, :], valid[:, :], NEG / 2, None, ALU.is_gt).then_inc(own.sem, own.one())
            own.restart()
        prog["dve"].append(mask1)
        statistics(X, m.mv, m.rstd, 1e-5, ready=True)
        prog["pe"].append(lambda p: loaded(p, "layer1_attention"))
        m.cx_phase = 0

        def kv1_piece(j):
            def f(p, bank, i, u):
                for c in range(4):
                    ins = p.matmul(bank[:, c * P:(c + 1) * P], Wkv1[:, (4 * j + c) * P:(4 * j + c + 1) * P], m.cT[:, :],
                                   start=True, stop=True)
                return ins
            return f

        def k1_keep(j):
            def f(s, bank, i, u, own):
                return s.activation(m.KT[:, 4 * j:4 * j + 4, :], bank.rearrange("p (c q) -> p c q", c=4), ACT.Copy)
            return f

        def v1_piece(b):
            def f(p, bank, i, u):
                w = Wkv1[:, 1024:2048].rearrange("p (c h d) -> p c h d", c=8, h=2)
                for h in range(2):
                    ins = p.matmul(bank[64 * h:64 * h + 64, :].rearrange("p (c d) -> p c d", c=8),
                                   m.cT[:, 64 * b:64 * b + 64], w[:, :, h, :], start=True, stop=True)
                return ins
            return f

        def v1_keep(b):
            def f(s, bank, i, u, own):
                return s.activation(m.V[:, u, b, :], bank, ACT.Copy)
            return f

        def finish_biased(gate, bias):
            def f(v, own, i):
                v.tensor_tensor(TMPO[:, :], m.OPS[:, 0:128], bias[:, :], ALU.add).then_inc(own.sem, own.one())
                v.wait_ge(own.sem, own.n)
                return v.scalar_tensor_tensor(tile_of(X, i), TMPO[:, :], m.tg[:, gate:gate + 1], tile_of(X, i),
                                              ALU.mult, ALU.add)
            return f

        def next_ctx():
            k = m.cx_phase
            m.cx_phase += 1
            return k * 8 * NT

        run(Attention(ctx="load", cx_base=next_ctx(), many_k=True, scale=64 ** -0.5,
                 mask=lambda i: cm[:, bass.ds(i, 1), :].unsqueeze(1),
                 rowscale=lambda i: valid[:, bass.ds(i, 1)],
                 pieces=[dict(pe=q_piece(Wq1, 0), act=q_keep(0)), dict(pe=q_piece(Wq1, 1), act=q_keep(1)),
                         dict(pe=kv1_piece(0), act=k1_keep(0)), dict(pe=kv1_piece(1), act=k1_keep(1)),
                         dict(pe=v1_piece(0), act=v1_keep(0)), dict(pe=v1_piece(1), act=v1_keep(1))],
                 q_ready=["kept0", "kept1", "kept2", "kept3"], v_ready=["kept4", "kept5"], w_out=Wo1,
                 normalise=normalise(X), finish=finish_biased(1, bo1), out=X))
        barrier()
        again()
        CAP = int(np.ceil(B * S / E * 1.25))
        statistics(X, m.mv, m.rstd, 1e-5, ready=True)
        prog["dve"].append(lambda v: loaded(v, "layer1_masks"))
        routing(wgT[:, 1, :], None, norm_x, bias=br1[:, :])
        softmax_and_ranks()
        top2_weights(False)
        s_chosen, s_counted = sem("chosen"), sem("counted")

        def chosen(v):
            own = Own(v, m.own_dve)
            v.tensor_scalar(SEL[:, 0, :], RW[:, :], 0.0, None, ALU.is_gt).then_inc(s_chosen, 1)
            v.wait_ge(s_counted, 1)
            cnt = m.PS[:, 512:640].rearrange("p (t e) -> p t e", e=E)
            a = [m.R1[:, 0:128].rearrange("p (t e) -> p t e", e=E), m.R2[:, 0:128].rearrange("p (t e) -> p t e", e=E)]
            v.tensor_copy(a[0], cnt).then_inc(own.sem, own.one())
            v.wait_ge(own.sem, own.n)
            for k, d in enumerate((1, 2, 4, 8)):
                x, y = a[k % 2], a[1 - k % 2]
                v.tensor_copy(y[:, 0:d, :], x[:, 0:d, :]).then_inc(own.sem, own.one())
                v.tensor_tensor(y[:, d:NT, :], x[:, d:NT, :], x[:, 0:NT - d, :], ALU.add).then_inc(own.sem, own.one())
                v.wait_ge(own.sem, own.n)
            v.tensor_tensor(a[0], a[0], cnt, ALU.subtract).then_inc(own.sem, own.one())
            v.wait_ge(own.sem, own.n)
            v.tensor_tensor(a[0], a[0], m.PS[:, 0:128].rearrange("p (t e) -> p t e", e=E), ALU.add).then_inc(own.sem, own.one())
            v.wait_ge(own.sem, own.n)
            v.tensor_scalar(m.R1[:, 0:128], m.R1[:, 0:128], float(CAP), None, ALU.is_lt).then_inc(own.sem, own.one())
            v.wait_ge(own.sem, own.n)
            v.tensor_tensor(RW[:, :], RW[:, :], m.R1[:, 0:128], ALU.mult).then_inc(own.sem, own.one())
            v.wait_ge(own.sem, own.n)
            own.restart()
        prog["dve"].append(chosen)

        def count(p):
            p.wait_ge(s_chosen, 1)
            p.matmul(m.PS[:, 0:128], m.before[:, :], SEL[:, 0, :], start=True, stop=True)
            p.matmul(m.PS[:, 512:640], m.ones[:, :], SEL[:, 0, :], start=True, stop=True).then_inc(s_counted, 1)
        prog["pe"].append(count)
        prog["pe"].append(lambda p: (loaded(p, "layer1_experts"), loaded(p, "layer1_expert_out")))
        experts(P, lambda e, c: WiE[:, e, c * P:(c + 1) * P], None, lambda e, c: WoE[:, e, c, :], None,
                norm_x, 5, None)
        narrow_buffers()
        RB.again()
        RA.again()
        TMPO = RA.cut([P, D])
        RA.at = NEXT_A
        nat2 = RA.cut([P, 6, D])
        wT2 = RA.cut([P, 5, D])
        bq2, bk2 = RA.cut([P, 1]), RA.cut([P, 1])
        bv2 = RA.cut([P, D])
        bo2 = RA.cut([P, D])
        wr1, br1c, wr2, br2 = RA.cut([P, 32]), RA.cut([P, 1]), RA.cut([P, E]), RA.cut([P, E])
        hr = RA.cut([P, P])
        wh1, bh1, wh2c, wh2, bh2 = RA.cut([P, 32]), RA.cut([P, 1]), RA.cut([P, 1]), RA.cut([P, P]), RA.cut([P, 1])
        e1, be1 = RA.cut([P, 2, 512]), RA.cut([P, 4])
        e2, be2 = RA.cut([P, 4, 384]), RA.cut([P, 384])
        s1, bs1 = RA.cut([P, 2, 64]), RA.cut([P, 1])
        s2, bs2 = RA.cut([P, 384]), RA.cut([P, 3])
        f1, bf1, f2, bf2 = RA.cut([P, 256]), RA.cut([P, 2]), RA.cut([P, 2, D]), RA.cut([P, 1])
        iw, mu, sw = RA.cut([P, 1]), RA.cut([P, 1]), RA.cut([P, 1])
        wq3, wk3, wv3, wo3, bo3 = (RA.cut([P, D]), RA.cut([P, E, D]), RA.cut([P, E, D]), RA.cut([P, 2, D]),
                                   RA.cut([P, D]))
        kt3, qt3 = RA.cut([P, NT, S]), RA.cut([P, NT])
        pad = RA.cut([P, NT, S])
        BK = RA.cut([P, NT * P])
        cmT = RA.cut([P, E, P])
        nat3 = RA.cut([P, 2, 512])
        pad8 = RA.cut([P, NT * S // 4])
        LEFT_A = RA.at
        tok_row = t["itok_BxS2_0_7"].rearrange("b s -> (b s)")
        load("layer2_attention", [(nat2[:, i, :], t["L2_xattn_W" + n]) for i, n in enumerate("qkvo")]
             + [(bq2[:, :], col(t["L2_xattn_bq"])), (bk2[:, :], col(t["L2_xattn_bk"])),
                (bv2[:, :], row(t["L2_xattn_bv"], D)),
                (bo2[:, :], row(t["L2_xattn_bo"], D))])
        A2 = "L2_ffn_"
        load("layer2_ffn", [
            (wr1[:, :], t[A2 + "w_r1"]), (br1c[0:32], col(t[A2 + "b_r1"])), (wr2[0:32], t[A2 + "w_r2"]),
            (br2[:, :], row(t[A2 + "b_r2"], E)), (wh1[:, :], t[A2 + "w_h1"]), (bh1[0:32], col(t[A2 + "b_h1"])),
            (wh2c[0:32], t[A2 + "w_h2"]), (bh2[:, :], row(t[A2 + "b_h2"], 1))]
            + [(e1[:, k, :].rearrange("p (e h) -> p e h", e=E), t[A2 + "expert_w1"].rearrange("e (k p) h -> k p e h", k=2)[k])
               for k in range(2)]
            + [(be1[:, :], t[A2 + "expert_b1"].rearrange("(c a) h -> (a h) c", a=2)),
               (e2[:, :, :], t[A2 + "expert_w2"].rearrange("(c a) h o -> (a h) c o", a=2)),
               (be2[0:E], t[A2 + "expert_b2"]), (be2[E:P], t["const_zeros"][E:P]),
               (s1[:, :, :], t[A2 + "w_s1"].rearrange("(k p) h -> p k h", p=P)), (bs1[0:64], col(t[A2 + "b_s1"])),
               (s2[0:64], t[A2 + "w_s2"]), (bs2[:, :], t[A2 + "b_s2"].rearrange("(j p) -> p j", p=P)),
               (f1[:, :], t[A2 + "w_f1"]), (bf1[:, :], t[A2 + "b_f1"].rearrange("(j p) -> p j", p=P)),
               (f2[:, :, :], t[A2 + "w_f2"].rearrange("(k p) d -> p k d", p=P)), (bf2[:, :], col(t[A2 + "b_f2"])),
               (iw[:, :], col(t[A2 + "integration_weight"])), (mu[:, :], col(t[A2 + "mu"])),
               (sw[:, :], row(t[A2 + "shared_weight"], 1))])
        load("layer3", [
            (wq3[:, :], t["L3_xattn_Wq"]), (wk3[:, :, :], t["L3_xattn_Wk_b"].rearrange("e d k -> d e k")),
            (wv3[:, :, :], t["L3_xattn_Wv_b"].rearrange("e d k -> d e k")), (wo3[:, :, :], t["const_zeros"][:, 0:2 * D].rearrange("p (g d) -> p g d", g=2)),
            (bo3[:, :], row(t["L3_xattn_bo"], D)), (qt3[:, :], of_queries("fside_BxS2_0")),
            (kt3[0:64], of_keys("fside_BxS2_0", 0)), (kt3[64:128], of_keys("fside_BxS2_0", 1)),
            (pad8.bitcast(I32)[0:64].rearrange("p (t k) -> p t k", t=NT), of_keys("mask_BxS2_bf0", 0, S // 4)),
            (pad8.bitcast(I32)[64:128].rearrange("p (t k) -> p t k", t=NT), of_keys("mask_BxS2_bf0", 1, S // 4)),
            (cmT[:, :, :].rearrange("p e q -> p (e q)").bitcast(I32), row(tok_row[0:1024], 1024)),
            (pad[:, :, :].rearrange("p t k -> p (t k)").bitcast(I32), row(tok_row[1024:2048], 1024)),
            (nat3[:, 0, :].rearrange("p (c d) -> p c d", c=4), t["L3_ffn_w1"].rearrange("(c p) d -> p c d", p=P)),
            (nat3[:, 1, :], t["L3_ffn_w2"])])

        s_spread = sem("output_weights_spread")

        def spread_wo(g):
            loaded(g, "layer2_attention")
            g.memset(nat2[:, 4:6, :], 0.0).then_inc(s_spread, 1)
            g.wait_ge(s_spread, 1)
            wide_o = nat2[:, 4:6, :].rearrange("p g (c x) -> p (g c) x", x=32)
            src = nat2[:, 3, :].rearrange("p (h c x) -> p h c x", h=2, x=8)
            for h in range(2):
                g.tensor_copy(wide_o[:, :, 8 * h:8 * h + 8], src[:, h]).then_inc(s_spread, 1)
        prog["pool"].append(spread_wo)
        s_pool3 = sem("layer3_masks_prepared")

        def masks3_pool(g):
            loaded(g, "layer3")
            flat_cm = cmT[:, :, :].rearrange("p e q -> p (e q)")
            flat_pad = pad[:, :, :].rearrange("p t k -> p (t k)")
            g.tensor_copy(BK[:, 0:1024], flat_cm.bitcast(I32)).then_inc(s_pool3, 1)
            g.tensor_copy(BK[:, 1024:2048], flat_pad.bitcast(I32)).then_inc(s_pool3, 1)
            g.wait_ge(s_pool3, 2)
            g.tensor_copy(flat_pad, pad8.bitcast(U8)).then_inc(s_pool3, 1)
            g.tensor_tensor(kt3[:, :, :], qt3[:, :].unsqueeze(2).to_broadcast([P, NT, S]), kt3[:, :, :], ALU.subtract)\
                .then_inc(s_pool3, 1)
            g.wait_ge(s_pool3, 4)
            g.tensor_scalar(kt3[:, :, :], kt3[:, :, :], 0.0, None, ALU.is_lt).then_inc(s_pool3, 1)
            g.wait_ge(s_pool3, 5)
            g.tensor_tensor(kt3[:, :, :], kt3[:, :, :], pad[:, :, :], ALU.add).then_inc(s_pool3, 1)
            g.wait_ge(s_pool3, 6)
            g.tensor_scalar(kt3[:, :, :], kt3[:, :, :], 0.0, -NEG, ALU.is_gt, ALU.mult).then_inc(s_pool3, 1)
            g.wait_ge(s_pool3, 7)
            g.tensor_scalar(kt3[:, :, :], kt3[:, :, :], NEG, None, ALU.add).then_inc(s_pool3, 1)
        prog["pool"].append(masks3_pool)

        s_wo = sem("loaded_layer3_output")

        def load_wo(q):
            loaded(q, "layer3")
            for c in range(4):
                for h in range(2):
                    src = t["L3_xattn_Wo"].rearrange("(h g c x) d -> h c x g d", h=2, g=2, c=4)[h][c]
                    q.dma_start(wo3[32 * c + 8 * h:32 * c + 8 * h + 8, :, :], src).then_inc(s_wo, 16)
        prog["sp"].append(load_wo)
        group_barrier()

        prog["pe"].append(lambda p: loaded(p, "layer2_attention"))
        turn([nat2[:, i, :] for i in range(3)], (wT2[:, 0:3, :], flat(3)))
        prog["pe"].append(lambda p: p.wait_ge(s_spread, 3))
        turn([nat2[:, 4 + i, :] for i in range(2)], (wT2[:, 3:5, :], flat(2)))
        kept_weights()
        prog["act"].append(lambda s: loaded(s, "layer2_attention"))
        prog["dve"].append(lambda s: loaded(s, "layer2_attention"))
        statistics(X, m.mv, m.rstd, 1e-5, ready=True)

        def one(w, src):
            def f(p, bank, i, u):
                return p.matmul(bank[:, 0:P], w, src[:, :], start=True, stop=True)
            return f

        def to_buffer(dst, bias=None):
            def f(s, bank):
                if bias is None:
                    return s.activation(dst, bank[:, 0:P], ACT.Copy)
                return s.activation(dst, bank[:, 0:P], ACT.Identity, bias=bias)
            return f

        def v2_piece(p, bank, i, u):
            return p.matmul(bank[:, 0:P], m.cT[:, :], wT2[:, 2, :], start=True, stop=True)

        def v2_keep(v, spread_v, bank, u):
            def put(dst, src, h, b):
                bias = bv2[64 * b:64 * b + 64, 64 * h:64 * h + 64].rearrange("p (c x) -> p c x", c=8)
                return v.tensor_tensor(dst, src, bias, ALU.add)
            return spread_v(put, bank, u)
        run(Attention(heads="narrow", ctx="load", cx_base=next_ctx(), scale=float(1 / np.sqrt(np.float32(8))),
                      pieces=[dict(pe=one(wT2[:, 0, :], m.xT), act=to_buffer(m.QB[:, :], bq2[:, :])),
                              dict(pe=one(wT2[:, 1, :], m.cT), act=to_buffer(m.KB[:, :], bk2[:, :])),
                              dict(pe=v2_piece, dve=v2_keep)],
                      w_out=wT2[:, 3:5, :], normalise=normalise(X), finish=finish_biased(2, bo2), out=X))
        barrier()
        again()
        statistics(X, m.mv, m.rstd, 1e-5, ready=True)
        for eng in ("pe", "act", "dve", "pool"):
            prog[eng].append(lambda x: loaded(x, "layer2_ffn"))
        s_prep = sem("layer2_prepared")

        def prep2_dve(v):
            own = Own(v, m.own_dve)
            v.tensor_scalar(sw[:, :], sw[:, :], 0.5, 0.5, ALU.mult, ALU.add).then_inc(own.sem, own.one())
            v.wait_ge(own.sem, own.n)
            own.restart()

        def prep2_act(s):
            s.activation(sw[:, :], sw[:, :], ACT.Tanh, scale=0.5).then_inc(s_prep, 1)
            s.activation(wh2[0:32, :], wh2c[0:32, 0:1].to_broadcast([32, P]), ACT.Copy).then_inc(s_prep, 1)
            s.activation(bh2[:, :], bh2[:, :], ACT.Copy, scale=0.5).then_inc(s_prep, 1)
            s.activation(hb2[:, :], bs2[:, :], ACT.Copy, scale=0.5).then_inc(s_prep, 1)
        hb2 = sb("hb2", [P, 3])
        prog["act"].append(prep2_act)
        prog["dve"].append(lambda v: v.wait_ge(s_prep, 1))
        prog["dve"].append(prep2_dve)
        prog["pe"].append(lambda p: p.wait_ge(s_prep, 4))
        prog["act"].append(lambda s: s.wait_ge(s_prep, 4))
        routing(wr2[0:32, :], None, norm_x, bias=br2[:, :], hidden=(wr1[:, :], br1c[0:32]))
        softmax_and_ranks()
        top2_weights(True)
        W = GT // 2
        WORK.again()
        RB.again()
        RA.at = D

        class Stream:
            def __init__(self, x):
                self.x = x
                if x:
                    assert RA.at <= NEXT_A
                    RA.at = LEFT_A
                self.name = "even" if x == 0 else "odd"
                self.xn = WORK.cut([P, 2, D])
                self.IT, self.VT = WORK.cut([P, W]), WORK.cut([P, W])
                self.HS, self.HG = WORK.cut([P, W]), WORK.cut([P, 4, W])
                self.OH, self.WH = WORK.cut([P, 2, W]), WORK.cut([P, 2, W])
                self.S4 = WORK.cut([P, 4, 2 * E])
                self.ERR, self.XN, self.H1, self.TH = (WORK.cut([P, W]) for _ in range(4))
                self.F1 = WORK.cut([P, 2, W])
                self.MK, self.MH = RB.cut([P, 2, 4, W]), RB.cut([P, 2, 4, W])
                self.WW = RA.cut([P, 3, W])
                self.TAG = RA.cut([P, 2, 3, W])
                self.ZB, self.AB = RA.cut([P, 3, W]), RA.cut([P, 3, W])
                self.bank = ([m.TPS[:, :], m.RING[:, 0:512], m.RING[:, 512:1024], m.PS[:, 0:512]] if x == 0 else
                             [m.PS[:, 512:1024], m.PTP[:, 0:512], m.PTP[:, 512:1024], m.OPS[:, :]])
                self.sem = {n: sem(self.name + "_" + n) for n in per}

            def nth(self, name, g, k):
                return per[name] * g + k + (1 if name in ahead else 0)

        per = dict(normed=1, turned=1, kept=1, sel_ready=1, sel_turned=1, sel_kept=1, spread=5, spread_kept=5,
                   hid=6, hid_gelu=10, masked0=8, masked1=8, steer=10, steer_kept=10, soft=2, x_next=2, refine=4,
                   refine_gelu=6, refined=2, halted=2, it_done=2, end_turned=1, done=1)
        ahead = ("done", "turned", "sel_turned")
        st = [Stream(0), Stream(1)]
        slots = [(0, 0), (1, 0), (0, 1), (1, 1)]

        def half(bank, k):
            return bank[:, k * W:(k + 1) * W]

        def pe(p):
            def mm(out, l, r, start=True, stop=True):
                return p.matmul(out, l, r, start=start, stop=stop)

            def begin(y, g):
                p.wait_ge(y.sem["normed"], y.nth("normed", g, 1))
                p.wait_ge(y.sem["done"], y.nth("done", g, 0))
                for i in range(2):
                    ins = p.transpose(y.bank[0][:, i * P:(i + 1) * P], y.xn[:, i, :], m.ident[:, :])
                ins.then_inc(y.sem["turned"], 1)
                p.wait_ge(y.sem["sel_ready"], y.nth("sel_ready", g, 1))
                for k in range(4):
                    for i in range(2):
                        o = (k % 2) * W + i * P
                        ins = p.transpose(y.bank[1 + k // 2][0:E, o:o + P], y.S4[:, k, i * E:(i + 1) * E], m.ident[:, :])
                ins.then_inc(y.sem["sel_turned"], 1)
                p.wait_ge(y.sem["sel_kept"], y.nth("sel_kept", g, 1))
                for j in range(5):
                    if j >= 2:
                        p.wait_ge(y.sem["spread_kept"], y.nth("spread_kept", g, j - 1))
                    for k in range(2):
                        c = 2 * j + k
                        if c < 8:
                            ins = mm(half(y.bank[3 - j % 2], k), m.pick[:, (c % 4) * P:(c % 4 + 1) * P], y.OH[:, c // 4, :])
                        else:
                            ins = mm(half(y.bank[3 - j % 2], k), m.ones[:, :], y.WH[:, k, :])
                    ins.then_inc(y.sem["spread"], 1)

            def hidden(y, g, it):
                if it:
                    p.wait_ge(y.sem["it_done"], y.nth("it_done", g, 1))
                else:
                    p.wait_ge(y.sem["spread_kept"], y.nth("spread_kept", g, 5))
                    p.wait_ge(y.sem["kept"], y.nth("kept", g, 1))
                for j in range(5):
                    o = half(y.bank[j // 2], j % 2)
                    for k, c in enumerate((y.IT, y.VT)):
                        l = s1[:, k, :] if j == 0 else e1[:, k, (j - 1) * P:j * P]
                        ins = mm(o[0:64, :] if j == 0 else o, l, c[:, :], k == 0, k == 1)
                    if j in (1, 3, 4):
                        ins.then_inc(y.sem["hid"], 1)

            def steer(y, g, it, r, part):
                bank = y.bank[3] if r == 0 else y.bank[r - 1]
                if part == 1:
                    bank = y.bank[3] if r == 2 else y.bank[2]
                o = half(bank, part // 2 if part != 1 else r % 2)
                if r == 0:
                    return mm(o, s2[0:64, part * P:(part + 1) * P], y.HS[0:64, :])
                for c in range(4):
                    mm(o, e2[:, c, part * P:(part + 1) * P], y.MH[:, r - 1, c, :], c == 0, False)
                return mm(o, be2[:, part * P:(part + 1) * P], y.OH[:, r - 1, :], False, True)

            def alpha_and_gate(y, g, it, r):
                steer(y, g, it, r, 0)
                steer(y, g, it, r, 2).then_inc(y.sem["steer"], 1)

            def refine(y, g, it):
                p.wait_ge(y.sem["x_next"], y.nth("x_next", g, it + 1))
                for j in range(2):
                    ins = mm(half(y.bank[0], j), f1[:, j * P:(j + 1) * P], y.XN[:, :])
                ins.then_inc(y.sem["refine"], 1)
                mm(y.bank[1][0:32, 0:W], wh1[:, :], y.XN[:, :]).then_inc(y.sem["refine"], 1)

            def refined(y, g, it):
                p.wait_ge(y.sem["refine_gelu"], y.nth("refine_gelu", g, 3 * it + 3))
                mm(half(y.bank[2], 0), wh2[0:32, :], y.H1[0:32, :])
                for k in range(2):
                    ins = mm(half(y.bank[3], 0), f2[:, k, :], y.F1[:, k, :], k == 0, k == 1)
                ins.then_inc(y.sem["refined"], 1)

            def end(y, g):
                p.wait_ge(y.sem["it_done"], y.nth("it_done", g, 2))
                for i in range(2):
                    ins = p.transpose(y.bank[0][:, i * P:(i + 1) * P], y.IT[:, i * P:(i + 1) * P], m.ident[:, :])
                ins.then_inc(y.sem["end_turned"], 1)

            def group(g, last=False):
                for k, (x, it) in enumerate(slots):
                    y = st[x]
                    z, zit = (st[slots[k - 1][0]], slots[k - 1][1]) if k else (None, None)
                    hidden(y, g, it)
                    if k == 0:
                        begin(st[1], g)
                    p.wait_ge(y.sem["hid_gelu"], y.nth("hid_gelu", g, 5 * it + 5))
                    alpha_and_gate(y, g, it, 0)
                    steer(y, g, it, 0, 1)
                    p.wait_ge(y.sem["masked0"], y.nth("masked0", g, 4 * it + 4))
                    alpha_and_gate(y, g, it, 1)
                    steer(y, g, it, 1, 1).then_inc(y.sem["steer"], 1)
                    if k:
                        refine(z, g, zit)
                    p.wait_ge(y.sem["masked1"], y.nth("masked1", g, 4 * it + 4))
                    alpha_and_gate(y, g, it, 2)
                    if k:
                        refined(z, g, zit)
                    p.wait_ge(y.sem["steer_kept"], y.nth("steer_kept", g, 5 * it + 1))
                    steer(y, g, it, 2, 1).then_inc(y.sem["steer"], 1)
                end(st[0], g)
                if not last:
                    begin(st[0], g + 1)
                refine(st[1], g, 1)
                refined(st[1], g, 1)
                end(st[1], g)
            begin(st[0], 0)
            with p.Fori(0, NG - 1) as g:
                group(g)
            group(NG - 1, True)

        def act(s):
            def begin(y, g):
                s.wait_ge(y.sem["turned"], y.nth("turned", g, 1))
                s.activation(y.IT[:, :], half(y.bank[0], 0), ACT.Copy).then_inc(y.sem["kept"], 1)
                s.wait_ge(y.sem["sel_turned"], y.nth("sel_turned", g, 1))
                s.activation(y.OH[0:E, :, :], y.bank[1][0:E, :].rearrange("p (k q) -> p k q", k=2), ACT.Copy)
                s.activation(y.WH[0:E, :, :], y.bank[2][0:E, :].rearrange("p (k q) -> p k q", k=2), ACT.Copy)\
                    .then_inc(y.sem["sel_kept"], 1)
                for j in range(5):
                    s.wait_ge(y.sem["spread"], y.nth("spread", g, j + 1))
                    dst = y.MK[:, j // 2, 2 * (j % 2):2 * (j % 2) + 2, :] if j < 4 else y.WW[:, 1:3, :]
                    s.activation(dst, y.bank[3 - j % 2].rearrange("p (k q) -> p k q", k=2), ACT.Copy)\
                        .then_inc(y.sem["spread_kept"], 1)

            def softplus(y, g, it):
                s.preload_act_table_set("natural_log_exp_and_others")
                s.wait_ge(y.sem["steer_kept"], y.nth("steer_kept", g, 5 * it + 5))
                s.activation(y.AB[:, :, :], y.ZB[:, :, :], ACT.Abs).then_inc(m.own_act, 1)
                s.wait_ge(m.own_act, 1)
                s.activation(y.AB[:, :, :], y.AB[:, :, :], ACT.Exp, scale=-1.0).then_inc(m.own_act, 1)
                s.wait_ge(m.own_act, 2)
                s.activation(y.AB[:, :, :], y.AB[:, :, :], ACT.Ln, bias=1.0).then_inc(y.sem["soft"], 1)
                s.sem_clear(m.own_act)

            def hidden(y, g, it):
                for j in range(5):
                    if j % 2 == 0:
                        s.wait_ge(y.sem["hid"], y.nth("hid", g, 3 * it + j // 2 + 1))
                    o = half(y.bank[j // 2], j % 2)
                    if j == 0:
                        ins = s.activation(y.HS[0:64, :], o[0:64, :], ACT.Gelu, bias=bs1[0:64])
                    else:
                        ins = s.activation(y.HG[:, j - 1, :], o, ACT.Gelu, bias=be1[:, j - 1:j])
                    ins.then_inc(y.sem["hid_gelu"], 1)

            def shared_gates(y, g, it):
                s.wait_ge(y.sem["steer"], y.nth("steer", g, 5 * it + 1))
                s.activation(y.TAG[:, 0, 0, :], half(y.bank[3], 0), ACT.Tanh, bias=hb2[:, 0:1], scale=0.5)
                s.activation(y.TAG[:, 1, 0, :], half(y.bank[3], 1), ACT.Tanh, bias=hb2[:, 2:3], scale=0.5)\
                    .then_inc(y.sem["steer_kept"], 1)

            def slot_gates(y, g, it, r):
                s.wait_ge(y.sem["steer"], y.nth("steer", g, 5 * it + 2 * r))
                s.activation(y.TAG[:, :, r, :], y.bank[r - 1].rearrange("p (k q) -> p k q", k=2), ACT.Tanh, scale=0.5)\
                    .then_inc(y.sem["steer_kept"], 1)

            def first_betas(y, g, it):
                s.wait_ge(y.sem["steer"], y.nth("steer", g, 5 * it + 3))
                s.activation(y.ZB[:, 0, :], half(y.bank[2], 0), ACT.Identity, bias=bs2[:, 1:2])
                s.activation(y.ZB[:, 1, :], half(y.bank[2], 1), ACT.Copy).then_inc(y.sem["steer_kept"], 1)

            def last_beta(y, g, it):
                s.wait_ge(y.sem["steer"], y.nth("steer", g, 5 * it + 5))
                s.activation(y.ZB[:, 2, :], half(y.bank[3], 0), ACT.Copy).then_inc(y.sem["steer_kept"], 1)

            def refine(y, g, it):
                s.wait_ge(y.sem["refine"], y.nth("refine", g, 2 * it + 1))
                for j in range(2):
                    s.activation(y.F1[:, j, :], half(y.bank[0], j), ACT.Gelu, bias=bf1[:, j:j + 1])\
                        .then_inc(y.sem["refine_gelu"], 1)
                s.wait_ge(y.sem["refine"], y.nth("refine", g, 2 * it + 2))
                s.activation(y.H1[0:32, :], y.bank[1][0:32, 0:W], ACT.Gelu, bias=bh1[0:32])\
                    .then_inc(y.sem["refine_gelu"], 1)

            def halting(y, g, it):
                s.wait_ge(y.sem["refined"], y.nth("refined", g, it + 1))
                s.activation(y.TH[:, :], half(y.bank[2], 0), ACT.Tanh, bias=bh2[:, 0:1], scale=0.5)\
                    .then_inc(y.sem["halted"], 1)

            def group(g, last=False):
                for k, (x, it) in enumerate(slots):
                    y = st[x]
                    z, zit = (st[slots[k - 1][0]], slots[k - 1][1]) if k else (None, None)
                    if k:
                        softplus(z, g, zit)
                    hidden(y, g, it)
                    if k == 0:
                        begin(st[1], g)
                    shared_gates(y, g, it)
                    slot_gates(y, g, it, 1)
                    first_betas(y, g, it)
                    if k:
                        refine(z, g, zit)
                    slot_gates(y, g, it, 2)
                    if k:
                        halting(z, g, zit)
                    last_beta(y, g, it)
                softplus(st[1], g, 1)
                if not last:
                    begin(st[0], g + 1)
                refine(st[1], g, 1)
                halting(st[1], g, 1)
            begin(st[0], 0)
            with s.Fori(0, NG - 1) as g:
                group(g)
            group(NG - 1, True)

        def dve(v):
            own = Own(v, m.own_dve)

            def chain(ins):
                ins.then_inc(own.sem, own.one())
                v.wait_ge(own.sem, own.n)

            def wide(x):
                return x.unsqueeze(1).to_broadcast([P, 3, W])
            for y in st:
                v.memset(y.OH[:, :, :], 0.0).then_inc(y.sem["done"], 1)
                v.memset(y.WH[:, :, :], 0.0).then_inc(y.sem["turned"], 1)
                v.memset(y.WW[:, 0, :], 0.0).then_inc(y.sem["sel_turned"], 1)
                for name in ahead:
                    v.wait_ge(y.sem[name], 1)
                chain(v.tensor_scalar(y.WW[:, 0, :], y.WW[:, 0, :], sw[:, 0:1], None, ALU.add))
            own.restart()

            def begin(y, g):
                v.wait_ge(y.sem["turned"], y.nth("turned", g, 0))
                for i in range(2):
                    ins = norm_tile(v, y.xn[:, i, :], X, 4 * g + 2 * y.x + i, mv2, m.rstd)
                ins.then_inc(y.sem["normed"], 1)
                v.memset(y.VT[:, :], 0.0).then_inc(own.sem, own.one())
                v.wait_ge(y.sem["sel_turned"], y.nth("sel_turned", g, 0))
                at = (4 * g + 2 * y.x) * E
                for k in range(2):
                    sel = SEL[:, k, bass.ds(at, 2 * E)]
                    v.tensor_scalar(y.S4[:, k, :], sel, 1.0, None, ALU.mult)
                    ins = v.tensor_tensor(y.S4[:, 2 + k, :], sel, RW[:, bass.ds(at, 2 * E)], ALU.mult)
                ins.then_inc(y.sem["sel_ready"], 1)

            def slot_weights(y, g):
                v.wait_ge(y.sem["spread_kept"], y.nth("spread_kept", g, 5))
                chain(v.tensor_tensor(y.TAG[:, 0, 1:3, :], y.WW[:, 1:3, :],
                                      sw[:, 0:1].unsqueeze(1).to_broadcast([P, 2, W]), ALU.mult))
                chain(v.tensor_tensor(y.WW[:, 1:3, :], y.WW[:, 1:3, :], y.TAG[:, 0, 1:3, :], ALU.subtract))

            def masks(y, g, it):
                for c in range(4):
                    v.wait_ge(y.sem["hid_gelu"], y.nth("hid_gelu", g, 5 * it + c + 2))
                    v.tensor_tensor(y.MH[:, 0, c, :], y.HG[:, c, :], y.MK[:, 0, c, :], ALU.mult)\
                        .then_inc(y.sem["masked0"], 1)

            def update1(y, g, it):
                TA, TG = y.TAG[:, 0], y.TAG[:, 1]
                v.tensor_scalar(y.ERR[:, :], y.IT[:, :], mu[:, 0:1], None, ALU.subtract).then_inc(own.sem, own.one())
                v.wait_ge(y.sem["steer_kept"], y.nth("steer_kept", g, 5 * it + 5))
                v.tensor_scalar(TA, TA, 0.5, 0.5, ALU.mult, ALU.add).then_inc(own.sem, own.one())
                chain(v.tensor_scalar(TG, TG, 0.05, 0.05, ALU.mult, ALU.add))
                v.tensor_tensor(TA, TA, wide(y.VT[:, :]), ALU.mult).then_inc(own.sem, own.one())
                v.wait_ge(y.sem["soft"], y.nth("soft", g, it + 1))
                chain(v.scalar_tensor_tensor(y.ZB.rearrange("p r q -> p (r q)"), y.ZB.rearrange("p r q -> p (r q)"), 0.0,
                                             y.AB.rearrange("p r q -> p (r q)"), ALU.max, ALU.add))
                chain(v.tensor_tensor(y.ZB, y.ZB, wide(y.ERR[:, :]), ALU.mult))

            def update2(y, g, it):
                TA, TG = y.TAG[:, 0], y.TAG[:, 1]
                chain(v.tensor_tensor(TA, TA, y.ZB, ALU.subtract))
                chain(v.tensor_tensor(TG, TG, TA, ALU.mult))
                chain(v.tensor_tensor(TG, TG, wide(y.IT[:, :]), ALU.add))
                chain(v.tensor_tensor(TG, TG, y.WW, ALU.mult))
                chain(v.tensor_tensor(y.XN[:, :], TG[:, 0, :], TG[:, 1, :], ALU.add))
                v.tensor_tensor(y.XN[:, :], y.XN[:, :], TG[:, 2, :], ALU.add).then_inc(y.sem["x_next"], 1)
                if it == 0:
                    chain(v.tensor_tensor(TA, TA, y.WW, ALU.mult))
                    chain(v.tensor_tensor(y.VT[:, :], TA[:, 0, :], TA[:, 1, :], ALU.add))
                    chain(v.tensor_tensor(y.VT[:, :], y.VT[:, :], TA[:, 2, :], ALU.add))

            def iterate(y, g, it):
                v.wait_ge(y.sem["halted"], y.nth("halted", g, it + 1))
                chain(v.tensor_scalar(y.TH[:, :], y.TH[:, :], 0.5, 0.5, ALU.mult, ALU.add))
                chain(v.scalar_tensor_tensor(y.TH[:, :], half(y.bank[3], 0), bf2[:, 0:1], y.TH[:, :], ALU.add, ALU.mult))
                own.restart()
                v.scalar_tensor_tensor(y.IT[:, :], y.TH[:, :], iw[:, 0:1], y.IT[:, :], ALU.mult, ALU.add)\
                    .then_inc(y.sem["it_done"], 1)
                v.wait_ge(y.sem["it_done"], y.nth("it_done", g, it + 1))

            def end(y, g):
                v.wait_ge(y.sem["end_turned"], y.nth("end_turned", g, 1))
                at = bass.ds((4 * g + 2 * y.x) * D, W)
                v.scalar_tensor_tensor(X[:, at], half(y.bank[0], 0), m.tg[:, 6:7], X[:, at], ALU.mult, ALU.add)\
                    .then_inc(own.sem, own.one())
                own.restart()
                for i in range(2):
                    tile = 4 * g + 2 * y.x + i
                    ins = v.bn_stats(m.st[:, bass.ds(tile, 1), :].rearrange("p a s -> p (a s)"),
                                     X[:, bass.ds(tile * D, D)])
                ins.then_inc(y.sem["done"], 1)

            def group(g, last=False):
                begin(st[1], g)
                slot_weights(st[0], g)
                masks(st[0], g, 0)
                slot_weights(st[1], g)
                own.restart()
                for k, (x, it) in list(enumerate(slots))[1:]:
                    z, zit = st[slots[k - 1][0]], slots[k - 1][1]
                    update1(z, g, zit)
                    masks(st[x], g, it)
                    update2(z, g, zit)
                    iterate(z, g, zit)
                end(st[0], g)
                if not last:
                    begin(st[0], g + 1)
                update1(st[1], g, 1)
                update2(st[1], g, 1)
                iterate(st[1], g, 1)
                end(st[1], g)
            begin(st[0], 0)
            own.restart()
            with v.Fori(0, NG - 1) as g:
                group(g)
            group(NG - 1, True)
            for y in st:
                v.wait_ge(y.sem["done"], NG + 1)

        def pool(q):
            with q.Fori(0, NG) as g:
                for x, it in slots:
                    y = st[x]
                    for c in range(4):
                        q.wait_ge(y.sem["hid_gelu"], y.nth("hid_gelu", g, 5 * it + c + 2))
                        q.tensor_tensor(y.MH[:, 1, c, :], y.HG[:, c, :], y.MK[:, 1, c, :], ALU.mult)\
                            .then_inc(y.sem["masked1"], 1)
        for k, f in (("pe", pe), ("act", act), ("dve", dve), ("pool", pool)):
            prog[k].append(f)
        for k in prog:
            for y in st:
                prog[k].append(lambda eng, y=y: eng.wait_ge(y.sem["done"], NG + 1))
        narrow_buffers()
        RB.again()
        IWT1 = RB.cut([P, 256]).bitcast(BF16)
        IWT2 = RB.cut([P, 256]).bitcast(BF16)
        AW = RB.cut([P, 2, 512])
        sums3, s3, r3 = RB.cut([P, 2]), RB.cut([P, 2]), RB.cut([P, 2])
        s_abs, s_total = sem("magnitudes_summed"), sem("magnitudes_totalled")

        prog["pe"].append(lambda p: p.wait_ge(s_wo, 16 * 8))

        def prep3(v):
            loaded(v, "layer3")
            v.wait_ge(s_pool3, 8)
            own = Own(v, m.own_dve)
            v.tensor_scalar(AW[:, :, :], nat3[:, :, :], -1.0, None, ALU.mult).then_inc(own.sem, own.one())
            v.wait_ge(own.sem, own.n)
            v.tensor_tensor(AW[:, :, :], AW[:, :, :], nat3[:, :, :], ALU.max).then_inc(own.sem, own.one())
            v.wait_ge(own.sem, own.n)
            v.tensor_reduce(sums3[:, :], AW[:, :, :], AX.X, ALU.add).then_inc(s_abs, 1)
            v.wait_ge(s_total, 1)
            v.tensor_scalar(s3[:, :], m.OPS[:, 0:2], 1.0 / (512 * D), 1e-5, ALU.mult, ALU.max).then_inc(own.sem, own.one())
            v.wait_ge(own.sem, own.n)
            v.reciprocal(r3[:, :], s3[:, :]).then_inc(own.sem, own.one())
            v.wait_ge(own.sem, own.n)
            v.tensor_tensor(nat3[:, :, :], nat3[:, :, :], r3[:, :].unsqueeze(2).to_broadcast([P, 2, 512]),
                                     ALU.mult).then_inc(own.sem, own.one())
            v.wait_ge(own.sem, own.n)
            v.tensor_scalar(nat3[:, :, :], nat3[:, :, :], MAGIC, MAGIC, ALU.add, ALU.subtract).then_inc(own.sem, own.one())
            v.wait_ge(own.sem, own.n)
            v.tensor_scalar(nat3[:, :, :], nat3[:, :, :], -1.0, 1.0, ALU.max, ALU.min).then_inc(own.sem, own.one())
            v.wait_ge(own.sem, own.n)
            v.tensor_scalar(s3[:, :], s3[:, :], 1.0 / 127.0, None, ALU.mult).then_inc(own.sem, own.one())
            v.wait_ge(own.sem, own.n)
            v.tensor_tensor(s3[:, 1:2], s3[:, 1:2], m.tg[:, 7:8], ALU.mult).then_inc(s_quant, 1)
            v.wait_ge(s_quant, n_q3)
            own.restart()

        def total3(p):
            loaded(p, "layer3")
            p.wait_ge(s_abs, 1)
            p.matmul(m.OPS[:, 0:2], m.ones[:, :], sums3[:, :], start=True, stop=True).then_inc(s_total, 1)
            p.wait_ge(s_quant, n_q3)
        n_q3 = m.n_quant = m.n_quant + 1
        prog["dve"].append(prep3)
        prog["pe"].append(total3)
        turn([nat3[:, 0, c * P:(c + 1) * P] for c in range(4)], (IWT1, lambda b: b))
        turn([nat3[:, 1, c * P:(c + 1) * P] for c in range(4)], (IWT2, lambda b: b))
        kept_weights()
        statistics(X, m.mv, m.rstd, 1e-5, ready=True)

        def masked_context(v, own, i, u):
            v.wait_ge(ev["xT"].sem, ev["xT"].base + i + 1)
            for e in range(E):
                ins = v.scalar_tensor_tensor(cmT[:, e, :], BK[:, bass.ds(i * P, P)], float(e), m.cT[:, :],
                                             ALU.is_equal, ALU.mult)
            ins.then_inc(ev["masked_ctx"].sem, 1)

        def k3_piece(p, bank, i, u):
            for e in range(E):
                ins = p.matmul(bank[:, 0:P], wk3[:, e, :], cmT[:, e, :], start=(e == 0), stop=(e == E - 1))
            return ins

        def v3_piece(p, bank, i, u):
            for e in range(E):
                ins = p.matmul(bank[:, 0:P], cmT[:, e, :], wv3[:, e, :], start=(e == 0), stop=(e == E - 1))
            return ins

        def v3_keep(s, spread_v, bank, u):
            return spread_v(lambda dst, src, h, b: s.activation(dst, src, ACT.Copy), bank, u)
        run(Attention(heads="narrow", ctx="load", cx_base=next_ctx(), scale=float(1 / np.sqrt(np.float32(8))),
                      extra=["masked_ctx"], dve_front=masked_context,
                      mask=lambda i: kt3[:, bass.ds(i, 1), :].unsqueeze(1),
                      pieces=[dict(pe=one(wq3, m.xT), act=to_buffer(m.QB[:, :])),
                              dict(pe=k3_piece, act=to_buffer(m.KB[:, :]), needs=["masked_ctx"]),
                              dict(pe=v3_piece, act=v3_keep)],
                      w_out=wo3, normalise=normalise(X), finish=finish_biased(3, bo3), out=X))
        barrier()

        statistics(X, m.mv, m.rstd, 1e-5, ready=True)
        bits = {n: sem("ternary_" + n) for n in ("rows_quantised", "rows_turned", "rows_kept", "up", "hidden",
                                                 "hidden_quantised", "hidden_turned", "hidden_kept", "down", "done")}
        WORK.again()
        XQ = WORK.cut([P, NT, D])
        HQ = WORK.cut([P, 2, 2, 512])
        XQT = RB.cut([P, P]).bitcast(BF16)
        HQT = RB.cut([P, 512]).bitcast(BF16)
        sx = RB.cut([P, 3, NT])
        sh = RB.cut([P, 2, 5, 2])
        NP = NT // 2

        def eight_bits(v, own, x, hi, lo, inv, sc, s):
            def then(ins):
                ins.then_inc(own.sem, own.one())
                v.wait_ge(own.sem, own.n)
            v.tensor_reduce(hi, x, AX.X, ALU.max).then_inc(own.sem, own.one())
            then(v.tensor_reduce(lo, x, AX.X, ALU.min))
            then(v.scalar_tensor_tensor(hi, lo, -1.0, hi, ALU.mult, ALU.max))
            then(v.tensor_scalar(hi, hi, 1e-5, None, ALU.max))
            v.tensor_scalar(sc, hi, s, None, ALU.mult).then_inc(own.sem, own.one())
            then(v.reciprocal(inv, hi))
            then(v.tensor_scalar(inv, inv, 127.0, None, ALU.mult))

        def pe(p):
            def step(n, u, on):
                if on[1]:
                    t = n + 1
                    p.wait_ge(bits["rows_quantised"], t + 1)
                    if some(t):
                        p.wait_ge(bits["rows_kept"], t)
                    for i in range(2):
                        ins = p.transpose(m.TPS[:, i * P:(i + 1) * P], XR[:, i, :], m.ident[:, :])
                    ins.then_inc(bits["rows_turned"], 1)
                if on[0]:
                    t = n
                    p.wait_ge(bits["hidden_quantised"], t + 1)
                    if some(t):
                        p.wait_ge(bits["hidden_kept"], t)
                    for i in range(2):
                        for c in range(4):
                            ins = p.transpose(m.PS[:, i * 512 + c * P:i * 512 + (c + 1) * P],
                                              HQ[:, u, i, c * P:(c + 1) * P], m.ident[:, :])
                    ins.then_inc(bits["hidden_turned"], 1)
                if on[1]:
                    t = n + 1
                    p.wait_ge(bits["rows_kept"], t + 1)
                    if some(t):
                        p.wait_ge(bits["hidden"], t)
                    for i in range(2):
                        ins = p.matmul(m.RING[:, i * 512:i * 512 + 512], XQT[:, i * P:(i + 1) * P], IWT1,
                                       start=True, stop=True)
                    ins.then_inc(bits["up"], 1)
                if on[0]:
                    t = n
                    p.wait_ge(bits["hidden_kept"], t + 1)
                    if some(t):
                        p.wait_ge(bits["done"], t)
                    for i in range(2):
                        for c in range(4):
                            ins = p.matmul(m.OPS[:, i * D:(i + 1) * D], HQT[:, i * 512 + c * P:i * 512 + (c + 1) * P],
                                           IWT2[:, c * P:(c + 1) * P], start=(c == 0), stop=(c == 3))
                    ins.then_inc(bits["down"], 1)
            pipeline(p, None, step, NP)

        def act(s):
            def step(n, u, on):
                if on[1]:
                    t = n + 1
                    s.wait_ge(bits["rows_turned"], t + 1)
                    if some(t):
                        s.wait_ge(bits["up"], t)
                    s.activation(XQT, m.TPS[:, 0:2 * P], ACT.Copy).then_inc(bits["rows_kept"], 1)
                if on[0]:
                    s.wait_ge(bits["hidden_turned"], n + 1)
                    if some(n):
                        s.wait_ge(bits["down"], n)
                    s.activation(HQT, m.PS[:, :], ACT.Copy).then_inc(bits["hidden_kept"], 1)
                if on[1]:
                    t, w = n + 1, 1 - u
                    s.wait_ge(bits["up"], t + 1)
                    if some(t - 1):
                        s.wait_ge(bits["hidden_turned"], t - 1)
                    for i in range(2):
                        ins = s.activation(HQ[:, w, i, :], m.RING[:, i * 512:i * 512 + 512], ACT.Gelu,
                                           scale=sh[:, w, 4, i:i + 1])
                    ins.then_inc(bits["hidden"], 1)
            pipeline(s, None, step, NP)

        def dve(v):
            own = Own(v, m.own_dve)
            for t in range(NT):
                norm_tile(v, XQ[:, t, :], X, t, mv2, m.rstd).then_inc(own.sem, own.one())
            v.wait_ge(own.sem, own.n)
            hi, lo, sc = sx[:, 0, :], sx[:, 1, :], sx[:, 2, :]
            eight_bits(v, own, XQ[:, :, :], hi, lo, lo, sc, s3[:, 0:1])
            own.restart()

            def step(n, u, on):
                if on[2]:
                    t = n + 2
                    if some(t):
                        v.wait_ge(bits["rows_turned"], t)
                    if some(t - 1):
                        v.wait_ge(bits["hidden"], t - 1)
                    v.tensor_scalar(sh[:, u, 4, :], sc[:, bass.ds(2 * t, 2)], 1.0, None, ALU.mult)\
                        .then_inc(own.sem, own.one())
                    for i in range(2):
                        x = XQ[:, bass.ds(2 * t + i, 1), :].rearrange("p a d -> p (a d)")
                        v.tensor_scalar(XR[:, i, :], x, lo[:, bass.ds(2 * t + i, 1)], MAGIC, ALU.mult, ALU.add)\
                            .then_inc(own.sem, own.one())
                    v.wait_ge(own.sem, own.n)
                    v.tensor_scalar(XR[:, :, :], XR[:, :, :], MAGIC, -128.0, ALU.subtract, ALU.max).then_inc(own.sem, own.one())
                    v.wait_ge(own.sem, own.n)
                    v.tensor_scalar(XR[:, :, :], XR[:, :, :], 127.0, None, ALU.min).then_inc(bits["rows_quantised"], 1)
                if on[1]:
                    w = 1 - u
                    v.wait_ge(bits["hidden"], n + 2)
                    h = HQ[:, w]
                    eight_bits(v, own, h, sh[:, w, 0, :], sh[:, w, 1, :], sh[:, w, 2, :], sh[:, w, 3, :], s3[:, 1:2])
                    for i in range(2):
                        v.tensor_scalar(h[:, i, :], h[:, i, :], sh[:, w, 2, i:i + 1], MAGIC, ALU.mult, ALU.add)\
                            .then_inc(own.sem, own.one())
                    v.wait_ge(own.sem, own.n)
                    v.tensor_scalar(h, h, MAGIC, -128.0, ALU.subtract, ALU.max).then_inc(own.sem, own.one())
                    v.wait_ge(own.sem, own.n)
                    v.tensor_scalar(h, h, 127.0, None, ALU.min).then_inc(bits["hidden_quantised"], 1)
                if on[0]:
                    v.wait_ge(bits["down"], n + 1)
                    for i in range(2):
                        at = bass.ds((2 * n + i) * D, D)
                        ins = v.scalar_tensor_tensor(X[:, at], m.OPS[:, i * D:(i + 1) * D], sh[:, u, 3, i:i + 1], X[:, at],
                                                     ALU.mult, ALU.add)
                    ins.then_inc(bits["done"], 1)
            pipeline(v, own, step, NP)
        XR = RB.cut([P, 2, D])
        for k, f in (("pe", pe), ("act", act), ("dve", dve)):
            prog[k].append(f)
        for k in prog:
            prog[k].append(lambda eng: eng.wait_ge(bits["done"], NP))
        def store(q):
            q.dma_start(out.rearrange("(t b) s d -> (b s) t d", b=TILE_B), X[:, :].rearrange("p (t d) -> p t d", d=D))\
                .then_inc(s_stored, 16)
            q.wait_ge(s_stored, 16)
        prog["sp"].append(store)

        block = ctx.enter_context(nc.Block())

        @block.sync
        def _(eng):
            for f in prog["sp"]:
                f(eng)

        @block.scalar
        def _(eng):
            for f in prog["act"]:
                f(eng)

        @block.vector
        def _(eng):
            for f in prog["dve"]:
                f(eng)

        @block.gpsimd
        def _(eng):
            for f in prog["pool"]:
                f(eng)

        @block.tensor
        def _(eng):
            for f in prog["pe"]:
                f(eng)


def kernel(**inputs):
    import concourse.bacc as _bacc
    from concourse.bass_utils import run_bass_kernel_spmd as _run

    nc = _bacc.Bacc("TRN2", target_bir_lowering=False, num_devices=1)
    arrays, aps = {}, {}
    given = {name: np.ascontiguousarray(a) for name, a in inputs.items()}
    given.update({"const_" + name: a for name, a in CONST.items()})
    for name, a in given.items():
        if a.dtype == np.bool_:
            a = a.view(np.int32)
        if a.ndim == 0:
            a = a.reshape(1)
        arrays[f"in_{name}"] = a
        aps[name] = nc.dram_tensor(f"in_{name}", a.shape, mybir.dt.from_np(a.dtype), kind="ExternalInput").ap()
    out = nc.dram_tensor("out_x", (B, S, D), F32, kind="ExternalOutput").ap()
    program(nc, aps, out)
    r = _run(nc, [arrays], core_ids=[0])
    return r.results[0]["out_x"]
```
